# Optimizing a Trainium2 kernel written in Bass

```python
import numpy as np
import jax
import jax.numpy as jnp

def _softmax(x, axis=-1):
    return jax.nn.softmax(x, axis=axis)

def _gelu(x):
    return jax.nn.gelu(x, approximate=True)

def _silu(x):
    return jax.nn.silu(x)

def _sigmoid(x):
    return jax.nn.sigmoid(x)

def _layernorm(x, axis=-1, eps=1e-05):
    m = jnp.mean(x, axis=axis, keepdims=True)
    v = jnp.var(x, axis=axis, keepdims=True)
    return (x - m) / jnp.sqrt(v + eps)

def _scatter_add(tgt, idx, src, axis=0):
    return tgt.at[idx].add(src)

def _segment_sum(src, seg, n):
    return jax.ops.segment_sum(src, seg, n)
kernel_name = 'mk_gps_d2_gnn_r16_dc8b11'

def setup_inputs(seed: int=0):
    np.random.seed(seed)
    _w = jnp.asarray

    def _rec_inputs():
        import jax
        import jax.numpy as jnp
        _gk = jax.random.key(seed)
        x = -0.0003713 + 1 * jax.random.normal(jax.random.fold_in(_gk, 1), (6250, 256), jnp.float32)
        _s = jax.random.randint(jax.random.fold_in(_gk, 2), (50000,), 0, 6250, jnp.int32)
        _d = jax.random.randint(jax.random.fold_in(_gk, 3), (50000,), 0, 6250, jnp.int32)
        _loop = jnp.arange(6250, dtype=jnp.int32)
        src = jnp.concatenate([_s, _d, _loop])
        dst = jnp.concatenate([_d, _s, _loop])
        _o = jnp.argsort(dst, stable=True)
        src = src[_o]
        dst = dst[_o]
        edge_attr_4 = 0.00117183 + 1.0004 * jax.random.normal(jax.random.fold_in(_gk, 12), (106250, 4), jnp.float32)
        edge_attr_8 = -0.000615933 + 0.999959 * jax.random.normal(jax.random.fold_in(_gk, 13), (106250, 8), jnp.float32)
        node_vec1 = jax.random.uniform(jax.random.fold_in(_gk, 15), (6250, 1), jnp.float32, 0.0, 1)
        return (x, src, dst, edge_attr_4, edge_attr_8, node_vec1)
    x, src, dst, edge_attr_4, edge_attr_8, node_vec1 = _rec_inputs()

    def _L0_gnn_setup():
        import jax, jax.numpy as jnp
        import numpy as np
        N_NODES = 3125
        N_EDGES = 50000
        DIM_IN = 256
        HEADS = 4
        DIM_OUT = 64
        NEG_SLOPE = 0.2
        key = jax.random.key(seed)
        k_x, k_e, k_w, k_as, k_ad = jax.random.split(key, 5)
        glorot = (6.0 / (DIM_IN + HEADS * DIM_OUT)) ** 0.5
        return {'x': jax.random.normal(k_x, (N_NODES, DIM_IN), dtype=jnp.float32), 'W': jax.random.uniform(k_w, (DIM_IN, HEADS * DIM_OUT), dtype=jnp.float32, minval=-glorot, maxval=glorot), 'att_src': jax.random.normal(k_as, (HEADS, DIM_OUT), dtype=jnp.float32) * 0.1, 'att_dst': jax.random.normal(k_ad, (HEADS, DIM_OUT), dtype=jnp.float32) * 0.1, 'bias': jnp.zeros((HEADS * DIM_OUT,), dtype=jnp.float32), 'edge_index': jax.random.randint(k_e, (2, N_EDGES), 0, N_NODES, dtype=jnp.int64)}
    _L0_gnn_all = _L0_gnn_setup()
    _L0_gnn_in = {k: v for k, v in _L0_gnn_all.items() if k in ('W', 'att_src', 'att_dst', 'bias')}
    del _L0_gnn_all

    def _L0_mix_setup():
        import jax, jax.numpy as jnp
        import numpy as np
        MIDC = 256
        HEADS = 8
        HEADC = MIDC // HEADS
        EPS = 1e-05

        def _ln(x, gamma, beta):
            mu = jnp.mean(x, axis=-1, keepdims=True)
            var = jnp.var(x, axis=-1, keepdims=True)
            return (x - mu) * jax.lax.rsqrt(var + EPS) * gamma + beta
        key = jax.random.key(seed)
        ks = jax.random.split(key, 8)
        B, HW, C = (8, 256, MIDC)
        s = 1.0 / np.sqrt(C)
        return {'x': jax.random.normal(ks[0], (B, HW, C), jnp.float32), 'w_qkv': jax.random.normal(ks[1], (C, 3 * C), jnp.float32) * s, 'b_qkv': jnp.zeros((3 * C,), jnp.float32), 'kln_g': jnp.ones((HEADC,), jnp.float32), 'kln_b': jnp.zeros((HEADC,), jnp.float32), 'vln_g': jnp.ones((HEADC,), jnp.float32), 'vln_b': jnp.zeros((HEADC,), jnp.float32), 'w1': jax.random.normal(ks[2], (C, C), jnp.float32) * s, 'b1': jnp.zeros((C,), jnp.float32), 'w2': jax.random.normal(ks[3], (C, C), jnp.float32) * s, 'b2': jnp.zeros((C,), jnp.float32)}
    _L0_mix_all = _L0_mix_setup()
    _L0_mix_in = {k: v for k, v in _L0_mix_all.items() if k in ('w_qkv', 'b_qkv', 'kln_g', 'kln_b', 'vln_g', 'vln_b', 'w1', 'b1', 'w2', 'b2')}
    del _L0_mix_all

    def _L0_ffn_setup():
        import math
        import jax, jax.numpy as jnp
        import numpy as np
        CAPACITY_FACTOR = 1.25
        TOP_K = 2
        LN_EPS = 1e-05

        def _layer_norm(x, gamma, beta):
            mu = jnp.mean(x, axis=-1, keepdims=True)
            var = jnp.var(x, axis=-1, keepdims=True)
            return (x - mu) * jax.lax.rsqrt(var + LN_EPS) * gamma + beta
        key = jax.random.key(seed)
        ks = jax.random.split(key, 4)
        B, S, D, F, E = (8, 256, 256, 512, 8)
        x = jax.random.normal(ks[0], (B, S, D), dtype=jnp.float32)
        Wr = jax.random.normal(ks[1], (D, E), dtype=jnp.float32) / np.sqrt(D)
        br = jnp.zeros((E,), jnp.float32)
        W1 = jax.random.normal(ks[2], (E, D, F), dtype=jnp.float32) / np.sqrt(D)
        b1 = jnp.zeros((E, F), jnp.float32)
        W2 = jax.random.normal(ks[3], (E, F, D), dtype=jnp.float32) / np.sqrt(F)
        b2 = jnp.zeros((E, D), jnp.float32)
        gamma = jnp.ones((D,), jnp.float32)
        beta = jnp.zeros((D,), jnp.float32)
        return {'x': x, 'Wr': Wr, 'br': br, 'W1': W1, 'b1': b1, 'W2': W2, 'b2': b2, 'gamma': gamma, 'beta': beta}
    _L0_ffn_all = _L0_ffn_setup()
    _L0_ffn_in = {k: v for k, v in _L0_ffn_all.items() if k in ('Wr', 'br', 'W1', 'b1', 'W2', 'b2', 'gamma', 'beta')}
    del _L0_ffn_all

    def _L1_gnn_setup():
        import jax, jax.numpy as jnp
        import numpy as np
        import math
        N = 1875
        E = 37500
        MUL = 64
        NES = 8
        FCN = 64
        NUM_NEIGHBORS = 20.0
        SILU_NORM = 1.679
        INV_SQRT3 = 1.0 / math.sqrt(3.0)

        def _split(x):
            return (x[:, :MUL], x[:, MUL:].reshape(-1, MUL, 3))
        key = jax.random.key(seed)
        ks = jax.random.split(key, 16)
        inp = {'node_input': jax.random.normal(ks[0], (N, 4 * MUL), jnp.float32), 'node_attr': jnp.ones((N, 1), jnp.float32), 'edge_src': jax.random.randint(ks[1], (E,), 0, N), 'edge_dst': jax.random.randint(ks[2], (E,), 0, N), 'edge_attr': jax.random.normal(ks[3], (E, 4), jnp.float32), 'edge_scalars': jax.random.normal(ks[4], (E, NES), jnp.float32), 'sc_w0': jax.random.normal(ks[5], (MUL, MUL), jnp.float32), 'sc_w1': jax.random.normal(ks[6], (MUL, MUL), jnp.float32), 'lin1_w0': jax.random.normal(ks[7], (MUL, MUL), jnp.float32), 'lin1_w1': jax.random.normal(ks[8], (MUL, MUL), jnp.float32), 'fc_w1': jax.random.normal(ks[9], (NES, FCN), jnp.float32), 'fc_w2': jax.random.normal(ks[10], (FCN, 4 * MUL), jnp.float32), 'lin2_w00': jax.random.normal(ks[11], (MUL, MUL), jnp.float32), 'lin2_w01': jax.random.normal(ks[12], (MUL, MUL), jnp.float32), 'lin2_w10': jax.random.normal(ks[13], (MUL, MUL), jnp.float32), 'lin2_w11': jax.random.normal(ks[14], (MUL, MUL), jnp.float32)}
        return inp
    _L1_gnn_all = _L1_gnn_setup()
    _L1_gnn_in = {k: v for k, v in _L1_gnn_all.items() if k in ('sc_w0', 'sc_w1', 'lin1_w0', 'lin1_w1', 'fc_w1', 'fc_w2', 'lin2_w00', 'lin2_w01', 'lin2_w10', 'lin2_w11')}
    del _L1_gnn_all

    def _L1_mix_setup():
        import jax, jax.numpy as jnp
        import numpy as np
        HEADS = 8
        DIM_HEAD = 64
        EPS = 1e-05

        def _inst_norm_lastdim(t):
            mu = jnp.mean(t, axis=-1, keepdims=True)
            var = jnp.mean(jnp.square(t - mu), axis=-1, keepdims=True)
            return (t - mu) * jax.lax.rsqrt(var + EPS)
        key = jax.random.key(seed)
        k1, k2, k3, k4 = jax.random.split(key, 4)
        b, n, dim = (4, 512, 256)
        inner = HEADS * DIM_HEAD
        x = jax.random.normal(k1, (b, n, dim), dtype=jnp.float32)
        Wqkv = jax.random.normal(k2, (3 * inner, dim), dtype=jnp.float32) * (1.0 / np.sqrt(dim))
        Wout = jax.random.normal(k3, (dim, inner), dtype=jnp.float32) * (1.0 / np.sqrt(inner))
        bout = jax.random.normal(k4, (dim,), dtype=jnp.float32) * 0.01
        return {'x': x, 'Wqkv': Wqkv, 'Wout': Wout, 'bout': bout}
    _L1_mix_all = _L1_mix_setup()
    _L1_mix_in = {k: v for k, v in _L1_mix_all.items() if k in ('Wqkv', 'Wout', 'bout')}
    del _L1_mix_all

    def _L1_ffn_setup():
        import jax, jax.numpy as jnp
        import numpy as np
        B, S, D = (8, 256, 256)
        H = 4 * D
        CAPACITY = 0.5
        key = jax.random.key(seed)
        ks = jax.random.split(key, 6)
        x = jax.random.normal(ks[0], (B, S, D), dtype=jnp.float32)
        attention_mask = jnp.zeros((B, 1, 1, S), dtype=jnp.float32)
        wr = jax.random.normal(ks[1], (D, 1), dtype=jnp.float32) * 0.02
        br = jnp.zeros((1,), dtype=jnp.float32)
        w1 = jax.random.normal(ks[2], (D, H), dtype=jnp.float32) * 0.02
        b1 = jnp.zeros((H,), dtype=jnp.float32)
        w2 = jax.random.normal(ks[3], (H, D), dtype=jnp.float32) * 0.02
        b2 = jnp.zeros((D,), dtype=jnp.float32)
        return {'x': x, 'attention_mask': attention_mask, 'wr': wr, 'br': br, 'w1': w1, 'b1': b1, 'w2': w2, 'b2': b2}
    _L1_ffn_all = _L1_ffn_setup()
    _L1_ffn_in = {k: v for k, v in _L1_ffn_all.items() if k in ('attention_mask', 'wr', 'br', 'w1', 'b1', 'w2', 'b2')}
    del _L1_ffn_all
    return {'x': x, 'src': src, 'dst': dst, 'edge_attr_4': edge_attr_4, 'edge_attr_8': edge_attr_8, 'node_vec1': node_vec1, 'L0_gnn_W': _L0_gnn_in['W'], 'L0_gnn_att_src': _L0_gnn_in['att_src'], 'L0_gnn_att_dst': _L0_gnn_in['att_dst'], 'L0_gnn_bias': _L0_gnn_in['bias'], 'L0_mix_w_qkv': _L0_mix_in['w_qkv'], 'L0_mix_b_qkv': _L0_mix_in['b_qkv'], 'L0_mix_kln_g': _L0_mix_in['kln_g'], 'L0_mix_kln_b': _L0_mix_in['kln_b'], 'L0_mix_vln_g': _L0_mix_in['vln_g'], 'L0_mix_vln_b': _L0_mix_in['vln_b'], 'L0_mix_w1': _L0_mix_in['w1'], 'L0_mix_b1': _L0_mix_in['b1'], 'L0_mix_w2': _L0_mix_in['w2'], 'L0_mix_b2': _L0_mix_in['b2'], 'L0_ffn_Wr': _L0_ffn_in['Wr'], 'L0_ffn_br': _L0_ffn_in['br'], 'L0_ffn_W1': _L0_ffn_in['W1'], 'L0_ffn_b1': _L0_ffn_in['b1'], 'L0_ffn_W2': _L0_ffn_in['W2'], 'L0_ffn_b2': _L0_ffn_in['b2'], 'L0_ffn_gamma': _L0_ffn_in['gamma'], 'L0_ffn_beta': _L0_ffn_in['beta'], 'L1_gnn_sc_w0': _L1_gnn_in['sc_w0'], 'L1_gnn_sc_w1': _L1_gnn_in['sc_w1'], 'L1_gnn_lin1_w0': _L1_gnn_in['lin1_w0'], 'L1_gnn_lin1_w1': _L1_gnn_in['lin1_w1'], 'L1_gnn_fc_w1': _L1_gnn_in['fc_w1'], 'L1_gnn_fc_w2': _L1_gnn_in['fc_w2'], 'L1_gnn_lin2_w00': _L1_gnn_in['lin2_w00'], 'L1_gnn_lin2_w01': _L1_gnn_in['lin2_w01'], 'L1_gnn_lin2_w10': _L1_gnn_in['lin2_w10'], 'L1_gnn_lin2_w11': _L1_gnn_in['lin2_w11'], 'L1_mix_Wqkv': _L1_mix_in['Wqkv'], 'L1_mix_Wout': _L1_mix_in['Wout'], 'L1_mix_bout': _L1_mix_in['bout'], 'L1_ffn_attention_mask': _L1_ffn_in['attention_mask'], 'L1_ffn_wr': _L1_ffn_in['wr'], 'L1_ffn_br': _L1_ffn_in['br'], 'L1_ffn_w1': _L1_ffn_in['w1'], 'L1_ffn_b1': _L1_ffn_in['b1'], 'L1_ffn_w2': _L1_ffn_in['w2'], 'L1_ffn_b2': _L1_ffn_in['b2']}

def reference(x, src, dst, edge_attr_4, edge_attr_8, node_vec1, L0_gnn_W, L0_gnn_att_src, L0_gnn_att_dst, L0_gnn_bias, L0_mix_w_qkv, L0_mix_b_qkv, L0_mix_kln_g, L0_mix_kln_b, L0_mix_vln_g, L0_mix_vln_b, L0_mix_w1, L0_mix_b1, L0_mix_w2, L0_mix_b2, L0_ffn_Wr, L0_ffn_br, L0_ffn_W1, L0_ffn_b1, L0_ffn_W2, L0_ffn_b2, L0_ffn_gamma, L0_ffn_beta, L1_gnn_sc_w0, L1_gnn_sc_w1, L1_gnn_lin1_w0, L1_gnn_lin1_w1, L1_gnn_fc_w1, L1_gnn_fc_w2, L1_gnn_lin2_w00, L1_gnn_lin2_w01, L1_gnn_lin2_w10, L1_gnn_lin2_w11, L1_mix_Wqkv, L1_mix_Wout, L1_mix_bout, L1_ffn_attention_mask, L1_ffn_wr, L1_ffn_br, L1_ffn_w1, L1_ffn_b1, L1_ffn_w2, L1_ffn_b2):
    import jax
    import jax.numpy as jnp

    def _L0_gnn_ref(x, W, att_src, att_dst, bias, edge_index):
        import jax, jax.numpy as jnp
        import numpy as np
        N_NODES = 3125
        N_EDGES = 50000
        DIM_IN = 256
        HEADS = 4
        DIM_OUT = 64
        NEG_SLOPE = 0.2
        N = x.shape[0]
        H, C = att_src.shape
        loops = jnp.arange(N, dtype=edge_index.dtype)
        src = jnp.concatenate([edge_index[0], loops])
        dst = jnp.concatenate([edge_index[1], loops])
        h = (x @ W).reshape(N, H, C)
        a_src = jnp.einsum('nhc,hc->nh', h, att_src)
        a_dst = jnp.einsum('nhc,hc->nh', h, att_dst)
        e = jax.nn.leaky_relu(a_src[src] + a_dst[dst], NEG_SLOPE)
        e_max = jax.ops.segment_max(e, dst, num_segments=N)
        e_exp = jnp.exp(e - e_max[dst])
        e_sum = jax.ops.segment_sum(e_exp, dst, num_segments=N)
        alpha = e_exp / (e_sum[dst] + 1e-16)
        out = jax.ops.segment_sum(h[src] * alpha[:, :, None], dst, num_segments=N)
        return out.reshape(N, H * C) + bias

    def _L0_mix_ref(x, w_qkv, b_qkv, kln_g, kln_b, vln_g, vln_b, w1, b1, w2, b2):
        import jax, jax.numpy as jnp
        import numpy as np
        MIDC = 256
        HEADS = 8
        HEADC = MIDC // HEADS
        EPS = 1e-05

        def _ln(x, gamma, beta):
            mu = jnp.mean(x, axis=-1, keepdims=True)
            var = jnp.var(x, axis=-1, keepdims=True)
            return (x - mu) * jax.lax.rsqrt(var + EPS) * gamma + beta
        B, HW, C = x.shape
        bias = x
        qkv = (x @ w_qkv + b_qkv).reshape(B, HW, HEADS, 3 * HEADC)
        qkv = qkv.transpose(0, 2, 1, 3)
        q, k, v = jnp.split(qkv, 3, axis=-1)
        k = _ln(k, kln_g, kln_b)
        v = _ln(v, vln_g, vln_b)
        kv = jnp.einsum('bhnd,bhne->bhde', k, v) / HW
        out = jnp.einsum('bhnd,bhde->bhne', q, kv)
        out = out.transpose(0, 2, 1, 3).reshape(B, HW, C)
        ret = out + bias
        h = jax.nn.gelu(ret @ w1 + b1, approximate=False)
        return h @ w2 + b2 + bias

    def _L0_ffn_ref(x, Wr, br, W1, b1, W2, b2, gamma, beta):
        import math
        import jax, jax.numpy as jnp
        import numpy as np
        CAPACITY_FACTOR = 1.25
        TOP_K = 2
        LN_EPS = 1e-05

        def _layer_norm(x, gamma, beta):
            mu = jnp.mean(x, axis=-1, keepdims=True)
            var = jnp.var(x, axis=-1, keepdims=True)
            return (x - mu) * jax.lax.rsqrt(var + LN_EPS) * gamma + beta
        B, S, D = x.shape
        E = Wr.shape[1]
        N = B * S
        K = TOP_K
        logits = jnp.mean(x, axis=1) @ Wr + br
        routing_weights = jax.nn.softmax(logits, axis=-1)
        capacity = float(math.ceil(N * CAPACITY_FACTOR / E))
        expected_loads = routing_weights.sum(axis=0) * (N / B)
        scale = jnp.where(expected_loads > capacity, capacity / expected_loads, 1.0)
        routing_weights = jax.nn.softmax(routing_weights * scale, axis=-1)
        rw_tok = jnp.broadcast_to(routing_weights[:, None, :], (B, S, E)).reshape(N, E)
        top_w, top_i = jax.lax.top_k(rw_tok, K)
        top_w = jax.nn.softmax(top_w, axis=-1)
        xf = x.reshape(N, D)
        h = jax.nn.gelu(jnp.einsum('nd,edf->enf', xf, W1) + b1[:, None, :], approximate=False)
        y = jnp.einsum('enf,efd->end', h, W2) + b2[:, None, :]
        w_dense = jnp.zeros((N, E), x.dtype).at[jnp.arange(N)[:, None], top_i].add(top_w)
        out = jnp.einsum('ne,end->nd', w_dense, y).reshape(B, S, D)
        out = _layer_norm(out + x, gamma, beta)
        return out

    def _L1_gnn_ref(node_input, node_attr, edge_src, edge_dst, edge_attr, edge_scalars, sc_w0, sc_w1, lin1_w0, lin1_w1, fc_w1, fc_w2, lin2_w00, lin2_w01, lin2_w10, lin2_w11):
        import jax, jax.numpy as jnp
        import numpy as np
        import math
        N = 1875
        E = 37500
        MUL = 64
        NES = 8
        FCN = 64
        NUM_NEIGHBORS = 20.0
        SILU_NORM = 1.679
        INV_SQRT3 = 1.0 / math.sqrt(3.0)

        def _split(x):
            return (x[:, :MUL], x[:, MUL:].reshape(-1, MUL, 3))
        n = node_input.shape[0]
        inv_mul = 1.0 / math.sqrt(MUL)
        x0, x1 = _split(node_input)
        a = node_attr
        s0 = x0 @ sc_w0 * a * inv_mul
        s1 = jnp.einsum('nuc,uv->nvc', x1, sc_w1) * a[:, :, None] * inv_mul
        y0 = x0 @ lin1_w0 * a * inv_mul
        y1 = jnp.einsum('nuc,uv->nvc', x1, lin1_w1) * a[:, :, None] * inv_mul
        h = jax.nn.silu(edge_scalars @ fc_w1 * (1.0 / math.sqrt(NES))) * SILU_NORM
        w = h @ fc_w2 * (1.0 / math.sqrt(FCN))
        w_a, w_b, w_c, w_d = (w[:, :MUL], w[:, MUL:2 * MUL], w[:, 2 * MUL:3 * MUL], w[:, 3 * MUL:])
        xg0 = y0[edge_src]
        xg1 = y1[edge_src]
        ea0 = edge_attr[:, :1]
        ea1 = edge_attr[:, 1:4]
        mid0 = w_a * xg0 * ea0
        mid1 = w_b * jnp.einsum('euc,ec->eu', xg1, ea1) * INV_SQRT3
        mid2 = (w_c * xg0)[:, :, None] * ea1[:, None, :]
        mid3 = (w_d * ea0)[:, :, None] * xg1
        mids = jnp.concatenate([mid0, mid1, mid2.reshape(-1, 3 * MUL), mid3.reshape(-1, 3 * MUL)], axis=1)
        agg = jax.ops.segment_sum(mids, edge_dst, num_segments=n)
        agg = agg * (1.0 / math.sqrt(NUM_NEIGHBORS))
        z0a = agg[:, :MUL]
        z0b = agg[:, MUL:2 * MUL]
        z1a = agg[:, 2 * MUL:5 * MUL].reshape(n, MUL, 3)
        z1b = agg[:, 5 * MUL:].reshape(n, MUL, 3)
        inv2 = 1.0 / math.sqrt(2 * MUL)
        o0 = (z0a @ lin2_w00 + z0b @ lin2_w01) * a * inv2
        o1 = (jnp.einsum('nuc,uv->nvc', z1a, lin2_w10) + jnp.einsum('nuc,uv->nvc', z1b, lin2_w11)) * a[:, :, None] * inv2
        c_s = math.sin(math.pi / 8.0)
        c_x = math.cos(math.pi / 8.0)
        out0 = c_s * s0 + c_x * o0
        out1 = c_s * s1 + c_x * o1
        return jnp.concatenate([out0, out1.reshape(n, 3 * MUL)], axis=1)

    def _L1_mix_ref(x, Wqkv, Wout, bout):
        import jax, jax.numpy as jnp
        import numpy as np
        HEADS = 8
        DIM_HEAD = 64
        EPS = 1e-05

        def _inst_norm_lastdim(t):
            mu = jnp.mean(t, axis=-1, keepdims=True)
            var = jnp.mean(jnp.square(t - mu), axis=-1, keepdims=True)
            return (t - mu) * jax.lax.rsqrt(var + EPS)
        b, n, dim = x.shape
        qkv = jnp.einsum('bnc,fc->bnf', x, Wqkv)
        q, k, v = jnp.split(qkv, 3, axis=-1)

        def to_heads(t):
            return t.reshape(b, n, HEADS, DIM_HEAD).transpose(0, 2, 1, 3)
        q, k, v = (to_heads(q), to_heads(k), to_heads(v))
        k = _inst_norm_lastdim(k)
        v = _inst_norm_lastdim(v)
        dots = jnp.einsum('bhnd,bhne->bhde', k, v)
        out = jnp.einsum('bhnd,bhde->bhne', q, dots) / n
        out = out.transpose(0, 2, 1, 3).reshape(b, n, HEADS * DIM_HEAD)
        return jnp.einsum('bnf,cf->bnc', out, Wout) + bout

    def _L1_ffn_ref(x, attention_mask, wr, br, w1, b1, w2, b2):
        import jax, jax.numpy as jnp
        import numpy as np
        B, S, D = (8, 256, 256)
        H = 4 * D
        CAPACITY = 0.5
        b, s, d = x.shape
        weights = (jnp.einsum('bsd,do->bso', x, wr) + br)[..., 0]
        k = max(1, int(CAPACITY * s))
        kk = k - 1 if k > 1 else 1
        _, idx = jax.lax.top_k(weights, k)
        sel_idx = idx[:, :kk]
        sel = jnp.take_along_axis(x, sel_idx[:, :, None], axis=1)
        h = jax.nn.gelu(jnp.einsum('bkd,dh->bkh', sel, w1) + b1)
        y = jnp.einsum('bkh,hd->bkd', h, w2) + b2
        w_sel = jnp.take_along_axis(weights, sel_idx, axis=1)
        y = y * w_sel[..., None]
        batch_idx = jnp.arange(b)[:, None]
        processed = jnp.zeros_like(x).at[batch_idx, sel_idx].set(y)
        return processed + x
    edge_index = jnp.stack([src, dst])
    xn = _layernorm(x, axis=-1)
    x = x + _L0_gnn_ref(xn, L0_gnn_W, L0_gnn_att_src, L0_gnn_att_dst, L0_gnn_bias, edge_index) + _L0_mix_ref(xn[None], L0_mix_w_qkv, L0_mix_b_qkv, L0_mix_kln_g, L0_mix_kln_b, L0_mix_vln_g, L0_mix_vln_b, L0_mix_w1, L0_mix_b1, L0_mix_w2, L0_mix_b2)[0]
    x = x + _L0_ffn_ref(_layernorm(x, axis=-1)[None], L0_ffn_Wr, L0_ffn_br, L0_ffn_W1, L0_ffn_b1, L0_ffn_W2, L0_ffn_b2, L0_ffn_gamma, L0_ffn_beta)[0]
    xn = _layernorm(x, axis=-1)
    x = x + _L1_gnn_ref(xn, node_vec1, src, dst, edge_attr_4, edge_attr_8, L1_gnn_sc_w0, L1_gnn_sc_w1, L1_gnn_lin1_w0, L1_gnn_lin1_w1, L1_gnn_fc_w1, L1_gnn_fc_w2, L1_gnn_lin2_w00, L1_gnn_lin2_w01, L1_gnn_lin2_w10, L1_gnn_lin2_w11) + _L1_mix_ref(xn[None], L1_mix_Wqkv, L1_mix_Wout, L1_mix_bout)[0]
    x = x + _L1_ffn_ref(_layernorm(x, axis=-1)[None], L1_ffn_attention_mask, L1_ffn_wr, L1_ffn_br, L1_ffn_w1, L1_ffn_b1, L1_ffn_w2, L1_ffn_b2)[0]
    return x

_drawn_inputs = setup_inputs


def setup_inputs(seed=0):
    import zlib

    import numpy as np

    out = dict(_drawn_inputs(seed))
    spreads = {'L0_gnn_bias': (0.0, 0.1),
     'L0_mix_b_qkv': (0.0, 0.1),
     'L0_mix_kln_g': (1.0, 0.6),
     'L0_mix_kln_b': (0.0, 0.44),
     'L0_mix_vln_g': (1.0, 0.586),
     'L0_mix_vln_b': (0.0, 0.396),
     'L0_mix_b1': (0.0, 0.1),
     'L0_mix_b2': (0.0, 0.1),
     'L0_ffn_br': (0.0, 0.8),
     'L0_ffn_b1': (0.0, 0.52),
     'L0_ffn_b2': (0.0, 0.323),
     'L0_ffn_gamma': (1.0, 0.2),
     'L0_ffn_beta': (0.0, 0.1),
     'L1_ffn_b1': (0.0, 0.8),
     'L1_ffn_b2': (0.0, 0.8)}
    factors = {'L1_mix_bout': 8.0, 'L1_ffn_wr': 7.259, 'L1_ffn_w1': 8.0, 'L1_ffn_w2': 7.75}
    for name, (base, spread) in spreads.items():
        noise = np.random.default_rng([zlib.crc32(name.encode()), seed]).standard_normal(out[name].shape)
        drawn = base * np.exp(spread * noise) if base else spread * noise
        out[name] = jnp.asarray(drawn.astype(out[name].dtype))
    for name, factor in factors.items():
        out[name] = (out[name] * factor).astype(out[name].dtype)
    return out
```

```python
from contextlib import ExitStack, contextmanager

import concourse.bass as bass
from concourse import mybir

F32 = mybir.dt.float32
I32 = mybir.dt.int32
U32 = mybir.dt.uint32
ALU = mybir.AluOpType
ACT = mybir.ActivationFunctionType
AX = mybir.AxisListType

N = 6250
C = 256
R = 125
TILES = N // R
CH = 2 * R
CHUNKS = N // CH
E = 106250
ETILES = E // R
GT = 5
GROUPS = ETILES // GT
W = 64
NPAD = N + W
QB = 85
NB = ETILES // QB
H0, D0 = 4, 64
TAB0 = C + H0
EPS = 1e-5
E8, F0 = 8, 512
F1 = 1024
CAPACITY = float(-(-N * 5 // (4 * E8)))
TOPK1 = N // 2 - 1
SEL = 112
INV_SQRT3 = 3.0 ** -0.5
COS8, SIN8 = 0.9238795325112867, 0.3826834323650898


def sweep(eng, n, body):
    for u in range(2):
        body(u, u % 2, u, u)
    pairs = (n - 3) // 2
    with eng.Fori(1, pairs + 1) as k:
        for r in range(2):
            body(k * 2 + r, r, 2, n - 2)
    for u in range(2 + 2 * pairs, n):
        body(u, u % 2, u, u)


def rows_dma(eng, out, in_, sem):
    eng.dma_start(out[0:SEL], in_[0:SEL]).then_inc(sem, 16)
    eng.dma_start(out[SEL:R], in_[SEL:R]).then_inc(sem, 16)


def hold(eng, sem, value):
    eng.wait_ge(sem, value)
    eng.nop(nofuse=True)


def ln_stats(nc, v, x, bn, mv, var_eps, s_var):
    for t in range(2):
        nc.vector.bn_stats(bn[:, t, :], x[:, t, :])
    v.drain()
    for t in range(2):
        nc.vector.bn_aggr(mv[:, t, :], bn[:, t, :])
    v.drain()
    nc.vector.tensor_scalar(var_eps[:, :], mv[:, :, 1], EPS, None, ALU.add).then_inc(s_var, 1)


def ln_apply(nc, v, xn, x, mv, rn, tiles=2):
    nc.vector.scalar_tensor_tensor(out=rn[:, :, 1], in0=mv[:, :, 0], scalar=-1.0, in1=rn[:, :, 0],
                                   op0=ALU.mult, op1=ALU.mult)
    v.drain()
    for t in range(tiles):
        last = nc.vector.tensor_scalar(xn[:, t, :], x[:, t, :], rn[:, t, 0:1], rn[:, t, 1:2], ALU.mult, ALU.add)
    return last


def front0(env):
    nc, a, sem, ident, ones, stats = (env[k] for k in ("nc", "a", "sem", "ident", "ones", "stats"))
    chunk_view = env["chunk_view"]
    g0, g0b = env["g0"], env["g0b"]
    x_v = chunk_view(env["x_in"])
    tab_v = chunk_view(env["tab0"])
    adst = env["dst_tab"]
    HD = 32
    with ExitStack() as ctx:
        sb = lambda n, s, d=F32: ctx.enter_context(nc.sbuf_tensor("f0_" + n, s, d))
        pb = lambda n, s: ctx.enter_context(nc.psum_tensor("f0_" + n, s, F32))
        wg = sb("wg", [128, 2, C])
        wga = sb("wga", [128, 2, C + 8])
        att = sb("att", [128, 2, C])
        tmp = sb("tmp", [128, 2, C])
        wqkv = sb("wqkv", [128, 2, 3 * C])
        bqkv = sb("bqkv", [128, 3 * C])
        wkv = sb("wkv", [128, 2, 2 * C])
        bkv = sb("bkv", [128, 2 * C])
        cm = sb("cm", [128, 3, 8])
        w1 = sb("w1", [128, 2, C])
        b1c = sb("b1c", [128, 2])
        bqc = sb("bqc", [128, 2])
        gv = sb("gv", [128, 2])
        gk = sb("gk", [128, 2, HD])
        xt = sb("xt", [R, 2, 2, C])
        xn = sb("xn", [R, 2, 2, C])
        bn = sb("bn", [R, 2, 6])
        mv = sb("mv", [R, 2, 2])
        ve = sb("ve", [R, 2])
        rn = sb("rn", [R, 2, 2])
        mhalf = sb("mhalf", [R, 2])
        xnT = sb("xnT", [128, 2, 2, CH])
        hrow = sb("hrow", [R, 2, 2, C + 8])
        adst_all = sb("adst_all", [R, TILES, 8])
        kvt = sb("kvt", [R, 2, 2 * C])
        sq = sb("sq", [R, 2 * C])
        ss = sb("ss", [R, 16])
        sd = sb("sd", [R, 16])
        ri = sb("ri", [R, 16])
        kvn = sb("kvn", [R, 2, 2 * C + 2])
        epst = sb("epst", [128, 1])
        pT = pb("pT", [128, 2, 512])
        pH = pb("pH", [128, 2, 512])
        pKV = pb("pKV", [128, 2, 512])
        pS = pb("pS", [128, 512])
        pK = pb("pK", [128, 512])
        s_w = sem("f0_weights")
        s_p = sem("f0_prepared")
        s_x = [sem(f"f0_x{i}") for i in range(2)]
        s_var = sem("f0_var")
        s_rstd = sem("f0_rstd")
        s_xn = sem("f0_xn")
        s_T = sem("f0_transposed")
        s_xnT = sem("f0_xnT")
        s_h = sem("f0_h")
        s_hrow = sem("f0_hrow")
        s_kv = sem("f0_kv")
        s_kvt = sem("f0_kvt")
        s_sq = sem("f0_sq")
        s_ss = sem("f0_ss")
        s_sd = sem("f0_sd")
        s_kvn = sem("f0_kvn")
        s_acc = sem("f0_accumulated")
        s_sx = [sem(f"f0_store_xnT{i}") for i in range(2)]
        s_st = [sem(f"f0_store_tab{i}") for i in range(2)]
        s_ad = sem("f0_store_dst")

        with nc.Block() as block:
            @block.sync
            def _(sp):
                sp.dma_start(wg[:, :, :], a["L0_gnn_W"].rearrange("(k p) n -> p k n", p=128)).then_inc(s_w, 16)
                for i, n in enumerate(("L0_gnn_att_src", "L0_gnn_att_dst")):
                    sp.dma_start(att[:, i, :], a[n].rearrange("(o h) c -> o (h c)", o=1).broadcast_to([128, C]))\
                      .then_inc(s_w, 16)
                sp.dma_start(wqkv[:, :, :], a["L0_mix_w_qkv"].rearrange("(k p) n -> p k n", p=128)).then_inc(s_w, 16)
                sp.dma_start(bqkv[:, :], a["L0_mix_b_qkv"].rearrange("(o n) -> o n", o=1).broadcast_to([128, 3 * C]))\
                  .then_inc(s_w, 16)
                sp.dma_start(w1[:, :, :], a["L0_mix_w1"].rearrange("(k p) n -> p k n", p=128)).then_inc(s_w, 16)
                sp.dma_start(b1c[:, :], a["L0_mix_b1"].rearrange("(k p) -> p k", p=128)).then_inc(s_w, 16)
                bq = a["L0_mix_b_qkv"].rearrange("(h s d o) -> h s d o", s=3, d=HD, o=1)
                for h in range(8):
                    sp.dma_start(bqc[HD * (h % 4):HD * (h % 4 + 1), h // 4:h // 4 + 1], bq[h, 0]).then_inc(s_w, 16)
                for h in range(4):
                    for i, n in enumerate(("L0_mix_vln_g", "L0_mix_vln_b")):
                        sp.dma_start(gv[HD * h:HD * (h + 1), i:i + 1], a[n].rearrange("(d o) -> d o", o=1))\
                          .then_inc(s_w, 16)
                for i, n in enumerate(("L0_mix_kln_g", "L0_mix_kln_b")):
                    sp.dma_start(gk[:, i, :], a[n].rearrange("(o d) -> o d", o=1).broadcast_to([128, HD]))\
                      .then_inc(s_w, 16)
                sp.wait_ge(s_w, 16 * 25)

        with nc.Block() as block:
            @block.gpsimd
            def _(pool):
                nc.gpsimd.memset(mhalf[:, :], -0.5)
                nc.gpsimd.memset(epst[:, :], EPS)
                nc.gpsimd.memset(kvn[:, :, :], 1.0)
                pool.drain()

            @block.vector
            def _(v):
                for i in range(2):
                    for k in range(2):
                        nc.vector.tensor_tensor(out=tmp[:, k, :], in0=wg[:, k, :], in1=att[:, i, :], op=ALU.mult)
                    v.drain()
                    for k in range(2):
                        nc.vector.tensor_reduce(wga[:, k, C + 4 * i:C + 4 * i + 4],
                                                tmp[:, k, :].rearrange("p (h c) -> p h c", h=H0), AX.X, ALU.add)
                    v.drain()
                nc.vector.tensor_copy(wga[:, :, 0:C], wg[:, :, :])
                for s in (1, 2):
                    for k in range(3):
                        src = wqkv[:, k, :] if k < 2 else bqkv[:, :]
                        dst = (wkv[:, k, :] if k < 2 else bkv[:, :])[:, (s - 1) * C:s * C]
                        src = src.rearrange("p (h s d) -> p h s d", s=3, d=HD)[:, :, s, :]
                        nc.vector.tensor_reduce(cm[:, k, :], src, AX.X, ALU.add)
                        v.drain()
                        nc.vector.tensor_scalar(cm[:, k, :], cm[:, k, :], -1.0 / HD, None, ALU.mult)
                        v.drain()
                        nc.vector.tensor_tensor(out=dst.rearrange("p (h d) -> p h d", d=HD), in0=src,
                                                in1=cm[:, k, :].unsqueeze(2).broadcast_to([128, 8, HD]), op=ALU.add)
                        v.drain()

        with nc.Block() as block:
            @block.sync
            def _(sp):
                def load(u, s):
                    rows_dma(sp, xt[:, s, :, :], x_v[u].rearrange("p t c -> p t c"), s_x[s])

                def step(u, s, lo, hi):
                    if lo >= 2:
                        sp.wait_ge(s_xn, u - 1)
                    load(u, s)
                    if lo >= 1:
                        o = u - 1
                        sp.wait_ge(s_xnT, o + 1)
                        sp.dma_start(env["xnT_d"][0][:, :, bass.ds(o * CH, CH)], xnT[:, 1 - s, :, :])\
                          .then_inc(s_sx[1 - s], 16)
                        sp.wait_ge(s_hrow, 2 * o + 2)
                        rows_dma(sp, tab_v[o][:, :, :], hrow[:, 1 - s, :, 0:TAB0], s_st[1 - s])
                sweep(sp, CHUNKS, step)
                o, s = CHUNKS - 1, (CHUNKS - 1) % 2
                sp.wait_ge(s_xnT, o + 1)
                sp.dma_start(env["xnT_d"][0][:, :, o * CH:(o + 1) * CH], xnT[:, s, :, :]).then_inc(s_sx[s], 16)
                sp.wait_ge(s_hrow, 2 * o + 2)
                rows_dma(sp, tab_v[o][:, :, :], hrow[:, s, :, 0:TAB0], s_st[s])
                for i in range(2):
                    n = (CHUNKS + 1 - i) // 2
                    sp.wait_ge(s_sx[i], 16 * n)
                    sp.wait_ge(s_st[i], 32 * n)

            @block.gpsimd
            def _(pool):
                def step(u, s, lo, hi):
                    hold(pool, s_var, u + 1)
                    nc.gpsimd.tensor_tensor(out=rn[:, :, 0], in0=ve[:, :], in1=mhalf[:, :], op=ALU.pow)\
                      .then_inc(s_rstd, 1)
                sweep(pool, CHUNKS, step)

            @block.vector
            def _(v):
                def keys_values(u, s):
                    for t in range(2):
                        i = 2 * u + t
                        v.wait_ge(s_kv, i + 1)
                        nc.vector.tensor_tensor(out=kvt[:, t, :], in0=pKV[0:R, t, :], in1=bkv[0:R, :], op=ALU.add)\
                          .then_inc(s_kvt, 1)
                    for t in range(2):
                        i = 2 * u + t
                        v.wait_ge(s_sq, i + 1)
                        nc.vector.tensor_reduce(ss[:, :], sq[:, :].rearrange("p (g d) -> p g d", d=HD), AX.X, ALU.add)\
                          .then_inc(s_ss, 1)
                        v.wait_ge(s_sd, i + 1)
                        nc.vector.reciprocal(ri[:, :], sd[:, :])
                        v.drain()
                        if t == 1 or not isinstance(u, int) or u > 0:
                            pass
                        kvn_k = kvn[:, t, 0:2 * 129].rearrange("p (g m) -> p g m", g=2)
                        for g in range(2):
                            nc.vector.tensor_tensor(
                                out=kvn_k[:, g, 0:128].rearrange("p (h d) -> p h d", d=HD),
                                in0=kvt[:, t, 128 * g:128 * g + 128].rearrange("p (h d) -> p h d", d=HD),
                                in1=ri[:, 4 * g:4 * g + 4].unsqueeze(2).broadcast_to([R, 4, HD]), op=ALU.mult)
                        nc.vector.tensor_tensor(
                            out=kvn[:, t, 258:514].rearrange("p (h d) -> p h d", d=HD),
                            in0=kvt[:, t, C:2 * C].rearrange("p (h d) -> p h d", d=HD),
                            in1=ri[:, 8:16].unsqueeze(2).broadcast_to([R, 8, HD]), op=ALU.mult).then_inc(s_kvn, 1)

                def step(u, s, lo, hi):
                    v.wait_ge(s_x[s], (u // 2 + 1) * 32)
                    ln_stats(nc, v, xt[:, s, :, :], bn, mv, ve, s_var)
                    v.wait_ge(s_rstd, u + 1)
                    if lo >= 2:
                        v.wait_ge(s_T, u - 1)
                    ln_apply(nc, v, xn[:, s, :, :], xt[:, s, :, :], mv, rn).then_inc(s_xn, 1)
                    nc.vector.tensor_copy(stats[:, bass.ds(u * 2, 2), :], rn[:, :, :])
                    if lo >= 1:
                        if lo >= 2:
                            v.wait_ge(s_acc, 2 * u - 2)
                        keys_values(u - 1, 1 - s)
                sweep(v, CHUNKS, step)
                v.wait_ge(s_acc, 2 * CHUNKS - 2)
                keys_values(CHUNKS - 1, (CHUNKS - 1) % 2)

            @block.scalar
            def _(act):
                def step(u, s, lo, hi):
                    if lo >= 2:
                        hold(act, s_sx[s], (u // 2) * 16)
                    hold(act, s_T, u + 1)
                    nc.scalar.copy(xnT[:, s, :, :], pT[:, s, 0:2 * CH].rearrange("p (k n) -> p k n", k=2))\
                      .then_inc(s_xnT, 1)
                    if lo >= 2:
                        hold(act, s_st[s], (u // 2) * 32)
                    for t in range(2):
                        i = 2 * u + t
                        hold(act, s_h, i + 1)
                        nc.scalar.copy(hrow[:, s, t, :], pH[0:R, t, 0:C + 8]).then_inc(s_hrow, 1)
                        act.drain()
                        nc.scalar.copy(adst_all[:, bass.ds(i, 1), :], hrow[:, s, t:t + 1, C:C + 8])
                    for t in range(2):
                        i = 2 * u + t
                        hold(act, s_kvt, i + 1)
                        if t == 1 or lo >= 1:
                            hold(act, s_ss, i)
                        nc.scalar.activation(sq[:, :], kvt[:, t, :], ACT.Square).then_inc(s_sq, 1)
                        hold(act, s_ss, i + 1)
                        nc.scalar.activation(sd[:, :], ss[:, :], ACT.Sqrt, bias=epst[0:R, :], scale=1.0 / HD)\
                          .then_inc(s_sd, 1)
                sweep(act, CHUNKS, step)

            @block.tensor
            def _(pe):
                def transposes(u, s, lo):
                    pe.wait_ge(s_xn, u + 1)
                    if lo >= 2:
                        pe.wait_ge(s_xnT, u - 1)
                    for k in range(2):
                        for t in range(2):
                            last = nc.tensor.transpose(pT[:, s, k * CH + t * R:k * CH + t * R + R],
                                                       xn[:, s, t, 128 * k:128 * k + 128], ident[0:R, 0:R])
                    last.then_inc(s_T, 1)

                def products(u, s, lo):
                    pe.wait_ge(s_xnT, u + 1)
                    for t in range(2):
                        i = 2 * u + t
                        if lo >= 1:
                            pe.wait_ge(s_hrow, i - 1)
                        for k in range(2):
                            last = nc.tensor.matmul(pH[0:R, t, 0:C + 8], xnT[:, s, k, t * R:t * R + R], wga[:, k, :],
                                                    start=k == 0, stop=k == 1)
                        last.then_inc(s_h, 1)
                    for t in range(2):
                        i = 2 * u + t
                        if lo >= 1:
                            pe.wait_ge(s_kvt, i - 1)
                        for k in range(2):
                            last = nc.tensor.matmul(pKV[0:R, t, :], xnT[:, s, k, t * R:t * R + R], wkv[:, k, :],
                                                    start=k == 0, stop=k == 1)
                        last.then_inc(s_kv, 1)

                def sums(u, s):
                    for t in range(2):
                        i = 2 * u + t
                        pe.wait_ge(s_kvn, i + 1)
                        for g in range(2):
                            nc.tensor.matmul(pS[:, 129 * g:129 * g + 129], kvn[:, t, 258 + 128 * g:386 + 128 * g],
                                             kvn[:, t, 129 * g:129 * g + 129], start=False, stop=False,
                                             skip_group_check=True)
                        last = nc.tensor.matmul(pK[:, 0:258], ones[0:R, :], kvn[:, t, 0:258], start=False, stop=False,
                                                skip_group_check=True)
                        last.then_inc(s_acc, 1)

                def step(u, s, lo, hi):
                    if hi <= CHUNKS - 2:
                        transposes(u + 1, 1 - s, lo + 1)
                    products(u, s, lo)
                    if lo >= 1:
                        sums(u - 1, 1 - s)

                nc.tensor.matmul(pS[:, 0:258], env["zeros"][0:1, 0:128], env["zeros"][0:1, 0:258], start=True, stop=False,
                                 skip_group_check=True)
                nc.tensor.matmul(pK[:, 0:258], env["zeros"][0:1, 0:128], env["zeros"][0:1, 0:258], start=True, stop=False,
                                 skip_group_check=True)
                transposes(0, 0, 0)
                sweep(pe, CHUNKS, step)
                sums(CHUNKS - 1, (CHUNKS - 1) % 2)
                pe.drain()

        kvT = sb("kvT", [128, 2, 128])
        mask = sb("mask", [128, 128])
        sA = sb("sA", [128, 2, 128])
        sv = sb("sv", [128, 2])
        m1 = sb("m1", [128, 2, C])
        wqT = sb("wqT", [128, 2, C])
        wq = sb("wq", [128, 2, C])
        amax = sb("amax", [R, 8])
        amaxT = sb("amaxT", [8, R])
        am1 = sb("am1", [8, 1])
        amr = sb("amr", [1, 8])
        amb = sb("amb", [128, 8])
        dtab = sb("dtab", [R, TILES, 8])
        g_ = sb("g_", [R, TILES, 4])
        zpad = sb("zpad", [W, 8])
        s_f = {k: sem("fold_" + k) for k in ("mask", "mask1", "wq", "qt", "qtc", "kvT", "m", "mc", "g", "am", "amT", "am1", "amr",
                                            "amrc", "amb", "dt", "zp", "gb")}
        with nc.Block() as block:
            @block.gpsimd
            def _(pool):
                nc.gpsimd.memset(mask[:, :], 0.0).then_inc(s_f["mask"], 1)
                nc.gpsimd.memset(zpad[:, :], 0.0).then_inc(s_f["zp"], 1)
                pool.wait_ge(s_f["mask"], 1)
                pool.drain()
                for h in range(4):
                    nc.gpsimd.memset(mask[HD * h:HD * (h + 1), HD * h:HD * (h + 1)], 1.0 / N)
                    pool.drain()
                pool.drain().then_inc(s_f["mask1"], 1)

            @block.tensor
            def _(pe):
                pe.wait_ge(s_f["wq"], 1)
                for g in range(2):
                    for k in range(2):
                        last = nc.tensor.transpose(pT[:, g, 128 * k:128 * k + 128],
                                                   wq[:, k, 128 * g:128 * g + 128], ident[:, :])
                last.then_inc(s_f["qt"], 1)
                pe.wait_ge(s_f["kvT"], 1)
                for g in range(2):
                    last = nc.tensor.matmul(pH[:, g, 0:C], kvT[:, g, :], w1[:, g, :], start=True, stop=True)
                last.then_inc(s_f["m"], 1)
                pe.wait_ge(s_f["mc"], 1)
                pe.wait_ge(s_f["qtc"], 1)
                for k in range(2):
                    for g in range(2):
                        last = nc.tensor.matmul(pKV[:, k, 0:C], wqT[:, g, 128 * k:128 * k + 128], m1[:, g, :],
                                                start=g == 0, stop=g == 1)
                for f in range(2):
                    for g in range(2):
                        last = nc.tensor.matmul(pT[:, 0, f:f + 1], m1[:, g, 128 * f:128 * f + 128], bqc[:, g:g + 1],
                                                start=g == 0, stop=g == 1)
                last.then_inc(s_f["g"], 1)
                pe.wait_ge(s_f["am"], 1)
                nc.tensor.transpose(pT[0:8, 1, 0:R], amax[:, :], ident[0:R, 0:R]).then_inc(s_f["amT"], 1)
                pe.wait_ge(s_f["am1"], 1)
                nc.tensor.transpose(pT[0:1, 1, 128:136], am1[:, :], ident[0:8, 0:8]).then_inc(s_f["amr"], 1)
                pe.wait_ge(s_f["amrc"], 1)
                nc.tensor.matmul(pT[:, 1, 256:264], ones[0:1, :], amr[:, :], start=True, stop=True).then_inc(s_f["amb"], 1)

            @block.vector
            def _(v):
                for k in range(2):
                    last = nc.vector.tensor_copy(
                        wq[:, k, :].rearrange("p (h d) -> p h d", d=HD),
                        wqkv[:, k, :].rearrange("p (h s d) -> p h s d", s=3, d=HD)[:, :, 0, :])
                last.then_inc(s_f["wq"], 1)
                v.wait_ge(s_f["qt"], 1)
                nc.vector.tensor_copy(wqT[:, :, :], pT[:, :, 0:C]).then_inc(s_f["qtc"], 1)
                v.wait_ge(s_f["mask1"], 1)
                for g in range(2):
                    S = pS[:, 129 * g:129 * g + 128]
                    gkb = gk[:, 0, :].unsqueeze(1).broadcast_to([128, 4, HD])
                    bkb = gk[:, 1, :].unsqueeze(1).broadcast_to([128, 4, HD])
                    nc.vector.tensor_scalar(sA[:, 0, :], S, gv[:, 0:1], None, ALU.mult)
                    v.drain()
                    nc.vector.scalar_tensor_tensor(out=sA[:, 1, :], in0=pK[:, 129 * g:129 * g + 128], scalar=gv[:, 1:2],
                                                   in1=sA[:, 0, :], op0=ALU.mult, op1=ALU.add)
                    v.drain()
                    nc.vector.tensor_tensor(out=sA[:, 0, :].rearrange("p (h d) -> p h d", h=4),
                                            in0=sA[:, 1, :].rearrange("p (h d) -> p h d", h=4), in1=gkb, op=ALU.mult)
                    nc.vector.tensor_scalar(sv[:, 0:1], gv[:, 1:2], float(N), None, ALU.mult)
                    v.drain()
                    nc.vector.scalar_tensor_tensor(out=sv[:, 1:2], in0=pS[:, 129 * g + 128:129 * g + 129],
                                                   scalar=gv[:, 0:1], in1=sv[:, 0:1], op0=ALU.mult, op1=ALU.add)
                    v.drain()
                    nc.vector.scalar_tensor_tensor(out=sA[:, 1, :].rearrange("p (h d) -> p h d", h=4), in0=bkb,
                                                   scalar=sv[:, 1:2], in1=sA[:, 0, :].rearrange("p (h d) -> p h d", h=4),
                                                   op0=ALU.mult, op1=ALU.add)
                    v.drain()
                    nc.vector.tensor_tensor(out=kvT[:, g, :], in0=sA[:, 1, :], in1=mask[:, :], op=ALU.mult)
                    v.drain()
                v.drain().then_inc(s_f["kvT"], 1)
                v.wait_ge(s_f["m"], 1)
                nc.vector.tensor_copy(m1[:, :, :], pH[:, :, 0:C]).then_inc(s_f["mc"], 1)
                v.wait_ge(s_f["g"], 1)
                nc.vector.tensor_tensor(out=g0[:, :, :], in0=pKV[:, :, 0:C], in1=w1[:, :, :], op=ALU.add)
                nc.vector.tensor_tensor(out=g0b[:, :], in0=pT[:, 0, 0:2], in1=b1c[:, :], op=ALU.add)
                nc.vector.tensor_reduce(amax[:, :], adst_all[:, :, :].rearrange("p t c -> p c t"), AX.X, ALU.max)\
                  .then_inc(s_f["am"], 1)
                v.wait_ge(s_f["amT"], 1)
                nc.vector.tensor_reduce(am1[:, :], pT[0:8, 1, 0:R], AX.X, ALU.max).then_inc(s_f["am1"], 1)
                v.wait_ge(s_f["amr"], 1)
                nc.vector.tensor_copy(amr[:, :], pT[0:1, 1, 128:136]).then_inc(s_f["amrc"], 1)
                v.wait_ge(s_f["amb"], 1)
                nc.vector.tensor_copy(amb[:, :], pT[:, 1, 256:264])
                v.drain()
                nc.vector.tensor_tensor(out=g_[:, :, :], in0=adst_all[:, :, 4:8],
                                        in1=amb[0:R, 0:4].unsqueeze(1).broadcast_to([R, TILES, 4]), op=ALU.add)
                nc.vector.tensor_copy(dtab[:, :, 0:4], adst_all[:, :, 4:8])
                v.drain()
                nc.vector.scalar_tensor_tensor(out=dtab[:, :, 4:8], in0=g_[:, :, :], scalar=0.2, in1=g_[:, :, :],
                                               op0=ALU.mult, op1=ALU.max)
                v.drain().then_inc(s_f["dt"], 1)
                pself = env["pself"]
                nc.vector.tensor_tensor(out=g_[:, :, :], in0=adst_all[:, :, 0:4], in1=adst_all[:, :, 4:8], op=ALU.add)
                v.drain()
                nc.vector.scalar_tensor_tensor(out=pself[:, :, :], in0=g_[:, :, :], scalar=0.2, in1=g_[:, :, :],
                                               op0=ALU.mult, op1=ALU.max)
                v.drain()
                nc.vector.tensor_tensor(out=g_[:, :, :], in0=pself[:, :, :], in1=dtab[:, :, 4:8], op=ALU.subtract)
                v.drain().then_inc(s_f["gb"], 1)

            @block.scalar
            def _(act):
                act.wait_ge(s_f["gb"], 1)
                nc.scalar.activation(env["pself"][:, :, :], g_[:, :, :], ACT.Exp)
                act.drain()

            @block.sync
            def _(sp):
                sp.wait_ge(s_f["zp"], 1)
                sp.dma_start(adst[N:NPAD, :], zpad[:, :]).then_inc(s_ad, 16)
                sp.wait_ge(s_f["dt"], 1)
                rows_dma(sp, adst[0:N, :].rearrange("(t p) c -> p t c", p=R), dtab[:, :, :], s_ad)
                sp.wait_ge(s_ad, 48)


def edge_indices(env):
    nc, a, sem, ident = (env[k] for k in ("nc", "a", "sem", "ident"))
    srcI, dstRel, baseF, spanI = (env[k] for k in ("srcI", "dstRel", "baseF", "spanI"))
    GQ = GROUPS // 2
    with ExitStack() as ctx:
        sb = lambda n, s, d=F32: ctx.enter_context(nc.sbuf_tensor("ei_" + n, s, d))
        st = sb("st", [QB, 2, NB, R], I32)
        stf = sb("stf", [QB, 2, NB, R])
        gi = sb("gi", [GQ, 2, GT * R], I32)
        gf = sb("gf", [GQ, 2, GT * R])
        gm = sb("gm", [GQ, 2, 2])
        grow = sb("grow", [1, 2, GROUPS])
        gB = sb("gB", [R, GROUPS])
        sp_ = sb("sp", [1, GROUPS])
        dstT = sb("dstT", [R, ETILES])
        pt = ctx.enter_context(nc.psum_tensor("ei_pt", [128, 8, 512], F32))
        s_ld, s_cv, s_mm, s_st, s_row, s_t, s_ev = (sem("ei_" + n) for n in
                                                    ("load", "floats", "minmax", "store", "rows", "T", "copied"))
        gd = env["gf_d"]
        with nc.Block() as block:
            @block.sync
            def _(sp):
                for i, n in enumerate(("dst", "src")):
                    sp.dma_start(st[:, i, :, :], a[n].rearrange("(b q e) -> q b e", q=QB, e=R)).then_inc(s_ld, 16)
                sp.dma_start(gi[:, :, :], a["dst"].rearrange("(b q e) -> q b e", q=GQ, e=GT * R)).then_inc(s_ld, 16)
                sp.wait_ge(s_mm, 1)
                for i in range(2):
                    sp.dma_start(gd[i].rearrange("(b q o) -> q b o", q=GQ, o=1), gm[:, :, i:i + 1]).then_inc(s_st, 16)
                sp.wait_ge(s_st, 32)
                sp.dma_start(grow[:, :, :], gd.rearrange("(o i) g -> o i g", o=1)).then_inc(s_row, 16)
                sp.dma_start(gB[:, :], gd[0:1, :].broadcast_to([R, GROUPS])).then_inc(s_row, 16)
                sp.wait_ge(s_row, 32)

            @block.vector
            def _(v):
                v.wait_ge(s_ld, 48)
                nc.vector.tensor_copy(gf[:, :, :], gi[:, :, :])
                v.drain()
                nc.vector.tensor_reduce(gm[:, :, 0], gf[:, :, :], AX.X, ALU.min)
                nc.vector.tensor_reduce(gm[:, :, 1], gf[:, :, :], AX.X, ALU.max)
                v.drain().then_inc(s_mm, 1)
                nc.vector.tensor_copy(stf[:, :, :, :], st[:, :, :, :]).then_inc(s_cv, 1)
                for i, dst in enumerate((dstT, srcI)):
                    for b in range(NB):
                        n = NB * i + b
                        v.wait_ge(s_t, n + 1)
                        nc.vector.tensor_copy(dst[:, QB * b:QB * (b + 1)], pt[0:R, n % 8, 0:QB]).then_inc(s_ev, 1)
                v.wait_ge(s_row, 32)
                nc.vector.tensor_copy(baseF[:, :], grow[:, 0, :])
                nc.vector.tensor_tensor(out=sp_[:, :], in0=grow[:, 1, :], in1=grow[:, 0, :], op=ALU.subtract)
                v.drain()
                nc.vector.tensor_reduce(spanI[:, :], sp_[:, :], AX.X, ALU.max)
                nc.vector.tensor_tensor(out=dstRel[:, :].rearrange("p (g j) -> p g j", j=GT),
                                        in0=dstT[:, :].rearrange("p (g j) -> p g j", j=GT),
                                        in1=gB[:, :].unsqueeze(2).broadcast_to([R, GROUPS, GT]), op=ALU.subtract)
                v.drain()

            @block.tensor
            def _(pe):
                pe.wait_ge(s_cv, 1)
                for n in range(2 * NB):
                    if n >= 8:
                        pe.wait_ge(s_ev, n - 7)
                    nc.tensor.transpose(pt[0:R, n % 8, 0:QB], stf[:, n // NB, n % NB, :], ident[0:QB, 0:QB])\
                      .then_inc(s_t, 1)


def edge_passes(env, layer, zero, one_pass, dma_sems, sems):
    nc, sem = env["nc"], env["sem"]
    iotaI, iotaW, baseI, baseF, spanI = (env[k] for k in ("iotaI", "iotaW", "baseI", "baseF", "spanI"))
    s_i = sem(f"window_iota{layer}")
    with nc.Block() as block:
        @block.gpsimd
        def _(pool):
            nc.gpsimd.iota(iotaI[:, :], pattern=[[1, W]], base=0, channel_multiplier=0).then_inc(s_i, 1)

        @block.vector
        def _(v):
            for t in zero:
                nc.vector.memset(t, 0.0)
            nc.vector.tensor_copy(baseI[:, :], baseF[:, :])
            v.wait_ge(s_i, 1)
            nc.vector.tensor_copy(iotaW[:, :], iotaI[:, :])
            v.drain()
    span = nc.values_load(spanI[0:1, 0:1], min_val=0, max_val=N - 1)
    with nc.Fori(0, span + 1, W):
        one_pass()
        with nc.Block() as block:
            @block.vector
            def _(v):
                nc.vector.tensor_scalar(iotaW[:, :], iotaW[:, :], float(W), None, ALU.add)
                nc.vector.tensor_scalar(baseI[:, :], baseI[:, :], float(W), float(N), ALU.add, ALU.min)
                v.drain()

            @block.gpsimd
            def _(pool):
                nc.gpsimd.inc_swdge_sem(dma_sems, [GROUPS // 2 * GT * 16] * 2, mode="sub")
                for s in sems:
                    pool.sem_clear(s)


def one_hots(nc, env, out, g):
    return nc.vector.tensor_tensor(
        out=out, in0=env["iotaW"][:, :].unsqueeze(1).broadcast_to([R, GT, W]),
        in1=env["dstRel"][:, bass.ds(g * GT, GT)].unsqueeze(2).broadcast_to([R, GT, W]), op=ALU.is_equal)


def edges0(env, acc, den):
    nc, sem, ident = (env[k] for k in ("nc", "sem", "ident"))
    srcI, baseI = env["srcI"], env["baseI"]
    with ExitStack() as ctx:
        sb = lambda n, s, d=F32: ctx.enter_context(nc.sbuf_tensor("e0_" + n, s, d))
        pb = lambda n, s: ctx.enter_context(nc.psum_tensor("e0_" + n, s, F32))
        ix = sb("ix", [R, 2, GT], I32)
        rows = sb("rows", [R, 2, GT, TAB0])
        dw = sb("dw", [W, 2, 8])
        oh = sb("oh", [R, 2, GT, W])
        ohT = sb("ohT", [W, GT, R])
        ee = sb("ee", [R, 3, GT, H0])
        pr = sb("pr", [R, 2, GT, H0])
        msg = sb("msg", [R, GT, C])
        pT = pb("pT", [W, 1024])
        pE = pb("pE", [R, 2, 512])
        pU = pb("pU", [128, 2, 512])
        pD = pb("pD", [H0, 2, 512])
        s_gat = [sem(f"e0_rows{i}", software_dma=True) for i in range(2)]
        s_dw = [sem("e0_dw0"), sem("e0_dw1")]
        s_ix, s_oh, s_T, s_ohT, s_E, s_ed, s_p, s_msg, s_acc, s_add = (
            sem("e0_" + n) for n in ("ix", "oh", "T", "ohT", "E", "logits", "p", "msg", "acc", "added"))

        def one_pass():
            with nc.Block() as block:
                @block.gpsimd
                def _(pool):
                    def step(g, s, lo, hi):
                        hold(pool, s_ix, g + 1)
                        for j in range(GT):
                            nc.gpsimd.indirect_dma_start(
                                out=rows[:, s, j, :], out_offset=None, in_=env["tab0"],
                                in_offset=bass.IndirectOffsetOnAxis(ap=ix[:, s, j:j + 1], axis=0))\
                              .then_inc(s_gat[s], 16)
                    sweep(pool, GROUPS, step)

                @block.sync
                def _(sp):
                    def step(g, s, lo, hi):
                        base = sp.value_load(baseI[0:1, bass.ds(g, 1)], min_val=0, max_val=N)
                        if lo >= 2:
                            sp.wait_ge(s_E, g - 1)
                        sp.dma_start(dw[:, s, :], env["dst_tab"][bass.ds(base, W), :]).then_inc(s_dw[s], 16)
                    sweep(sp, GROUPS, step)

                @block.scalar
                def _(act):
                    def stage(g, s, lo):
                        if lo >= 2:
                            hold(act, s_msg, g - 1)
                        nc.scalar.copy(ix[:, s, :], srcI[:, bass.ds(g * GT, GT)]).then_inc(s_ix, 1)

                    def turn(g, lo):
                        if lo >= 1:
                            hold(act, s_E, g)
                        hold(act, s_T, g + 1)
                        nc.scalar.copy(ohT[:, :, :], pT[:, 0:128 * GT].rearrange("p (j e) -> p j e", e=128)[:, :, 0:R])\
                          .then_inc(s_ohT, 1)

                    def step(g, s, lo, hi):
                        if lo == 0:
                            stage(0, 0, 0)
                            turn(0, 0)
                        if hi <= GROUPS - 2:
                            stage(g + 1, 1 - s, lo + 1)
                            turn(g + 1, lo + 1)
                        if lo >= 2:
                            hold(act, s_acc, g - 1)
                        hold(act, s_ed, g + 1)
                        nc.scalar.activation(pr[:, s, :, :], ee[:, 2, :, :], ACT.Exp).then_inc(s_p, 1)
                    sweep(act, GROUPS, step)

                @block.vector
                def _(v):
                    def hots(g, s, lo):
                        if lo >= 2:
                            v.wait_ge(s_acc, g - 1)
                        one_hots(nc, env, oh[:, s, :, :], g).then_inc(s_oh, 1)

                    def add(g, s):
                        base = v.value_load(baseI[0:1, bass.ds(g, 1)], min_val=0, max_val=N)
                        v.wait_ge(s_acc, g + 1)
                        w = acc[:, :, bass.ds(base, W)]
                        nc.vector.tensor_tensor(out=w, in0=w, in1=pU[:, s, 0:2 * W].rearrange("p (k n) -> p k n", k=2),
                                                op=ALU.add)
                        w = den[:, bass.ds(base, W)]
                        nc.vector.tensor_tensor(out=w, in0=w, in1=pD[:, s, 0:W], op=ALU.add).then_inc(s_add, 1)

                    def step(g, s, lo, hi):
                        if lo == 0:
                            hots(0, 0, 0)
                        v.wait_ge(s_gat[s], (g // 2 + 1) * 16 * GT)
                        v.wait_ge(s_E, g + 1)
                        lg = pE[:, s, 0:8 * GT].rearrange("p (j c) -> p j c", c=8)
                        nc.vector.tensor_tensor(out=ee[:, 0, :, :], in0=rows[:, s, :, C:C + H0], in1=lg[:, :, 0:H0],
                                                op=ALU.add)
                        v.drain()
                        nc.vector.scalar_tensor_tensor(out=ee[:, 1, :, :], in0=ee[:, 0, :, :], scalar=0.2,
                                                       in1=ee[:, 0, :, :], op0=ALU.mult, op1=ALU.max)
                        v.drain()
                        nc.vector.tensor_tensor(out=ee[:, 0, :, :], in0=ee[:, 1, :, :], in1=lg[:, :, H0:8],
                                                op=ALU.subtract)
                        v.drain()
                        if lo >= 1:
                            v.wait_ge(s_p, g)
                        nc.vector.tensor_scalar(ee[:, 2, :, :], ee[:, 0, :, :], 0.0, None, ALU.min).then_inc(s_ed, 1)
                        if lo >= 2:
                            add(g - 2, s)
                        if hi <= GROUPS - 2:
                            hots(g + 1, 1 - s, lo + 1)
                        v.wait_ge(s_p, g + 1)
                        if lo >= 1:
                            v.wait_ge(s_acc, g)
                        nc.vector.tensor_tensor(
                            out=msg[:, :, :].rearrange("p j (h c) -> p j h c", h=H0),
                            in0=rows[:, s, :, 0:C].rearrange("p j (h c) -> p j h c", h=H0),
                            in1=pr[:, s, :, :].unsqueeze(3).broadcast_to([R, GT, H0, D0]), op=ALU.mult)\
                          .then_inc(s_msg, 1)
                        if lo == GROUPS - 1:
                            v.drain()
                            add(GROUPS - 2, 1 - s)
                            v.drain()
                            add(GROUPS - 1, s)
                            v.drain()
                    sweep(v, GROUPS, step)

                @block.tensor
                def _(pe):
                    def turn(g, s, lo):
                        if lo >= 1:
                            pe.wait_ge(s_ohT, g)
                        hold(pe, s_oh, g + 1)
                        for j in range(GT):
                            last = nc.tensor.transpose(pT[:, 128 * j:128 * j + R], oh[:, s, j, :], ident[0:R, 0:R])
                        last.then_inc(s_T, 1)

                    def logits(g, s, lo):
                        pe.wait_ge(s_ohT, g + 1)
                        pe.wait_ge(s_dw[s], (g // 2 + 1) * 16)
                        if lo >= 2:
                            pe.wait_ge(s_ed, g - 1)
                        for j in range(GT):
                            last = nc.tensor.matmul(pE[:, s, 8 * j:8 * j + 8], ohT[:, j, :], dw[:, s, :],
                                                    start=True, stop=True)
                        last.then_inc(s_E, 1)

                    def sums(g, s, lo):
                        pe.wait_ge(s_msg, g + 1)
                        if lo >= 2:
                            pe.wait_ge(s_add, g - 1)
                        for k in range(2):
                            for j in range(GT):
                                nc.tensor.matmul(pU[:, s, k * W:k * W + W], msg[:, j, 128 * k:128 * k + 128],
                                                 oh[:, s, j, :], start=j == 0, stop=j == GT - 1)
                        for j in range(GT):
                            last = nc.tensor.matmul(pD[:, s, 0:W], pr[:, s, j, :], oh[:, s, j, :],
                                                    start=j == 0, stop=j == GT - 1)
                        last.then_inc(s_acc, 1)

                    def step(g, s, lo, hi):
                        if lo == 0:
                            turn(0, 0, 0)
                            logits(0, 0, 0)
                        if lo >= 1:
                            sums(g - 1, 1 - s, lo - 1)
                        if hi <= GROUPS - 2:
                            turn(g + 1, 1 - s, lo + 1)
                            logits(g + 1, 1 - s, lo + 1)
                        if lo == GROUPS - 1:
                            sums(g, s, lo)
                    sweep(pe, GROUPS, step)

        edge_passes(env, 0, [acc[:, :, :], den[:, :]], one_pass, s_gat,
                    s_dw + [s_ix, s_oh, s_T, s_ohT, s_E, s_ed, s_p, s_msg, s_acc, s_add])


def row_bc(ap, parts):
    return ap.rearrange("(o n) -> o n", o=1).broadcast_to([parts, ap.shape[0]])


def back0(env, acc, den):
    nc, a, sem, ident, ones, stats = (env[k] for k in ("nc", "a", "sem", "ident", "ones", "stats"))
    cv = env["chunk_view"]
    g0, g0b, pself = env["g0"], env["g0b"], env["pself"]
    x_v, tab_v, x1_v = cv(env["x_in"]), cv(env["tab0"]), cv(env["x_d"][0])
    with ExitStack() as ctx:
        sb = lambda n, s, d=F32: ctx.enter_context(nc.sbuf_tensor("b0_" + n, s, d))
        pb = lambda n, s: ctx.enter_context(nc.psum_tensor("b0_" + n, s, F32))
        w2 = sb("w2", [128, 2, C])
        crow = sb("crow", [R, 2, C])
        xt = sb("xt", [R, 2, 2, C])
        ht = sb("ht", [R, 2, 2, TAB0])
        xnT = sb("xnT", [128, 2, 2, CH])
        us = sb("us", [128, 2, 2, CH])
        ds_ = sb("ds", [H0, 2, CH])
        gT = sb("gT", [128, 2, CH])
        dn = sb("dn", [R, 2, H0])
        sc = sb("sc", [R, 2, 2])
        ya = sb("ya", [R, 2, C])
        yb = sb("yb", [R, 2, C])
        xx = sb("xx", [R, 2, C])
        x1 = sb("x1", [R, 2, 2, C])
        xn1 = sb("xn1", [R, 2, 2, C])
        bn, mv, ve, rn, mhalf = (sb("bn", [R, 2, 6]), sb("mv", [R, 2, 2, 2]), sb("ve", [R, 2]), sb("rn", [R, 2, 2]),
                                 sb("mhalf", [R, 2]))
        xT = sb("xT", [128, 2, 2, CH])
        pU, pN, pH, pO, pT = (pb("pU", [R, 512]), pb("pN", [R, 512]), pb("pH", [128, 512]), pb("pO", [R, 512]),
                              pb("pT", [128, 512]))
        pSum = pb("pSum", [128, 512])
        s_w, s_z = sem("b0_weights"), sem("b0_consts")
        s_ld = [sem("b0_load0"), sem("b0_load1")]
        s_st = [sem("b0_store0"), sem("b0_store1")]
        s_sx = [sem("b0_storeT0"), sem("b0_storeT1")]
        s_us, s_U, s_H, s_g, s_O, s_x1, s_var, s_rstd, s_xn1, s_T, s_xT, s_rd, s_sum = (
            sem("b0_" + n) for n in ("sums", "U", "H", "gelu", "O", "x1", "var", "rstd", "xn1", "T", "xT", "read", "xsum"))

        with nc.Block() as block:
            @block.sync
            def _(sp):
                sp.dma_start(w2[:, :, :], a["L0_mix_w2"].rearrange("(k p) n -> p k n", p=128)).then_inc(s_w, 16)
                sp.dma_start(crow[:, 0, :], row_bc(a["L0_gnn_bias"], R)).then_inc(s_w, 16)
                sp.dma_start(crow[:, 1, :], row_bc(a["L0_mix_b2"], R)).then_inc(s_w, 16)
                sp.wait_ge(s_w, 48)

            @block.gpsimd
            def _(pool):
                nc.gpsimd.memset(mhalf[:, :], -0.5)
                pool.drain()

        with nc.Block() as block:
            @block.vector
            def _(v):
                nc.vector.tensor_tensor(out=crow[:, 0, :], in0=crow[:, 0, :], in1=crow[:, 1, :], op=ALU.add)
                v.drain()

        with nc.Block() as block:
            @block.sync
            def _(sp):
                def load(u, s):
                    rows_dma(sp, xt[:, s, :, :], x_v[u], s_ld[s])
                    rows_dma(sp, ht[:, s, :, :], tab_v[u], s_ld[s])
                    sp.dma_start(xnT[:, s, :, :], env["xnT_d"][0][:, :, bass.ds(u * CH, CH)]).then_inc(s_ld[s], 16)

                def store(u, s):
                    sp.wait_ge(s_x1, u + 1)
                    rows_dma(sp, x1_v[u], x1[:, s, :, :], s_st[s])
                    sp.wait_ge(s_xT, u + 1)
                    sp.dma_start(env["xnT_d"][1][:, :, bass.ds(u * CH, CH)], xT[:, s, :, :]).then_inc(s_sx[s], 16)

                def step(u, s, lo, hi):
                    if lo >= 2:
                        sp.wait_ge(s_rd, u - 1)
                        sp.wait_ge(s_H, u - 1)
                    load(u, s)
                    if lo >= 2:
                        store(u - 2, s)
                sweep(sp, CHUNKS, step)
                for u in (CHUNKS - 2, CHUNKS - 1):
                    store(u, u % 2)
                for i in range(2):
                    n = (CHUNKS + 1 - i) // 2
                    sp.wait_ge(s_st[i], 32 * n)
                    sp.wait_ge(s_sx[i], 16 * n)

            @block.scalar
            def _(act):
                def pick(u, s, lo):
                    if lo >= 2:
                        hold(act, s_U, u - 1)
                    nc.scalar.copy(us[:, s, :, :], acc[:, :, bass.ds(u * CH, CH)])
                    nc.scalar.copy(ds_[:, s, :], den[:, bass.ds(u * CH, CH)]).then_inc(s_us, 1)

                def turn(u, s, lo):
                    if lo >= 2:
                        hold(act, s_sx[s], (u // 2) * 16)
                    hold(act, s_T, u + 1)
                    nc.scalar.copy(xT[:, s, :, :], pT[:, 0:2 * CH].rearrange("p (k n) -> p k n", k=2)).then_inc(s_xT, 1)

                def step(u, s, lo, hi):
                    if lo == 0:
                        pick(0, 0, 0)
                    if hi <= CHUNKS - 2:
                        pick(u + 1, 1 - s, lo + 1)
                    if lo >= 1:
                        hold(act, s_O, u)
                    hold(act, s_H, u + 1)
                    for f in range(2):
                        last = nc.scalar.activation(gT[:, f, :], pH[:, f * CH:(f + 1) * CH], ACT.Gelu, bias=g0b[:, f:f + 1])
                    last.then_inc(s_g, 1)
                    if lo >= 1:
                        turn(u - 1, 1 - s, lo - 1)
                    if lo == CHUNKS - 1:
                        turn(u, s, lo)
                sweep(act, CHUNKS, step)

            @block.gpsimd
            def _(pool):
                def step(u, s, lo, hi):
                    hold(pool, s_var, u + 1)
                    nc.gpsimd.tensor_tensor(out=rn[:, :, 0], in0=ve[:, :], in1=mhalf[:, :], op=ALU.pow)\
                      .then_inc(s_rstd, 1)
                sweep(pool, CHUNKS, step)

            @block.vector
            def _(v):
                def finish(u, s, lo):
                    v.wait_ge(s_rstd, u + 1)
                    if lo >= 2:
                        v.wait_ge(s_sum, u - 1)
                    ln_apply(nc, v, xn1[:, s, :, :], x1[:, s, :, :], mv[:, s, :, :], rn).then_inc(s_xn1, 1)
                    nc.vector.tensor_copy(stats[:, bass.ds(u * 2, 2), :], rn[:, :, :])
                    v.drain()

                def step(u, s, lo, hi):
                    if lo >= 1:
                        finish(u - 1, 1 - s, lo - 1)
                    v.wait_ge(s_ld[s], (u // 2 + 1) * 80)
                    nc.vector.tensor_scalar(sc[:, :, 0], stats[:, bass.ds(u * 2, 2), 0], 1.0, None, ALU.add)
                    nc.vector.tensor_copy(sc[:, :, 1], stats[:, bass.ds(u * 2, 2), 1])
                    v.wait_ge(s_U, u + 1)
                    nc.vector.tensor_tensor(out=dn[:, :, :], in0=pN[:, 0:2 * H0].rearrange("p (t h) -> p t h", t=2),
                                            in1=pself[:, bass.ds(u * 2, 2), :], op=ALU.add)
                    v.drain()
                    for t in range(2):
                        nc.vector.tensor_scalar(xx[:, t, :], xt[:, s, t, :], sc[:, t, 0:1], sc[:, t, 1:2],
                                                ALU.mult, ALU.add)
                    nc.vector.reciprocal(dn[:, :, :], dn[:, :, :])
                    nc.vector.tensor_tensor(
                        out=ya[:, :, :].rearrange("p t (h c) -> p t h c", h=H0),
                        in0=ht[:, s, :, 0:C].rearrange("p t (h c) -> p t h c", h=H0),
                        in1=pself[:, bass.ds(u * 2, 2), :].unsqueeze(3).broadcast_to([R, 2, H0, D0]), op=ALU.mult)
                    v.drain()
                    nc.vector.tensor_tensor(out=yb[:, :, :], in0=ya[:, :, :],
                                            in1=pU[:, :].rearrange("p (t c) -> p t c", t=2), op=ALU.add)
                    v.drain().then_inc(s_rd, 1)
                    nc.vector.tensor_tensor(
                        out=ya[:, :, :].rearrange("p t (h c) -> p t h c", h=H0),
                        in0=yb[:, :, :].rearrange("p t (h c) -> p t h c", h=H0),
                        in1=dn[:, :, :].unsqueeze(3).broadcast_to([R, 2, H0, D0]), op=ALU.mult)
                    nc.vector.tensor_tensor(out=xx[:, :, :], in0=xx[:, :, :],
                                            in1=crow[:, 0, :].unsqueeze(1).broadcast_to([R, 2, C]), op=ALU.add)
                    v.drain()
                    nc.vector.tensor_tensor(out=yb[:, :, :], in0=ya[:, :, :], in1=xx[:, :, :], op=ALU.add)
                    v.drain()
                    v.wait_ge(s_O, u + 1)
                    if lo >= 2:
                        v.wait_ge(s_st[s], (u // 2) * 32)
                    nc.vector.tensor_tensor(out=x1[:, s, :, :], in0=yb[:, :, :],
                                            in1=pO[:, :].rearrange("p (t c) -> p t c", t=2), op=ALU.add)
                    v.drain().then_inc(s_x1, 1)
                    ln_stats(nc, v, x1[:, s, :, :], bn, mv[:, s, :, :], ve, s_var)
                    if lo == CHUNKS - 1:
                        finish(u, s, lo)
                sweep(v, CHUNKS, step)

            @block.tensor
            def _(pe):
                def front(u, s, lo):
                    pe.wait_ge(s_us, u + 1)
                    if lo >= 1:
                        pe.wait_ge(s_rd, u)
                    for t in range(2):
                        for k in range(2):
                            nc.tensor.transpose(pU[:, t * C + 128 * k:t * C + 128 * k + 128],
                                                us[:, s, k, t * R:t * R + R], ident[:, :])
                    for t in range(2):
                        last = nc.tensor.transpose(pN[:, t * H0:t * H0 + H0], ds_[:, s, t * R:t * R + R],
                                                   ident[0:H0, 0:H0])
                    last.then_inc(s_U, 1)
                    pe.wait_ge(s_ld[s], (u // 2 + 1) * 80)
                    if lo >= 1:
                        pe.wait_ge(s_g, u)
                    for f in range(2):
                        for k in range(2):
                            last = nc.tensor.matmul(pH[:, f * CH:(f + 1) * CH], g0[:, k, 128 * f:128 * f + 128],
                                                    xnT[:, s, k, :], start=k == 0, stop=k == 1)
                    last.then_inc(s_H, 1)

                def turn(u, s, lo):
                    pe.wait_ge(s_xn1, u + 1)
                    if lo >= 1:
                        pe.wait_ge(s_xT, u)
                    for k in range(2):
                        for t in range(2):
                            last = nc.tensor.transpose(pT[:, k * CH + t * R:k * CH + t * R + R],
                                                       xn1[:, s, t, 128 * k:128 * k + 128], ident[0:R, 0:R])
                    last.then_inc(s_T, 1)
                    for k in range(2):
                        for t in range(2):
                            last = nc.tensor.matmul(pSum[:, k:k + 1], xn1[:, s, t, 128 * k:128 * k + 128], ones[0:R, 0:1],
                                                    start=False, stop=False, skip_group_check=True)
                    last.then_inc(s_sum, 1)

                def step(u, s, lo, hi):
                    if lo == 0:
                        front(0, 0, 0)
                    pe.wait_ge(s_g, u + 1)
                    if lo >= 1:
                        pe.wait_ge(s_x1, u)
                    for t in range(2):
                        for f in range(2):
                            last = nc.tensor.matmul(pO[:, t * C:(t + 1) * C], gT[:, f, t * R:t * R + R], w2[:, f, :],
                                                    start=f == 0, stop=f == 1)
                    last.then_inc(s_O, 1)
                    if hi <= CHUNKS - 2:
                        front(u + 1, 1 - s, lo + 1)
                    if lo >= 1:
                        turn(u - 1, 1 - s, lo - 1)
                    if lo == CHUNKS - 1:
                        turn(u, s, lo)
                nc.tensor.matmul(pSum[:, 0:2], env["zeros"][0:1, 0:128], env["zeros"][0:1, 0:2], start=True, stop=False,
                                 skip_group_check=True)
                sweep(pe, CHUNKS, step)
                pe.drain()

        with nc.Block() as block:
            @block.vector
            def _(v):
                nc.vector.tensor_copy(env["x1sum"][:, :], pSum[:, 0:2])
                v.drain()


def ffn0(env):
    nc, a, sem, ident, ones, stats = (env[k] for k in ("nc", "a", "sem", "ident", "ones", "stats"))
    cv = env["chunk_view"]
    x1_v, x2_v = cv(env["x_d"][0]), cv(env["x_d"][1])
    NF = 2 * F0 // 128
    with ExitStack() as ctx:
        sb = lambda n, s, d=F32: ctx.enter_context(nc.sbuf_tensor("m_" + n, s, d))
        pb = lambda n, s: ctx.enter_context(nc.psum_tensor("m_" + n, s, F32))
        w1 = sb("w1", [128, 2, 2, F0])
        w2 = sb("w2", [128, NF, C])
        b1 = sb("b1", [128, NF])
        b2 = sb("b2", [R, 3, C])
        gam = sb("gam", [R, 2, C])
        wr = sb("wr", [128, 2, E8])
        br = sb("br", [1, E8])
        lg = sb("lg", [1, 8, E8])
        sm = sb("sm", [1, 8])
        ei = sb("ei", [1, 8], U32)
        wB = sb("wB", [128, 2])
        xnT = sb("xnT", [128, 2, 2, CH])
        x1 = sb("x1", [R, 2, 2, C])
        hT = sb("hT", [128, NF, CH])
        ya = sb("ya", [R, 2, C])
        yb = sb("yb", [R, 2, C])
        xnb = sb("xnb", [R, 2, C])
        x2 = sb("x2", [R, 2, 2, C])
        xn2 = sb("xn2", [R, 2, 2, C])
        sc = sb("sc", [R, 2, 2])
        bn, mv, ve, rn, mhalf = (sb("bn", [R, 2, 6]), sb("mv", [R, 2, 2]), sb("ve", [R, 2]), sb("rn", [R, 2, 2]),
                                 sb("mhalf", [R, 2]))
        xT = sb("xT", [128, 2, 2, CH])
        pH, pO, pT = pb("pH", [128, NF // 2, 512]), pb("pO", [R, 512]), pb("pT", [128, 512])
        s_w, s_l, s_act, s_l2, s_e, s_wb = (sem("m_" + n) for n in ("weights", "logits", "exp", "l2", "experts", "wB"))
        s_ld = [sem("m_load0"), sem("m_load1")]
        s_st = [sem("m_store0"), sem("m_store1")]
        s_sx = [sem("m_storeT0"), sem("m_storeT1")]
        s_H, s_g, s_O, s_Or, s_x2, s_var, s_rstd, s_xn2, s_T, s_xT = (
            sem("m_" + n) for n in ("H", "gelu", "O", "Oread", "x2", "var", "rstd", "xn2", "T", "xT"))

        with nc.Block() as block:
            @block.sync
            def _(sp):
                sp.dma_start(wr[:, :, :], a["L0_ffn_Wr"].rearrange("(k p) n -> p k n", p=128)).then_inc(s_w, 16)
                sp.dma_start(br[:, :], row_bc(a["L0_ffn_br"], 1)).then_inc(s_w, 16)
                sp.dma_start(gam[:, 0, :], row_bc(a["L0_ffn_gamma"], R)).then_inc(s_w, 16)
                sp.dma_start(gam[:, 1, :], row_bc(a["L0_ffn_beta"], R)).then_inc(s_w, 16)
                sp.wait_ge(s_w, 64)
                sp.wait_ge(s_e, 1)
                for j in range(2):
                    e = sp.value_load(ei[0:1, j:j + 1], min_val=0, max_val=E8 - 1)
                    ix = bass.ds(e, 1)
                    sp.dma_start(w1[:, j, :, :], a["L0_ffn_W1"][ix].rearrange("e (k p) f -> p (e k) f", p=128))\
                      .then_inc(s_w, 16)
                    sp.dma_start(w2[:, j * NF // 2:(j + 1) * NF // 2, :],
                                 a["L0_ffn_W2"][ix].rearrange("e (f p) n -> p (e f) n", p=128)).then_inc(s_w, 16)
                    sp.dma_start(b1[:, j * NF // 2:(j + 1) * NF // 2],
                                 a["L0_ffn_b1"][ix].rearrange("e (f p) -> p (e f)", p=128)).then_inc(s_w, 16)
                    sp.dma_start(b2[:, j, :], a["L0_ffn_b2"][ix].broadcast_to([R, C])).then_inc(s_w, 16)
                sp.wait_ge(s_w, 64 + 128)

            @block.gpsimd
            def _(pool):
                nc.gpsimd.memset(mhalf[:, :], -0.5)
                pool.drain()

            @block.tensor
            def _(pe):
                pe.wait_ge(s_w, 64)
                for k in range(2):
                    last = nc.tensor.matmul(pO[0:1, 0:E8], env["x1sum"][:, k:k + 1], wr[:, k, :], start=k == 0, stop=k == 1)
                last.then_inc(s_l, 1)
                pe.wait_ge(s_wb, 1)
                nc.tensor.matmul(pT[:, 0:2], ones[0:1, :], sm[0:1, 6:8], start=True, stop=True).then_inc(s_l, 1)

            @block.scalar
            def _(act):
                for n, (i, w) in enumerate(((1, E8), (3, E8), (6, 2))):
                    act.wait_ge(s_l2, n + 1)
                    nc.scalar.activation(lg[:, i, 0:w], lg[:, i, 0:w], ACT.Exp).then_inc(s_act, 1)

            @block.vector
            def _(v):
                ts, tt = nc.vector.tensor_scalar, nc.vector.tensor_tensor
                v.wait_ge(s_w, 64)
                v.wait_ge(s_l, 1)
                nc.vector.scalar_tensor_tensor(out=lg[:, 0, :], in0=pO[0:1, 0:E8], scalar=1.0 / N, in1=br[:, :],
                                               op0=ALU.mult, op1=ALU.add)
                v.drain()

                def softmax(src, dst, n, w, m):
                    nc.vector.tensor_reduce(sm[:, m:m + 1], lg[:, src, 0:w], AX.X, ALU.max)
                    v.drain()
                    ts(lg[:, dst, 0:w], lg[:, src, 0:w], sm[:, m:m + 1], None, ALU.subtract).then_inc(s_l2, 1)
                    v.wait_ge(s_act, n + 1)
                    nc.vector.tensor_reduce(sm[:, m + 1:m + 2], lg[:, dst, 0:w], AX.X, ALU.add)
                    v.drain()
                    nc.vector.reciprocal(sm[:, m + 1:m + 2], sm[:, m + 1:m + 2])
                    v.drain()

                softmax(0, 1, 0, E8, 0)
                ts(lg[:, 1, :], lg[:, 1, :], sm[:, 1:2], None, ALU.mult)
                v.drain()
                ts(lg[:, 2, :], lg[:, 1, :], float(N) / CAPACITY, None, ALU.mult)
                v.drain()
                nc.vector.reciprocal(lg[:, 2, :], lg[:, 2, :])
                v.drain()
                ts(lg[:, 2, :], lg[:, 2, :], 1.0, None, ALU.min)
                v.drain()
                tt(out=lg[:, 4, :], in0=lg[:, 1, :], in1=lg[:, 2, :], op=ALU.mult)
                v.drain()
                softmax(4, 3, 1, E8, 2)
                ts(lg[:, 3, :], lg[:, 3, :], sm[:, 3:4], None, ALU.mult)
                v.drain()
                nc.vector.max(lg[:, 5, :], lg[:, 3, :])
                v.drain()
                nc.vector.max_index(ei[:, :], lg[:, 5, :], lg[:, 3, :])
                v.drain().then_inc(s_e, 1)
                softmax(5, 6, 2, 2, 4)
                ts(sm[:, 6:8], lg[:, 6, 0:2], sm[:, 5:6], None, ALU.mult)
                v.drain().then_inc(s_wb, 1)
                v.wait_ge(s_l, 2)
                nc.vector.tensor_copy(wB[:, :], pT[:, 0:2])
                v.drain()
                v.wait_ge(s_w, 64 + 128)
                for j in range(2):
                    w = w2[:, j * NF // 2:(j + 1) * NF // 2, :]
                    ts(w, w, wB[:, j:j + 1], None, ALU.mult)
                ts(b2[:, 2, :], b2[:, 0, :], wB[0:R, 0:1], None, ALU.mult)
                v.drain()
                nc.vector.scalar_tensor_tensor(out=b2[:, 0, :], in0=b2[:, 1, :], scalar=wB[0:R, 1:2], in1=b2[:, 2, :],
                                               op0=ALU.mult, op1=ALU.add)
                v.drain()

        with nc.Block() as block:
            @block.sync
            def _(sp):
                def load(u, s):
                    rows_dma(sp, x1[:, s, :, :], x1_v[u], s_ld[s])
                    sp.dma_start(xnT[:, s, :, :], env["xnT_d"][1][:, :, bass.ds(u * CH, CH)]).then_inc(s_ld[s], 16)

                def store(u, s):
                    sp.wait_ge(s_x2, u + 1)
                    rows_dma(sp, x2_v[u], x2[:, s, :, :], s_st[s])
                    sp.wait_ge(s_xT, u + 1)
                    sp.dma_start(env["xnT_d"][2][:, :, bass.ds(u * CH, CH)], xT[:, s, :, :]).then_inc(s_sx[s], 16)

                def step(u, s, lo, hi):
                    if lo >= 2:
                        sp.wait_ge(s_x2, u - 1)
                        sp.wait_ge(s_H, u - 1)
                    load(u, s)
                    if lo >= 2:
                        store(u - 2, s)
                sweep(sp, CHUNKS, step)
                for u in (CHUNKS - 2, CHUNKS - 1):
                    store(u, u % 2)
                for i in range(2):
                    n = (CHUNKS + 1 - i) // 2
                    sp.wait_ge(s_st[i], 32 * n)
                    sp.wait_ge(s_sx[i], 16 * n)

            @block.scalar
            def _(act):
                def turn(u, s, lo):
                    if lo >= 2:
                        hold(act, s_sx[s], (u // 2) * 16)
                    hold(act, s_T, u + 1)
                    nc.scalar.copy(xT[:, s, :, :], pT[:, 0:2 * CH].rearrange("p (k n) -> p k n", k=2)).then_inc(s_xT, 1)

                def step(u, s, lo, hi):
                    if lo >= 1:
                        hold(act, s_O, u)
                    for f in range(NF):
                        if f % 2 == 0:
                            hold(act, s_H, NF // 2 * u + f // 2 + 1)
                        x = nc.scalar.activation(hT[:, f, :], pH[:, f // 2, (f % 2) * CH:(f % 2 + 1) * CH], ACT.Gelu,
                                                 bias=b1[:, f:f + 1])
                        if f % 2:
                            x.then_inc(s_g, 1)
                    if lo >= 1:
                        turn(u - 1, 1 - s, lo - 1)
                    if lo == CHUNKS - 1:
                        turn(u, s, lo)
                sweep(act, CHUNKS, step)

            @block.gpsimd
            def _(pool):
                def step(u, s, lo, hi):
                    for i in range(2):
                        hold(pool, s_var, 2 * u + i + 1)
                        nc.gpsimd.tensor_tensor(out=rn[:, :, 0], in0=ve[:, :], in1=mhalf[:, :], op=ALU.pow)\
                          .then_inc(s_rstd, 1)
                sweep(pool, CHUNKS, step)

            @block.vector
            def _(v):
                def step(u, s, lo, hi):
                    v.wait_ge(s_ld[s], (u // 2 + 1) * 48)
                    nc.vector.tensor_copy(sc[:, :, :], stats[:, bass.ds(u * 2, 2), :])
                    v.drain()
                    for t in range(2):
                        nc.vector.tensor_scalar(xnb[:, t, :], x1[:, s, t, :], sc[:, t, 0:1], sc[:, t, 1:2],
                                                ALU.mult, ALU.add)
                    v.drain()
                    nc.vector.tensor_tensor(out=ya[:, :, :], in0=xnb[:, :, :],
                                            in1=b2[:, 0, :].unsqueeze(1).broadcast_to([R, 2, C]), op=ALU.add)
                    v.drain()
                    v.wait_ge(s_O, u + 1)
                    nc.vector.tensor_tensor(out=yb[:, :, :], in0=ya[:, :, :],
                                            in1=pO[:, :].rearrange("p (t c) -> p t c", t=2), op=ALU.add)
                    v.drain().then_inc(s_Or, 1)
                    ln_stats(nc, v, yb, bn, mv, ve, s_var)
                    v.wait_ge(s_rstd, 2 * u + 1)
                    ln_apply(nc, v, ya, yb, mv, rn)
                    v.drain()
                    nc.vector.tensor_tensor(out=yb[:, :, :], in0=ya[:, :, :],
                                            in1=gam[:, 0, :].unsqueeze(1).broadcast_to([R, 2, C]), op=ALU.mult)
                    nc.vector.tensor_tensor(out=xnb[:, :, :], in0=x1[:, s, :, :],
                                            in1=gam[:, 1, :].unsqueeze(1).broadcast_to([R, 2, C]), op=ALU.add)
                    v.drain()
                    if lo >= 2:
                        v.wait_ge(s_st[s], (u // 2) * 32)
                    nc.vector.tensor_tensor(out=x2[:, s, :, :], in0=xnb[:, :, :], in1=yb[:, :, :], op=ALU.add)
                    v.drain().then_inc(s_x2, 1)
                    ln_stats(nc, v, x2[:, s, :, :], bn, mv, ve, s_var)
                    v.wait_ge(s_rstd, 2 * u + 2)
                    if lo >= 2:
                        v.wait_ge(s_T, u - 1)
                    ln_apply(nc, v, xn2[:, s, :, :], x2[:, s, :, :], mv, rn).then_inc(s_xn2, 1)
                    nc.vector.tensor_copy(stats[:, bass.ds(u * 2, 2), :], rn[:, :, :])
                    v.drain()
                sweep(v, CHUNKS, step)

            @block.tensor
            def _(pe):
                def hidden(u, s, lo):
                    pe.wait_ge(s_ld[s], (u // 2 + 1) * 48)
                    for f in range(NF):
                        if f % 2 == 0 and lo >= 1:
                            pe.wait_ge(s_g, NF // 2 * (u - 1) + f // 2 + 1)
                        j, c = f // (NF // 2), f % (NF // 2)
                        for k in range(2):
                            last = nc.tensor.matmul(pH[:, f // 2, (f % 2) * CH:(f % 2 + 1) * CH],
                                                    w1[:, j, k, 128 * c:128 * c + 128], xnT[:, s, k, :],
                                                    start=k == 0, stop=k == 1)
                        if f % 2:
                            last.then_inc(s_H, 1)

                def output(u, s, lo):
                    if lo >= 1:
                        pe.wait_ge(s_Or, u)
                    for t in range(2):
                        for f in range(NF):
                            if t == 0 and f % 2 == 0:
                                pe.wait_ge(s_g, NF // 2 * u + f // 2 + 1)
                            last = nc.tensor.matmul(pO[:, t * C:(t + 1) * C], hT[:, f, t * R:t * R + R], w2[:, f, :],
                                                    start=f == 0, stop=f == NF - 1)
                    last.then_inc(s_O, 1)

                def turn(u, s, lo):
                    pe.wait_ge(s_xn2, u + 1)
                    if lo >= 1:
                        pe.wait_ge(s_xT, u)
                    for k in range(2):
                        for t in range(2):
                            last = nc.tensor.transpose(pT[:, k * CH + t * R:k * CH + t * R + R],
                                                       xn2[:, s, t, 128 * k:128 * k + 128], ident[0:R, 0:R])
                    last.then_inc(s_T, 1)

                def step(u, s, lo, hi):
                    if lo == 0:
                        hidden(0, 0, 0)
                    if hi <= CHUNKS - 2:
                        hidden(u + 1, 1 - s, lo + 1)
                    output(u, s, lo)
                    if lo >= 1:
                        turn(u - 1, 1 - s, lo - 1)
                    if lo == CHUNKS - 1:
                        turn(u, s, lo)
                sweep(pe, CHUNKS, step)


def front1(env):
    nc, a, sem, ident, ones = (env[k] for k in ("nc", "a", "sem", "ident", "ones"))
    cv = env["chunk_view"]
    tab_v = cv(env["tab1"])
    g1, attr = env["g1"], env["attr"]
    HID = 512
    with ExitStack() as ctx:
        sb = lambda n, s, d=F32: ctx.enter_context(nc.sbuf_tensor("f1_" + n, s, d))
        wq = sb("wq", [128, 4, C])
        wk = sb("wk", [128, 8, C])
        wo = sb("wo", [128, 2, HID])
        wkv = sb("wkv", [128, 2, 2 * HID])
        woT = sb("woT", [128, 4, C])
        lin = sb("lin", [128, 2, C])
        cm = sb("cm", [128, 2, 16])
        xnT = sb("xnT", [128, 2, 2, CH])
        trow = sb("trow", [R, 2, 2, C])
        sq = sb("sq", [R, HID])
        ss = sb("ss", [R, 8])
        sd = sb("sd", [R, 8])
        ri = sb("ri", [R, 8])
        kvn = sb("kvn", [R, 2, 2 * HID])
        epst = sb("epst", [128, 1])
        mask = sb("mask", [128, 128])
        dT = sb("dT", [128, 4, 128])
        m1 = sb("m1", [128, 4, C])
        pb = lambda n, s: ctx.enter_context(nc.psum_tensor("f1_" + n, s, F32))
        pA, pKV, pY, pS = pb("pA", [128, 2, 512]), pb("pKV", [128, 3, 512]), pb("pY", [R, 512]), pb("pS", [128, 512])
        s_w, s_c, s_t, s_tc, s_m = (sem("f1_" + n) for n in ("weights", "consts", "T", "Tc", "mask"))
        s_ld = [sem("f1_load0"), sem("f1_load1")]
        s_st = [sem("f1_store0"), sem("f1_store1")]
        s_kv, s_sq, s_ss, s_sd, s_kvn, s_acc, s_Y, s_row = (
            sem("f1_" + n) for n in ("kv", "sq", "ss", "sd", "kvn", "acc", "Y", "rows"))
        s_dT, s_M, s_m1, s_G = (sem("f1_" + n) for n in ("dT", "M", "m1", "G"))
        wqkv = a["L1_mix_Wqkv"].rearrange("(i p) k -> p i k", p=128)

        with nc.Block() as block:
            @block.gpsimd
            def _(pool):
                nc.gpsimd.memset(lin[:, :, :], 0.0).then_inc(s_c, 1)
                nc.gpsimd.memset(epst[:, :], EPS)
                nc.gpsimd.memset(mask[:, :], 0.0)
                pool.drain()
                for h in range(2):
                    nc.gpsimd.memset(mask[64 * h:64 * h + 64, 64 * h:64 * h + 64], 1.0 / N)
                    pool.drain()

            @block.sync
            def _(sp):
                sp.dma_start(wq[:, :, :], wqkv[:, 0:4, :]).then_inc(s_w, 16)
                sp.dma_start(wk[:, :, :], wqkv[:, 4:12, :]).then_inc(s_w, 16)
                sp.dma_start(wo[:, :, :], a["L1_mix_Wout"].rearrange("(k p) f -> p k f", p=128)).then_inc(s_w, 16)
                sp.dma_start(attr[:, :], a["node_vec1"].rearrange("(t p) o -> p (t o)", p=R)).then_inc(s_w, 16)
                sp.wait_ge(s_c, 1)
                sp.dma_start(lin[0:64, 0, 0:64], a["L1_gnn_lin1_w0"]).then_inc(s_w, 16)
                for k, p, c, u, n in vector_rows():
                    sp.dma_start(lin[p:p + 3 * (n - 1) + 1:3, k, 64 + 64 * c:128 + 64 * c],
                                 a["L1_gnn_lin1_w1"][u:u + n, :]).then_inc(s_w, 16)
                sp.wait_ge(s_w, 16 * (5 + len(vector_rows())))

            @block.tensor
            def _(pe):
                n = 0
                pe.wait_ge(s_w, 16 * (5 + len(vector_rows())))
                for src, rows in ((wk, 8), (wo, 2)):
                    for i in range(rows):
                        for k in range(2 if rows == 8 else 4):
                            if n >= 2:
                                pe.wait_ge(s_tc, n - 1)
                            nc.tensor.transpose(pA[:, n % 2, 0:128], src[:, i, 128 * k:128 * k + 128], ident[:, :])\
                              .then_inc(s_t, 1)
                            n += 1

            @block.vector
            def _(v):
                n = 0
                for rows in (8, 2):
                    for i in range(rows):
                        for k in range(2 if rows == 8 else 4):
                            dst = wkv[:, k, 128 * i:128 * i + 128] if rows == 8 else woT[:, k, 128 * i:128 * i + 128]
                            v.wait_ge(s_t, n + 1)
                            nc.vector.tensor_copy(dst, pA[:, n % 2, 0:128]).then_inc(s_tc, 1)
                            n += 1
                v.drain()
                for k in range(2):
                    w = wkv[:, k, :].rearrange("p (h d) -> p h d", d=64)
                    nc.vector.tensor_reduce(cm[:, k, :], w, AX.X, ALU.add)
                    v.drain()
                    nc.vector.tensor_scalar(cm[:, k, :], cm[:, k, :], -1.0 / 64, None, ALU.mult)
                    v.drain()
                    nc.vector.tensor_tensor(out=w, in0=w, in1=cm[:, k, :].unsqueeze(2).broadcast_to([128, 16, 64]),
                                            op=ALU.add)
                    v.drain()
                nc.vector.tensor_scalar(lin[:, :, :], lin[:, :, :], 0.125, None, ALU.mult)
                v.drain()

        with nc.Block() as block:
            @block.sync
            def _(sp):
                def store(u, s):
                    sp.wait_ge(s_row, u + 1)
                    rows_dma(sp, tab_v[u], trow[:, s, :, :], s_st[s])

                def step(u, s, lo, hi):
                    if lo >= 2:
                        sp.wait_ge(s_Y, u - 1)
                    sp.dma_start(xnT[:, s, :, :], env["xnT_d"][2][:, :, bass.ds(u * CH, CH)]).then_inc(s_ld[s], 16)
                    if lo >= 1:
                        store(u - 1, 1 - s)
                    if lo == CHUNKS - 1:
                        store(u, s)
                sweep(sp, CHUNKS, step)
                for i in range(2):
                    sp.wait_ge(s_st[i], 32 * ((CHUNKS + 1 - i) // 2))

            @block.tensor
            def _(pe):
                def sums(u, t):
                    i = u * 2 + t
                    pe.wait_ge(s_kvn, 2 * i + 2)
                    for g in range(4):
                        last = nc.tensor.matmul(pS[:, 128 * g:128 * g + 128], kvn[:, t, HID + 128 * g:HID + 128 * g + 128],
                                                kvn[:, t, 128 * g:128 * g + 128], start=False, stop=False,
                                                skip_group_check=True)
                    last.then_inc(s_acc, 1)

                def step(u, s, lo, hi):
                    pe.wait_ge(s_ld[s], (u // 2 + 1) * 16)
                    for t in range(2):
                        for b in range(2):
                            hh = u * 4 + 2 * t + b
                            if lo >= 1 or t == 1:
                                pe.wait_ge(s_kvn, hh - 1)
                            for k in range(2):
                                last = nc.tensor.matmul(pKV[0:R, b, :], xnT[:, s, k, t * R:t * R + R],
                                                        wkv[:, k, HID * b:HID * b + HID], start=k == 0, stop=k == 1)
                            last.then_inc(s_kv, 1)
                        if t == 0:
                            if lo >= 1:
                                pe.wait_ge(s_row, u)
                            for q in range(2):
                                for k in range(2):
                                    last = nc.tensor.matmul(pY[:, q * C:q * C + C], xnT[:, s, k, q * R:q * R + R],
                                                            lin[:, k, :], start=k == 0, stop=k == 1)
                            if lo >= 1:
                                sums(u - 1, 1)
                        else:
                            sums(u, 0)
                    pe.drain().then_inc(s_Y, 1)

                nc.tensor.matmul(pS[:, :], env["zeros"][0:1, 0:128], env["zeros"][0:1, :], start=True, stop=False,
                                 skip_group_check=True)
                sweep(pe, CHUNKS, step)
                sums(CHUNKS - 1, 1)
                pe.drain()

            @block.scalar
            def _(act):
                def step(u, s, lo, hi):
                    for t in range(2):
                        for b in range(2):
                            hh = u * 4 + 2 * t + b
                            hold(act, s_kv, hh + 1)
                            if lo >= 1 or t + b > 0:
                                hold(act, s_ss, hh)
                            nc.scalar.activation(sq[:, :], pKV[0:R, b, :], ACT.Square).then_inc(s_sq, 1)
                            hold(act, s_ss, hh + 1)
                            nc.scalar.activation(sd[:, :], ss[:, :], ACT.Sqrt, bias=epst[0:R, :], scale=1.0 / 64)\
                              .then_inc(s_sd, 1)
                    if lo >= 2:
                        hold(act, s_st[s], (u // 2) * 32)
                    hold(act, s_Y, u + 1)
                    for t in range(2):
                        last = nc.scalar.activation(trow[:, s, t, :], pY[:, t * C:t * C + C], ACT.Copy,
                                                    scale=attr[:, bass.ds(u * 2 + t, 1)])
                    last.then_inc(s_row, 1)
                sweep(act, CHUNKS, step)

            @block.vector
            def _(v):
                def step(u, s, lo, hi):
                    for t in range(2):
                        for b in range(2):
                            hh = u * 4 + 2 * t + b
                            v.wait_ge(s_sq, hh + 1)
                            nc.vector.tensor_reduce(ss[:, :], sq[:, :].rearrange("p (h d) -> p h d", d=64), AX.X, ALU.add)\
                              .then_inc(s_ss, 1)
                            v.wait_ge(s_sd, hh + 1)
                            nc.vector.reciprocal(ri[:, :], sd[:, :])
                            v.drain()
                            if lo >= 1:
                                v.wait_ge(s_acc, u * 2 + t - 1)
                            nc.vector.tensor_tensor(
                                out=kvn[:, t, HID * b:HID * b + HID].rearrange("p (h d) -> p h d", d=64),
                                in0=pKV[0:R, b, :].rearrange("p (h d) -> p h d", d=64),
                                in1=ri[:, :].unsqueeze(2).broadcast_to([R, 8, 64]), op=ALU.mult).then_inc(s_kvn, 1)
                sweep(v, CHUNKS, step)

        with nc.Block() as block:
            @block.vector
            def _(v):
                for g in range(4):
                    nc.vector.tensor_tensor(out=dT[:, g, :], in0=pS[:, 128 * g:128 * g + 128], in1=mask[:, :], op=ALU.mult)
                v.drain().then_inc(s_dT, 1)
                for g in range(4):
                    v.wait_ge(s_M, g + 1)
                    nc.vector.tensor_copy(m1[:, g, :], pA[:, g % 2, 0:C]).then_inc(s_m1, 1)
                v.wait_ge(s_G, 1)
                nc.vector.tensor_copy(g1[:, :, :], pKV[:, 0:2, 0:C])
                v.drain()

            @block.tensor
            def _(pe):
                pe.wait_ge(s_dT, 1)
                for g in range(4):
                    if g >= 2:
                        pe.wait_ge(s_m1, g - 1)
                    nc.tensor.matmul(pA[:, g % 2, 0:C], dT[:, g, :], woT[:, g, :], start=True, stop=True).then_inc(s_M, 1)
                pe.wait_ge(s_m1, 4)
                for k in range(2):
                    for g in range(4):
                        last = nc.tensor.matmul(pKV[:, k, 0:C], wq[:, g, 128 * k:128 * k + 128], m1[:, g, :],
                                                start=g == 0, stop=g == 3)
                last.then_inc(s_G, 1)


def vector_rows():
    runs = []
    for c in range(3):
        for k in range(2):
            us = [u for u in range(64) if (64 + 3 * u + c) // 128 == k]
            runs.append((k, (64 + 3 * us[0] + c) % 128, c, us[0], len(us)))
    return runs


def edge_attrs(env, ea):
    nc, a, sem, ident = (env[k] for k in ("nc", "a", "sem", "ident"))
    with ExitStack() as ctx:
        st = ctx.enter_context(nc.sbuf_tensor("ea_st", [QB, NB, R * 4], F32))
        sc = ctx.enter_context(nc.sbuf_tensor("ea_sc", [QB, 4, NB, R], F32))
        pt = ctx.enter_context(nc.psum_tensor("ea_pt", [R, 8, 512], F32))
        s_ld, s_c, s_t, s_ev = sem("ea_load"), sem("ea_split"), sem("ea_T"), sem("ea_copied")
        with nc.Block() as block:
            @block.sync
            def _(sp):
                sp.dma_start(st[:, :, :], a["edge_attr_4"].rearrange("(b q e) c -> q b (e c)", q=QB, e=R)).then_inc(s_ld, 16)
                sp.wait_ge(s_ld, 16)

            @block.vector
            def _(v):
                v.wait_ge(s_ld, 16)
                for c in range(4):
                    nc.vector.tensor_copy(sc[:, c, :, :], st[:, :, :].rearrange("q b (e c) -> q b e c", c=4)[:, :, :, c])\
                      .then_inc(s_c, 1)
                for c in range(4):
                    for b in range(NB):
                        n = c * NB + b
                        v.wait_ge(s_t, n + 1)
                        nc.vector.tensor_copy(ea[:, QB * b:QB * (b + 1), c], pt[:, n % 8, 0:QB]).then_inc(s_ev, 1)
                v.drain()

            @block.tensor
            def _(pe):
                for c in range(4):
                    pe.wait_ge(s_c, c + 1)
                    for b in range(NB):
                        n = c * NB + b
                        if n >= 8:
                            pe.wait_ge(s_ev, n - 7)
                        nc.tensor.transpose(pt[:, n % 8, 0:QB], sc[:, c, b, :], ident[0:QB, 0:QB]).then_inc(s_t, 1)


def edges1(env, z, ea):
    nc, a, sem, ident = (env[k] for k in ("nc", "a", "sem", "ident"))
    srcI, baseI = env["srcI"], env["baseI"]
    PAIRS = (GT + 1) // 2
    with ExitStack() as ctx:
        sb = lambda n, s, d=F32: ctx.enter_context(nc.sbuf_tensor("e1_" + n, s, d))
        pb = lambda n, s: ctx.enter_context(nc.psum_tensor("e1_" + n, s, F32))
        ix = sb("ix", [R, 2, GT], I32)
        rows = sb("rows", [R, 2, GT, C])
        es = sb("es", [R, 2, GT, 8])
        esT = sb("esT", [8 * GT, 2, R])
        w1 = sb("w1", [8 * GT, PAIRS, 128])
        w2 = sb("w2", [128, 2, C])
        hT = sb("hT", [128, 2, PAIRS, R])
        ohu = sb("ohu", [R, GT, W])
        oh = sb("oh", [R, 2, GT, 4, W])
        msg = sb("msg", [R, 2, GT, 8, 64])
        pT, pH, pW, pZ = pb("pT", [8 * GT, 512]), pb("pH", [128, 512]), pb("pW", [R, 3, 512]), pb("pZ", [128, 2, 512])
        s_wt, s_wz = sem("e1_weights"), sem("e1_zeroed")
        s_gat = [sem(f"e1_rows{i}", software_dma=True) for i in range(2)]
        s_es = [sem("e1_es0"), sem("e1_es1")]
        s_ix, s_T, s_esT, s_F, s_h, s_W, s_msg, s_oh, s_acc, s_add = (
            sem("e1_" + n) for n in ("ix", "T", "esT", "F", "silu", "W", "msg", "oh", "acc", "added"))
        SILU_NORM = 1.679
        blk = lambda s, j, i: msg[:, s, j, :, :].rearrange("p b c -> p (b c)")[:, 64 * i:64 * i + 64]

        with nc.Block() as block:
            @block.gpsimd
            def _(pool):
                nc.gpsimd.memset(w1[:, :, :], 0.0)
                nc.gpsimd.memset(w2[:, :, :], 0.0)
                pool.drain().then_inc(s_wz, 1)

            @block.sync
            def _(sp):
                sp.wait_ge(s_wz, 1)
                for j in range(GT):
                    sp.dma_start(w1[8 * j:8 * j + 8, j // 2, 64 * (j % 2):64 * (j % 2) + 64], a["L1_gnn_fc_w1"])\
                      .then_inc(s_wt, 16)
                for r in range(2):
                    for i, b in enumerate((0, 3, 2, 1)):
                        sp.dma_start(w2[64 * r:64 * r + 64, r, 64 * i:64 * i + 64],
                                     a["L1_gnn_fc_w2"][:, 64 * b:64 * b + 64]).then_inc(s_wt, 16)
                sp.wait_ge(s_wt, 16 * (GT + 8))

        with nc.Block() as block:
            @block.vector
            def _(v):
                nc.vector.tensor_scalar(w2[:, :, :], w2[:, :, :], SILU_NORM / 8.0, None, ALU.mult)
                v.drain()
        es_v = a["edge_attr_8"].rearrange("(g j p) f -> g p j f", j=GT, p=R)

        def one_pass():
            with nc.Block() as block:
                @block.gpsimd
                def _(pool):
                    def step(g, s, lo, hi):
                        hold(pool, s_ix, g + 1)
                        for j in range(GT):
                            nc.gpsimd.indirect_dma_start(
                                out=rows[:, s, j, :], out_offset=None, in_=env["tab1"],
                                in_offset=bass.IndirectOffsetOnAxis(ap=ix[:, s, j:j + 1], axis=0))\
                              .then_inc(s_gat[s], 16)
                    sweep(pool, GROUPS, step)

                @block.sync
                def _(sp):
                    def step(g, s, lo, hi):
                        if lo >= 2:
                            sp.wait_ge(s_T, g - 1)
                        rows_dma(sp, es[:, s, :, :], es_v[g], s_es[s])
                    sweep(sp, GROUPS, step)

                @block.scalar
                def _(act):
                    def front(g, s, lo):
                        if lo >= 2:
                            hold(act, s_msg, PAIRS * (g - 1))
                        nc.scalar.copy(ix[:, s, :], srcI[:, bass.ds(g * GT, GT)]).then_inc(s_ix, 1)
                        hold(act, s_T, g + 1)
                        if lo >= 2:
                            hold(act, s_F, g - 1)
                        nc.scalar.copy(esT[:, s, :], pT[:, 0:R]).then_inc(s_esT, 1)
                        if lo >= 2:
                            hold(act, s_W, PAIRS * (g - 1))
                        hold(act, s_F, g + 1)
                        nc.scalar.activation(hT[:, s, :, :],
                                             pH[:, 0:128 * PAIRS].rearrange("p (i e) -> p i e", e=128)[:, :, 0:R],
                                             ACT.Silu, scale=8.0 ** -0.5).then_inc(s_h, 1)

                    sweep(act, GROUPS, lambda g, s, lo, hi: front(g, s, lo))

                @block.vector
                def _(v):
                    def add(g, s):
                        base = v.value_load(baseI[0:1, bass.ds(g, 1)], min_val=0, max_val=N)
                        v.wait_ge(s_acc, g + 1)
                        w = z[:, :, bass.ds(base, W)]
                        nc.vector.tensor_tensor(out=w, in0=w, in1=pZ[:, s, 0:4 * W].rearrange("p (k n) -> p k n", k=4),
                                                op=ALU.add).then_inc(s_add, 1)

                    def step(g, s, lo, hi):
                        if lo >= 2:
                            add(g - 2, s)
                        if lo >= 1:
                            v.wait_ge(s_oh, g)
                        one_hots(nc, env, ohu[:, :, :], g)
                        v.drain()
                        nc.vector.tensor_tensor(
                            out=oh[:, s, :, :, :], in0=ohu[:, :, :].unsqueeze(2).broadcast_to([R, GT, 4, W]),
                            in1=ea[:, bass.ds(g * GT, GT), :].unsqueeze(3).broadcast_to([R, GT, 4, W]), op=ALU.mult)\
                          .then_inc(s_oh, 1)
                        v.wait_ge(s_gat[s], (g // 2 + 1) * 16 * GT)
                        for j in range(GT):
                            if j % 2 == 0:
                                v.wait_ge(s_W, g * PAIRS + j // 2 + 1)
                            wj = pW[:, j // 2, 256 * (j % 2):256 * (j % 2) + 256]
                            wa = wj.rearrange("p (b q c) -> p b q c", b=2, q=2)
                            m = msg[:, s, j, :, :].rearrange("p (b q) c -> p b q c", b=2)
                            nc.vector.tensor_tensor(out=m[:, :, 0, :], in0=wa[:, :, 0, :],
                                                    in1=rows[:, s, j, 0:64].unsqueeze(1).broadcast_to([R, 2, 64]),
                                                    op=ALU.mult)
                            last = nc.vector.tensor_tensor(
                                out=m[:, :, 1:4, :], in0=wa[:, :, 1:2, :].broadcast_to([R, 2, 3, 64]),
                                in1=rows[:, s, j, 64:256].rearrange("p (q c) -> p q c", q=3).unsqueeze(1)
                                .broadcast_to([R, 2, 3, 64]), op=ALU.mult)
                            if j % 2 or j == GT - 1:
                                last.then_inc(s_msg, 1)
                        if lo == GROUPS - 1:
                            v.drain()
                            add(GROUPS - 2, 1 - s)
                            v.drain()
                            add(GROUPS - 1, s)
                            v.drain()
                    sweep(v, GROUPS, step)

                @block.tensor
                def _(pe):
                    def front(g, s, lo):
                        if lo >= 1:
                            pe.wait_ge(s_esT, g)
                        hold(pe, s_es[s], (g // 2 + 1) * 32)
                        nc.tensor.transpose(pT[:, 0:R], es[:, s, :, :].rearrange("p j f -> p (j f)"), ident[0:R, 0:R])\
                          .then_inc(s_T, 1)
                        if lo >= 1:
                            pe.wait_ge(s_h, g)
                        hold(pe, s_esT, g + 1)
                        for i in range(PAIRS):
                            last = nc.tensor.matmul(pH[:, 128 * i:128 * i + R], w1[:, i, :], esT[:, s, :],
                                                    start=True, stop=True)
                        last.then_inc(s_F, 1)

                    def second(g, s, lo):
                        pe.wait_ge(s_h, g + 1)
                        for j in range(GT):
                            if lo >= 1 and j % 2 == 0:
                                pe.wait_ge(s_msg, (g - 1) * PAIRS + j // 2 + 1)
                            last = nc.tensor.matmul(pW[:, j // 2, 256 * (j % 2):256 * (j % 2) + 256],
                                                    hT[:, s, j // 2, :], w2[:, j % 2, :], start=True, stop=True)
                            if j % 2 or j == GT - 1:
                                last.then_inc(s_W, 1)

                    def sums(g, s, lo):
                        pe.wait_ge(s_msg, (g + 1) * PAIRS)
                        pe.wait_ge(s_oh, g + 1)
                        if lo >= 2:
                            hold(pe, s_add, g - 1)
                        pz = lambda p, b: pZ[p:p + 64, s, W * b:W * b + W]
                        for b in range(2):
                            for j in range(GT):
                                m = msg[:, s, j, :, :].rearrange("p b c -> p (b c)")
                                nc.tensor.matmul(pZ[:, s, W * b:W * b + W], m[:, 128 * b:128 * b + 128],
                                                 oh[:, s, j, 0, :], start=j == 0, stop=j == GT - 1)
                        for c, (p, b) in enumerate(((0, 2), (64, 2), (0, 3))):
                            for j in range(GT):
                                nc.tensor.matmul(pz(p, b), blk(s, j, 4), oh[:, s, j, 1 + c, :],
                                                 start=j == 0, stop=j == GT - 1)
                        for j in range(GT):
                            for c in range(3):
                                last = nc.tensor.matmul(pz(64, 3), blk(s, j, 5 + c), oh[:, s, j, 1 + c, :],
                                                        start=j + c == 0, stop=j == GT - 1 and c == 2)
                        last.then_inc(s_acc, 1)

                    def step(g, s, lo, hi):
                        if lo == 0:
                            front(0, 0, 0)
                        if hi <= GROUPS - 2:
                            front(g + 1, 1 - s, lo + 1)
                        second(g, s, lo)
                        if lo >= 1:
                            sums(g - 1, 1 - s, lo - 1)
                        if lo == GROUPS - 1:
                            sums(g, s, lo)
                    sweep(pe, GROUPS, step)

        edge_passes(env, 1, [z[:, :, :]], one_pass, s_gat,
                    s_es + [s_ix, s_T, s_esT, s_F, s_h, s_W, s_msg, s_oh, s_acc, s_add])


def back1(env, z):
    nc, a, sem, ident, stats, attr = (env[k] for k in ("nc", "a", "sem", "ident", "stats", "attr"))
    cv = env["chunk_view"]
    x2_v, x3_v = cv(env["x_d"][1]), cv(env["x_d"][2])
    wsel = env["wsel"]
    INV2 = 128.0 ** -0.5
    with ExitStack() as ctx:
        sb = lambda n, s, d=F32: ctx.enter_context(nc.sbuf_tensor("b1_" + n, s, d))
        pb = lambda n, s: ctx.enter_context(nc.psum_tensor("b1_" + n, s, F32))
        sc_w = sb("sc", [128, 2, C])
        lin2 = sb("lin2", [128, 4, C])
        bout = sb("bout", [R, C])
        wr = sb("wr", [R, C])
        br = sb("br", [R, 1])
        xt = sb("xt", [R, 2, 2, C])
        xnT = sb("xnT", [128, 2, 2, CH])
        zs = sb("zs", [128, 2, 4, CH])
        ga = sb("ga", [R, 2, C])
        ya = sb("ya", [R, 2, C])
        x3 = sb("x3", [R, 2, C])
        yy = sb("yy", [R, 2, 2, C])
        xn = sb("xn", [R, 2, 2, C])
        pr = sb("pr", [R, 2, C])
        bn, mv, ve, rn, mhalf = (sb("bn", [R, 2, 6]), sb("mv", [R, 2, 2]), sb("ve", [R, 2]), sb("rn", [R, 2, 2]),
                                 sb("mhalf", [R, 2]))
        xT = sb("xT", [128, 2, 2, CH])
        pA, pB, pT = pb("pA", [R, 2, 512]), pb("pB", [R, 2, 512]), pb("pT", [128, 512])
        s_w, s_z = sem("b1_weights"), sem("b1_zeroed")
        s_ld = [sem("b1_load0"), sem("b1_load1")]
        s_st = [sem("b1_store0"), sem("b1_store1")]
        s_sx = [sem("b1_storeT0"), sem("b1_storeT1")]
        s_zs, s_A, s_ga, s_Br, s_var, s_rstd, s_xn, s_y, s_T, s_xT = (
            sem("b1_" + n) for n in ("zs", "A", "gated", "read", "var", "rstd", "xn", "y", "T", "xT"))
        vec = lambda t, k: t[:, k, 64:256].rearrange("p (v c) -> p v c", c=3)

        with nc.Block() as block:
            @block.gpsimd
            def _(pool):
                nc.gpsimd.memset(sc_w[:, :, :], 0.0)
                nc.gpsimd.memset(lin2[:, :, :], 0.0)
                nc.gpsimd.memset(mhalf[:, :], -0.5)
                pool.drain().then_inc(s_z, 1)

            @block.sync
            def _(sp):
                sp.dma_start(bout[:, :], row_bc(a["L1_mix_bout"], R)).then_inc(s_w, 16)
                sp.dma_start(wr[:, :], a["L1_ffn_wr"].rearrange("k o -> o k").broadcast_to([R, C])).then_inc(s_w, 16)
                sp.dma_start(br[:, :], a["L1_ffn_br"].rearrange("(o n) -> o n", o=1).broadcast_to([R, 1])).then_inc(s_w, 16)
                sp.wait_ge(s_z, 1)
                sp.dma_start(sc_w[0:64, 0, 0:64], a["L1_gnn_sc_w0"]).then_inc(s_w, 16)
                sp.dma_start(lin2[0:64, 0, 0:64], a["L1_gnn_lin2_w00"]).then_inc(s_w, 16)
                sp.dma_start(lin2[64:128, 3, 0:64], a["L1_gnn_lin2_w01"]).then_inc(s_w, 16)
                sp.wait_ge(s_w, 96)

        w10, w11, w1s = (ctx.enter_context(nc.sbuf_tensor("b1_" + n, [128, 64], F32)) for n in ("w10", "w11", "w1s"))
        ws1 = sb("ws1", [128, 2, 64])
        with nc.Block() as block:
            @block.sync
            def _(sp):
                for r in range(2):
                    sp.dma_start(w10[64 * r:64 * r + 64, :], a["L1_gnn_lin2_w10"]).then_inc(s_w, 16)
                    sp.dma_start(w11[64 * r:64 * r + 64, :], a["L1_gnn_lin2_w11"]).then_inc(s_w, 16)
                for k, p, c, u, n in vector_rows():
                    sp.dma_start(sc_w[p:p + 3 * (n - 1) + 1:3, k, 64 + c:64 + 3 * 63 + c + 1:3],
                                 a["L1_gnn_sc_w1"][u:u + n, :]).then_inc(s_w, 16)
                sp.wait_ge(s_w, 96 + 64 + 16 * len(vector_rows()))

        with nc.Block() as block:
            @block.vector
            def _(v):
                for (b, p), w, c in zip(((0, 64), (1, 0), (1, 64), (2, 0), (2, 64), (3, 0)), (w11,) * 3 + (w10,) * 3,
                                        (0, 1, 2) * 2):
                    nc.vector.tensor_copy(vec(lin2, b)[p:p + 64, :, c], w[p:p + 64, :])
                v.drain()
                nc.vector.tensor_scalar(sc_w[:, :, :], sc_w[:, :, :], SIN8 / 8.0, None, ALU.mult)
                nc.vector.tensor_scalar(lin2[:, :, :], lin2[:, :, :], COS8 * INV2 * 20.0 ** -0.5, None, ALU.mult)
                v.drain()
                nc.vector.tensor_scalar(lin2[64:128, 3, :], lin2[64:128, 3, :], INV_SQRT3, None, ALU.mult)
                v.drain()

        with nc.Block() as block:
            @block.sync
            def _(sp):
                def load(u, s):
                    rows_dma(sp, xt[:, s, :, :], x2_v[u], s_ld[s])
                    sp.dma_start(xnT[:, s, :, :], env["xnT_d"][2][:, :, bass.ds(u * CH, CH)]).then_inc(s_ld[s], 16)

                def store(u, s):
                    sp.wait_ge(s_y, u + 1)
                    rows_dma(sp, x3_v[u], yy[:, s, :, :], s_st[s])
                    sp.wait_ge(s_xT, u + 1)
                    sp.dma_start(env["xnT_d"][3][:, :, bass.ds(u * CH, CH)], xT[:, s, :, :]).then_inc(s_sx[s], 16)

                def step(u, s, lo, hi):
                    if lo >= 2:
                        sp.wait_ge(s_Br, u - 1)
                        sp.wait_ge(s_A, u - 1)
                    load(u, s)
                    if lo >= 2:
                        store(u - 2, s)
                sweep(sp, CHUNKS, step)
                for u in (CHUNKS - 2, CHUNKS - 1):
                    store(u, u % 2)
                for i in range(2):
                    n = (CHUNKS + 1 - i) // 2
                    sp.wait_ge(s_st[i], 32 * n)
                    sp.wait_ge(s_sx[i], 16 * n)

            @block.gpsimd
            def _(pool):
                def step(u, s, lo, hi):
                    hold(pool, s_var, u + 1)
                    nc.gpsimd.tensor_tensor(out=rn[:, :, 0], in0=ve[:, :], in1=mhalf[:, :], op=ALU.pow)\
                      .then_inc(s_rstd, 1)
                sweep(pool, CHUNKS, step)

            @block.scalar
            def _(act):
                def pick(u, s, lo):
                    if lo >= 2:
                        hold(act, s_A, u - 1)
                    nc.scalar.copy(zs[:, s, :, :], z[:, :, bass.ds(u * CH, CH)]).then_inc(s_zs, 1)

                def turn(u, s, lo):
                    if lo >= 2:
                        hold(act, s_sx[s], (u // 2) * 16)
                    hold(act, s_T, u + 1)
                    nc.scalar.copy(xT[:, s, :, :], pT[:, 0:2 * CH].rearrange("p (k n) -> p k n", k=2)).then_inc(s_xT, 1)

                def step(u, s, lo, hi):
                    if lo == 0:
                        pick(0, 0, 0)
                    if hi <= CHUNKS - 2:
                        pick(u + 1, 1 - s, lo + 1)
                    if lo >= 1:
                        hold(act, s_Br, u)
                    hold(act, s_A, u + 1)
                    for t in range(2):
                        last = nc.scalar.activation(ga[:, t, :], pA[:, s, t * C:t * C + C], ACT.Copy,
                                                    scale=attr[:, bass.ds(u * 2 + t, 1)])
                    last.then_inc(s_ga, 1)
                    if lo >= 1:
                        turn(u - 1, 1 - s, lo - 1)
                    if lo == CHUNKS - 1:
                        turn(u, s, lo)
                sweep(act, CHUNKS, step)

            @block.vector
            def _(v):
                def step(u, s, lo, hi):
                    v.wait_ge(s_ld[s], (u // 2 + 1) * 48)
                    nc.vector.tensor_tensor(out=ya[:, :, :], in0=xt[:, s, :, :],
                                            in1=bout[:, :].unsqueeze(1).broadcast_to([R, 2, C]), op=ALU.add)
                    v.wait_ge(s_ga, u + 1)
                    nc.vector.tensor_tensor(out=x3[:, :, :], in0=ga[:, :, :],
                                            in1=pB[:, s, :].rearrange("p (t c) -> p t c", t=2), op=ALU.add)
                    v.drain()
                    nc.vector.tensor_tensor(out=x3[:, :, :], in0=x3[:, :, :], in1=ya[:, :, :], op=ALU.add)
                    v.drain().then_inc(s_Br, 1)
                    ln_stats(nc, v, x3, bn, mv, ve, s_var)
                    v.wait_ge(s_rstd, u + 1)
                    if lo >= 2:
                        v.wait_ge(s_T, u - 1)
                    ln_apply(nc, v, xn[:, s, :, :], x3, mv, rn)
                    v.drain().then_inc(s_xn, 1)
                    if lo >= 2:
                        v.wait_ge(s_st[s], (u // 2) * 32)
                    nc.vector.tensor_tensor(out=yy[:, s, :, :], in0=x3[:, :, :], in1=xn[:, s, :, :], op=ALU.add)\
                      .then_inc(s_y, 1)
                    nc.vector.tensor_tensor(out=pr[:, :, :], in0=xn[:, s, :, :],
                                            in1=wr[:, :].unsqueeze(1).broadcast_to([R, 2, C]), op=ALU.mult)
                    v.drain()
                    nc.vector.tensor_reduce(wsel[:, bass.ds(u * 2, 2)], pr[:, :, :], AX.X, ALU.add)
                    v.drain()
                    if lo == CHUNKS - 1:
                        nc.vector.tensor_scalar(wsel[:, :], wsel[:, :], br[:, 0:1], None, ALU.add)
                        v.drain()
                sweep(v, CHUNKS, step)

            @block.tensor
            def _(pe):
                def products(u, s, lo):
                    pe.wait_ge(s_zs, u + 1)
                    pe.wait_ge(s_ld[s], (u // 2 + 1) * 48)
                    if lo >= 2:
                        pe.wait_ge(s_Br, u - 1)
                    for t in range(2):
                        tt = slice(t * R, t * R + R)
                        for k in range(2):
                            nc.tensor.matmul(pA[:, s, t * C:t * C + C], xnT[:, s, k, tt], sc_w[:, k, :],
                                             start=k == 0, stop=False)
                        for b in range(4):
                            nc.tensor.matmul(pA[:, s, t * C:t * C + C], zs[:, s, b, tt], lin2[:, b, :],
                                             start=False, stop=b == 3)
                        for k in range(2):
                            last = nc.tensor.matmul(pB[:, s, t * C:t * C + C], xnT[:, s, k, tt], env["g1"][:, k, :],
                                                    start=k == 0, stop=k == 1)
                    last.then_inc(s_A, 1)

                def turn(u, s, lo):
                    pe.wait_ge(s_xn, u + 1)
                    if lo >= 1:
                        pe.wait_ge(s_xT, u)
                    for k in range(2):
                        for t in range(2):
                            last = nc.tensor.transpose(pT[:, k * CH + t * R:k * CH + t * R + R],
                                                       xn[:, s, t, 128 * k:128 * k + 128], ident[0:R, 0:R])
                    last.then_inc(s_T, 1)

                def step(u, s, lo, hi):
                    products(u, s, lo)
                    if lo >= 1:
                        turn(u - 1, 1 - s, lo - 1)
                    if lo == CHUNKS - 1:
                        turn(u, s, lo)
                sweep(pe, CHUNKS, step)


def ffn1(env):
    nc, a, sem, ident, ones, wsel = (env[k] for k in ("nc", "a", "sem", "ident", "ones", "wsel"))
    cv = env["chunk_view"]
    yy_v, out_v = cv(env["x_d"][2]), cv(env["out"])
    NF = F1 // 128
    with ExitStack() as ctx:
        sb = lambda n, s, d=F32: ctx.enter_context(nc.sbuf_tensor("o_" + n, s, d))
        pb = lambda n, s: ctx.enter_context(nc.psum_tensor("o_" + n, s, F32))
        w1 = sb("w1", [128, 2, F1])
        w2 = sb("w2", [128, NF, C])
        b1 = sb("b1", [128, NF])
        b2 = sb("b2", [R, C])
        wrow = sb("wrow", [R, N])
        cmp_ = sb("cmp", [R, N], mybir.dt.bfloat16)
        low = sb("low", [R, R])
        eq = sb("eq", [R, R])
        cnt = sb("cnt", [R, 4])
        rank = sb("rank", [R, TILES])
        coef = sb("coef", [R, TILES])
        wc = sb("wc", [TILES, R])
        xnT = sb("xnT", [128, 2, 2, CH])
        hT = sb("hT", [128, NF, CH])
        yall = sb("yall", [R, TILES, C])
        yt = sb("yt", [R, 2, 2, C])
        ot = sb("ot", [R, 2, 2, C])
        pH, pO, pW = pb("pH", [128, NF // 2, 512]), pb("pO", [R, 2, 512]), pb("pW", [128, 512])
        s_w, s_wT, s_wTc, s_wst, s_wrow, s_low = (sem("o_" + n) for n in ("weights", "wT", "wTc", "wst", "wrow", "low"))
        s_ld = [sem("o_load0"), sem("o_load1")]
        s_l2 = [sem("o_rows0"), sem("o_rows1")]
        s_st = [sem("o_store0"), sem("o_store1")]
        s_H, s_g, s_O, s_y, s_rank, s_o = (sem("o_" + n) for n in ("H", "gelu", "O", "y", "rank", "out"))

        with nc.Block() as block:
            @block.sync
            def _(sp):
                sp.dma_start(w1[:, :, :], a["L1_ffn_w1"].rearrange("(k p) f -> p k f", p=128)).then_inc(s_w, 16)
                sp.dma_start(w2[:, :, :], a["L1_ffn_w2"].rearrange("(f p) n -> p f n", p=128)).then_inc(s_w, 16)
                sp.dma_start(b1[:, :], a["L1_ffn_b1"].rearrange("(f p) -> p f", p=128)).then_inc(s_w, 16)
                sp.dma_start(b2[:, :], row_bc(a["L1_ffn_b2"], R)).then_inc(s_w, 16)
                sp.wait_ge(s_wTc, 1)
                sp.dma_start(env["w_d"].rearrange("o (t p) -> (o t) p", p=R), wc[:, :]).then_inc(s_wst, 16)
                sp.wait_ge(s_wst, 16)
                sp.dma_start(wrow[:, :], env["w_d"].broadcast_to([R, N])).then_inc(s_wrow, 16)
                sp.wait_ge(s_wrow, 16)
                sp.wait_ge(s_w, 64)

            @block.tensor
            def _(pe):
                nc.tensor.transpose(pW[0:TILES, 0:R], wsel[:, :], ident[0:R, 0:R]).then_inc(s_wT, 1)

            @block.vector
            def _(v):
                v.wait_ge(s_wT, 1)
                nc.vector.tensor_copy(wc[:, :], pW[0:TILES, 0:R]).then_inc(s_wTc, 1)

            @block.gpsimd
            def _(pool):
                nc.gpsimd.memset(low[:, :], 1.0)
                pool.drain()
                nc.gpsimd.affine_select(out=low[:, :], in_=low[:, :], compare_op=ALU.is_gt, fill=0.0, base=0,
                                        pattern=[[-1, R]], channel_multiplier=1)
                pool.drain()

        def rank_tile(v, i):
            w = wsel[:, i:i + 1]
            lo_, hi_ = i * R, (i + 1) * R
            own = wrow[:, lo_:hi_]
            nc.vector.tensor_scalar(eq[:, :], own, w, None, ALU.is_equal)
            nc.vector.tensor_scalar(cmp_[:, lo_:hi_], own, w, 0.0, ALU.is_gt, ALU.add, accum_out=cnt[:, 0:1])
            if i == 0:
                nc.vector.memset(cnt[:, 1:2], 0.0)
            else:
                nc.vector.tensor_scalar(cmp_[:, 0:lo_], wrow[:, 0:lo_], w, 0.0, ALU.is_ge, ALU.add,
                                        accum_out=cnt[:, 1:2])
            if i == TILES - 1:
                nc.vector.memset(cnt[:, 2:3], 0.0)
            else:
                nc.vector.tensor_scalar(cmp_[:, hi_:N], wrow[:, hi_:N], w, 0.0, ALU.is_gt, ALU.add,
                                        accum_out=cnt[:, 2:3])
            v.drain()
            nc.vector.tensor_tensor(out=eq[:, :], in0=eq[:, :], in1=low[:, :], op=ALU.mult)
            v.drain()
            nc.vector.tensor_reduce(cnt[:, 3:4], eq[:, :], AX.X, ALU.add)
            v.drain()
            nc.vector.tensor_reduce(rank[:, i:i + 1], cnt[:, :], AX.X, ALU.add)
            v.drain()

        with nc.Block() as block:
            @block.sync
            def _(sp):
                def step(u, s, lo, hi):
                    if lo >= 2:
                        sp.wait_ge(s_H, (u - 1) * (NF // 2))
                    sp.dma_start(xnT[:, s, :, :], env["xnT_d"][3][:, :, bass.ds(u * CH, CH)]).then_inc(s_ld[s], 16)
                sweep(sp, CHUNKS, step)

                def final(u, s, lo, hi):
                    if lo >= 2:
                        sp.wait_ge(s_o, u - 1)
                    rows_dma(sp, yt[:, s, :, :], yy_v[u], s_l2[s])
                    if lo >= 1:
                        sp.wait_ge(s_o, u)
                        rows_dma(sp, out_v[u - 1], ot[:, 1 - s, :, :], s_st[1 - s])
                    if lo == CHUNKS - 1:
                        sp.wait_ge(s_o, u + 1)
                        rows_dma(sp, out_v[u], ot[:, s, :, :], s_st[s])
                sweep(sp, CHUNKS, final)
                for i in range(2):
                    sp.wait_ge(s_st[i], 32 * ((CHUNKS + 1 - i) // 2))

            @block.scalar
            def _(act):
                def step(u, s, lo, hi):
                    if lo >= 1:
                        hold(act, s_O, u)
                    for f in range(NF):
                        if f % 2 == 0:
                            hold(act, s_H, NF // 2 * u + f // 2 + 1)
                        x = nc.scalar.activation(hT[:, f, :], pH[:, f // 2, (f % 2) * CH:(f % 2 + 1) * CH],
                                                 ACT.Gelu_apprx_tanh, bias=b1[:, f:f + 1])
                        if f % 2:
                            x.then_inc(s_g, 1)
                    if lo >= 1:
                        nc.scalar.copy(yall[:, bass.ds(u * 2 - 2, 2), :], pO[:, 1 - s, :].rearrange("p (t c) -> p t c", t=2))\
                          .then_inc(s_y, 1)
                    if lo == CHUNKS - 1:
                        hold(act, s_O, u + 1)
                        nc.scalar.copy(yall[:, 2 * u:2 * u + 2, :], pO[:, s, :].rearrange("p (t c) -> p t c", t=2))\
                          .then_inc(s_y, 1)
                sweep(act, CHUNKS, step)

            @block.tensor
            def _(pe):
                def hidden(u, s, lo):
                    pe.wait_ge(s_ld[s], (u // 2 + 1) * 16)
                    for f in range(NF):
                        if f % 2 == 0 and lo >= 1:
                            pe.wait_ge(s_g, NF // 2 * (u - 1) + f // 2 + 1)
                        for k in range(2):
                            last = nc.tensor.matmul(pH[:, f // 2, (f % 2) * CH:(f % 2 + 1) * CH],
                                                    w1[:, k, 128 * f:128 * f + 128], xnT[:, s, k, :],
                                                    start=k == 0, stop=k == 1)
                        if f % 2:
                            last.then_inc(s_H, 1)

                def step(u, s, lo, hi):
                    if lo == 0:
                        hidden(0, 0, 0)
                    if hi <= CHUNKS - 2:
                        hidden(u + 1, 1 - s, lo + 1)
                    if lo >= 2:
                        pe.wait_ge(s_y, u - 1)
                    for t in range(2):
                        for f in range(NF):
                            if t == 0 and f % 2 == 0:
                                pe.wait_ge(s_g, NF // 2 * u + f // 2 + 1)
                            last = nc.tensor.matmul(pO[:, s, t * C:(t + 1) * C], hT[:, f, t * R:t * R + R], w2[:, f, :],
                                                    start=f == 0, stop=f == NF - 1)
                    last.then_inc(s_O, 1)
                sweep(pe, CHUNKS, step)

            @block.vector
            def _(v):
                for i in range(TILES):
                    rank_tile(v, i)
                nc.vector.scalar_tensor_tensor(out=coef[:, :], in0=rank[:, :], scalar=float(TOPK1), in1=wsel[:, :],
                                               op0=ALU.is_lt, op1=ALU.mult)
                v.drain()
                v.wait_ge(s_y, CHUNKS)

                def final(u, s, lo, hi):
                    y = yall[:, bass.ds(u * 2, 2), :]
                    nc.vector.tensor_tensor(out=y, in0=y, in1=b2[:, :].unsqueeze(1).broadcast_to([R, 2, C]), op=ALU.add)
                    v.drain()
                    nc.vector.tensor_tensor(out=y, in0=y, in1=coef[:, bass.ds(u * 2, 2)].unsqueeze(2)
                                            .broadcast_to([R, 2, C]), op=ALU.mult)
                    v.drain()
                    v.wait_ge(s_l2[s], (u // 2 + 1) * 32)
                    if lo >= 2:
                        v.wait_ge(s_st[s], (u // 2) * 32)
                    nc.vector.tensor_tensor(out=ot[:, s, :, :], in0=y, in1=yt[:, s, :, :], op=ALU.add).then_inc(s_o, 1)
                sweep(v, CHUNKS, final)


@contextmanager
def phase(env):
    nc, used = env["nc"], []
    with ExitStack() as ctx:
        def sem(name, software_dma=False):
            s = ctx.enter_context(nc.semaphore(name))
            if not software_dma:
                used.append(s)
            return s

        env["sem"] = sem
        yield
        with nc.Block() as block:
            @block.gpsimd
            def _(pool):
                for s in used:
                    pool.sem_clear(s)


def gps_kernel(nc, a, out):
    def dram(name, shape, dt=F32):
        return nc.dram_tensor(name, shape, dt).ap()

    def chunk_view(t):
        return t.rearrange("(u t p) c -> u p t c", t=2, p=R)

    with nc.allow_non_contiguous_dma(reason="bias columns and rows of a strided weight"), ExitStack() as ctx:
        sb = lambda n, s, d=F32: ctx.enter_context(nc.sbuf_tensor(n, s, d))
        env = dict(
            nc=nc, a=a, chunk_view=chunk_view, x_in=a["x"], out=out,
            tab0=dram("tab0", (N, TAB0)),
            dst_tab=dram("dst_tab", (NPAD, 2 * H0)),
            tab1=dram("tab1", (N, C)),
            xnT_d=[dram(f"xnT{i}", (128, 2, N)) for i in range(4)],
            x_d=[dram(f"xres{i}", (N, C)) for i in range(3)],
            gf_d=dram("group_range", (2, GROUPS)),
            w_d=dram("route_weight", (1, N)),
            ident=sb("ident", [128, 128]), ones=sb("ones", [128, 128]), zeros=sb("zeros", [1, 512]),
            stats=sb("stats", [R, TILES, 2]),
            spanI=sb("span", [1, 1], I32),
            g0=sb("mix0_g", [128, 2, C]), g0b=sb("mix0_b", [128, 2]), g1=sb("mix1_g", [128, 2, C]),
            pself=sb("pself", [R, TILES, H0]),
            x1sum=sb("x1sum", [128, 2]), attr=sb("node_attr", [R, TILES]), wsel=sb("wsel", [R, TILES]),
            srcI=sb("src", [R, ETILES], I32),
            dstRel=sb("dst_rel", [R, ETILES]),
            baseF=sb("base_f", [1, GROUPS]), baseI=sb("base", [1, GROUPS], I32),
            iotaI=sb("iota_i", [R, W], I32), iotaW=sb("iota", [R, W]))
        ident, ones, zeros = env["ident"], env["ones"], env["zeros"]
        s_zero = ctx.enter_context(nc.semaphore("const_zeroed"))
        with nc.Block() as block:
            @block.gpsimd
            def _(pool):
                nc.gpsimd.memset(ident[:, :], 0.0).then_inc(s_zero, 1)
                nc.gpsimd.memset(ones[:, :], 1.0)
                nc.gpsimd.memset(zeros[:, :], 0.0)
                pool.wait_ge(s_zero, 1)
                nc.gpsimd.affine_select(out=ident[:, :], in_=ident[:, :], compare_op=ALU.not_equal, fill=1.0,
                                        base=0, pattern=[[-1, 128]], channel_multiplier=1)
                pool.drain()
        with phase(env):
            edge_indices(env)
        with phase(env):
            front0(env)
        with ExitStack() as first:
            acc = first.enter_context(nc.sbuf_tensor("sum0", [128, 2, NPAD], F32))
            den = first.enter_context(nc.sbuf_tensor("den0", [H0, NPAD], F32))
            with phase(env):
                edges0(env, acc, den)
            with phase(env):
                back0(env, acc, den)
        with phase(env):
            ffn0(env)
        with phase(env):
            front1(env)
        with ExitStack() as second:
            z = second.enter_context(nc.sbuf_tensor("sum1", [128, 4, NPAD], F32))
            with ExitStack() as attrs:
                ea = attrs.enter_context(nc.sbuf_tensor("edge_attr", [R, ETILES, 4], F32))
                with phase(env):
                    edge_attrs(env, ea)
                with phase(env):
                    edges1(env, z, ea)
            with phase(env):
                back1(env, z)
        with phase(env):
            ffn1(env)


def kernel(**inputs):
    import numpy as np
    import concourse.bacc as bacc
    from concourse.bass_utils import run_bass_kernel_spmd

    nc = bacc.Bacc("TRN2", target_bir_lowering=False, num_devices=1)
    arrays, aps = {}, {}
    for name, value in inputs.items():
        if name == "L1_ffn_attention_mask":
            continue
        value = np.ascontiguousarray(value)
        arrays["in_" + name] = value
        aps[name] = nc.dram_tensor("in_" + name, value.shape, mybir.dt.from_np(value.dtype), kind="ExternalInput").ap()
    out = nc.dram_tensor("out_nodes", (N, C), F32, kind="ExternalOutput").ap()
    gps_kernel(nc, aps, out)
    result = run_bass_kernel_spmd(nc, [arrays], core_ids=[0])
    return result.results[0]["out_nodes"]
```

```python
from contextlib import ExitStack, contextmanager

import concourse.bass as bass
from concourse import mybir

F32 = mybir.dt.float32
I32 = mybir.dt.int32
BF16 = mybir.dt.bfloat16
U32 = mybir.dt.uint32
ALU = mybir.AluOpType
ACT = mybir.ActivationFunctionType
AX = mybir.AxisListType

N = 6250
C = 256
R = 125
TILES = N // R
CH = 2 * R
CHUNKS = N // CH
E = 106250
ETILES = E // R
GT = 5
GROUPS = ETILES // GT
SLOTS = 6
AHEAD = 3
W = 64
NPAD = N + W
QB = 85
NB = ETILES // QB
H0, D0 = 4, 64
TAB0 = C + H0
EPS = 1e-5
E8, F0 = 8, 512
F1 = 1024
CAPACITY = float(-(-N * 5 // (4 * E8)))
TOPK1 = N // 2 - 1
SEL = 112
INV_SQRT3 = 3.0 ** -0.5
COS8, SIN8 = 0.9238795325112867, 0.3826834323650898


def sweep(eng, n, body, m=2, ahead=1):
    for u in range(m):
        body(u, u % m, u, u)
    blocks = (n - ahead - m) // m
    with eng.Fori(1, blocks + 1) as k:
        for r in range(m):
            body(k * m + r, r, m, m * blocks + m - 1)
    for u in range(m + m * blocks, n):
        body(u, u % m, u, u)


def rows_dma(eng, out, in_, sem):
    eng.dma_start(out[0:SEL], in_[0:SEL]).then_inc(sem, 16)
    eng.dma_start(out[SEL:R], in_[SEL:R]).then_inc(sem, 16)


def hold(eng, sem, value):
    eng.wait_ge(sem, value)
    eng.nop(nofuse=True)


def ln_stats(nc, v, x, bn, mv, var_eps, s_var):
    for t in range(2):
        nc.vector.bn_stats(bn[:, t, :], x[:, t, :])
    v.drain()
    for t in range(2):
        nc.vector.bn_aggr(mv[:, t, :], bn[:, t, :])
    v.drain()
    nc.vector.tensor_scalar(var_eps[:, :], mv[:, :, 1], EPS, None, ALU.add).then_inc(s_var, 1)


def ln_apply(nc, v, xn, x, mv, rn, tiles=2):
    nc.vector.scalar_tensor_tensor(out=rn[:, :, 1], in0=mv[:, :, 0], scalar=-1.0, in1=rn[:, :, 0],
                                   op0=ALU.mult, op1=ALU.mult)
    v.drain()
    for t in range(tiles):
        last = nc.vector.tensor_scalar(xn[:, t, :], x[:, t, :], rn[:, t, 0:1], rn[:, t, 1:2], ALU.mult, ALU.add)
    return last


def front0(env):
    nc, a, sem, ident, ones, stats = (env[k] for k in ("nc", "a", "sem", "ident", "ones", "stats"))
    chunk_view = env["chunk_view"]
    g0, g0b = env["g0"], env["g0b"]
    x_v = chunk_view(env["x_in"])
    tab_v = chunk_view(env["tab0"])
    adst = env["dst_tab"]
    HD = 32
    with ExitStack() as ctx:
        sb = lambda n, s, d=F32: ctx.enter_context(nc.sbuf_tensor("f0_" + n, s, d))
        pb = lambda n, s: ctx.enter_context(nc.psum_tensor("f0_" + n, s, F32))
        wg = sb("wg", [128, 2, C])
        wga = sb("wga", [128, 2, C + 8])
        att = sb("att", [128, 2, C])
        tmp = sb("tmp", [128, 2, C])
        wqkv = sb("wqkv", [128, 2, 3 * C])
        bqkv = sb("bqkv", [128, 3 * C])
        wkv = sb("wkv", [128, 2, 2 * C])
        bkv = sb("bkv", [128, 2 * C])
        cm = sb("cm", [128, 3, 8])
        w1 = sb("w1", [128, 2, C])
        b1c = sb("b1c", [128, 2])
        bqc = sb("bqc", [128, 2])
        gv = sb("gv", [128, 2])
        gk = sb("gk", [128, 2, HD])
        xt = sb("xt", [R, 2, 2, C])
        xn = sb("xn", [R, 2, 2, C])
        bn = sb("bn", [R, 2, 6])
        mv = sb("mv", [R, 2, 2])
        ve = sb("ve", [R, 2])
        rn = sb("rn", [R, 2, 2])
        mhalf = sb("mhalf", [R, 2])
        xnT = sb("xnT", [128, 2, 2, CH])
        hrow = sb("hrow", [R, 2, 2, C + 8])
        adst_all = sb("adst_all", [R, TILES, 8])
        kvt = sb("kvt", [R, 2, 2 * C])
        sq = sb("sq", [R, 2, 2 * C])
        ss = sb("ss", [R, 2, 16])
        sd = sb("sd", [R, 2, 16])
        ri = sb("ri", [R, 2, 16])
        kvn = sb("kvn", [R, 2, 2 * C + 2])
        epst = sb("epst", [128, 1])
        pT = pb("pT", [128, 2, 512])
        pH = pb("pH", [128, 2, 512])
        pKV = pb("pKV", [128, 2, 512])
        pS = pb("pS", [128, 512])
        pK = pb("pK", [128, 512])
        s_w = sem("f0_weights")
        s_p = sem("f0_prepared")
        s_x = [sem(f"f0_x{i}") for i in range(2)]
        s_var = sem("f0_var")
        s_rstd = sem("f0_rstd")
        s_xn = sem("f0_xn")
        s_T = sem("f0_transposed")
        s_xnT = sem("f0_xnT")
        s_h = sem("f0_h")
        s_hrow = sem("f0_hrow")
        s_kv = sem("f0_kv")
        s_kvt = sem("f0_kvt")
        s_sq = sem("f0_sq")
        s_ss = sem("f0_ss")
        s_sd = sem("f0_sd")
        s_kvn = sem("f0_kvn")
        s_acc = sem("f0_accumulated")
        s_sx = [sem(f"f0_store_xnT{i}") for i in range(2)]
        s_st = [sem(f"f0_store_tab{i}") for i in range(2)]
        s_ad = sem("f0_store_dst")

        with nc.Block() as block:
            @block.sync
            def _(sp):
                sp.dma_start(wg[:, :, :], a["L0_gnn_W"].rearrange("(k p) n -> p k n", p=128)).then_inc(s_w, 16)
                for i, n in enumerate(("L0_gnn_att_src", "L0_gnn_att_dst")):
                    sp.dma_start(att[:, i, :], a[n].rearrange("(o h) c -> o (h c)", o=1).broadcast_to([128, C]))\
                      .then_inc(s_w, 16)
                sp.dma_start(wqkv[:, :, :], a["L0_mix_w_qkv"].rearrange("(k p) n -> p k n", p=128)).then_inc(s_w, 16)
                sp.dma_start(bqkv[:, :], a["L0_mix_b_qkv"].rearrange("(o n) -> o n", o=1).broadcast_to([128, 3 * C]))\
                  .then_inc(s_w, 16)
                sp.dma_start(w1[:, :, :], a["L0_mix_w1"].rearrange("(k p) n -> p k n", p=128)).then_inc(s_w, 16)
                sp.dma_start(b1c[:, :], a["L0_mix_b1"].rearrange("(k p) -> p k", p=128)).then_inc(s_w, 16)
                bq = a["L0_mix_b_qkv"].rearrange("(h s d o) -> h s d o", s=3, d=HD, o=1)
                for h in range(8):
                    sp.dma_start(bqc[HD * (h % 4):HD * (h % 4 + 1), h // 4:h // 4 + 1], bq[h, 0]).then_inc(s_w, 16)
                for h in range(4):
                    for i, n in enumerate(("L0_mix_vln_g", "L0_mix_vln_b")):
                        sp.dma_start(gv[HD * h:HD * (h + 1), i:i + 1], a[n].rearrange("(d o) -> d o", o=1))\
                          .then_inc(s_w, 16)
                for i, n in enumerate(("L0_mix_kln_g", "L0_mix_kln_b")):
                    sp.dma_start(gk[:, i, :], a[n].rearrange("(o d) -> o d", o=1).broadcast_to([128, HD]))\
                      .then_inc(s_w, 16)
                sp.wait_ge(s_w, 16 * 25)

        with nc.Block() as block:
            @block.gpsimd
            def _(pool):
                nc.gpsimd.memset(mhalf[:, :], -0.5)
                nc.gpsimd.memset(epst[:, :], EPS)
                nc.gpsimd.memset(kvn[:, :, :], 1.0)
                pool.drain()

            @block.vector
            def _(v):
                for i in range(2):
                    for k in range(2):
                        nc.vector.tensor_tensor(out=tmp[:, k, :], in0=wg[:, k, :], in1=att[:, i, :], op=ALU.mult)
                    v.drain()
                    for k in range(2):
                        nc.vector.tensor_reduce(wga[:, k, C + 4 * i:C + 4 * i + 4],
                                                tmp[:, k, :].rearrange("p (h c) -> p h c", h=H0), AX.X, ALU.add)
                    v.drain()
                nc.vector.tensor_copy(wga[:, :, 0:C], wg[:, :, :])
                for s in (1, 2):
                    for k in range(3):
                        src = wqkv[:, k, :] if k < 2 else bqkv[:, :]
                        dst = (wkv[:, k, :] if k < 2 else bkv[:, :])[:, (s - 1) * C:s * C]
                        src = src.rearrange("p (h s d) -> p h s d", s=3, d=HD)[:, :, s, :]
                        nc.vector.tensor_reduce(cm[:, k, :], src, AX.X, ALU.add)
                        v.drain()
                        nc.vector.tensor_scalar(cm[:, k, :], cm[:, k, :], -1.0 / HD, None, ALU.mult)
                        v.drain()
                        nc.vector.tensor_tensor(out=dst.rearrange("p (h d) -> p h d", d=HD), in0=src,
                                                in1=cm[:, k, :].unsqueeze(2).broadcast_to([128, 8, HD]), op=ALU.add)
                        v.drain()

        with nc.Block() as block:
            @block.sync
            def _(sp):
                def load(u, s):
                    rows_dma(sp, xt[:, s, :, :], x_v[u].rearrange("p t c -> p t c"), s_x[s])

                def step(u, s, lo, hi):
                    if lo >= 2:
                        sp.wait_ge(s_xn, u - 1)
                    load(u, s)
                    if lo >= 1:
                        o = u - 1
                        sp.wait_ge(s_xnT, o + 1)
                        sp.dma_start(env["xnT_d"][0][:, :, bass.ds(o * CH, CH)], xnT[:, 1 - s, :, :])\
                          .then_inc(s_sx[1 - s], 16)
                        sp.wait_ge(s_hrow, 2 * o + 2)
                        rows_dma(sp, tab_v[o][:, :, :], hrow[:, 1 - s, :, 0:TAB0], s_st[1 - s])
                sweep(sp, CHUNKS, step)
                o, s = CHUNKS - 1, (CHUNKS - 1) % 2
                sp.wait_ge(s_xnT, o + 1)
                sp.dma_start(env["xnT_d"][0][:, :, o * CH:(o + 1) * CH], xnT[:, s, :, :]).then_inc(s_sx[s], 16)
                sp.wait_ge(s_hrow, 2 * o + 2)
                rows_dma(sp, tab_v[o][:, :, :], hrow[:, s, :, 0:TAB0], s_st[s])
                for i in range(2):
                    n = (CHUNKS + 1 - i) // 2
                    sp.wait_ge(s_sx[i], 16 * n)
                    sp.wait_ge(s_st[i], 32 * n)

            @block.gpsimd
            def _(pool):
                def step(u, s, lo, hi):
                    hold(pool, s_var, u + 1)
                    nc.gpsimd.tensor_tensor(out=rn[:, :, 0], in0=ve[:, :], in1=mhalf[:, :], op=ALU.pow)\
                      .then_inc(s_rstd, 1)
                sweep(pool, CHUNKS, step)

            @block.vector
            def _(v):
                def keys_values(u, lo):
                    if lo >= 1:
                        v.wait_ge(s_kvn, 2 * u)
                    for t in range(2):
                        i = 2 * u + t
                        v.wait_ge(s_kv, i + 1)
                        nc.vector.tensor_tensor(out=kvt[:, t, :], in0=pKV[0:R, t, :], in1=bkv[0:R, :], op=ALU.add)\
                          .then_inc(s_kvt, 1)
                    for t in range(2):
                        v.wait_ge(s_sq, 2 * u + t + 1)
                        nc.vector.tensor_reduce(ss[:, t, :], sq[:, t, :].rearrange("p (g d) -> p g d", d=HD), AX.X,
                                                ALU.add).then_inc(s_ss, 1)
                    v.wait_ge(s_sd, u + 1)
                    nc.vector.reciprocal(ri[:, :, :], sd[:, :, :])
                    v.drain()
                    if lo >= 1:
                        v.wait_ge(s_acc, 2 * u)
                    for t in range(2):
                        kvn_k = kvn[:, t, 0:2 * 129].rearrange("p (g m) -> p g m", g=2)
                        for g in range(2):
                            nc.vector.tensor_tensor(
                                out=kvn_k[:, g, 0:128].rearrange("p (h d) -> p h d", d=HD),
                                in0=kvt[:, t, 128 * g:128 * g + 128].rearrange("p (h d) -> p h d", d=HD),
                                in1=ri[:, t, 4 * g:4 * g + 4].unsqueeze(2).broadcast_to([R, 4, HD]), op=ALU.mult)
                        nc.vector.tensor_tensor(
                            out=kvn[:, t, 258:514].rearrange("p (h d) -> p h d", d=HD),
                            in0=kvt[:, t, C:2 * C].rearrange("p (h d) -> p h d", d=HD),
                            in1=ri[:, t, 8:16].unsqueeze(2).broadcast_to([R, 8, HD]), op=ALU.mult).then_inc(s_kvn, 1)

                def step(u, s, lo, hi):
                    v.wait_ge(s_x[s], (u // 2 + 1) * 32)
                    ln_stats(nc, v, xt[:, s, :, :], bn, mv, ve, s_var)
                    v.wait_ge(s_rstd, u + 1)
                    if lo >= 2:
                        v.wait_ge(s_T, u - 1)
                    ln_apply(nc, v, xn[:, s, :, :], xt[:, s, :, :], mv, rn).then_inc(s_xn, 1)
                    nc.vector.tensor_copy(stats[:, bass.ds(u * 2, 2), :], rn[:, :, :])
                    if lo >= 1:
                        keys_values(u - 1, lo - 1)
                sweep(v, CHUNKS, step)
                keys_values(CHUNKS - 1, CHUNKS - 1)

            @block.scalar
            def _(act):
                def turn(u, s, lo):
                    if lo >= 2:
                        hold(act, s_sx[s], (u // 2) * 16)
                    hold(act, s_T, u + 1)
                    nc.scalar.copy(xnT[:, s, :, :], pT[:, s, 0:2 * CH].rearrange("p (k n) -> p k n", k=2))\
                      .then_inc(s_xnT, 1)

                def step(u, s, lo, hi):
                    if lo == 0:
                        turn(0, 0, 0)
                    if lo >= 2:
                        hold(act, s_st[s], (u // 2) * 32)
                    for t in range(2):
                        hold(act, s_h, 2 * u + t + 1)
                        nc.scalar.copy(hrow[:, s, t, :], pH[0:R, t, 0:C + 8]).then_inc(s_hrow, 1)
                    act.drain()
                    nc.scalar.copy(adst_all[:, bass.ds(2 * u, 2), :], hrow[:, s, :, C:C + 8])
                    if hi <= CHUNKS - 2:
                        turn(u + 1, 1 - s, lo + 1)
                    for t in range(2):
                        hold(act, s_kvt, 2 * u + t + 1)
                        nc.scalar.activation(sq[:, t, :], kvt[:, t, :], ACT.Square).then_inc(s_sq, 1)
                    hold(act, s_ss, 2 * u + 2)
                    nc.scalar.activation(sd[:, :, :], ss[:, :, :], ACT.Sqrt, bias=epst[0:R, :], scale=1.0 / HD)\
                      .then_inc(s_sd, 1)
                sweep(act, CHUNKS, step)

            @block.tensor
            def _(pe):
                def transposes(u, s, lo):
                    pe.wait_ge(s_xn, u + 1)
                    if lo >= 2:
                        pe.wait_ge(s_xnT, u - 1)
                    for k in range(2):
                        for t in range(2):
                            last = nc.tensor.transpose(pT[:, s, k * CH + t * R:k * CH + t * R + R],
                                                       xn[:, s, t, 128 * k:128 * k + 128], ident[0:R, 0:R])
                    last.then_inc(s_T, 1)

                def products(u, s, lo):
                    pe.wait_ge(s_xnT, u + 1)
                    for t in range(2):
                        i = 2 * u + t
                        if lo >= 1:
                            pe.wait_ge(s_hrow, i - 1)
                        for k in range(2):
                            last = nc.tensor.matmul(pH[0:R, t, 0:C + 8], xnT[:, s, k, t * R:t * R + R], wga[:, k, :],
                                                    start=k == 0, stop=k == 1)
                        last.then_inc(s_h, 1)
                    for t in range(2):
                        i = 2 * u + t
                        if lo >= 1:
                            pe.wait_ge(s_kvt, i - 1)
                        for k in range(2):
                            last = nc.tensor.matmul(pKV[0:R, t, :], xnT[:, s, k, t * R:t * R + R], wkv[:, k, :],
                                                    start=k == 0, stop=k == 1)
                        last.then_inc(s_kv, 1)

                def sums(u, s):
                    for t in range(2):
                        i = 2 * u + t
                        pe.wait_ge(s_kvn, i + 1)
                        for g in range(2):
                            nc.tensor.matmul(pS[:, 129 * g:129 * g + 129], kvn[:, t, 258 + 128 * g:386 + 128 * g],
                                             kvn[:, t, 129 * g:129 * g + 129], start=False, stop=False,
                                             skip_group_check=True)
                        last = nc.tensor.matmul(pK[:, 0:258], ones[0:R, :], kvn[:, t, 0:258], start=False, stop=False,
                                                skip_group_check=True)
                        last.then_inc(s_acc, 1)

                def step(u, s, lo, hi):
                    products(u, s, lo)
                    if hi <= CHUNKS - 2:
                        transposes(u + 1, 1 - s, lo + 1)
                    if lo >= 1:
                        sums(u - 1, 1 - s)

                nc.tensor.matmul(pS[:, 0:258], env["zeros"][0:1, 0:128], env["zeros"][0:1, 0:258], start=True, stop=False,
                                 skip_group_check=True)
                nc.tensor.matmul(pK[:, 0:258], env["zeros"][0:1, 0:128], env["zeros"][0:1, 0:258], start=True, stop=False,
                                 skip_group_check=True)
                transposes(0, 0, 0)
                sweep(pe, CHUNKS, step)
                sums(CHUNKS - 1, (CHUNKS - 1) % 2)
                pe.drain()

        kvT = sb("kvT", [128, 2, 128])
        mask = sb("mask", [128, 128])
        sA = sb("sA", [128, 2, 128])
        sv = sb("sv", [128, 2])
        m1 = sb("m1", [128, 2, C])
        wqT = sb("wqT", [128, 2, C])
        wq = sb("wq", [128, 2, C])
        amax = sb("amax", [R, 8])
        amaxT = sb("amaxT", [8, R])
        am1 = sb("am1", [8, 1])
        amr = sb("amr", [1, 8])
        amb = sb("amb", [128, 8])
        dtab = sb("dtab", [R, TILES, 8])
        g_ = sb("g_", [R, TILES, 4])
        dpart = sb("dpart", [R, TILES, 3, 8], BF16)
        drest = sb("drest", [R, 2, TILES, 8])
        zpad = sb("zpad", [W, 24], BF16)
        s_f = {k: sem("fold_" + k) for k in ("mask", "mask1", "wq", "qt", "qtc", "kvT", "m", "mc", "g", "am", "amT", "am1", "amr",
                                            "amrc", "amb", "dt", "zp", "gb")}
        with nc.Block() as block:
            @block.gpsimd
            def _(pool):
                nc.gpsimd.memset(mask[:, :], 0.0).then_inc(s_f["mask"], 1)
                nc.gpsimd.memset(zpad[:, :], 0.0).then_inc(s_f["zp"], 1)
                pool.wait_ge(s_f["mask"], 1)
                pool.drain()
                for h in range(4):
                    nc.gpsimd.memset(mask[HD * h:HD * (h + 1), HD * h:HD * (h + 1)], 1.0 / N)
                    pool.drain()
                pool.drain().then_inc(s_f["mask1"], 1)

            @block.tensor
            def _(pe):
                pe.wait_ge(s_f["wq"], 1)
                for g in range(2):
                    for k in range(2):
                        last = nc.tensor.transpose(pT[:, g, 128 * k:128 * k + 128],
                                                   wq[:, k, 128 * g:128 * g + 128], ident[:, :])
                last.then_inc(s_f["qt"], 1)
                pe.wait_ge(s_f["kvT"], 1)
                for g in range(2):
                    last = nc.tensor.matmul(pH[:, g, 0:C], kvT[:, g, :], w1[:, g, :], start=True, stop=True)
                last.then_inc(s_f["m"], 1)
                pe.wait_ge(s_f["mc"], 1)
                pe.wait_ge(s_f["qtc"], 1)
                for k in range(2):
                    for g in range(2):
                        last = nc.tensor.matmul(pKV[:, k, 0:C], wqT[:, g, 128 * k:128 * k + 128], m1[:, g, :],
                                                start=g == 0, stop=g == 1)
                for f in range(2):
                    for g in range(2):
                        last = nc.tensor.matmul(pT[:, 0, f:f + 1], m1[:, g, 128 * f:128 * f + 128], bqc[:, g:g + 1],
                                                start=g == 0, stop=g == 1)
                last.then_inc(s_f["g"], 1)
                pe.wait_ge(s_f["am"], 1)
                nc.tensor.transpose(pT[0:8, 1, 0:R], amax[:, :], ident[0:R, 0:R]).then_inc(s_f["amT"], 1)
                pe.wait_ge(s_f["am1"], 1)
                nc.tensor.transpose(pT[0:1, 1, 128:136], am1[:, :], ident[0:8, 0:8]).then_inc(s_f["amr"], 1)
                pe.wait_ge(s_f["amrc"], 1)
                nc.tensor.matmul(pT[:, 1, 256:264], ones[0:1, :], amr[:, :], start=True, stop=True).then_inc(s_f["amb"], 1)

            @block.vector
            def _(v):
                for k in range(2):
                    last = nc.vector.tensor_copy(
                        wq[:, k, :].rearrange("p (h d) -> p h d", d=HD),
                        wqkv[:, k, :].rearrange("p (h s d) -> p h s d", s=3, d=HD)[:, :, 0, :])
                last.then_inc(s_f["wq"], 1)
                v.wait_ge(s_f["qt"], 1)
                nc.vector.tensor_copy(wqT[:, :, :], pT[:, :, 0:C]).then_inc(s_f["qtc"], 1)
                v.wait_ge(s_f["mask1"], 1)
                for g in range(2):
                    S = pS[:, 129 * g:129 * g + 128]
                    gkb = gk[:, 0, :].unsqueeze(1).broadcast_to([128, 4, HD])
                    bkb = gk[:, 1, :].unsqueeze(1).broadcast_to([128, 4, HD])
                    nc.vector.tensor_scalar(sA[:, 0, :], S, gv[:, 0:1], None, ALU.mult)
                    v.drain()
                    nc.vector.scalar_tensor_tensor(out=sA[:, 1, :], in0=pK[:, 129 * g:129 * g + 128], scalar=gv[:, 1:2],
                                                   in1=sA[:, 0, :], op0=ALU.mult, op1=ALU.add)
                    v.drain()
                    nc.vector.tensor_tensor(out=sA[:, 0, :].rearrange("p (h d) -> p h d", h=4),
                                            in0=sA[:, 1, :].rearrange("p (h d) -> p h d", h=4), in1=gkb, op=ALU.mult)
                    nc.vector.tensor_scalar(sv[:, 0:1], gv[:, 1:2], float(N), None, ALU.mult)
                    v.drain()
                    nc.vector.scalar_tensor_tensor(out=sv[:, 1:2], in0=pS[:, 129 * g + 128:129 * g + 129],
                                                   scalar=gv[:, 0:1], in1=sv[:, 0:1], op0=ALU.mult, op1=ALU.add)
                    v.drain()
                    nc.vector.scalar_tensor_tensor(out=sA[:, 1, :].rearrange("p (h d) -> p h d", h=4), in0=bkb,
                                                   scalar=sv[:, 1:2], in1=sA[:, 0, :].rearrange("p (h d) -> p h d", h=4),
                                                   op0=ALU.mult, op1=ALU.add)
                    v.drain()
                    nc.vector.tensor_tensor(out=kvT[:, g, :], in0=sA[:, 1, :], in1=mask[:, :], op=ALU.mult)
                    v.drain()
                v.drain().then_inc(s_f["kvT"], 1)
                v.wait_ge(s_f["m"], 1)
                nc.vector.tensor_copy(m1[:, :, :], pH[:, :, 0:C]).then_inc(s_f["mc"], 1)
                v.wait_ge(s_f["g"], 1)
                nc.vector.tensor_tensor(out=g0[:, :, :], in0=pKV[:, :, 0:C], in1=w1[:, :, :], op=ALU.add)
                nc.vector.tensor_tensor(out=g0b[:, :], in0=pT[:, 0, 0:2], in1=b1c[:, :], op=ALU.add)
                nc.vector.tensor_reduce(amax[:, :], adst_all[:, :, :].rearrange("p t c -> p c t"), AX.X, ALU.max)\
                  .then_inc(s_f["am"], 1)
                v.wait_ge(s_f["amT"], 1)
                nc.vector.tensor_reduce(am1[:, :], pT[0:8, 1, 0:R], AX.X, ALU.max).then_inc(s_f["am1"], 1)
                v.wait_ge(s_f["amr"], 1)
                nc.vector.tensor_copy(amr[:, :], pT[0:1, 1, 128:136]).then_inc(s_f["amrc"], 1)
                v.wait_ge(s_f["amb"], 1)
                nc.vector.tensor_copy(amb[:, :], pT[:, 1, 256:264])
                v.drain()
                nc.vector.tensor_tensor(out=g_[:, :, :], in0=adst_all[:, :, 4:8],
                                        in1=amb[0:R, 0:4].unsqueeze(1).broadcast_to([R, TILES, 4]), op=ALU.add)
                nc.vector.tensor_copy(dtab[:, :, 0:4], adst_all[:, :, 4:8])
                v.drain()
                nc.vector.scalar_tensor_tensor(out=dtab[:, :, 4:8], in0=g_[:, :, :], scalar=0.2, in1=g_[:, :, :],
                                               op0=ALU.mult, op1=ALU.max)
                v.drain()
                rest = dtab[:, :, :]
                for i in range(3):
                    nc.vector.tensor_copy(dpart[:, :, i, :], rest)
                    v.drain()
                    if i < 2:
                        nc.vector.tensor_tensor(out=drest[:, i, :, :], in0=rest,
                                                in1=dpart[:, :, i, :], op=ALU.subtract)
                        v.drain()
                        rest = drest[:, i, :, :]
                v.drain().then_inc(s_f["dt"], 1)
                pself = env["pself"]
                nc.vector.tensor_tensor(out=g_[:, :, :], in0=adst_all[:, :, 0:4], in1=adst_all[:, :, 4:8], op=ALU.add)
                v.drain()
                nc.vector.scalar_tensor_tensor(out=pself[:, :, :], in0=g_[:, :, :], scalar=0.2, in1=g_[:, :, :],
                                               op0=ALU.mult, op1=ALU.max)
                v.drain()
                nc.vector.tensor_tensor(out=g_[:, :, :], in0=pself[:, :, :], in1=dtab[:, :, 4:8], op=ALU.subtract)
                v.drain().then_inc(s_f["gb"], 1)

            @block.scalar
            def _(act):
                act.wait_ge(s_f["gb"], 1)
                nc.scalar.activation(env["pself"][:, :, :], g_[:, :, :], ACT.Exp)
                act.drain()

            @block.sync
            def _(sp):
                sp.wait_ge(s_f["zp"], 1)
                sp.dma_start(adst[N:NPAD, :], zpad[:, :]).then_inc(s_ad, 16)
                sp.wait_ge(s_f["dt"], 1)
                rows_dma(sp, adst[0:N, :].rearrange("(t p) c -> p t c", p=R),
                         dpart[:, :, :, :].rearrange("p t i c -> p t (i c)"), s_ad)
                sp.wait_ge(s_ad, 48)


def edge_indices(env):
    nc, a, sem, ident = (env[k] for k in ("nc", "a", "sem", "ident"))
    srcI, dstRel, baseF, spanI = (env[k] for k in ("srcI", "dstRel", "baseF", "spanI"))
    GQ = GROUPS // 2
    with ExitStack() as ctx:
        sb = lambda n, s, d=F32: ctx.enter_context(nc.sbuf_tensor("ei_" + n, s, d))
        st = sb("st", [QB, 2, NB, R], I32)
        stf = sb("stf", [QB, 2, NB, R])
        gi = sb("gi", [GQ, 2, GT * R], I32)
        gf = sb("gf", [GQ, 2, GT * R])
        gm = sb("gm", [GQ, 2, 2])
        grow = sb("grow", [1, 2, GROUPS])
        gB = sb("gB", [R, GROUPS])
        sp_ = sb("sp", [1, GROUPS])
        dstT = sb("dstT", [R, ETILES])
        pt = ctx.enter_context(nc.psum_tensor("ei_pt", [128, 8, 512], F32))
        s_ld, s_cv, s_mm, s_st, s_row, s_t, s_ev = (sem("ei_" + n) for n in
                                                    ("load", "floats", "minmax", "store", "rows", "T", "copied"))
        gd = env["gf_d"]
        with nc.Block() as block:
            @block.sync
            def _(sp):
                for i, n in enumerate(("dst", "src")):
                    sp.dma_start(st[:, i, :, :], a[n].rearrange("(b q e) -> q b e", q=QB, e=R)).then_inc(s_ld, 16)
                sp.dma_start(gi[:, :, :], a["dst"].rearrange("(b q e) -> q b e", q=GQ, e=GT * R)).then_inc(s_ld, 16)
                sp.wait_ge(s_mm, 1)
                for i in range(2):
                    sp.dma_start(gd[i].rearrange("(b q o) -> q b o", q=GQ, o=1), gm[:, :, i:i + 1]).then_inc(s_st, 16)
                sp.wait_ge(s_st, 32)
                sp.dma_start(grow[:, :, :], gd.rearrange("(o i) g -> o i g", o=1)).then_inc(s_row, 16)
                sp.dma_start(gB[:, :], gd[0:1, :].broadcast_to([R, GROUPS])).then_inc(s_row, 16)
                sp.wait_ge(s_row, 32)

            @block.vector
            def _(v):
                v.wait_ge(s_ld, 48)
                nc.vector.tensor_copy(gf[:, :, :], gi[:, :, :])
                v.drain()
                nc.vector.tensor_reduce(gm[:, :, 0], gf[:, :, :], AX.X, ALU.min)
                nc.vector.tensor_reduce(gm[:, :, 1], gf[:, :, :], AX.X, ALU.max)
                v.drain().then_inc(s_mm, 1)
                nc.vector.tensor_copy(stf[:, :, :, :], st[:, :, :, :]).then_inc(s_cv, 1)
                for i, dst in enumerate((dstT, srcI)):
                    for b in range(NB):
                        n = NB * i + b
                        v.wait_ge(s_t, n + 1)
                        nc.vector.tensor_copy(dst[:, QB * b:QB * (b + 1)], pt[0:R, n % 8, 0:QB]).then_inc(s_ev, 1)
                v.wait_ge(s_row, 32)
                nc.vector.tensor_copy(baseF[:, :], grow[:, 0, :])
                nc.vector.tensor_tensor(out=sp_[:, :], in0=grow[:, 1, :], in1=grow[:, 0, :], op=ALU.subtract)
                v.drain()
                nc.vector.tensor_reduce(spanI[:, :], sp_[:, :], AX.X, ALU.max)
                nc.vector.tensor_tensor(out=dstRel[:, :].rearrange("p (g j) -> p g j", j=GT),
                                        in0=dstT[:, :].rearrange("p (g j) -> p g j", j=GT),
                                        in1=gB[:, :].unsqueeze(2).broadcast_to([R, GROUPS, GT]), op=ALU.subtract)
                v.drain()

            @block.tensor
            def _(pe):
                pe.wait_ge(s_cv, 1)
                for n in range(2 * NB):
                    if n >= 8:
                        pe.wait_ge(s_ev, n - 7)
                    nc.tensor.transpose(pt[0:R, n % 8, 0:QB], stf[:, n // NB, n % NB, :], ident[0:QB, 0:QB])\
                      .then_inc(s_t, 1)


def edge_passes(env, layer, zero, one_pass, dma_sems, sems):
    nc, sem = env["nc"], env["sem"]
    iotaI, iotaW, baseI, baseF, spanI = (env[k] for k in ("iotaI", "iotaW", "baseI", "baseF", "spanI"))
    s_i = sem(f"window_iota{layer}")
    with nc.Block() as block:
        @block.gpsimd
        def _(pool):
            nc.gpsimd.iota(iotaI[:, :], pattern=[[1, W]], base=0, channel_multiplier=0).then_inc(s_i, 1)

        @block.vector
        def _(v):
            for t in zero:
                nc.vector.memset(t, 0.0)
            nc.vector.tensor_copy(baseI[:, :], baseF[:, :])
            v.wait_ge(s_i, 1)
            nc.vector.tensor_copy(iotaW[:, :], iotaI[:, :])
            v.drain()
    span = nc.values_load(spanI[0:1, 0:1], min_val=0, max_val=N - 1)
    with nc.Fori(0, span + 1, W):
        one_pass()
        with nc.Block() as block:
            @block.vector
            def _(v):
                nc.vector.tensor_scalar(iotaW[:, :], iotaW[:, :], float(W), None, ALU.add)
                nc.vector.tensor_scalar(baseI[:, :], baseI[:, :], float(W), float(N), ALU.add, ALU.min)
                v.drain()

            @block.gpsimd
            def _(pool):
                m = len(dma_sems)
                nc.gpsimd.inc_swdge_sem(dma_sems, [-(-(GROUPS - i) // m) * GT * 16 for i in range(m)], mode="sub")
                for s in sems:
                    pool.sem_clear(s)


def one_hots(nc, env, out, g):
    return nc.vector.tensor_tensor(
        out=out, in0=env["iotaW"][:, :].unsqueeze(1).broadcast_to([R, GT, W]),
        in1=env["dstRel"][:, bass.ds(g * GT, GT)].unsqueeze(2).broadcast_to([R, GT, W]), op=ALU.is_equal)


def edges0(env, acc, den):
    nc, sem, ident = (env[k] for k in ("nc", "sem", "ident"))
    srcI, baseI = env["srcI"], env["baseI"]
    with ExitStack() as ctx:
        sb = lambda n, s, d=F32: ctx.enter_context(nc.sbuf_tensor("e0_" + n, s, d))
        pb = lambda n, s: ctx.enter_context(nc.psum_tensor("e0_" + n, s, F32))
        ix = sb("ix", [R, SLOTS, GT], I32)
        rows = sb("rows", [R, SLOTS, GT, TAB0])
        dw = sb("dw", [W, SLOTS, 24], BF16)
        oh = sb("oh", [R, SLOTS, GT, W])
        ohT = sb("ohT", [W, 2, GT, R], BF16)
        lg = sb("lg", [R, GT, 8])
        ee = sb("ee", [R, 4, GT, H0])
        msg = sb("msg", [R, 3, GT, TAB0])
        us = sb("us", [128, 2, TAB0])
        eye2 = sb("eye2", [128, W])
        pT = pb("pT", [W, 1024])
        pE = pb("pE", [R, 2, 512])
        pU = pb("pU", [128, 2, 512])
        pF = pb("pF", [128, 2, 512])
        s_gat = [sem(f"e0_rows{i}", software_dma=True) for i in range(SLOTS)]
        s_dw = [sem(f"e0_dw{i}") for i in range(SLOTS)]
        s_ix, s_oh, s_T, s_ohT, s_E, s_lg, s_ed, s_p, s_msg, s_acc, s_us, s_flip, s_add = (
            sem("e0_" + n) for n in ("ix", "oh", "T", "ohT", "E", "logits", "exponents", "p", "msg", "acc", "copied",
                                     "flip", "added"))
        with nc.Block() as block:
            @block.vector
            def _(v):
                nc.vector.tensor_tensor(out=eye2[:, :], in0=ident[:, 0:W], in1=ident[:, W:2 * W], op=ALU.add)
                v.drain()

        def one_pass():
            with nc.Block() as block:
                @block.gpsimd
                def _(pool):
                    def step(g, s, lo, hi):
                        hold(pool, s_ix, g + 1)
                        for j in range(GT):
                            nc.gpsimd.indirect_dma_start(
                                out=rows[:, s, j, :], out_offset=None, in_=env["tab0"],
                                in_offset=bass.IndirectOffsetOnAxis(ap=ix[:, s, j:j + 1], axis=0))\
                              .then_inc(s_gat[s], 16)
                    sweep(pool, GROUPS, step, SLOTS, AHEAD)

                @block.sync
                def _(sp):
                    def step(g, s, lo, hi):
                        base = sp.value_load(baseI[0:1, bass.ds(g, 1)], min_val=0, max_val=N)
                        if lo >= SLOTS:
                            sp.wait_ge(s_E, g - SLOTS + 1)
                        sp.dma_start(dw[:, s, :], env["dst_tab"][bass.ds(base, W), :]).then_inc(s_dw[s], 16)
                    sweep(sp, GROUPS, step, SLOTS, AHEAD)

                @block.scalar
                def _(act):
                    def stage(g, s, lo):
                        if lo >= SLOTS:
                            hold(act, s_msg, g - SLOTS + 1)
                        nc.scalar.copy(ix[:, s, :], srcI[:, bass.ds(g * GT, GT)]).then_inc(s_ix, 1)

                    def turn(g, s, lo):
                        if lo >= 2:
                            hold(act, s_E, g - 1)
                        hold(act, s_T, g + 1)
                        nc.scalar.copy(ohT[:, s % 2, :, :],
                                       pT[:, 0:128 * GT].rearrange("p (j e) -> p j e", e=128)[:, :, 0:R])\
                          .then_inc(s_ohT, 1)

                    def copied(g, s, lo):
                        if lo >= 2:
                            hold(act, s_flip, g - 1)
                        hold(act, s_acc, g + 1)
                        nc.scalar.copy(us[:, s % 2, :], pU[:, s % 2, 0:TAB0]).then_inc(s_us, 1)

                    def step(g, s, lo, hi):
                        if lo == 0:
                            for i in range(3):
                                stage(i, i, i)
                            for i in range(2):
                                turn(i, i, i)
                        if hi <= GROUPS - 3:
                            turn(g + 2, (s + 2) % SLOTS, lo + 2)
                        if lo >= 3:
                            hold(act, s_acc, g - 2)
                        hold(act, s_ed, g + 1)
                        nc.scalar.activation(msg[:, s % 3, :, C:TAB0], ee[:, 2 + s % 2, :, :], ACT.Exp).then_inc(s_p, 1)
                        if lo >= 2:
                            copied(g - 2, s, lo - 2)
                        if hi <= GROUPS - 4:
                            stage(g + 3, (s + 3) % SLOTS, lo + 3)
                        if lo == GROUPS - 1:
                            copied(g - 1, s + 1, lo)
                            copied(g, s, lo)
                    sweep(act, GROUPS, step, SLOTS, AHEAD)

                @block.vector
                def _(v):
                    def hots(g, s, lo):
                        if lo >= SLOTS:
                            v.wait_ge(s_acc, g - SLOTS + 1)
                        one_hots(nc, env, oh[:, s, :, :], g).then_inc(s_oh, 1)

                    def add(g, s):
                        base = v.value_load(baseI[0:1, bass.ds(g, 1)], min_val=0, max_val=N)
                        v.wait_ge(s_flip, g + 1)
                        w = acc[:, :, bass.ds(base, W)]
                        nc.vector.tensor_tensor(out=w, in0=w,
                                                in1=pF[:, s % 2, 0:2 * W].rearrange("p (k n) -> p k n", k=2), op=ALU.add)
                        w = den[:, bass.ds(base, W)]
                        nc.vector.tensor_tensor(out=w, in0=w, in1=pF[0:H0, s % 2, 2 * W:3 * W], op=ALU.add).then_inc(s_add, 1)

                    def exponents(g, s, lo):
                        v.wait_ge(s_gat[s], (g // SLOTS + 1) * 16 * GT)
                        if lo >= 1:
                            v.wait_ge(s_ed, g)
                        v.wait_ge(s_E, g + 1)
                        nc.vector.tensor_reduce(
                            lg[:, :, :], pE[:, s % 2, 0:24 * GT].rearrange("p (j i c) -> p j c i", i=3, c=8), AX.X,
                            ALU.add).then_inc(s_lg, 1)
                        v.drain()
                        nc.vector.tensor_tensor(out=ee[:, 0, :, :], in0=rows[:, s, :, C:C + H0], in1=lg[:, :, 0:H0],
                                                op=ALU.add)
                        v.drain()
                        nc.vector.scalar_tensor_tensor(out=ee[:, 1, :, :], in0=ee[:, 0, :, :], scalar=0.2,
                                                       in1=ee[:, 0, :, :], op0=ALU.mult, op1=ALU.max)
                        v.drain()
                        nc.vector.tensor_tensor(out=ee[:, 0, :, :], in0=ee[:, 1, :, :], in1=lg[:, :, H0:8],
                                                op=ALU.subtract)
                        v.drain()
                        if lo >= 2:
                            v.wait_ge(s_p, g - 1)
                        nc.vector.tensor_scalar(ee[:, 2 + s % 2, :, :], ee[:, 0, :, :], 0.0, None, ALU.min)\
                          .then_inc(s_ed, 1)

                    def messages(g, s, lo):
                        v.wait_ge(s_p, g + 1)
                        nc.vector.tensor_tensor(
                            out=msg[:, s % 3, :, 0:C].rearrange("p j (h c) -> p j h c", h=H0),
                            in0=rows[:, s, :, 0:C].rearrange("p j (h c) -> p j h c", h=H0),
                            in1=msg[:, s % 3, :, C:TAB0].unsqueeze(3).broadcast_to([R, GT, H0, D0]), op=ALU.mult)\
                          .then_inc(s_msg, 1)

                    def step(g, s, lo, hi):
                        if lo == 0:
                            hots(0, 0, 0)
                            hots(1, 1, 1)
                        if hi <= GROUPS - 3:
                            hots(g + 2, (s + 2) % SLOTS, lo + 2)
                        exponents(g, s, lo)
                        if lo >= 4:
                            add(g - 4, s)
                        if lo >= 1:
                            messages(g - 1, (s - 1) % SLOTS, lo - 1)
                        if lo == GROUPS - 1:
                            messages(g, s, lo)
                            for i in (3, 2, 1, 0):
                                v.drain()
                                add(g - i, s + i)
                            v.drain()
                    sweep(v, GROUPS, step, SLOTS, AHEAD)

                @block.tensor
                def _(pe):
                    def turn(g, s, lo):
                        if lo >= 1:
                            pe.wait_ge(s_ohT, g)
                        hold(pe, s_oh, g + 1)
                        for j in range(GT):
                            last = nc.tensor.transpose(pT[:, 128 * j:128 * j + R], oh[:, s, j, :], ident[0:R, 0:R])
                        last.then_inc(s_T, 1)

                    def logits(g, s, lo):
                        pe.wait_ge(s_ohT, g + 1)
                        pe.wait_ge(s_dw[s], (g // SLOTS + 1) * 16)
                        if lo >= 2:
                            pe.wait_ge(s_lg, g - 1)
                        for j in range(GT):
                            last = nc.tensor.matmul(pE[:, s % 2, 24 * j:24 * j + 24], ohT[:, s % 2, j, :], dw[:, s, :],
                                                    start=True, stop=True)
                        last.then_inc(s_E, 1)

                    def sums(g, s, lo):
                        pe.wait_ge(s_msg, g + 1)
                        if lo >= 2:
                            pe.wait_ge(s_us, g - 1)
                        for j in range(GT):
                            h = W * (j % 2)
                            last = nc.tensor.matmul(pU[h:h + W, s % 2, 0:TAB0], oh[:, s, j, :], msg[:, s % 3, j, :],
                                                    start=j < 2, stop=j >= GT - 2)
                        last.then_inc(s_acc, 1)

                    def flip(g, s, lo):
                        pe.wait_ge(s_us, g + 1)
                        if lo >= 2:
                            pe.wait_ge(s_add, g - 1)
                        for k in range(2):
                            nc.tensor.matmul(pF[:, s % 2, k * W:k * W + W], us[:, s % 2, 128 * k:128 * k + 128],
                                             eye2[:, :], start=True, stop=True)
                        nc.tensor.matmul(pF[0:H0, s % 2, 2 * W:3 * W], us[:, s % 2, C:TAB0], eye2[:, :],
                                         start=True, stop=True).then_inc(s_flip, 1)

                    def step(g, s, lo, hi):
                        if lo == 0:
                            turn(0, 0, 0)
                            turn(1, 1, 1)
                            logits(0, 0, 0)
                        if hi <= GROUPS - 3:
                            turn(g + 2, (s + 2) % SLOTS, lo + 2)
                        if lo >= 2:
                            sums(g - 2, (s - 2) % SLOTS, lo - 2)
                        if lo >= 3:
                            flip(g - 3, s + 1, lo - 3)
                        if hi <= GROUPS - 2:
                            logits(g + 1, (s + 1) % SLOTS, lo + 1)
                        if lo == GROUPS - 1:
                            sums(g - 1, (s - 1) % SLOTS, lo - 1)
                            flip(g - 2, s, lo)
                            sums(g, s, lo)
                            flip(g - 1, s + 1, lo)
                            flip(g, s, lo)
                    sweep(pe, GROUPS, step, SLOTS, AHEAD)

        edge_passes(env, 0, [acc[:, :, :], den[:, :]], one_pass, s_gat,
                    s_dw + [s_ix, s_oh, s_T, s_ohT, s_E, s_lg, s_ed, s_p, s_msg, s_acc, s_us, s_flip, s_add])


def row_bc(ap, parts):
    return ap.rearrange("(o n) -> o n", o=1).broadcast_to([parts, ap.shape[0]])


def back0(env, acc, den):
    nc, a, sem, ident, ones, stats = (env[k] for k in ("nc", "a", "sem", "ident", "ones", "stats"))
    cv = env["chunk_view"]
    g0, g0b, pself = env["g0"], env["g0b"], env["pself"]
    x_v, tab_v, x1_v = cv(env["x_in"]), cv(env["tab0"]), cv(env["x_d"][0])
    with ExitStack() as ctx:
        sb = lambda n, s, d=F32: ctx.enter_context(nc.sbuf_tensor("b0_" + n, s, d))
        pb = lambda n, s: ctx.enter_context(nc.psum_tensor("b0_" + n, s, F32))
        w2 = sb("w2", [128, 2, C])
        crow = sb("crow", [R, 2, C])
        xt = sb("xt", [R, 2, 2, C])
        ht = sb("ht", [R, 2, 2, TAB0])
        xnT = sb("xnT", [128, 2, 2, CH])
        us = sb("us", [128, 2, 2, CH])
        ds_ = sb("ds", [H0, 2, CH])
        gT = sb("gT", [128, 2, CH])
        dn = sb("dn", [R, 2, H0])
        sc = sb("sc", [R, 2, 2])
        ya = sb("ya", [R, 2, C])
        yb = sb("yb", [R, 2, C])
        xx = sb("xx", [R, 2, C])
        x1 = sb("x1", [R, 2, 2, C])
        xn1 = sb("xn1", [R, 2, 2, C])
        bn, mv, ve, rn, mhalf = (sb("bn", [R, 2, 6]), sb("mv", [R, 2, 2, 2]), sb("ve", [R, 2]), sb("rn", [R, 2, 2]),
                                 sb("mhalf", [R, 2]))
        xT = sb("xT", [128, 2, 2, CH])
        pU, pN, pH, pO, pT = (pb("pU", [R, 512]), pb("pN", [R, 512]), pb("pH", [128, 512]), pb("pO", [R, 512]),
                              pb("pT", [128, 512]))
        pSum = pb("pSum", [128, 512])
        s_w, s_z = sem("b0_weights"), sem("b0_consts")
        s_ld = [sem("b0_load0"), sem("b0_load1")]
        s_st = [sem("b0_store0"), sem("b0_store1")]
        s_sx = [sem("b0_storeT0"), sem("b0_storeT1")]
        s_us, s_U, s_H, s_g, s_O, s_x1, s_var, s_rstd, s_xn1, s_T, s_xT, s_rd, s_sum = (
            sem("b0_" + n) for n in ("sums", "U", "H", "gelu", "O", "x1", "var", "rstd", "xn1", "T", "xT", "read", "xsum"))

        with nc.Block() as block:
            @block.sync
            def _(sp):
                sp.dma_start(w2[:, :, :], a["L0_mix_w2"].rearrange("(k p) n -> p k n", p=128)).then_inc(s_w, 16)
                sp.dma_start(crow[:, 0, :], row_bc(a["L0_gnn_bias"], R)).then_inc(s_w, 16)
                sp.dma_start(crow[:, 1, :], row_bc(a["L0_mix_b2"], R)).then_inc(s_w, 16)
                sp.wait_ge(s_w, 48)

            @block.gpsimd
            def _(pool):
                nc.gpsimd.memset(mhalf[:, :], -0.5)
                pool.drain()

        with nc.Block() as block:
            @block.vector
            def _(v):
                nc.vector.tensor_tensor(out=crow[:, 0, :], in0=crow[:, 0, :], in1=crow[:, 1, :], op=ALU.add)
                v.drain()

        with nc.Block() as block:
            @block.sync
            def _(sp):
                def load(u, s):
                    rows_dma(sp, xt[:, s, :, :], x_v[u], s_ld[s])
                    rows_dma(sp, ht[:, s, :, :], tab_v[u], s_ld[s])
                    sp.dma_start(xnT[:, s, :, :], env["xnT_d"][0][:, :, bass.ds(u * CH, CH)]).then_inc(s_ld[s], 16)

                def store(u, s):
                    sp.wait_ge(s_x1, u + 1)
                    rows_dma(sp, x1_v[u], x1[:, s, :, :], s_st[s])
                    sp.wait_ge(s_xT, u + 1)
                    sp.dma_start(env["xnT_d"][1][:, :, bass.ds(u * CH, CH)], xT[:, s, :, :]).then_inc(s_sx[s], 16)

                def step(u, s, lo, hi):
                    if lo >= 2:
                        sp.wait_ge(s_rd, u - 1)
                        sp.wait_ge(s_H, u - 1)
                    load(u, s)
                    if lo >= 2:
                        store(u - 2, s)
                sweep(sp, CHUNKS, step)
                for u in (CHUNKS - 2, CHUNKS - 1):
                    store(u, u % 2)
                for i in range(2):
                    n = (CHUNKS + 1 - i) // 2
                    sp.wait_ge(s_st[i], 32 * n)
                    sp.wait_ge(s_sx[i], 16 * n)

            @block.scalar
            def _(act):
                def pick(u, s, lo):
                    if lo >= 2:
                        hold(act, s_U, u - 1)
                    nc.scalar.copy(us[:, s, :, :], acc[:, :, bass.ds(u * CH, CH)])
                    nc.scalar.copy(ds_[:, s, :], den[:, bass.ds(u * CH, CH)]).then_inc(s_us, 1)

                def turn(u, s, lo):
                    if lo >= 2:
                        hold(act, s_sx[s], (u // 2) * 16)
                    hold(act, s_T, u + 1)
                    nc.scalar.copy(xT[:, s, :, :], pT[:, 0:2 * CH].rearrange("p (k n) -> p k n", k=2)).then_inc(s_xT, 1)

                def step(u, s, lo, hi):
                    if lo == 0:
                        pick(0, 0, 0)
                    if hi <= CHUNKS - 2:
                        pick(u + 1, 1 - s, lo + 1)
                    if lo >= 1:
                        hold(act, s_O, u)
                    hold(act, s_H, u + 1)
                    for f in range(2):
                        last = nc.scalar.activation(gT[:, f, :], pH[:, f * CH:(f + 1) * CH], ACT.Gelu, bias=g0b[:, f:f + 1])
                    last.then_inc(s_g, 1)
                    if lo >= 1:
                        turn(u - 1, 1 - s, lo - 1)
                    if lo == CHUNKS - 1:
                        turn(u, s, lo)
                sweep(act, CHUNKS, step)

            @block.gpsimd
            def _(pool):
                def step(u, s, lo, hi):
                    hold(pool, s_var, u + 1)
                    nc.gpsimd.tensor_tensor(out=rn[:, :, 0], in0=ve[:, :], in1=mhalf[:, :], op=ALU.pow)\
                      .then_inc(s_rstd, 1)
                sweep(pool, CHUNKS, step)

            @block.vector
            def _(v):
                def finish(u, s, lo):
                    v.wait_ge(s_rstd, u + 1)
                    if lo >= 2:
                        v.wait_ge(s_sum, u - 1)
                    ln_apply(nc, v, xn1[:, s, :, :], x1[:, s, :, :], mv[:, s, :, :], rn).then_inc(s_xn1, 1)
                    nc.vector.tensor_copy(stats[:, bass.ds(u * 2, 2), :], rn[:, :, :])
                    v.drain()

                def step(u, s, lo, hi):
                    if lo >= 1:
                        finish(u - 1, 1 - s, lo - 1)
                    v.wait_ge(s_ld[s], (u // 2 + 1) * 80)
                    nc.vector.tensor_scalar(sc[:, :, 0], stats[:, bass.ds(u * 2, 2), 0], 1.0, None, ALU.add)
                    nc.vector.tensor_copy(sc[:, :, 1], stats[:, bass.ds(u * 2, 2), 1])
                    v.wait_ge(s_U, u + 1)
                    nc.vector.tensor_tensor(out=dn[:, :, :], in0=pN[:, 0:2 * H0].rearrange("p (t h) -> p t h", t=2),
                                            in1=pself[:, bass.ds(u * 2, 2), :], op=ALU.add)
                    v.drain()
                    for t in range(2):
                        nc.vector.tensor_scalar(xx[:, t, :], xt[:, s, t, :], sc[:, t, 0:1], sc[:, t, 1:2],
                                                ALU.mult, ALU.add)
                    nc.vector.reciprocal(dn[:, :, :], dn[:, :, :])
                    nc.vector.tensor_tensor(
                        out=ya[:, :, :].rearrange("p t (h c) -> p t h c", h=H0),
                        in0=ht[:, s, :, 0:C].rearrange("p t (h c) -> p t h c", h=H0),
                        in1=pself[:, bass.ds(u * 2, 2), :].unsqueeze(3).broadcast_to([R, 2, H0, D0]), op=ALU.mult)
                    v.drain()
                    nc.vector.tensor_tensor(out=yb[:, :, :], in0=ya[:, :, :],
                                            in1=pU[:, :].rearrange("p (t c) -> p t c", t=2), op=ALU.add)
                    v.drain().then_inc(s_rd, 1)
                    nc.vector.tensor_tensor(
                        out=ya[:, :, :].rearrange("p t (h c) -> p t h c", h=H0),
                        in0=yb[:, :, :].rearrange("p t (h c) -> p t h c", h=H0),
                        in1=dn[:, :, :].unsqueeze(3).broadcast_to([R, 2, H0, D0]), op=ALU.mult)
                    nc.vector.tensor_tensor(out=xx[:, :, :], in0=xx[:, :, :],
                                            in1=crow[:, 0, :].unsqueeze(1).broadcast_to([R, 2, C]), op=ALU.add)
                    v.drain()
                    nc.vector.tensor_tensor(out=yb[:, :, :], in0=ya[:, :, :], in1=xx[:, :, :], op=ALU.add)
                    v.drain()
                    v.wait_ge(s_O, u + 1)
                    if lo >= 2:
                        v.wait_ge(s_st[s], (u // 2) * 32)
                    nc.vector.tensor_tensor(out=x1[:, s, :, :], in0=yb[:, :, :],
                                            in1=pO[:, :].rearrange("p (t c) -> p t c", t=2), op=ALU.add)
                    v.drain().then_inc(s_x1, 1)
                    ln_stats(nc, v, x1[:, s, :, :], bn, mv[:, s, :, :], ve, s_var)
                    if lo == CHUNKS - 1:
                        finish(u, s, lo)
                sweep(v, CHUNKS, step)

            @block.tensor
            def _(pe):
                def front(u, s, lo):
                    pe.wait_ge(s_us, u + 1)
                    if lo >= 1:
                        pe.wait_ge(s_rd, u)
                    for t in range(2):
                        for k in range(2):
                            nc.tensor.transpose(pU[:, t * C + 128 * k:t * C + 128 * k + 128],
                                                us[:, s, k, t * R:t * R + R], ident[:, :])
                    for t in range(2):
                        last = nc.tensor.transpose(pN[:, t * H0:t * H0 + H0], ds_[:, s, t * R:t * R + R],
                                                   ident[0:H0, 0:H0])
                    last.then_inc(s_U, 1)
                    pe.wait_ge(s_ld[s], (u // 2 + 1) * 80)
                    if lo >= 1:
                        pe.wait_ge(s_g, u)
                    for f in range(2):
                        for k in range(2):
                            last = nc.tensor.matmul(pH[:, f * CH:(f + 1) * CH], g0[:, k, 128 * f:128 * f + 128],
                                                    xnT[:, s, k, :], start=k == 0, stop=k == 1)
                    last.then_inc(s_H, 1)

                def turn(u, s, lo):
                    pe.wait_ge(s_xn1, u + 1)
                    if lo >= 1:
                        pe.wait_ge(s_xT, u)
                    for k in range(2):
                        for t in range(2):
                            last = nc.tensor.transpose(pT[:, k * CH + t * R:k * CH + t * R + R],
                                                       xn1[:, s, t, 128 * k:128 * k + 128], ident[0:R, 0:R])
                    last.then_inc(s_T, 1)
                    for k in range(2):
                        for t in range(2):
                            last = nc.tensor.matmul(pSum[:, k:k + 1], xn1[:, s, t, 128 * k:128 * k + 128], ones[0:R, 0:1],
                                                    start=False, stop=False, skip_group_check=True)
                    last.then_inc(s_sum, 1)

                def step(u, s, lo, hi):
                    if lo == 0:
                        front(0, 0, 0)
                    pe.wait_ge(s_g, u + 1)
                    if lo >= 1:
                        pe.wait_ge(s_x1, u)
                    for t in range(2):
                        for f in range(2):
                            last = nc.tensor.matmul(pO[:, t * C:(t + 1) * C], gT[:, f, t * R:t * R + R], w2[:, f, :],
                                                    start=f == 0, stop=f == 1)
                    last.then_inc(s_O, 1)
                    if hi <= CHUNKS - 2:
                        front(u + 1, 1 - s, lo + 1)
                    if lo >= 1:
                        turn(u - 1, 1 - s, lo - 1)
                    if lo == CHUNKS - 1:
                        turn(u, s, lo)
                nc.tensor.matmul(pSum[:, 0:2], env["zeros"][0:1, 0:128], env["zeros"][0:1, 0:2], start=True, stop=False,
                                 skip_group_check=True)
                sweep(pe, CHUNKS, step)
                pe.drain()

        with nc.Block() as block:
            @block.vector
            def _(v):
                nc.vector.tensor_copy(env["x1sum"][:, :], pSum[:, 0:2])
                v.drain()


def ffn0(env):
    nc, a, sem, ident, ones, stats = (env[k] for k in ("nc", "a", "sem", "ident", "ones", "stats"))
    cv = env["chunk_view"]
    x1_v, x2_v = cv(env["x_d"][0]), cv(env["x_d"][1])
    NF = 2 * F0 // 128
    with ExitStack() as ctx:
        sb = lambda n, s, d=F32: ctx.enter_context(nc.sbuf_tensor("m_" + n, s, d))
        pb = lambda n, s: ctx.enter_context(nc.psum_tensor("m_" + n, s, F32))
        w1 = sb("w1", [128, 2, 2, F0])
        w2 = sb("w2", [128, NF, C])
        b1 = sb("b1", [128, NF])
        b2 = sb("b2", [R, 3, C])
        gam = sb("gam", [R, 2, C])
        wr = sb("wr", [128, 2, E8])
        br = sb("br", [1, E8])
        lg = sb("lg", [1, 8, E8])
        sm = sb("sm", [1, 8])
        ei = sb("ei", [1, 8], U32)
        wB = sb("wB", [128, 2])
        xnT = sb("xnT", [128, 4, 2, CH])
        x1 = sb("x1", [R, 4, 2, C])
        hT = sb("hT", [128, 2, NF, CH])
        ya = sb("ya", [R, 2, C])
        yb = sb("yb", [R, 2, C])
        xnb = sb("xnb", [R, 2, C])
        x2 = sb("x2", [R, 2, 2, C])
        xn2 = sb("xn2", [R, 2, 2, C])
        sc = sb("sc", [R, 2, 2])
        bn, mv, ve, rn, mhalf = (sb("bn", [R, 2, 6]), sb("mv", [R, 2, 2]), sb("ve", [R, 2]), sb("rn", [R, 2, 2]),
                                 sb("mhalf", [R, 2]))
        xT = sb("xT", [128, 2, 2, CH])
        pH, pO, pT = pb("pH", [128, NF // 2, 512]), pb("pO", [R, 512]), pb("pT", [128, 512])
        s_w, s_l, s_act, s_l2, s_e, s_wb = (sem("m_" + n) for n in ("weights", "logits", "exp", "l2", "experts", "wB"))
        s_ld = [sem(f"m_load{i}") for i in range(4)]
        s_st = [sem("m_store0"), sem("m_store1")]
        s_sx = [sem("m_storeT0"), sem("m_storeT1")]
        s_H, s_g, s_O, s_Or, s_x2, s_var, s_rstd, s_xn2, s_T, s_xT = (
            sem("m_" + n) for n in ("H", "gelu", "O", "Oread", "x2", "var", "rstd", "xn2", "T", "xT"))

        with nc.Block() as block:
            @block.sync
            def _(sp):
                sp.dma_start(wr[:, :, :], a["L0_ffn_Wr"].rearrange("(k p) n -> p k n", p=128)).then_inc(s_w, 16)
                sp.dma_start(br[:, :], row_bc(a["L0_ffn_br"], 1)).then_inc(s_w, 16)
                sp.dma_start(gam[:, 0, :], row_bc(a["L0_ffn_gamma"], R)).then_inc(s_w, 16)
                sp.dma_start(gam[:, 1, :], row_bc(a["L0_ffn_beta"], R)).then_inc(s_w, 16)
                sp.wait_ge(s_w, 64)
                sp.wait_ge(s_e, 1)
                for j in range(2):
                    e = sp.value_load(ei[0:1, j:j + 1], min_val=0, max_val=E8 - 1)
                    ix = bass.ds(e, 1)
                    sp.dma_start(w1[:, j, :, :], a["L0_ffn_W1"][ix].rearrange("e (k p) f -> p (e k) f", p=128))\
                      .then_inc(s_w, 16)
                    sp.dma_start(w2[:, j * NF // 2:(j + 1) * NF // 2, :],
                                 a["L0_ffn_W2"][ix].rearrange("e (f p) n -> p (e f) n", p=128)).then_inc(s_w, 16)
                    sp.dma_start(b1[:, j * NF // 2:(j + 1) * NF // 2],
                                 a["L0_ffn_b1"][ix].rearrange("e (f p) -> p (e f)", p=128)).then_inc(s_w, 16)
                    sp.dma_start(b2[:, j, :], a["L0_ffn_b2"][ix].broadcast_to([R, C])).then_inc(s_w, 16)
                sp.wait_ge(s_w, 64 + 128)

            @block.gpsimd
            def _(pool):
                nc.gpsimd.memset(mhalf[:, :], -0.5)
                pool.drain()

            @block.tensor
            def _(pe):
                pe.wait_ge(s_w, 64)
                for k in range(2):
                    last = nc.tensor.matmul(pO[0:1, 0:E8], env["x1sum"][:, k:k + 1], wr[:, k, :], start=k == 0, stop=k == 1)
                last.then_inc(s_l, 1)
                pe.wait_ge(s_wb, 1)
                nc.tensor.matmul(pT[:, 0:2], ones[0:1, :], sm[0:1, 6:8], start=True, stop=True).then_inc(s_l, 1)

            @block.scalar
            def _(act):
                for n, (i, w) in enumerate(((1, E8), (3, E8), (6, 2))):
                    act.wait_ge(s_l2, n + 1)
                    nc.scalar.activation(lg[:, i, 0:w], lg[:, i, 0:w], ACT.Exp).then_inc(s_act, 1)

            @block.vector
            def _(v):
                ts, tt = nc.vector.tensor_scalar, nc.vector.tensor_tensor
                v.wait_ge(s_w, 64)
                v.wait_ge(s_l, 1)
                nc.vector.scalar_tensor_tensor(out=lg[:, 0, :], in0=pO[0:1, 0:E8], scalar=1.0 / N, in1=br[:, :],
                                               op0=ALU.mult, op1=ALU.add)
                v.drain()

                def softmax(src, dst, n, w, m):
                    nc.vector.tensor_reduce(sm[:, m:m + 1], lg[:, src, 0:w], AX.X, ALU.max)
                    v.drain()
                    ts(lg[:, dst, 0:w], lg[:, src, 0:w], sm[:, m:m + 1], None, ALU.subtract).then_inc(s_l2, 1)
                    v.wait_ge(s_act, n + 1)
                    nc.vector.tensor_reduce(sm[:, m + 1:m + 2], lg[:, dst, 0:w], AX.X, ALU.add)
                    v.drain()
                    nc.vector.reciprocal(sm[:, m + 1:m + 2], sm[:, m + 1:m + 2])
                    v.drain()

                softmax(0, 1, 0, E8, 0)
                ts(lg[:, 1, :], lg[:, 1, :], sm[:, 1:2], None, ALU.mult)
                v.drain()
                ts(lg[:, 2, :], lg[:, 1, :], float(N) / CAPACITY, None, ALU.mult)
                v.drain()
                nc.vector.reciprocal(lg[:, 2, :], lg[:, 2, :])
                v.drain()
                ts(lg[:, 2, :], lg[:, 2, :], 1.0, None, ALU.min)
                v.drain()
                tt(out=lg[:, 4, :], in0=lg[:, 1, :], in1=lg[:, 2, :], op=ALU.mult)
                v.drain()
                softmax(4, 3, 1, E8, 2)
                ts(lg[:, 3, :], lg[:, 3, :], sm[:, 3:4], None, ALU.mult)
                v.drain()
                nc.vector.max(lg[:, 5, :], lg[:, 3, :])
                v.drain()
                nc.vector.max_index(ei[:, :], lg[:, 5, :], lg[:, 3, :])
                v.drain().then_inc(s_e, 1)
                softmax(5, 6, 2, 2, 4)
                ts(sm[:, 6:8], lg[:, 6, 0:2], sm[:, 5:6], None, ALU.mult)
                v.drain().then_inc(s_wb, 1)
                v.wait_ge(s_l, 2)
                nc.vector.tensor_copy(wB[:, :], pT[:, 0:2])
                v.drain()
                v.wait_ge(s_w, 64 + 128)
                for j in range(2):
                    w = w2[:, j * NF // 2:(j + 1) * NF // 2, :]
                    ts(w, w, wB[:, j:j + 1], None, ALU.mult)
                ts(b2[:, 2, :], b2[:, 0, :], wB[0:R, 0:1], None, ALU.mult)
                v.drain()
                nc.vector.scalar_tensor_tensor(out=b2[:, 0, :], in0=b2[:, 1, :], scalar=wB[0:R, 1:2], in1=b2[:, 2, :],
                                               op0=ALU.mult, op1=ALU.add)
                v.drain()

        with nc.Block() as block:
            @block.sync
            def _(sp):
                def load(u, s):
                    rows_dma(sp, x1[:, s, :, :], x1_v[u], s_ld[s])
                    sp.dma_start(xnT[:, s, :, :], env["xnT_d"][1][:, :, bass.ds(u * CH, CH)]).then_inc(s_ld[s], 16)

                def store(u, s):
                    sp.wait_ge(s_x2, u + 1)
                    rows_dma(sp, x2_v[u], x2[:, s, :, :], s_st[s])
                    sp.wait_ge(s_xT, u + 1)
                    sp.dma_start(env["xnT_d"][2][:, :, bass.ds(u * CH, CH)], xT[:, s, :, :]).then_inc(s_sx[s], 16)

                def step(u, s, lo, hi):
                    if lo >= 4:
                        sp.wait_ge(s_x2, u - 3)
                    load(u, s)
                    if lo >= 3:
                        store(u - 3, (s + 1) % 2)
                sweep(sp, CHUNKS, step, 4)
                for u in range(CHUNKS - 3, CHUNKS):
                    store(u, u % 2)
                for i in range(2):
                    n = (CHUNKS + 1 - i) // 2
                    sp.wait_ge(s_st[i], 32 * n)
                    sp.wait_ge(s_sx[i], 16 * n)

            @block.scalar
            def _(act):
                def turn(u, s, lo):
                    if lo >= 2:
                        hold(act, s_sx[s], (u // 2) * 16)
                    hold(act, s_T, u + 1)
                    nc.scalar.copy(xT[:, s, :, :], pT[:, 0:2 * CH].rearrange("p (k n) -> p k n", k=2)).then_inc(s_xT, 1)

                def step(u, s, lo, hi):
                    if lo >= 2:
                        hold(act, s_O, u - 1)
                    for f in range(NF):
                        if f % 2 == 0:
                            hold(act, s_H, NF // 2 * u + f // 2 + 1)
                        x = nc.scalar.activation(hT[:, s, f, :], pH[:, f // 2, (f % 2) * CH:(f % 2 + 1) * CH], ACT.Gelu,
                                                 bias=b1[:, f:f + 1])
                        if f % 2:
                            x.then_inc(s_g, 1)
                    if lo >= 1:
                        turn(u - 1, 1 - s, lo - 1)
                    if lo == CHUNKS - 1:
                        turn(u, s, lo)
                sweep(act, CHUNKS, step)

            @block.gpsimd
            def _(pool):
                def step(u, s, lo, hi):
                    for i in range(2):
                        hold(pool, s_var, 2 * u + i + 1)
                        nc.gpsimd.tensor_tensor(out=rn[:, :, 0], in0=ve[:, :], in1=mhalf[:, :], op=ALU.pow)\
                          .then_inc(s_rstd, 1)
                sweep(pool, CHUNKS, step)

            @block.vector
            def _(v):
                def step(u, q, lo, hi):
                    s = q % 2
                    v.wait_ge(s_ld[q], (u // 4 + 1) * 48)
                    nc.vector.tensor_copy(sc[:, :, :], stats[:, bass.ds(u * 2, 2), :])
                    v.drain()
                    for t in range(2):
                        nc.vector.tensor_scalar(xnb[:, t, :], x1[:, q, t, :], sc[:, t, 0:1], sc[:, t, 1:2],
                                                ALU.mult, ALU.add)
                    v.drain()
                    nc.vector.tensor_tensor(out=ya[:, :, :], in0=xnb[:, :, :],
                                            in1=b2[:, 0, :].unsqueeze(1).broadcast_to([R, 2, C]), op=ALU.add)
                    v.drain()
                    v.wait_ge(s_O, u + 1)
                    nc.vector.tensor_tensor(out=yb[:, :, :], in0=ya[:, :, :],
                                            in1=pO[:, :].rearrange("p (t c) -> p t c", t=2), op=ALU.add)
                    v.drain().then_inc(s_Or, 1)
                    ln_stats(nc, v, yb, bn, mv, ve, s_var)
                    v.wait_ge(s_rstd, 2 * u + 1)
                    ln_apply(nc, v, ya, yb, mv, rn)
                    v.drain()
                    nc.vector.tensor_tensor(out=yb[:, :, :], in0=ya[:, :, :],
                                            in1=gam[:, 0, :].unsqueeze(1).broadcast_to([R, 2, C]), op=ALU.mult)
                    nc.vector.tensor_tensor(out=xnb[:, :, :], in0=x1[:, q, :, :],
                                            in1=gam[:, 1, :].unsqueeze(1).broadcast_to([R, 2, C]), op=ALU.add)
                    v.drain()
                    if lo >= 2:
                        v.wait_ge(s_st[s], (u // 2) * 32)
                    nc.vector.tensor_tensor(out=x2[:, s, :, :], in0=xnb[:, :, :], in1=yb[:, :, :], op=ALU.add)
                    v.drain().then_inc(s_x2, 1)
                    ln_stats(nc, v, x2[:, s, :, :], bn, mv, ve, s_var)
                    v.wait_ge(s_rstd, 2 * u + 2)
                    if lo >= 2:
                        v.wait_ge(s_T, u - 1)
                    ln_apply(nc, v, xn2[:, s, :, :], x2[:, s, :, :], mv, rn).then_inc(s_xn2, 1)
                    nc.vector.tensor_copy(stats[:, bass.ds(u * 2, 2), :], rn[:, :, :])
                    v.drain()
                sweep(v, CHUNKS, step, 4)

            @block.tensor
            def _(pe):
                def hidden(u, s, lo):
                    pe.wait_ge(s_ld[s], (u // 4 + 1) * 48)
                    for f in range(NF):
                        if f % 2 == 0 and lo >= 1:
                            pe.wait_ge(s_g, NF // 2 * (u - 1) + f // 2 + 1)
                        j, c = f // (NF // 2), f % (NF // 2)
                        for k in range(2):
                            last = nc.tensor.matmul(pH[:, f // 2, (f % 2) * CH:(f % 2 + 1) * CH],
                                                    w1[:, j, k, 128 * c:128 * c + 128], xnT[:, s, k, :],
                                                    start=k == 0, stop=k == 1)
                        if f % 2:
                            last.then_inc(s_H, 1)

                def output(u, s, lo):
                    if lo >= 1:
                        pe.wait_ge(s_Or, u)
                    for t in range(2):
                        for f in range(NF):
                            if t == 0 and f % 2 == 0:
                                pe.wait_ge(s_g, NF // 2 * u + f // 2 + 1)
                            last = nc.tensor.matmul(pO[:, t * C:(t + 1) * C], hT[:, s % 2, f, t * R:t * R + R], w2[:, f, :],
                                                    start=f == 0, stop=f == NF - 1)
                    last.then_inc(s_O, 1)

                def turn(u, s, lo):
                    pe.wait_ge(s_xn2, u + 1)
                    if lo >= 1:
                        pe.wait_ge(s_xT, u)
                    for k in range(2):
                        for t in range(2):
                            last = nc.tensor.transpose(pT[:, k * CH + t * R:k * CH + t * R + R],
                                                       xn2[:, s, t, 128 * k:128 * k + 128], ident[0:R, 0:R])
                    last.then_inc(s_T, 1)

                def step(u, s, lo, hi):
                    if lo == 0:
                        hidden(0, 0, 0)
                    if hi <= CHUNKS - 2:
                        hidden(u + 1, (s + 1) % 4, lo + 1)
                    output(u, s, lo)
                    if lo >= 1:
                        turn(u - 1, (s + 1) % 2, lo - 1)
                    if lo == CHUNKS - 1:
                        turn(u, s % 2, lo)
                sweep(pe, CHUNKS, step, 4)


def front1(env):
    nc, a, sem, ident, ones = (env[k] for k in ("nc", "a", "sem", "ident", "ones"))
    cv = env["chunk_view"]
    tab_v = cv(env["tab1"])
    g1, attr = env["g1"], env["attr"]
    HID = 512
    with ExitStack() as ctx:
        sb = lambda n, s, d=F32: ctx.enter_context(nc.sbuf_tensor("f1_" + n, s, d))
        wq = sb("wq", [128, 4, C])
        wk = sb("wk", [128, 8, C])
        wo = sb("wo", [128, 2, HID])
        wkv = sb("wkv", [128, 2, 2 * HID])
        woT = sb("woT", [128, 4, C])
        lin = sb("lin", [128, 2, C])
        cm = sb("cm", [128, 2, 16])
        xnT = sb("xnT", [128, 2, 2, CH])
        trow = sb("trow", [R, 2, 2, C])
        sq = sb("sq", [R, HID])
        ss = sb("ss", [R, 8])
        sd = sb("sd", [R, 8])
        ri = sb("ri", [R, 8])
        kvn = sb("kvn", [R, 2, 2 * HID])
        epst = sb("epst", [128, 1])
        mask = sb("mask", [128, 128])
        dT = sb("dT", [128, 4, 128])
        m1 = sb("m1", [128, 4, C])
        pb = lambda n, s: ctx.enter_context(nc.psum_tensor("f1_" + n, s, F32))
        pA, pKV, pY, pS = pb("pA", [128, 2, 512]), pb("pKV", [128, 3, 512]), pb("pY", [R, 512]), pb("pS", [128, 512])
        s_w, s_c, s_t, s_tc, s_m = (sem("f1_" + n) for n in ("weights", "consts", "T", "Tc", "mask"))
        s_ld = [sem("f1_load0"), sem("f1_load1")]
        s_st = [sem("f1_store0"), sem("f1_store1")]
        s_kv, s_sq, s_ss, s_sd, s_kvn, s_acc, s_Y, s_row = (
            sem("f1_" + n) for n in ("kv", "sq", "ss", "sd", "kvn", "acc", "Y", "rows"))
        s_dT, s_M, s_m1, s_G = (sem("f1_" + n) for n in ("dT", "M", "m1", "G"))
        wqkv = a["L1_mix_Wqkv"].rearrange("(i p) k -> p i k", p=128)

        with nc.Block() as block:
            @block.gpsimd
            def _(pool):
                nc.gpsimd.memset(lin[:, :, :], 0.0).then_inc(s_c, 1)
                nc.gpsimd.memset(epst[:, :], EPS)
                nc.gpsimd.memset(mask[:, :], 0.0)
                pool.drain()
                for h in range(2):
                    nc.gpsimd.memset(mask[64 * h:64 * h + 64, 64 * h:64 * h + 64], 1.0 / N)
                    pool.drain()

            @block.sync
            def _(sp):
                sp.dma_start(wq[:, :, :], wqkv[:, 0:4, :]).then_inc(s_w, 16)
                sp.dma_start(wk[:, :, :], wqkv[:, 4:12, :]).then_inc(s_w, 16)
                sp.dma_start(wo[:, :, :], a["L1_mix_Wout"].rearrange("(k p) f -> p k f", p=128)).then_inc(s_w, 16)
                sp.dma_start(attr[:, :], a["node_vec1"].rearrange("(t p) o -> p (t o)", p=R)).then_inc(s_w, 16)
                sp.wait_ge(s_c, 1)
                sp.dma_start(lin[0:64, 0, 0:64], a["L1_gnn_lin1_w0"]).then_inc(s_w, 16)
                for k, p, c, u, n in vector_rows():
                    sp.dma_start(lin[p:p + 3 * (n - 1) + 1:3, k, 64 + 64 * c:128 + 64 * c],
                                 a["L1_gnn_lin1_w1"][u:u + n, :]).then_inc(s_w, 16)
                sp.wait_ge(s_w, 16 * (5 + len(vector_rows())))

            @block.tensor
            def _(pe):
                n = 0
                pe.wait_ge(s_w, 16 * (5 + len(vector_rows())))
                for src, rows in ((wk, 8), (wo, 2)):
                    for i in range(rows):
                        for k in range(2 if rows == 8 else 4):
                            if n >= 2:
                                pe.wait_ge(s_tc, n - 1)
                            nc.tensor.transpose(pA[:, n % 2, 0:128], src[:, i, 128 * k:128 * k + 128], ident[:, :])\
                              .then_inc(s_t, 1)
                            n += 1

            @block.vector
            def _(v):
                n = 0
                for rows in (8, 2):
                    for i in range(rows):
                        for k in range(2 if rows == 8 else 4):
                            dst = wkv[:, k, 128 * i:128 * i + 128] if rows == 8 else woT[:, k, 128 * i:128 * i + 128]
                            v.wait_ge(s_t, n + 1)
                            nc.vector.tensor_copy(dst, pA[:, n % 2, 0:128]).then_inc(s_tc, 1)
                            n += 1
                v.drain()
                for k in range(2):
                    w = wkv[:, k, :].rearrange("p (h d) -> p h d", d=64)
                    nc.vector.tensor_reduce(cm[:, k, :], w, AX.X, ALU.add)
                    v.drain()
                    nc.vector.tensor_scalar(cm[:, k, :], cm[:, k, :], -1.0 / 64, None, ALU.mult)
                    v.drain()
                    nc.vector.tensor_tensor(out=w, in0=w, in1=cm[:, k, :].unsqueeze(2).broadcast_to([128, 16, 64]),
                                            op=ALU.add)
                    v.drain()
                nc.vector.tensor_scalar(lin[:, :, :], lin[:, :, :], 0.125, None, ALU.mult)
                v.drain()

        with nc.Block() as block:
            @block.sync
            def _(sp):
                def store(u, s):
                    sp.wait_ge(s_row, u + 1)
                    rows_dma(sp, tab_v[u], trow[:, s, :, :], s_st[s])

                def step(u, s, lo, hi):
                    if lo >= 2:
                        sp.wait_ge(s_Y, u - 1)
                    sp.dma_start(xnT[:, s, :, :], env["xnT_d"][2][:, :, bass.ds(u * CH, CH)]).then_inc(s_ld[s], 16)
                    if lo >= 1:
                        store(u - 1, 1 - s)
                    if lo == CHUNKS - 1:
                        store(u, s)
                sweep(sp, CHUNKS, step)
                for i in range(2):
                    sp.wait_ge(s_st[i], 32 * ((CHUNKS + 1 - i) // 2))

            @block.tensor
            def _(pe):
                def sums(u, t):
                    i = u * 2 + t
                    pe.wait_ge(s_kvn, 2 * i + 2)
                    for g in range(4):
                        last = nc.tensor.matmul(pS[:, 128 * g:128 * g + 128], kvn[:, t, HID + 128 * g:HID + 128 * g + 128],
                                                kvn[:, t, 128 * g:128 * g + 128], start=False, stop=False,
                                                skip_group_check=True)
                    last.then_inc(s_acc, 1)

                def step(u, s, lo, hi):
                    pe.wait_ge(s_ld[s], (u // 2 + 1) * 16)
                    for t in range(2):
                        for b in range(2):
                            hh = u * 4 + 2 * t + b
                            if lo >= 1 or t == 1:
                                pe.wait_ge(s_kvn, hh - 1)
                            for k in range(2):
                                last = nc.tensor.matmul(pKV[0:R, b, :], xnT[:, s, k, t * R:t * R + R],
                                                        wkv[:, k, HID * b:HID * b + HID], start=k == 0, stop=k == 1)
                            last.then_inc(s_kv, 1)
                        if t == 0:
                            if lo >= 1:
                                pe.wait_ge(s_row, u)
                            for q in range(2):
                                for k in range(2):
                                    last = nc.tensor.matmul(pY[:, q * C:q * C + C], xnT[:, s, k, q * R:q * R + R],
                                                            lin[:, k, :], start=k == 0, stop=k == 1)
                            if lo >= 1:
                                sums(u - 1, 1)
                        else:
                            sums(u, 0)
                    pe.drain().then_inc(s_Y, 1)

                nc.tensor.matmul(pS[:, :], env["zeros"][0:1, 0:128], env["zeros"][0:1, :], start=True, stop=False,
                                 skip_group_check=True)
                sweep(pe, CHUNKS, step)
                sums(CHUNKS - 1, 1)
                pe.drain()

            @block.scalar
            def _(act):
                def step(u, s, lo, hi):
                    for t in range(2):
                        for b in range(2):
                            hh = u * 4 + 2 * t + b
                            hold(act, s_kv, hh + 1)
                            if lo >= 1 or t + b > 0:
                                hold(act, s_ss, hh)
                            nc.scalar.activation(sq[:, :], pKV[0:R, b, :], ACT.Square).then_inc(s_sq, 1)
                            hold(act, s_ss, hh + 1)
                            nc.scalar.activation(sd[:, :], ss[:, :], ACT.Sqrt, bias=epst[0:R, :], scale=1.0 / 64)\
                              .then_inc(s_sd, 1)
                    if lo >= 2:
                        hold(act, s_st[s], (u // 2) * 32)
                    hold(act, s_Y, u + 1)
                    for t in range(2):
                        last = nc.scalar.activation(trow[:, s, t, :], pY[:, t * C:t * C + C], ACT.Copy,
                                                    scale=attr[:, bass.ds(u * 2 + t, 1)])
                    last.then_inc(s_row, 1)
                sweep(act, CHUNKS, step)

            @block.vector
            def _(v):
                def step(u, s, lo, hi):
                    for t in range(2):
                        for b in range(2):
                            hh = u * 4 + 2 * t + b
                            v.wait_ge(s_sq, hh + 1)
                            nc.vector.tensor_reduce(ss[:, :], sq[:, :].rearrange("p (h d) -> p h d", d=64), AX.X, ALU.add)\
                              .then_inc(s_ss, 1)
                            v.wait_ge(s_sd, hh + 1)
                            nc.vector.reciprocal(ri[:, :], sd[:, :])
                            v.drain()
                            if lo >= 1:
                                v.wait_ge(s_acc, u * 2 + t - 1)
                            nc.vector.tensor_tensor(
                                out=kvn[:, t, HID * b:HID * b + HID].rearrange("p (h d) -> p h d", d=64),
                                in0=pKV[0:R, b, :].rearrange("p (h d) -> p h d", d=64),
                                in1=ri[:, :].unsqueeze(2).broadcast_to([R, 8, 64]), op=ALU.mult).then_inc(s_kvn, 1)
                sweep(v, CHUNKS, step)

        with nc.Block() as block:
            @block.vector
            def _(v):
                for g in range(4):
                    nc.vector.tensor_tensor(out=dT[:, g, :], in0=pS[:, 128 * g:128 * g + 128], in1=mask[:, :], op=ALU.mult)
                v.drain().then_inc(s_dT, 1)
                for g in range(4):
                    v.wait_ge(s_M, g + 1)
                    nc.vector.tensor_copy(m1[:, g, :], pA[:, g % 2, 0:C]).then_inc(s_m1, 1)
                v.wait_ge(s_G, 1)
                nc.vector.tensor_copy(g1[:, :, :], pKV[:, 0:2, 0:C])
                v.drain()

            @block.tensor
            def _(pe):
                pe.wait_ge(s_dT, 1)
                for g in range(4):
                    if g >= 2:
                        pe.wait_ge(s_m1, g - 1)
                    nc.tensor.matmul(pA[:, g % 2, 0:C], dT[:, g, :], woT[:, g, :], start=True, stop=True).then_inc(s_M, 1)
                pe.wait_ge(s_m1, 4)
                for k in range(2):
                    for g in range(4):
                        last = nc.tensor.matmul(pKV[:, k, 0:C], wq[:, g, 128 * k:128 * k + 128], m1[:, g, :],
                                                start=g == 0, stop=g == 3)
                last.then_inc(s_G, 1)


def vector_rows():
    runs = []
    for c in range(3):
        for k in range(2):
            us = [u for u in range(64) if (64 + 3 * u + c) // 128 == k]
            runs.append((k, (64 + 3 * us[0] + c) % 128, c, us[0], len(us)))
    return runs


def edge_attrs(env, ea):
    nc, a, sem, ident = (env[k] for k in ("nc", "a", "sem", "ident"))
    with ExitStack() as ctx:
        st = ctx.enter_context(nc.sbuf_tensor("ea_st", [QB, NB, R * 4], F32))
        sc = ctx.enter_context(nc.sbuf_tensor("ea_sc", [QB, 4, NB, R], F32))
        pt = ctx.enter_context(nc.psum_tensor("ea_pt", [R, 8, 512], F32))
        s_ld, s_c, s_t, s_ev = sem("ea_load"), sem("ea_split"), sem("ea_T"), sem("ea_copied")
        with nc.Block() as block:
            @block.sync
            def _(sp):
                sp.dma_start(st[:, :, :], a["edge_attr_4"].rearrange("(b q e) c -> q b (e c)", q=QB, e=R)).then_inc(s_ld, 16)
                sp.wait_ge(s_ld, 16)

            @block.vector
            def _(v):
                v.wait_ge(s_ld, 16)
                for c in range(4):
                    nc.vector.tensor_copy(sc[:, c, :, :], st[:, :, :].rearrange("q b (e c) -> q b e c", c=4)[:, :, :, c])\
                      .then_inc(s_c, 1)
                for c in range(4):
                    for b in range(NB):
                        n = c * NB + b
                        v.wait_ge(s_t, n + 1)
                        nc.vector.tensor_copy(ea[:, QB * b:QB * (b + 1), c], pt[:, n % 8, 0:QB]).then_inc(s_ev, 1)
                v.drain()

            @block.tensor
            def _(pe):
                for c in range(4):
                    pe.wait_ge(s_c, c + 1)
                    for b in range(NB):
                        n = c * NB + b
                        if n >= 8:
                            pe.wait_ge(s_ev, n - 7)
                        nc.tensor.transpose(pt[:, n % 8, 0:QB], sc[:, c, b, :], ident[0:QB, 0:QB]).then_inc(s_t, 1)


def edges1(env, z, ea):
    nc, a, sem, ident = (env[k] for k in ("nc", "a", "sem", "ident"))
    srcI, baseI = env["srcI"], env["baseI"]
    PAIRS = (GT + 1) // 2
    with ExitStack() as ctx:
        sb = lambda n, s, d=F32: ctx.enter_context(nc.sbuf_tensor("e1_" + n, s, d))
        pb = lambda n, s: ctx.enter_context(nc.psum_tensor("e1_" + n, s, F32))
        ix = sb("ix", [R, SLOTS, GT], I32)
        rows = sb("rows", [R, 3, GT, C])
        es = sb("es", [R, SLOTS, GT, 8])
        esT = sb("esT", [8 * GT, 2, R])
        w1 = sb("w1", [8 * GT, PAIRS, 128])
        w2 = sb("w2", [128, 2, C])
        hT = sb("hT", [128, 2, PAIRS, R])
        ohu = sb("ohu", [R, GT, W])
        oh = sb("oh", [R, 2, GT, 4, W])
        msg = sb("msg", [R, 2, GT, 8, 64])
        us = sb("us", [128, 2, 512])
        eye2 = sb("eye2", [128, W])
        pH = pb("pH", [128, 512])
        pT = pH[0:8 * GT, 128 * PAIRS:128 * PAIRS + R]
        pW, pU, pF = pb("pW", [R, 3, 512]), pb("pU", [128, 2, 512]), pb("pF", [128, 2, 512])
        s_wt, s_wz = sem("e1_weights"), sem("e1_zeroed")
        s_gat = [sem(f"e1_rows{i}", software_dma=True) for i in range(SLOTS)]
        s_es = [sem(f"e1_es{i}") for i in range(SLOTS)]
        s_ix, s_T, s_esT, s_F, s_h, s_W, s_msg, s_oh, s_acc, s_us, s_flip, s_add = (
            sem("e1_" + n) for n in ("ix", "T", "esT", "F", "silu", "W", "msg", "oh", "acc", "copied", "flip", "added"))
        SILU_NORM = 1.679
        blk = lambda s, j, i: msg[:, s, j, :, :].rearrange("p b c -> p (b c)")[:, 64 * i:64 * i + 64]

        with nc.Block() as block:
            @block.gpsimd
            def _(pool):
                nc.gpsimd.memset(w1[:, :, :], 0.0)
                nc.gpsimd.memset(w2[:, :, :], 0.0)
                pool.drain().then_inc(s_wz, 1)

            @block.sync
            def _(sp):
                sp.wait_ge(s_wz, 1)
                for j in range(GT):
                    sp.dma_start(w1[8 * j:8 * j + 8, j // 2, 64 * (j % 2):64 * (j % 2) + 64], a["L1_gnn_fc_w1"])\
                      .then_inc(s_wt, 16)
                for r in range(2):
                    for i, b in enumerate((0, 3, 2, 1)):
                        sp.dma_start(w2[64 * r:64 * r + 64, r, 64 * i:64 * i + 64],
                                     a["L1_gnn_fc_w2"][:, 64 * b:64 * b + 64]).then_inc(s_wt, 16)
                sp.wait_ge(s_wt, 16 * (GT + 8))

        with nc.Block() as block:
            @block.vector
            def _(v):
                nc.vector.tensor_scalar(w2[:, :, :], w2[:, :, :], SILU_NORM / 8.0, None, ALU.mult)
                nc.vector.tensor_tensor(out=eye2[:, :], in0=ident[:, 0:W], in1=ident[:, W:2 * W], op=ALU.add)
                v.drain()
        es_v = a["edge_attr_8"].rearrange("(g j p) f -> g p j f", j=GT, p=R)

        def one_pass():
            with nc.Block() as block:
                @block.gpsimd
                def _(pool):
                    def step(g, s, lo, hi):
                        hold(pool, s_ix, g + 1)
                        for j in range(GT):
                            nc.gpsimd.indirect_dma_start(
                                out=rows[:, s % 3, j, :], out_offset=None, in_=env["tab1"],
                                in_offset=bass.IndirectOffsetOnAxis(ap=ix[:, s, j:j + 1], axis=0))\
                              .then_inc(s_gat[s], 16)
                    sweep(pool, GROUPS, step, SLOTS, AHEAD)

                @block.sync
                def _(sp):
                    def step(g, s, lo, hi):
                        if lo >= SLOTS:
                            sp.wait_ge(s_T, g - SLOTS + 1)
                        rows_dma(sp, es[:, s, :, :], es_v[g], s_es[s])
                    sweep(sp, GROUPS, step, SLOTS, AHEAD)

                @block.scalar
                def _(act):
                    def stage(g, s, lo):
                        if lo >= 3:
                            hold(act, s_msg, PAIRS * (g - 2))
                        nc.scalar.copy(ix[:, s, :], srcI[:, bass.ds(g * GT, GT)]).then_inc(s_ix, 1)

                    def front(g, s, lo):
                        if lo >= 2:
                            hold(act, s_F, g - 1)
                        hold(act, s_T, g + 1)
                        nc.scalar.copy(esT[:, s % 2, :], pT).then_inc(s_esT, 1)
                        if lo >= 2:
                            hold(act, s_W, PAIRS * (g - 1))
                        hold(act, s_F, g + 1)
                        nc.scalar.activation(hT[:, s % 2, :, :],
                                             pH[:, 0:128 * PAIRS].rearrange("p (i e) -> p i e", e=128)[:, :, 0:R],
                                             ACT.Silu, scale=8.0 ** -0.5).then_inc(s_h, 1)

                    def copied(g, s, lo):
                        if lo >= 2:
                            hold(act, s_flip, g - 1)
                        hold(act, s_acc, g + 1)
                        nc.scalar.copy(us[:, s % 2, :], pU[:, s % 2, :]).then_inc(s_us, 1)

                    def step(g, s, lo, hi):
                        if lo == 0:
                            for i in range(3):
                                stage(i, i, i)
                            front(0, 0, 0)
                        if lo >= 1 and hi <= GROUPS - 3:
                            stage(g + 2, (s + 2) % SLOTS, lo + 2)
                        if hi <= GROUPS - 2:
                            front(g + 1, (s + 1) % SLOTS, lo + 1)
                        if lo >= 1:
                            copied(g - 1, s + 1, lo - 1)
                        if lo == GROUPS - 1:
                            copied(g, s, lo)
                    sweep(act, GROUPS, step, SLOTS, AHEAD)

                @block.vector
                def _(v):
                    def add(g, s):
                        base = v.value_load(baseI[0:1, bass.ds(g, 1)], min_val=0, max_val=N)
                        v.wait_ge(s_flip, g + 1)
                        w = z[:, :, bass.ds(base, W)]
                        nc.vector.tensor_tensor(out=w, in0=w,
                                                in1=pF[:, s % 2, 0:4 * W].rearrange("p (k n) -> p k n", k=4),
                                                op=ALU.add).then_inc(s_add, 1)

                    def step(g, s, lo, hi):
                        if lo >= 1:
                            v.wait_ge(s_oh, g)
                        one_hots(nc, env, ohu[:, :, :], g)
                        v.drain()
                        if lo >= 2:
                            v.wait_ge(s_acc, g - 1)
                        nc.vector.tensor_tensor(
                            out=oh[:, s % 2, :, :, :], in0=ohu[:, :, :].unsqueeze(2).broadcast_to([R, GT, 4, W]),
                            in1=ea[:, bass.ds(g * GT, GT), :].unsqueeze(3).broadcast_to([R, GT, 4, W]), op=ALU.mult)\
                          .then_inc(s_oh, 1)
                        v.wait_ge(s_gat[s], (g // SLOTS + 1) * 16 * GT)
                        for j in range(GT):
                            if j % 2 == 0:
                                v.wait_ge(s_W, g * PAIRS + j // 2 + 1)
                            wj = pW[:, j // 2, 256 * (j % 2):256 * (j % 2) + 256]
                            wa = wj.rearrange("p (b q c) -> p b q c", b=2, q=2)
                            m = msg[:, s % 2, j, :, :].rearrange("p (b q) c -> p b q c", b=2)
                            nc.vector.tensor_tensor(out=m[:, :, 0, :], in0=wa[:, :, 0, :],
                                                    in1=rows[:, s % 3, j, 0:64].unsqueeze(1).broadcast_to([R, 2, 64]),
                                                    op=ALU.mult)
                            last = nc.vector.tensor_tensor(
                                out=m[:, :, 1:4, :], in0=wa[:, :, 1:2, :].broadcast_to([R, 2, 3, 64]),
                                in1=rows[:, s % 3, j, 64:256].rearrange("p (q c) -> p q c", q=3).unsqueeze(1)
                                .broadcast_to([R, 2, 3, 64]), op=ALU.mult)
                            if j % 2 or j == GT - 1:
                                last.then_inc(s_msg, 1)
                        if lo >= 3:
                            add(g - 3, s + 1)
                        if lo == GROUPS - 1:
                            for i in (2, 1, 0):
                                v.drain()
                                add(g - i, s + i)
                            v.drain()
                    sweep(v, GROUPS, step, SLOTS, AHEAD)

                @block.tensor
                def _(pe):
                    def front(g, s, lo):
                        if lo >= 1:
                            pe.wait_ge(s_h, g)
                        hold(pe, s_es[s], (g // SLOTS + 1) * 32)
                        nc.tensor.transpose(pT, es[:, s, :, :].rearrange("p j f -> p (j f)"), ident[0:R, 0:R])\
                          .then_inc(s_T, 1)

                    def first(g, s):
                        hold(pe, s_esT, g + 1)
                        for i in range(PAIRS):
                            last = nc.tensor.matmul(pH[:, 128 * i:128 * i + R], w1[:, i, :], esT[:, s % 2, :],
                                                    start=True, stop=True)
                        last.then_inc(s_F, 1)

                    def second(g, s, lo):
                        pe.wait_ge(s_h, g + 1)
                        for j in range(GT):
                            if lo >= 1 and j % 2 == 0:
                                pe.wait_ge(s_msg, (g - 1) * PAIRS + j // 2 + 1)
                            last = nc.tensor.matmul(pW[:, j // 2, 256 * (j % 2):256 * (j % 2) + 256],
                                                    hT[:, s % 2, j // 2, :], w2[:, j % 2, :], start=True, stop=True)
                            if j % 2 or j == GT - 1:
                                last.then_inc(s_W, 1)

                    def sums(g, s, lo):
                        pe.wait_ge(s_msg, (g + 1) * PAIRS)
                        pe.wait_ge(s_oh, g + 1)
                        if lo >= 2:
                            hold(pe, s_us, g - 1)
                        for pair in range(0, GT, 2):
                            for c in range(4):
                                for j in range(pair, min(pair + 2, GT)):
                                    h = W * (j % 2 if j < GT - 1 else c in (1, 2))
                                    m = msg[:, s % 2, j, :, :]
                                    u8 = pU[h:h + W, s % 2, :].rearrange("p (b c) -> p b c", b=8)
                                    last = nc.tensor.matmul(
                                        u8[:, 0:4, :] if c == 0 else u8[:, 3 + c:8:4 - c, :], oh[:, s % 2, j, c, :],
                                        m[:, 0:4, :] if c == 0 else m[:, 4:5 + c:c, :],
                                        start=pair + c == 0, stop=j == GT - 1 and c >= 2, skip_group_check=True)
                        last.then_inc(s_acc, 1)

                    def flip(g, s, lo):
                        pe.wait_ge(s_us, g + 1)
                        if lo >= 2:
                            pe.wait_ge(s_add, g - 1)
                        for k in range(4):
                            last = nc.tensor.matmul(pF[:, s % 2, k * W:k * W + W], us[:, s % 2, 128 * k:128 * k + 128],
                                                    eye2[:, :], start=True, stop=True)
                        last.then_inc(s_flip, 1)

                    def step(g, s, lo, hi):
                        if lo == 0:
                            front(0, 0, 0)
                            first(0, 0)
                        if hi <= GROUPS - 2:
                            front(g + 1, (s + 1) % SLOTS, lo + 1)
                        second(g, s, lo)
                        if hi <= GROUPS - 2:
                            first(g + 1, s + 1)
                        if lo >= 1:
                            sums(g - 1, s + 1, lo - 1)
                        if lo >= 2:
                            flip(g - 2, s, lo - 2)
                        if lo == GROUPS - 1:
                            flip(g - 1, s + 1, lo)
                            sums(g, s, lo)
                            flip(g, s, lo)
                    sweep(pe, GROUPS, step, SLOTS, AHEAD)

        edge_passes(env, 1, [z[:, :, :]], one_pass, s_gat,
                    s_es + [s_ix, s_T, s_esT, s_F, s_h, s_W, s_msg, s_oh, s_acc, s_us, s_flip, s_add])


def back1(env, z):
    nc, a, sem, ident, stats, attr = (env[k] for k in ("nc", "a", "sem", "ident", "stats", "attr"))
    cv = env["chunk_view"]
    x2_v, x3_v = cv(env["x_d"][1]), cv(env["x_d"][2])
    wsel = env["wsel"]
    INV2 = 128.0 ** -0.5
    with ExitStack() as ctx:
        sb = lambda n, s, d=F32: ctx.enter_context(nc.sbuf_tensor("b1_" + n, s, d))
        pb = lambda n, s: ctx.enter_context(nc.psum_tensor("b1_" + n, s, F32))
        sc_w = sb("sc", [128, 2, C])
        lin2 = sb("lin2", [128, 4, C])
        bout = sb("bout", [R, C])
        wr = sb("wr", [R, C])
        br = sb("br", [R, 1])
        xt = sb("xt", [R, 2, 2, C])
        xnT = sb("xnT", [128, 2, 2, CH])
        zs = sb("zs", [128, 2, 4, CH])
        ga = sb("ga", [R, 2, C])
        ya = sb("ya", [R, 2, C])
        x3 = sb("x3", [R, 2, C])
        yy = sb("yy", [R, 2, 2, C])
        xn = sb("xn", [R, 2, 2, C])
        pr = sb("pr", [R, 2, C])
        bn, mv, ve, rn, mhalf = (sb("bn", [R, 2, 6]), sb("mv", [R, 2, 2]), sb("ve", [R, 2]), sb("rn", [R, 2, 2]),
                                 sb("mhalf", [R, 2]))
        xT = sb("xT", [128, 2, 2, CH])
        pA, pB, pT = pb("pA", [R, 2, 512]), pb("pB", [R, 2, 512]), pb("pT", [128, 512])
        s_w, s_z = sem("b1_weights"), sem("b1_zeroed")
        s_ld = [sem("b1_load0"), sem("b1_load1")]
        s_st = [sem("b1_store0"), sem("b1_store1")]
        s_sx = [sem("b1_storeT0"), sem("b1_storeT1")]
        s_zs, s_A, s_ga, s_Br, s_var, s_rstd, s_xn, s_y, s_T, s_xT = (
            sem("b1_" + n) for n in ("zs", "A", "gated", "read", "var", "rstd", "xn", "y", "T", "xT"))
        vec = lambda t, k: t[:, k, 64:256].rearrange("p (v c) -> p v c", c=3)

        with nc.Block() as block:
            @block.gpsimd
            def _(pool):
                nc.gpsimd.memset(sc_w[:, :, :], 0.0)
                nc.gpsimd.memset(lin2[:, :, :], 0.0)
                nc.gpsimd.memset(mhalf[:, :], -0.5)
                pool.drain().then_inc(s_z, 1)

            @block.sync
            def _(sp):
                sp.dma_start(bout[:, :], row_bc(a["L1_mix_bout"], R)).then_inc(s_w, 16)
                sp.dma_start(wr[:, :], a["L1_ffn_wr"].rearrange("k o -> o k").broadcast_to([R, C])).then_inc(s_w, 16)
                sp.dma_start(br[:, :], a["L1_ffn_br"].rearrange("(o n) -> o n", o=1).broadcast_to([R, 1])).then_inc(s_w, 16)
                sp.wait_ge(s_z, 1)
                sp.dma_start(sc_w[0:64, 0, 0:64], a["L1_gnn_sc_w0"]).then_inc(s_w, 16)
                sp.dma_start(lin2[0:64, 0, 0:64], a["L1_gnn_lin2_w00"]).then_inc(s_w, 16)
                sp.dma_start(lin2[64:128, 3, 0:64], a["L1_gnn_lin2_w01"]).then_inc(s_w, 16)
                sp.wait_ge(s_w, 96)

        w10, w11, w1s = (ctx.enter_context(nc.sbuf_tensor("b1_" + n, [128, 64], F32)) for n in ("w10", "w11", "w1s"))
        ws1 = sb("ws1", [128, 2, 64])
        with nc.Block() as block:
            @block.sync
            def _(sp):
                for r in range(2):
                    sp.dma_start(w10[64 * r:64 * r + 64, :], a["L1_gnn_lin2_w10"]).then_inc(s_w, 16)
                    sp.dma_start(w11[64 * r:64 * r + 64, :], a["L1_gnn_lin2_w11"]).then_inc(s_w, 16)
                for k, p, c, u, n in vector_rows():
                    sp.dma_start(sc_w[p:p + 3 * (n - 1) + 1:3, k, 64 + c:64 + 3 * 63 + c + 1:3],
                                 a["L1_gnn_sc_w1"][u:u + n, :]).then_inc(s_w, 16)
                sp.wait_ge(s_w, 96 + 64 + 16 * len(vector_rows()))

        with nc.Block() as block:
            @block.vector
            def _(v):
                for (b, p), w, c in zip(((0, 64), (1, 0), (1, 64), (2, 0), (2, 64), (3, 0)), (w11,) * 3 + (w10,) * 3,
                                        (0, 1, 2) * 2):
                    nc.vector.tensor_copy(vec(lin2, b)[p:p + 64, :, c], w[p:p + 64, :])
                v.drain()
                nc.vector.tensor_scalar(sc_w[:, :, :], sc_w[:, :, :], SIN8 / 8.0, None, ALU.mult)
                nc.vector.tensor_scalar(lin2[:, :, :], lin2[:, :, :], COS8 * INV2 * 20.0 ** -0.5, None, ALU.mult)
                v.drain()
                nc.vector.tensor_scalar(lin2[64:128, 3, :], lin2[64:128, 3, :], INV_SQRT3, None, ALU.mult)
                v.drain()

        with nc.Block() as block:
            @block.sync
            def _(sp):
                def load(u, s):
                    rows_dma(sp, xt[:, s, :, :], x2_v[u], s_ld[s])
                    sp.dma_start(xnT[:, s, :, :], env["xnT_d"][2][:, :, bass.ds(u * CH, CH)]).then_inc(s_ld[s], 16)

                def store(u, s):
                    sp.wait_ge(s_y, u + 1)
                    rows_dma(sp, x3_v[u], yy[:, s, :, :], s_st[s])
                    sp.wait_ge(s_xT, u + 1)
                    sp.dma_start(env["xnT_d"][3][:, :, bass.ds(u * CH, CH)], xT[:, s, :, :]).then_inc(s_sx[s], 16)

                def step(u, s, lo, hi):
                    if lo >= 2:
                        sp.wait_ge(s_Br, u - 1)
                        sp.wait_ge(s_A, u - 1)
                    load(u, s)
                    if lo >= 2:
                        store(u - 2, s)
                sweep(sp, CHUNKS, step)
                for u in (CHUNKS - 2, CHUNKS - 1):
                    store(u, u % 2)
                for i in range(2):
                    n = (CHUNKS + 1 - i) // 2
                    sp.wait_ge(s_st[i], 32 * n)
                    sp.wait_ge(s_sx[i], 16 * n)

            @block.gpsimd
            def _(pool):
                def step(u, s, lo, hi):
                    hold(pool, s_var, u + 1)
                    nc.gpsimd.tensor_tensor(out=rn[:, :, 0], in0=ve[:, :], in1=mhalf[:, :], op=ALU.pow)\
                      .then_inc(s_rstd, 1)
                sweep(pool, CHUNKS, step)

            @block.scalar
            def _(act):
                def pick(u, s, lo):
                    if lo >= 2:
                        hold(act, s_A, u - 1)
                    nc.scalar.copy(zs[:, s, :, :], z[:, :, bass.ds(u * CH, CH)]).then_inc(s_zs, 1)

                def turn(u, s, lo):
                    if lo >= 2:
                        hold(act, s_sx[s], (u // 2) * 16)
                    hold(act, s_T, u + 1)
                    nc.scalar.copy(xT[:, s, :, :], pT[:, 0:2 * CH].rearrange("p (k n) -> p k n", k=2)).then_inc(s_xT, 1)

                def step(u, s, lo, hi):
                    if lo == 0:
                        pick(0, 0, 0)
                    if hi <= CHUNKS - 2:
                        pick(u + 1, 1 - s, lo + 1)
                    if lo >= 1:
                        hold(act, s_Br, u)
                    hold(act, s_A, u + 1)
                    for t in range(2):
                        last = nc.scalar.activation(ga[:, t, :], pA[:, s, t * C:t * C + C], ACT.Copy,
                                                    scale=attr[:, bass.ds(u * 2 + t, 1)])
                    last.then_inc(s_ga, 1)
                    if lo >= 1:
                        turn(u - 1, 1 - s, lo - 1)
                    if lo == CHUNKS - 1:
                        turn(u, s, lo)
                sweep(act, CHUNKS, step)

            @block.vector
            def _(v):
                def step(u, s, lo, hi):
                    v.wait_ge(s_ld[s], (u // 2 + 1) * 48)
                    nc.vector.tensor_tensor(out=ya[:, :, :], in0=xt[:, s, :, :],
                                            in1=bout[:, :].unsqueeze(1).broadcast_to([R, 2, C]), op=ALU.add)
                    v.wait_ge(s_ga, u + 1)
                    nc.vector.tensor_tensor(out=x3[:, :, :], in0=ga[:, :, :],
                                            in1=pB[:, s, :].rearrange("p (t c) -> p t c", t=2), op=ALU.add)
                    v.drain()
                    nc.vector.tensor_tensor(out=x3[:, :, :], in0=x3[:, :, :], in1=ya[:, :, :], op=ALU.add)
                    v.drain().then_inc(s_Br, 1)
                    ln_stats(nc, v, x3, bn, mv, ve, s_var)
                    v.wait_ge(s_rstd, u + 1)
                    if lo >= 2:
                        v.wait_ge(s_T, u - 1)
                    ln_apply(nc, v, xn[:, s, :, :], x3, mv, rn)
                    v.drain().then_inc(s_xn, 1)
                    if lo >= 2:
                        v.wait_ge(s_st[s], (u // 2) * 32)
                    nc.vector.tensor_tensor(out=yy[:, s, :, :], in0=x3[:, :, :], in1=xn[:, s, :, :], op=ALU.add)\
                      .then_inc(s_y, 1)
                    nc.vector.tensor_tensor(out=pr[:, :, :], in0=xn[:, s, :, :],
                                            in1=wr[:, :].unsqueeze(1).broadcast_to([R, 2, C]), op=ALU.mult)
                    v.drain()
                    nc.vector.tensor_reduce(wsel[:, bass.ds(u * 2, 2)], pr[:, :, :], AX.X, ALU.add)
                    v.drain()
                    if lo == CHUNKS - 1:
                        nc.vector.tensor_scalar(wsel[:, :], wsel[:, :], br[:, 0:1], None, ALU.add)
                        v.drain()
                sweep(v, CHUNKS, step)

            @block.tensor
            def _(pe):
                def products(u, s, lo):
                    pe.wait_ge(s_zs, u + 1)
                    pe.wait_ge(s_ld[s], (u // 2 + 1) * 48)
                    if lo >= 2:
                        pe.wait_ge(s_Br, u - 1)
                    for t in range(2):
                        tt = slice(t * R, t * R + R)
                        for k in range(2):
                            nc.tensor.matmul(pA[:, s, t * C:t * C + C], xnT[:, s, k, tt], sc_w[:, k, :],
                                             start=k == 0, stop=False)
                        for b in range(4):
                            nc.tensor.matmul(pA[:, s, t * C:t * C + C], zs[:, s, b, tt], lin2[:, b, :],
                                             start=False, stop=b == 3)
                        for k in range(2):
                            last = nc.tensor.matmul(pB[:, s, t * C:t * C + C], xnT[:, s, k, tt], env["g1"][:, k, :],
                                                    start=k == 0, stop=k == 1)
                    last.then_inc(s_A, 1)

                def turn(u, s, lo):
                    pe.wait_ge(s_xn, u + 1)
                    if lo >= 1:
                        pe.wait_ge(s_xT, u)
                    for k in range(2):
                        for t in range(2):
                            last = nc.tensor.transpose(pT[:, k * CH + t * R:k * CH + t * R + R],
                                                       xn[:, s, t, 128 * k:128 * k + 128], ident[0:R, 0:R])
                    last.then_inc(s_T, 1)

                def step(u, s, lo, hi):
                    products(u, s, lo)
                    if lo >= 1:
                        turn(u - 1, 1 - s, lo - 1)
                    if lo == CHUNKS - 1:
                        turn(u, s, lo)
                sweep(pe, CHUNKS, step)


def ffn1(env):
    nc, a, sem, ident, ones, wsel = (env[k] for k in ("nc", "a", "sem", "ident", "ones", "wsel"))
    cv = env["chunk_view"]
    yy_v, out_v = cv(env["x_d"][2]), cv(env["out"])
    NF = F1 // 128
    with ExitStack() as ctx:
        sb = lambda n, s, d=F32: ctx.enter_context(nc.sbuf_tensor("o_" + n, s, d))
        pb = lambda n, s: ctx.enter_context(nc.psum_tensor("o_" + n, s, F32))
        w1 = sb("w1", [128, 2, F1])
        w2 = sb("w2", [128, NF, C])
        b1 = sb("b1", [128, NF])
        b2 = sb("b2", [R, C])
        wrow = sb("wrow", [R, N])
        cmp_ = sb("cmp", [R, N], mybir.dt.bfloat16)
        low = sb("low", [R, R])
        eq = sb("eq", [R, R])
        cnt = sb("cnt", [R, 4])
        rank = sb("rank", [R, TILES])
        coef = sb("coef", [R, TILES])
        wc = sb("wc", [TILES, R])
        xnT = sb("xnT", [128, 2, 2, CH])
        hT = sb("hT", [128, NF, CH])
        yall = sb("yall", [R, TILES, C])
        yt = sb("yt", [R, 2, 2, C])
        ot = sb("ot", [R, 2, 2, C])
        pH, pO, pW = pb("pH", [128, NF // 2, 512]), pb("pO", [R, 2, 512]), pb("pW", [128, 512])
        s_w, s_wT, s_wTc, s_wst, s_wrow, s_low = (sem("o_" + n) for n in ("weights", "wT", "wTc", "wst", "wrow", "low"))
        s_ld = [sem("o_load0"), sem("o_load1")]
        s_l2 = [sem("o_rows0"), sem("o_rows1")]
        s_st = [sem("o_store0"), sem("o_store1")]
        s_H, s_g, s_O, s_y, s_rank, s_o = (sem("o_" + n) for n in ("H", "gelu", "O", "y", "rank", "out"))

        with nc.Block() as block:
            @block.sync
            def _(sp):
                sp.dma_start(w1[:, :, :], a["L1_ffn_w1"].rearrange("(k p) f -> p k f", p=128)).then_inc(s_w, 16)
                sp.dma_start(w2[:, :, :], a["L1_ffn_w2"].rearrange("(f p) n -> p f n", p=128)).then_inc(s_w, 16)
                sp.dma_start(b1[:, :], a["L1_ffn_b1"].rearrange("(f p) -> p f", p=128)).then_inc(s_w, 16)
                sp.dma_start(b2[:, :], row_bc(a["L1_ffn_b2"], R)).then_inc(s_w, 16)
                sp.wait_ge(s_wTc, 1)
                sp.dma_start(env["w_d"].rearrange("o (t p) -> (o t) p", p=R), wc[:, :]).then_inc(s_wst, 16)
                sp.wait_ge(s_wst, 16)
                sp.dma_start(wrow[:, :], env["w_d"].broadcast_to([R, N])).then_inc(s_wrow, 16)
                sp.wait_ge(s_wrow, 16)
                sp.wait_ge(s_w, 64)

            @block.tensor
            def _(pe):
                nc.tensor.transpose(pW[0:TILES, 0:R], wsel[:, :], ident[0:R, 0:R]).then_inc(s_wT, 1)

            @block.vector
            def _(v):
                v.wait_ge(s_wT, 1)
                nc.vector.tensor_copy(wc[:, :], pW[0:TILES, 0:R]).then_inc(s_wTc, 1)

            @block.gpsimd
            def _(pool):
                nc.gpsimd.memset(low[:, :], 1.0)
                pool.drain()
                nc.gpsimd.affine_select(out=low[:, :], in_=low[:, :], compare_op=ALU.is_gt, fill=0.0, base=0,
                                        pattern=[[-1, R]], channel_multiplier=1)
                pool.drain()

        def rank_tile(v, i):
            w = wsel[:, i:i + 1]
            lo_, hi_ = i * R, (i + 1) * R
            own = wrow[:, lo_:hi_]
            nc.vector.tensor_scalar(eq[:, :], own, w, None, ALU.is_equal)
            nc.vector.tensor_scalar(cmp_[:, lo_:hi_], own, w, 0.0, ALU.is_gt, ALU.add, accum_out=cnt[:, 0:1])
            if i == 0:
                nc.vector.memset(cnt[:, 1:2], 0.0)
            else:
                nc.vector.tensor_scalar(cmp_[:, 0:lo_], wrow[:, 0:lo_], w, 0.0, ALU.is_ge, ALU.add,
                                        accum_out=cnt[:, 1:2])
            if i == TILES - 1:
                nc.vector.memset(cnt[:, 2:3], 0.0)
            else:
                nc.vector.tensor_scalar(cmp_[:, hi_:N], wrow[:, hi_:N], w, 0.0, ALU.is_gt, ALU.add,
                                        accum_out=cnt[:, 2:3])
            v.drain()
            nc.vector.tensor_tensor(out=eq[:, :], in0=eq[:, :], in1=low[:, :], op=ALU.mult)
            v.drain()
            nc.vector.tensor_reduce(cnt[:, 3:4], eq[:, :], AX.X, ALU.add)
            v.drain()
            nc.vector.tensor_reduce(rank[:, i:i + 1], cnt[:, :], AX.X, ALU.add)
            v.drain()

        with nc.Block() as block:
            @block.sync
            def _(sp):
                def step(u, s, lo, hi):
                    if lo >= 2:
                        sp.wait_ge(s_H, (u - 1) * (NF // 2))
                    sp.dma_start(xnT[:, s, :, :], env["xnT_d"][3][:, :, bass.ds(u * CH, CH)]).then_inc(s_ld[s], 16)
                sweep(sp, CHUNKS, step)

                def final(u, s, lo, hi):
                    if lo >= 2:
                        sp.wait_ge(s_o, u - 1)
                    rows_dma(sp, yt[:, s, :, :], yy_v[u], s_l2[s])
                    if lo >= 1:
                        sp.wait_ge(s_o, u)
                        rows_dma(sp, out_v[u - 1], ot[:, 1 - s, :, :], s_st[1 - s])
                    if lo == CHUNKS - 1:
                        sp.wait_ge(s_o, u + 1)
                        rows_dma(sp, out_v[u], ot[:, s, :, :], s_st[s])
                sweep(sp, CHUNKS, final)
                for i in range(2):
                    sp.wait_ge(s_st[i], 32 * ((CHUNKS + 1 - i) // 2))

            @block.scalar
            def _(act):
                def step(u, s, lo, hi):
                    if lo >= 1:
                        hold(act, s_O, u)
                    for f in range(NF):
                        if f % 2 == 0:
                            hold(act, s_H, NF // 2 * u + f // 2 + 1)
                        x = nc.scalar.activation(hT[:, f, :], pH[:, f // 2, (f % 2) * CH:(f % 2 + 1) * CH],
                                                 ACT.Gelu_apprx_tanh, bias=b1[:, f:f + 1])
                        if f % 2:
                            x.then_inc(s_g, 1)
                    if lo >= 1:
                        nc.scalar.copy(yall[:, bass.ds(u * 2 - 2, 2), :], pO[:, 1 - s, :].rearrange("p (t c) -> p t c", t=2))\
                          .then_inc(s_y, 1)
                    if lo == CHUNKS - 1:
                        hold(act, s_O, u + 1)
                        nc.scalar.copy(yall[:, 2 * u:2 * u + 2, :], pO[:, s, :].rearrange("p (t c) -> p t c", t=2))\
                          .then_inc(s_y, 1)
                sweep(act, CHUNKS, step)

            @block.tensor
            def _(pe):
                def hidden(u, s, lo):
                    pe.wait_ge(s_ld[s], (u // 2 + 1) * 16)
                    for f in range(NF):
                        if f % 2 == 0 and lo >= 1:
                            pe.wait_ge(s_g, NF // 2 * (u - 1) + f // 2 + 1)
                        for k in range(2):
                            last = nc.tensor.matmul(pH[:, f // 2, (f % 2) * CH:(f % 2 + 1) * CH],
                                                    w1[:, k, 128 * f:128 * f + 128], xnT[:, s, k, :],
                                                    start=k == 0, stop=k == 1)
                        if f % 2:
                            last.then_inc(s_H, 1)

                def step(u, s, lo, hi):
                    if lo == 0:
                        hidden(0, 0, 0)
                    if hi <= CHUNKS - 2:
                        hidden(u + 1, 1 - s, lo + 1)
                    if lo >= 2:
                        pe.wait_ge(s_y, u - 1)
                    for t in range(2):
                        for f in range(NF):
                            if t == 0 and f % 2 == 0:
                                pe.wait_ge(s_g, NF // 2 * u + f // 2 + 1)
                            last = nc.tensor.matmul(pO[:, s, t * C:(t + 1) * C], hT[:, f, t * R:t * R + R], w2[:, f, :],
                                                    start=f == 0, stop=f == NF - 1)
                    last.then_inc(s_O, 1)
                sweep(pe, CHUNKS, step)

            @block.vector
            def _(v):
                for i in range(TILES):
                    rank_tile(v, i)
                nc.vector.scalar_tensor_tensor(out=coef[:, :], in0=rank[:, :], scalar=float(TOPK1), in1=wsel[:, :],
                                               op0=ALU.is_lt, op1=ALU.mult)
                v.drain()
                v.wait_ge(s_y, CHUNKS)

                def final(u, s, lo, hi):
                    y = yall[:, bass.ds(u * 2, 2), :]
                    nc.vector.tensor_tensor(out=y, in0=y, in1=b2[:, :].unsqueeze(1).broadcast_to([R, 2, C]), op=ALU.add)
                    v.drain()
                    nc.vector.tensor_tensor(out=y, in0=y, in1=coef[:, bass.ds(u * 2, 2)].unsqueeze(2)
                                            .broadcast_to([R, 2, C]), op=ALU.mult)
                    v.drain()
                    v.wait_ge(s_l2[s], (u // 2 + 1) * 32)
                    if lo >= 2:
                        v.wait_ge(s_st[s], (u // 2) * 32)
                    nc.vector.tensor_tensor(out=ot[:, s, :, :], in0=y, in1=yt[:, s, :, :], op=ALU.add).then_inc(s_o, 1)
                sweep(v, CHUNKS, final)


@contextmanager
def phase(env):
    nc, used = env["nc"], []
    with ExitStack() as ctx:
        def sem(name, software_dma=False):
            s = ctx.enter_context(nc.semaphore(name))
            if not software_dma:
                used.append(s)
            return s

        env["sem"] = sem
        yield
        with nc.Block() as block:
            @block.gpsimd
            def _(pool):
                for s in used:
                    pool.sem_clear(s)


def gps_kernel(nc, a, out):
    def dram(name, shape, dt=F32):
        return nc.dram_tensor(name, shape, dt).ap()

    def chunk_view(t):
        return t.rearrange("(u t p) c -> u p t c", t=2, p=R)

    with nc.allow_non_contiguous_dma(reason="bias columns and rows of a strided weight"), ExitStack() as ctx:
        sb = lambda n, s, d=F32: ctx.enter_context(nc.sbuf_tensor(n, s, d))
        env = dict(
            nc=nc, a=a, chunk_view=chunk_view, x_in=a["x"], out=out,
            tab0=dram("tab0", (N, TAB0)),
            dst_tab=dram("dst_tab", (NPAD, 24), BF16),
            tab1=dram("tab1", (N, C)),
            xnT_d=[dram(f"xnT{i}", (128, 2, N)) for i in range(4)],
            x_d=[dram(f"xres{i}", (N, C)) for i in range(3)],
            gf_d=dram("group_range", (2, GROUPS)),
            w_d=dram("route_weight", (1, N)),
            ident=sb("ident", [128, 128]), ones=sb("ones", [128, 128]), zeros=sb("zeros", [1, 512]),
            stats=sb("stats", [R, TILES, 2]),
            spanI=sb("span", [1, 1], I32),
            g0=sb("mix0_g", [128, 2, C]), g0b=sb("mix0_b", [128, 2]), g1=sb("mix1_g", [128, 2, C]),
            pself=sb("pself", [R, TILES, H0]),
            x1sum=sb("x1sum", [128, 2]), attr=sb("node_attr", [R, TILES]), wsel=sb("wsel", [R, TILES]),
            srcI=sb("src", [R, ETILES], I32),
            dstRel=sb("dst_rel", [R, ETILES]),
            baseF=sb("base_f", [1, GROUPS]), baseI=sb("base", [1, GROUPS], I32),
            iotaI=sb("iota_i", [R, W], I32), iotaW=sb("iota", [R, W]))
        ident, ones, zeros = env["ident"], env["ones"], env["zeros"]
        s_zero = ctx.enter_context(nc.semaphore("const_zeroed"))
        with nc.Block() as block:
            @block.gpsimd
            def _(pool):
                nc.gpsimd.memset(ident[:, :], 0.0).then_inc(s_zero, 1)
                nc.gpsimd.memset(ones[:, :], 1.0)
                nc.gpsimd.memset(zeros[:, :], 0.0)
                pool.wait_ge(s_zero, 1)
                nc.gpsimd.affine_select(out=ident[:, :], in_=ident[:, :], compare_op=ALU.not_equal, fill=1.0,
                                        base=0, pattern=[[-1, 128]], channel_multiplier=1)
                pool.drain()
        with phase(env):
            edge_indices(env)
        with phase(env):
            front0(env)
        with ExitStack() as first:
            acc = first.enter_context(nc.sbuf_tensor("sum0", [128, 2, NPAD], F32))
            den = first.enter_context(nc.sbuf_tensor("den0", [H0, NPAD], F32))
            with phase(env):
                edges0(env, acc, den)
            with phase(env):
                back0(env, acc, den)
        with phase(env):
            ffn0(env)
        with phase(env):
            front1(env)
        with ExitStack() as second:
            z = second.enter_context(nc.sbuf_tensor("sum1", [128, 4, NPAD], F32))
            with ExitStack() as attrs:
                ea = attrs.enter_context(nc.sbuf_tensor("edge_attr", [R, ETILES, 4], F32))
                with phase(env):
                    edge_attrs(env, ea)
                with phase(env):
                    edges1(env, z, ea)
            with phase(env):
                back1(env, z)
        with phase(env):
            ffn1(env)


def kernel(**inputs):
    import numpy as np
    import concourse.bacc as bacc
    from concourse.bass_utils import run_bass_kernel_spmd

    nc = bacc.Bacc("TRN2", target_bir_lowering=False, num_devices=1)
    arrays, aps = {}, {}
    for name, value in inputs.items():
        if name == "L1_ffn_attention_mask":
            continue
        value = np.ascontiguousarray(value)
        arrays["in_" + name] = value
        aps[name] = nc.dram_tensor("in_" + name, value.shape, mybir.dt.from_np(value.dtype), kind="ExternalInput").ap()
    out = nc.dram_tensor("out_nodes", (N, C), F32, kind="ExternalOutput").ap()
    gps_kernel(nc, aps, out)
    result = run_bass_kernel_spmd(nc, [arrays], core_ids=[0])
    return result.results[0]["out_nodes"]
```

```python
from contextlib import ExitStack, contextmanager

import concourse.bass as bass
from concourse import mybir

F32 = mybir.dt.float32
I32 = mybir.dt.int32
BF16 = mybir.dt.bfloat16
U32 = mybir.dt.uint32
U16 = mybir.dt.uint16
ALU = mybir.AluOpType
ACT = mybir.ActivationFunctionType
AX = mybir.AxisListType

N = 6250
C = 256
R = 125
TILES = N // R
CH = 2 * R
CHUNKS = N // CH
E = 106250
ETILES = E // R
GT = 5
GROUPS = ETILES // GT
SLOTS = 6
AHEAD = 3
W = 64
NPAD = N + W
QB = 85
NB = ETILES // QB
H0, D0 = 4, 64
TAB0 = C + H0
EPS = 1e-5
E8, F0 = 8, 512
F1 = 1024
CAPACITY = float(-(-N * 5 // (4 * E8)))
KEPT = N // 2
TOPK1 = KEPT - 1
SEL = 112
INV_SQRT3 = 3.0 ** -0.5
COS8, SIN8 = 0.9238795325112867, 0.3826834323650898


def sweep(eng, n, body, m=2, ahead=1):
    for u in range(m):
        body(u, u % m, u, u)
    blocks = (n - ahead - m) // m
    with eng.Fori(1, blocks + 1) as k:
        for r in range(m):
            body(k * m + r, r, m, m * blocks + m - 1)
    for u in range(m + m * blocks, n):
        body(u, u % m, u, u)


def rows_dma(eng, out, in_, sem):
    eng.dma_start(out[0:SEL], in_[0:SEL]).then_inc(sem, 16)
    eng.dma_start(out[SEL:R], in_[SEL:R]).then_inc(sem, 16)


def hold(eng, sem, value):
    eng.wait_ge(sem, value)
    eng.nop(nofuse=True)


def ln_stats(nc, v, x, bn, mv, var_eps, s_var):
    for t in range(2):
        nc.vector.bn_stats(bn[:, t, :], x[:, t, :])
    v.drain()
    for t in range(2):
        nc.vector.bn_aggr(mv[:, t, :], bn[:, t, :])
    v.drain()
    nc.vector.tensor_scalar(var_eps[:, :], mv[:, :, 1], EPS, None, ALU.add).then_inc(s_var, 1)


def ln_apply(nc, v, xn, x, mv, rn, tiles=2):
    nc.vector.scalar_tensor_tensor(out=rn[:, :, 1], in0=mv[:, :, 0], scalar=-1.0, in1=rn[:, :, 0],
                                   op0=ALU.mult, op1=ALU.mult)
    v.drain()
    for t in range(tiles):
        last = nc.vector.tensor_scalar(xn[:, t, :], x[:, t, :], rn[:, t, 0:1], rn[:, t, 1:2], ALU.mult, ALU.add)
    return last


def front0(env):
    nc, a, sem, ident, ones, stats = (env[k] for k in ("nc", "a", "sem", "ident", "ones", "stats"))
    chunk_view = env["chunk_view"]
    g0, g0b = env["g0"], env["g0b"]
    x_v = chunk_view(env["x_in"])
    tab_v = chunk_view(env["tab0"])
    adst = env["dst_tab"]
    HD = 32
    with ExitStack() as ctx:
        sb = lambda n, s, d=F32: ctx.enter_context(nc.sbuf_tensor("f0_" + n, s, d))
        pb = lambda n, s: ctx.enter_context(nc.psum_tensor("f0_" + n, s, F32))
        wg = sb("wg", [128, 2, C])
        wga = sb("wga", [128, 2, C + 8])
        att = sb("att", [128, 2, C])
        tmp = sb("tmp", [128, 2, C])
        wqkv = sb("wqkv", [128, 3, 3 * C])
        wkv = sb("wkv", [128, 3, 2 * C])
        cm = sb("cm", [128, 3, 8])
        w1 = sb("w1", [128, 2, C])
        b1c = sb("b1c", [128, 2])
        bqc = sb("bqc", [128, 2])
        gv = sb("gv", [128, 2])
        gk = sb("gk", [128, 2, HD])
        xt = sb("xt", [R, 2, 2, C])
        xn = sb("xn", [R, 2, 2, C])
        bn = sb("bn", [R, 2, 6])
        mv = sb("mv", [R, 2, 2])
        ve = sb("ve", [R, 2])
        rn = sb("rn", [R, 2, 2])
        mhalf = sb("mhalf", [R, 2])
        xnT = sb("xnT", [128, 2, 2, CH])
        hrow = sb("hrow", [R, 2, 2, C + 8])
        adst_all = sb("adst_all", [R, TILES, 8])
        kvt = sb("kvt", [R, 2, 2 * C])
        sq = sb("sq", [R, 2, 2 * C])
        ss = sb("ss", [R, 2, 16])
        sd = sb("sd", [R, 2, 16])
        ri = sb("ri", [R, 2, 16])
        kvn = sb("kvn", [R, 2, 2 * C + 2])
        epst = sb("epst", [128, 1])
        pT = pb("pT", [128, 2, 512])
        pH = pb("pH", [128, 2, 512])
        pKV = pb("pKV", [128, 2, 512])
        pS = pb("pS", [128, 512])
        pK = pb("pK", [128, 512])
        s_w = sem("f0_weights")
        s_wf = sem("f0_fold_weights")
        s_p = sem("f0_prepared")
        s_x = [sem(f"f0_x{i}") for i in range(2)]
        s_var = sem("f0_var")
        s_rstd = sem("f0_rstd")
        s_xn = sem("f0_xn")
        s_T = sem("f0_transposed")
        s_xnT = sem("f0_xnT")
        s_h = sem("f0_h")
        s_hrow = sem("f0_hrow")
        s_kv = sem("f0_kv")
        s_kvt = sem("f0_kvt")
        s_sq = sem("f0_sq")
        s_ss = sem("f0_ss")
        s_sd = sem("f0_sd")
        s_kvn = sem("f0_kvn")
        s_acc = sem("f0_accumulated")
        s_sx = [sem(f"f0_store_xnT{i}") for i in range(2)]
        s_st = [sem(f"f0_store_tab{i}") for i in range(2)]
        s_ad = sem("f0_store_dst")

        with nc.Block() as block:
            @block.sync
            def _(sp):
                sp.dma_start(wg[:, :, :], a["L0_gnn_W"].rearrange("(k p) n -> p k n", p=128)).then_inc(s_w, 16)
                for i, n in enumerate(("L0_gnn_att_src", "L0_gnn_att_dst")):
                    sp.dma_start(att[:, i, :], a[n].rearrange("(o h) c -> o (h c)", o=1).broadcast_to([128, C]))\
                      .then_inc(s_w, 16)
                sp.dma_start(wqkv[:, 0:2, :], a["L0_mix_w_qkv"].rearrange("(k p) n -> p k n", p=128)).then_inc(s_w, 16)
                sp.dma_start(wqkv[:, 2, :], a["L0_mix_b_qkv"].rearrange("(o n) -> o n", o=1).broadcast_to([128, 3 * C]))\
                  .then_inc(s_w, 16)
                sp.wait_ge(s_w, 16 * 5)

        with nc.Block() as block:
            @block.gpsimd
            def _(pool):
                nc.gpsimd.memset(mhalf[:, :], -0.5)
                nc.gpsimd.memset(epst[:, :], EPS)
                nc.gpsimd.memset(kvn[:, :, :], 1.0)
                pool.drain()

            @block.vector
            def _(v):
                for i in range(2):
                    for k in range(2):
                        nc.vector.tensor_tensor(out=tmp[:, k, :], in0=wg[:, k, :], in1=att[:, i, :], op=ALU.mult)
                    v.drain()
                    for k in range(2):
                        nc.vector.tensor_reduce(wga[:, k, C + 4 * i:C + 4 * i + 4],
                                                tmp[:, k, :].rearrange("p (h c) -> p h c", h=H0), AX.X, ALU.add)
                    v.drain()
                nc.vector.tensor_copy(wga[:, :, 0:C], wg[:, :, :])
                for s in (1, 2):
                    src = wqkv[:, :, :].rearrange("p k (h s d) -> p k h s d", s=3, d=HD)[:, :, :, s, :]
                    dst = wkv[:, :, (s - 1) * C:s * C].rearrange("p k (h d) -> p k h d", d=HD)
                    nc.vector.tensor_reduce(cm[:, :, :], src, AX.X, ALU.add)
                    v.drain()
                    nc.vector.tensor_scalar(cm[:, :, :], cm[:, :, :], -1.0 / HD, None, ALU.mult)
                    v.drain()
                    for k in range(3):
                        nc.vector.tensor_tensor(out=dst[:, k, :, :], in0=src[:, k, :, :],
                                                in1=cm[:, k, :].unsqueeze(2).broadcast_to([128, 8, HD]), op=ALU.add)
                    v.drain()

        with nc.Block() as block:
            @block.sync
            def _(sp):
                def load(u, s):
                    rows_dma(sp, xt[:, s, :, :], x_v[u].rearrange("p t c -> p t c"), s_x[s])

                def store(u, s):
                    sp.wait_ge(s_xnT, u + 1)
                    sp.dma_start(env["xnT_d"][0][:, :, bass.ds(u * CH, CH)], xnT[:, s, :, :]).then_inc(s_sx[s], 16)
                    sp.wait_ge(s_hrow, 2 * u + 2)
                    rows_dma(sp, tab_v[u], hrow[:, s, :, 0:TAB0], s_st[s])

                def step(u, s, lo, hi):
                    if lo >= 2:
                        sp.wait_ge(s_xn, u - 1)
                    load(u, s % 2)
                    if lo >= 3:
                        store(u - 3, (s + 1) % 2)
                sweep(sp, CHUNKS, step, 4)
                for u in range(CHUNKS - 3, CHUNKS):
                    store(u, u % 2)
                for i in range(2):
                    n = (CHUNKS + 1 - i) // 2
                    sp.wait_ge(s_sx[i], 16 * n)
                    sp.wait_ge(s_st[i], 32 * n)

            @block.gpsimd
            def _(pool):
                def step(u, s, lo, hi):
                    hold(pool, s_var, u + 1)
                    nc.gpsimd.tensor_tensor(out=rn[:, :, 0], in0=ve[:, :], in1=mhalf[:, :], op=ALU.pow)\
                      .then_inc(s_rstd, 1)
                sweep(pool, CHUNKS, step)

            @block.vector
            def _(v):
                def norm_stats(u, s):
                    v.wait_ge(s_x[s], (u // 2 + 1) * 32)
                    ln_stats(nc, v, xt[:, s, :, :], bn, mv, ve, s_var)

                def norm_apply(u, s, lo):
                    v.wait_ge(s_rstd, u + 1)
                    if lo >= 2:
                        v.wait_ge(s_T, u - 1)
                    ln_apply(nc, v, xn[:, s, :, :], xt[:, s, :, :], mv, rn).then_inc(s_xn, 1)
                    nc.vector.tensor_copy(stats[:, bass.ds(u * 2, 2), :], rn[:, :, :])

                def step(u, s, lo, hi):
                    if lo == 0:
                        for i in range(2):
                            norm_stats(i, i)
                            norm_apply(i, i, i)
                            v.drain()
                    more = hi <= CHUNKS - 3
                    if lo >= 1:
                        v.wait_ge(s_kvn, 2 * u)
                    for t in range(2):
                        v.wait_ge(s_kv, 2 * u + t + 1)
                        nc.vector.tensor_tensor(out=kvt[:, t, :], in0=pKV[0:R, t, :], in1=wkv[0:R, 2, :], op=ALU.add)\
                          .then_inc(s_kvt, 1)
                    if more:
                        norm_stats(u + 2, s)
                    for t in range(2):
                        v.wait_ge(s_sq, 2 * u + t + 1)
                        nc.vector.tensor_reduce(ss[:, t, :], sq[:, t, :].rearrange("p (g d) -> p g d", d=HD), AX.X,
                                                ALU.add).then_inc(s_ss, 1)
                    if more:
                        norm_apply(u + 2, s, lo + 2)
                    v.wait_ge(s_sd, u + 1)
                    nc.vector.reciprocal(ri[:, :, :], sd[:, :, :])
                    v.drain()
                    if lo >= 1:
                        v.wait_ge(s_acc, 2 * u)
                    for t in range(2):
                        kvn_k = kvn[:, t, 0:2 * 129].rearrange("p (g m) -> p g m", g=2)
                        for g in range(2):
                            nc.vector.tensor_tensor(
                                out=kvn_k[:, g, 0:128].rearrange("p (h d) -> p h d", d=HD),
                                in0=kvt[:, t, 128 * g:128 * g + 128].rearrange("p (h d) -> p h d", d=HD),
                                in1=ri[:, t, 4 * g:4 * g + 4].unsqueeze(2).broadcast_to([R, 4, HD]), op=ALU.mult)
                        nc.vector.tensor_tensor(
                            out=kvn[:, t, 258:514].rearrange("p (h d) -> p h d", d=HD),
                            in0=kvt[:, t, C:2 * C].rearrange("p (h d) -> p h d", d=HD),
                            in1=ri[:, t, 8:16].unsqueeze(2).broadcast_to([R, 8, HD]), op=ALU.mult).then_inc(s_kvn, 1)
                sweep(v, CHUNKS, step, 2, 2)

            @block.scalar
            def _(act):
                act.dma_start(w1[:, :, :], a["L0_mix_w1"].rearrange("(k p) n -> p k n", p=128)).then_inc(s_wf, 16)
                act.dma_start(b1c[:, :], a["L0_mix_b1"].rearrange("(k p) -> p k", p=128)).then_inc(s_wf, 16)
                bq = a["L0_mix_b_qkv"].rearrange("(h s d o) -> h s d o", s=3, d=HD, o=1)
                for h in range(8):
                    act.dma_start(bqc[HD * (h % 4):HD * (h % 4 + 1), h // 4:h // 4 + 1], bq[h, 0]).then_inc(s_wf, 16)
                for h in range(4):
                    for i, n in enumerate(("L0_mix_vln_g", "L0_mix_vln_b")):
                        act.dma_start(gv[HD * h:HD * (h + 1), i:i + 1], a[n].rearrange("(d o) -> d o", o=1))\
                          .then_inc(s_wf, 16)
                for i, n in enumerate(("L0_mix_kln_g", "L0_mix_kln_b")):
                    act.dma_start(gk[:, i, :], a[n].rearrange("(o d) -> o d", o=1).broadcast_to([128, HD]))\
                      .then_inc(s_wf, 16)

                def turn(u, s, lo):
                    if lo >= 2:
                        hold(act, s_sx[s], (u // 2) * 16)
                    hold(act, s_T, u + 1)
                    nc.scalar.copy(xnT[:, s, :, :], pT[:, s, 0:2 * CH].rearrange("p (k n) -> p k n", k=2))\
                      .then_inc(s_xnT, 1)

                def step(u, s, lo, hi):
                    if lo == 0:
                        turn(0, 0, 0)
                    if lo >= 2:
                        hold(act, s_st[s], (u // 2) * 32)
                    for t in range(2):
                        hold(act, s_h, 2 * u + t + 1)
                        nc.scalar.copy(hrow[:, s, t, :], pH[0:R, t, 0:C + 8]).then_inc(s_hrow, 1)
                    act.drain()
                    nc.scalar.copy(adst_all[:, bass.ds(2 * u, 2), :], hrow[:, s, :, C:C + 8])
                    if hi <= CHUNKS - 2:
                        turn(u + 1, 1 - s, lo + 1)
                    for t in range(2):
                        hold(act, s_kvt, 2 * u + t + 1)
                        nc.scalar.activation(sq[:, t, :], kvt[:, t, :], ACT.Square).then_inc(s_sq, 1)
                    hold(act, s_ss, 2 * u + 2)
                    nc.scalar.activation(sd[:, :, :], ss[:, :, :], ACT.Sqrt, bias=epst[0:R, :], scale=1.0 / HD)\
                      .then_inc(s_sd, 1)
                sweep(act, CHUNKS, step)

            @block.tensor
            def _(pe):
                def transposes(u, s, lo):
                    pe.wait_ge(s_xn, u + 1)
                    if lo >= 2:
                        pe.wait_ge(s_xnT, u - 1)
                    for k in range(2):
                        for t in range(2):
                            last = nc.tensor.transpose(pT[:, s, k * CH + t * R:k * CH + t * R + R],
                                                       xn[:, s, t, 128 * k:128 * k + 128], ident[0:R, 0:R])
                    last.then_inc(s_T, 1)

                def products(u, s, lo):
                    pe.wait_ge(s_xnT, u + 1)
                    for t in range(2):
                        i = 2 * u + t
                        if lo >= 1:
                            pe.wait_ge(s_hrow, i - 1)
                        for k in range(2):
                            last = nc.tensor.matmul(pH[0:R, t, 0:C + 8], xnT[:, s, k, t * R:t * R + R], wga[:, k, :],
                                                    start=k == 0, stop=k == 1)
                        last.then_inc(s_h, 1)
                    for t in range(2):
                        i = 2 * u + t
                        if lo >= 1:
                            pe.wait_ge(s_kvt, i - 1)
                        for k in range(2):
                            last = nc.tensor.matmul(pKV[0:R, t, :], xnT[:, s, k, t * R:t * R + R], wkv[:, k, :],
                                                    start=k == 0, stop=k == 1)
                        last.then_inc(s_kv, 1)

                def sums(u, s):
                    for t in range(2):
                        i = 2 * u + t
                        pe.wait_ge(s_kvn, i + 1)
                        for g in range(2):
                            nc.tensor.matmul(pS[:, 129 * g:129 * g + 129], kvn[:, t, 258 + 128 * g:386 + 128 * g],
                                             kvn[:, t, 129 * g:129 * g + 129], start=False, stop=False,
                                             skip_group_check=True)
                        for g in range(2):
                            last = nc.tensor.matmul(pK[:, g:g + 1], kvn[:, t, 129 * g:129 * g + 128], ones[0:R, 0:1],
                                                    start=False, stop=False, skip_group_check=True)
                        last.then_inc(s_acc, 1)

                def step(u, s, lo, hi):
                    products(u, s, lo)
                    if hi <= CHUNKS - 2:
                        transposes(u + 1, 1 - s, lo + 1)
                    if lo >= 1:
                        sums(u - 1, 1 - s)

                nc.tensor.matmul(pS[:, 0:258], env["zeros"][0:1, 0:128], env["zeros"][0:1, 0:258], start=True, stop=False,
                                 skip_group_check=True)
                nc.tensor.matmul(pK[:, 0:2], env["zeros"][0:1, 0:128], env["zeros"][0:1, 0:2], start=True, stop=False,
                                 skip_group_check=True)
                transposes(0, 0, 0)
                sweep(pe, CHUNKS, step)
                sums(CHUNKS - 1, (CHUNKS - 1) % 2)
                pe.drain()

        kvT = sb("kvT", [128, 2, 128])
        ksum = sb("ksum", [128, 2])
        kdiag = sb("kdiag", [128, 2, 128])
        mask = sb("mask", [128, 128])
        sA = sb("sA", [128, 2, 128])
        sv = sb("sv", [128, 2])
        m1 = sb("m1", [128, 2, C])
        wqT = sb("wqT", [128, 2, C])
        wq = sb("wq", [128, 2, C])
        amax = sb("amax", [R, 8])
        amaxT = sb("amaxT", [8, R])
        am1 = sb("am1", [8, 1])
        amr = sb("amr", [1, 8])
        amb = sb("amb", [128, 8])
        dtab = sb("dtab", [R, TILES, 8])
        g_ = sb("g_", [R, TILES, 4])
        dpart = sb("dpart", [R, TILES, 3, 8], BF16)
        drest = sb("drest", [R, 2, TILES, 8])
        zpad = sb("zpad", [W, 24], BF16)
        s_f = {k: sem("fold_" + k) for k in ("mask", "mask1", "wq", "qt", "qtc", "kvT", "m", "mc", "g", "am", "amT", "am1", "amr",
                                            "amrc", "amb", "dt", "zp", "gb", "kd", "ks")}
        with nc.Block() as block:
            @block.gpsimd
            def _(pool):
                nc.gpsimd.memset(mask[:, :], 0.0).then_inc(s_f["mask"], 1)
                nc.gpsimd.memset(zpad[:, :], 0.0).then_inc(s_f["zp"], 1)
                pool.wait_ge(s_f["mask"], 1)
                pool.drain()
                for h in range(4):
                    nc.gpsimd.memset(mask[HD * h:HD * (h + 1), HD * h:HD * (h + 1)], 1.0 / N)
                    pool.drain()
                pool.drain().then_inc(s_f["mask1"], 1)

            @block.tensor
            def _(pe):
                pe.wait_ge(s_f["wq"], 1)
                for g in range(2):
                    for k in range(2):
                        last = nc.tensor.transpose(pT[:, g, 128 * k:128 * k + 128],
                                                   wq[:, k, 128 * g:128 * g + 128], ident[:, :])
                last.then_inc(s_f["qt"], 1)
                pe.wait_ge(s_f["kd"], 1)
                for g in range(2):
                    last = nc.tensor.matmul(pK[:, 128 + 128 * g:256 + 128 * g], ones[:, :], kdiag[:, g, :], start=True,
                                            stop=True, skip_group_check=True)
                last.then_inc(s_f["ks"], 1)
                pe.wait_ge(s_wf, 16 * 20)
                pe.wait_ge(s_f["kvT"], 1)
                for g in range(2):
                    last = nc.tensor.matmul(pH[:, g, 0:C], kvT[:, g, :], w1[:, g, :], start=True, stop=True)
                last.then_inc(s_f["m"], 1)
                pe.wait_ge(s_f["mc"], 1)
                pe.wait_ge(s_f["qtc"], 1)
                for k in range(2):
                    for g in range(2):
                        last = nc.tensor.matmul(pKV[:, k, 0:C], wqT[:, g, 128 * k:128 * k + 128], m1[:, g, :],
                                                start=g == 0, stop=g == 1)
                for f in range(2):
                    for g in range(2):
                        last = nc.tensor.matmul(pT[:, 0, f:f + 1], m1[:, g, 128 * f:128 * f + 128], bqc[:, g:g + 1],
                                                start=g == 0, stop=g == 1)
                last.then_inc(s_f["g"], 1)
                pe.wait_ge(s_f["am"], 1)
                nc.tensor.transpose(pT[0:8, 1, 0:R], amax[:, :], ident[0:R, 0:R]).then_inc(s_f["amT"], 1)
                pe.wait_ge(s_f["am1"], 1)
                nc.tensor.transpose(pT[0:1, 1, 128:136], am1[:, :], ident[0:8, 0:8]).then_inc(s_f["amr"], 1)
                pe.wait_ge(s_f["amrc"], 1)
                nc.tensor.matmul(pT[:, 1, 256:264], ones[0:1, :], amr[:, :], start=True, stop=True).then_inc(s_f["amb"], 1)

            @block.vector
            def _(v):
                for k in range(2):
                    last = nc.vector.tensor_copy(
                        wq[:, k, :].rearrange("p (h d) -> p h d", d=HD),
                        wqkv[:, k, :].rearrange("p (h s d) -> p h s d", s=3, d=HD)[:, :, 0, :])
                last.then_inc(s_f["wq"], 1)
                nc.vector.tensor_copy(ksum[:, :], pK[:, 0:2])
                v.drain()
                for g in range(2):
                    last = nc.vector.tensor_scalar(kdiag[:, g, :], ident[:, :], ksum[:, g:g + 1], None, ALU.mult)
                last.then_inc(s_f["kd"], 1)
                v.wait_ge(s_f["qt"], 1)
                nc.vector.tensor_copy(wqT[:, :, :], pT[:, :, 0:C]).then_inc(s_f["qtc"], 1)
                v.wait_ge(s_f["mask1"], 1)
                v.wait_ge(s_wf, 16 * 20)
                v.wait_ge(s_f["ks"], 1)
                for g in range(2):
                    S = pS[:, 129 * g:129 * g + 128]
                    gkb = gk[:, 0, :].unsqueeze(1).broadcast_to([128, 4, HD])
                    bkb = gk[:, 1, :].unsqueeze(1).broadcast_to([128, 4, HD])
                    nc.vector.tensor_scalar(sA[:, 0, :], S, gv[:, 0:1], None, ALU.mult)
                    v.drain()
                    nc.vector.scalar_tensor_tensor(out=sA[:, 1, :], in0=pK[:, 128 + 128 * g:256 + 128 * g], scalar=gv[:, 1:2],
                                                   in1=sA[:, 0, :], op0=ALU.mult, op1=ALU.add)
                    v.drain()
                    nc.vector.tensor_tensor(out=sA[:, 0, :].rearrange("p (h d) -> p h d", h=4),
                                            in0=sA[:, 1, :].rearrange("p (h d) -> p h d", h=4), in1=gkb, op=ALU.mult)
                    nc.vector.tensor_scalar(sv[:, 0:1], gv[:, 1:2], float(N), None, ALU.mult)
                    v.drain()
                    nc.vector.scalar_tensor_tensor(out=sv[:, 1:2], in0=pS[:, 129 * g + 128:129 * g + 129],
                                                   scalar=gv[:, 0:1], in1=sv[:, 0:1], op0=ALU.mult, op1=ALU.add)
                    v.drain()
                    nc.vector.scalar_tensor_tensor(out=sA[:, 1, :].rearrange("p (h d) -> p h d", h=4), in0=bkb,
                                                   scalar=sv[:, 1:2], in1=sA[:, 0, :].rearrange("p (h d) -> p h d", h=4),
                                                   op0=ALU.mult, op1=ALU.add)
                    v.drain()
                    nc.vector.tensor_tensor(out=kvT[:, g, :], in0=sA[:, 1, :], in1=mask[:, :], op=ALU.mult)
                    v.drain()
                v.drain().then_inc(s_f["kvT"], 1)
                v.wait_ge(s_f["m"], 1)
                nc.vector.tensor_copy(m1[:, :, :], pH[:, :, 0:C]).then_inc(s_f["mc"], 1)
                v.wait_ge(s_f["g"], 1)
                nc.vector.tensor_tensor(out=g0[:, :, :], in0=pKV[:, :, 0:C], in1=w1[:, :, :], op=ALU.add)
                nc.vector.tensor_tensor(out=g0b[:, :], in0=pT[:, 0, 0:2], in1=b1c[:, :], op=ALU.add)
                nc.vector.tensor_reduce(amax[:, :], adst_all[:, :, :].rearrange("p t c -> p c t"), AX.X, ALU.max)\
                  .then_inc(s_f["am"], 1)
                v.wait_ge(s_f["amT"], 1)
                nc.vector.tensor_reduce(am1[:, :], pT[0:8, 1, 0:R], AX.X, ALU.max).then_inc(s_f["am1"], 1)
                v.wait_ge(s_f["amr"], 1)
                nc.vector.tensor_copy(amr[:, :], pT[0:1, 1, 128:136]).then_inc(s_f["amrc"], 1)
                v.wait_ge(s_f["amb"], 1)
                nc.vector.tensor_copy(amb[:, :], pT[:, 1, 256:264])
                v.drain()
                nc.vector.tensor_tensor(out=g_[:, :, :], in0=adst_all[:, :, 4:8],
                                        in1=amb[0:R, 0:4].unsqueeze(1).broadcast_to([R, TILES, 4]), op=ALU.add)
                nc.vector.tensor_copy(dtab[:, :, 0:4], adst_all[:, :, 4:8])
                v.drain()
                nc.vector.scalar_tensor_tensor(out=dtab[:, :, 4:8], in0=g_[:, :, :], scalar=0.2, in1=g_[:, :, :],
                                               op0=ALU.mult, op1=ALU.max)
                v.drain()
                rest = dtab[:, :, :]
                for i in range(3):
                    nc.vector.tensor_copy(dpart[:, :, i, :], rest)
                    v.drain()
                    if i < 2:
                        nc.vector.tensor_tensor(out=drest[:, i, :, :], in0=rest,
                                                in1=dpart[:, :, i, :], op=ALU.subtract)
                        v.drain()
                        rest = drest[:, i, :, :]
                v.drain().then_inc(s_f["dt"], 1)
                pself = env["pself"]
                nc.vector.tensor_tensor(out=g_[:, :, :], in0=adst_all[:, :, 0:4], in1=adst_all[:, :, 4:8], op=ALU.add)
                v.drain()
                nc.vector.scalar_tensor_tensor(out=pself[:, :, :], in0=g_[:, :, :], scalar=0.2, in1=g_[:, :, :],
                                               op0=ALU.mult, op1=ALU.max)
                v.drain()
                nc.vector.tensor_tensor(out=g_[:, :, :], in0=pself[:, :, :], in1=dtab[:, :, 4:8], op=ALU.subtract)
                v.drain().then_inc(s_f["gb"], 1)

            @block.scalar
            def _(act):
                act.wait_ge(s_f["gb"], 1)
                nc.scalar.activation(env["pself"][:, :, :], g_[:, :, :], ACT.Exp)
                act.drain()

            @block.sync
            def _(sp):
                sp.wait_ge(s_f["zp"], 1)
                sp.dma_start(adst[N:NPAD, :], zpad[:, :]).then_inc(s_ad, 16)
                sp.wait_ge(s_f["dt"], 1)
                rows_dma(sp, adst[0:N, :].rearrange("(t p) c -> p t c", p=R),
                         dpart[:, :, :, :].rearrange("p t i c -> p t (i c)"), s_ad)
                sp.wait_ge(s_ad, 48)


def edge_indices(env):
    nc, a, sem, ident = (env[k] for k in ("nc", "a", "sem", "ident"))
    srcI, dstRel, baseF, spanI = (env[k] for k in ("srcI", "dstRel", "baseF", "spanI"))
    GQ = GROUPS // 2
    with ExitStack() as ctx:
        sb = lambda n, s, d=F32: ctx.enter_context(nc.sbuf_tensor("ei_" + n, s, d))
        st = sb("st", [QB, 2, NB, R], I32)
        stf = sb("stf", [QB, 2, NB, R])
        gi = sb("gi", [GQ, 2, GT * R], I32)
        gf = sb("gf", [GQ, 2, GT * R])
        gm = sb("gm", [GQ, 2, 2])
        grow = sb("grow", [1, 2, GROUPS])
        gB = sb("gB", [R, GROUPS])
        sp_ = sb("sp", [1, GROUPS])
        dstT = sb("dstT", [R, ETILES])
        pt = ctx.enter_context(nc.psum_tensor("ei_pt", [128, 8, 512], F32))
        s_ld, s_cv, s_mm, s_st, s_row, s_t, s_ev = (sem("ei_" + n) for n in
                                                    ("load", "floats", "minmax", "store", "rows", "T", "copied"))
        gd = env["gf_d"]
        with nc.Block() as block:
            @block.sync
            def _(sp):
                for i, n in enumerate(("dst", "src")):
                    sp.dma_start(st[:, i, :, :], a[n].rearrange("(b q e) -> q b e", q=QB, e=R)).then_inc(s_ld, 16)
                sp.dma_start(gi[:, :, :], a["dst"].rearrange("(b q e) -> q b e", q=GQ, e=GT * R)).then_inc(s_ld, 16)
                sp.wait_ge(s_mm, 1)
                for i in range(2):
                    sp.dma_start(gd[i].rearrange("(b q o) -> q b o", q=GQ, o=1), gm[:, :, i:i + 1]).then_inc(s_st, 16)
                sp.wait_ge(s_st, 32)
                sp.dma_start(grow[:, :, :], gd.rearrange("(o i) g -> o i g", o=1)).then_inc(s_row, 16)
                sp.dma_start(gB[:, :], gd[0:1, :].broadcast_to([R, GROUPS])).then_inc(s_row, 16)
                sp.wait_ge(s_row, 32)

            @block.vector
            def _(v):
                v.wait_ge(s_ld, 48)
                nc.vector.tensor_copy(gf[:, :, :], gi[:, :, :])
                v.drain()
                nc.vector.tensor_reduce(gm[:, :, 0], gf[:, :, :], AX.X, ALU.min)
                nc.vector.tensor_reduce(gm[:, :, 1], gf[:, :, :], AX.X, ALU.max)
                v.drain().then_inc(s_mm, 1)
                nc.vector.tensor_copy(stf[:, :, :, :], st[:, :, :, :]).then_inc(s_cv, 1)
                for i, dst in enumerate((dstT, srcI)):
                    for b in range(NB):
                        n = NB * i + b
                        v.wait_ge(s_t, n + 1)
                        nc.vector.tensor_copy(dst[:, QB * b:QB * (b + 1)], pt[0:R, n % 8, 0:QB]).then_inc(s_ev, 1)
                v.wait_ge(s_row, 32)
                nc.vector.tensor_copy(baseF[:, :], grow[:, 0, :])
                nc.vector.tensor_tensor(out=sp_[:, :], in0=grow[:, 1, :], in1=grow[:, 0, :], op=ALU.subtract)
                v.drain()
                nc.vector.tensor_reduce(spanI[:, :], sp_[:, :], AX.X, ALU.max)
                nc.vector.tensor_tensor(out=dstRel[:, :].rearrange("p (g j) -> p g j", j=GT),
                                        in0=dstT[:, :].rearrange("p (g j) -> p g j", j=GT),
                                        in1=gB[:, :].unsqueeze(2).broadcast_to([R, GROUPS, GT]), op=ALU.subtract)
                v.drain()

            @block.tensor
            def _(pe):
                pe.wait_ge(s_cv, 1)
                for n in range(2 * NB):
                    if n >= 8:
                        pe.wait_ge(s_ev, n - 7)
                    nc.tensor.transpose(pt[0:R, n % 8, 0:QB], stf[:, n // NB, n % NB, :], ident[0:QB, 0:QB])\
                      .then_inc(s_t, 1)


def edge_passes(env, layer, zero, one_pass, dma_sems, sems):
    nc, sem = env["nc"], env["sem"]
    iotaI, iotaW, baseI, baseF, spanI = (env[k] for k in ("iotaI", "iotaW", "baseI", "baseF", "spanI"))
    s_i = sem(f"window_iota{layer}")
    with nc.Block() as block:
        @block.gpsimd
        def _(pool):
            nc.gpsimd.iota(iotaI[:, :], pattern=[[1, W]], base=0, channel_multiplier=0).then_inc(s_i, 1)

        @block.vector
        def _(v):
            for t in zero:
                nc.vector.memset(t, 0.0)
            nc.vector.tensor_copy(baseI[:, :], baseF[:, :])
            v.wait_ge(s_i, 1)
            nc.vector.tensor_copy(iotaW[:, :], iotaI[:, :])
            v.drain()
    span = nc.values_load(spanI[0:1, 0:1], min_val=0, max_val=N - 1)
    with nc.Fori(0, span + 1, W):
        one_pass()
        with nc.Block() as block:
            @block.vector
            def _(v):
                nc.vector.tensor_scalar(iotaW[:, :], iotaW[:, :], float(W), None, ALU.add)
                nc.vector.tensor_scalar(baseI[:, :], baseI[:, :], float(W), float(N), ALU.add, ALU.min)
                v.drain()

            @block.gpsimd
            def _(pool):
                m = len(dma_sems)
                nc.gpsimd.inc_swdge_sem(dma_sems, [-(-(GROUPS - i) // m) * GT * 16 for i in range(m)], mode="sub")
                for s in sems:
                    pool.sem_clear(s)


def one_hots(nc, env, out, g):
    return nc.vector.tensor_tensor(
        out=out, in0=env["iotaW"][:, :].unsqueeze(1).broadcast_to([R, GT, W]),
        in1=env["dstRel"][:, bass.ds(g * GT, GT)].unsqueeze(2).broadcast_to([R, GT, W]), op=ALU.is_equal)


def edges0(env, acc, den):
    nc, sem, ident = (env[k] for k in ("nc", "sem", "ident"))
    srcI, baseI = env["srcI"], env["baseI"]
    with ExitStack() as ctx:
        sb = lambda n, s, d=F32: ctx.enter_context(nc.sbuf_tensor("e0_" + n, s, d))
        pb = lambda n, s: ctx.enter_context(nc.psum_tensor("e0_" + n, s, F32))
        ix = sb("ix", [R, SLOTS, GT], I32)
        rows = sb("rows", [R, SLOTS, GT, TAB0])
        dw = sb("dw", [W, SLOTS, 24], BF16)
        oh = sb("oh", [R, SLOTS, GT, W])
        ohT = sb("ohT", [W, 2, GT, R], BF16)
        lg = sb("lg", [R, GT, 8])
        ee = sb("ee", [R, 4, GT, H0])
        msg = sb("msg", [R, 3, GT, TAB0])
        us = sb("us", [128, 2, TAB0])
        eye2 = sb("eye2", [128, W])
        pT = pb("pT", [W, 1024])
        pE = pb("pE", [R, 2, 512])
        pU = pb("pU", [128, 2, 512])
        pF = pb("pF", [128, 2, 512])
        s_gat = env["s_rows"]
        s_dw = [sem(f"e0_dw{i}") for i in range(SLOTS)]
        s_ix, s_oh, s_T, s_ohT, s_E, s_lg, s_ed, s_p, s_msg, s_acc, s_us, s_flip, s_add = (
            sem("e0_" + n) for n in ("ix", "oh", "T", "ohT", "E", "logits", "exponents", "p", "msg", "acc", "copied",
                                     "flip", "added"))
        with nc.Block() as block:
            @block.vector
            def _(v):
                nc.vector.tensor_tensor(out=eye2[:, :], in0=ident[:, 0:W], in1=ident[:, W:2 * W], op=ALU.add)
                v.drain()

        def one_pass():
            with nc.Block() as block:
                @block.gpsimd
                def _(pool):
                    def step(g, s, lo, hi):
                        hold(pool, s_ix, g + 1)
                        for j in range(GT):
                            nc.gpsimd.indirect_dma_start(
                                out=rows[:, s, j, :], out_offset=None, in_=env["tab0"],
                                in_offset=bass.IndirectOffsetOnAxis(ap=ix[:, s, j:j + 1], axis=0))\
                              .then_inc(s_gat[s], 16)
                    sweep(pool, GROUPS, step, SLOTS, AHEAD)

                @block.sync
                def _(sp):
                    def step(g, s, lo, hi):
                        base = sp.value_load(baseI[0:1, bass.ds(g, 1)], min_val=0, max_val=N)
                        if lo >= SLOTS:
                            sp.wait_ge(s_E, g - SLOTS + 1)
                        sp.dma_start(dw[:, s, :], env["dst_tab"][bass.ds(base, W), :]).then_inc(s_dw[s], 16)
                    sweep(sp, GROUPS, step, SLOTS, AHEAD)

                @block.scalar
                def _(act):
                    def stage(g, s, lo):
                        if lo >= SLOTS:
                            hold(act, s_msg, g - SLOTS + 1)
                        nc.scalar.copy(ix[:, s, :], srcI[:, bass.ds(g * GT, GT)]).then_inc(s_ix, 1)

                    def turn(g, s, lo):
                        if lo >= 2:
                            hold(act, s_E, g - 1)
                        hold(act, s_T, g + 1)
                        nc.scalar.copy(ohT[:, s % 2, :, :],
                                       pT[:, 0:128 * GT].rearrange("p (j e) -> p j e", e=128)[:, :, 0:R])\
                          .then_inc(s_ohT, 1)

                    def copied(g, s, lo):
                        if lo >= 2:
                            hold(act, s_flip, g - 1)
                        hold(act, s_acc, g + 1)
                        nc.scalar.copy(us[:, s % 2, :], pU[:, s % 2, 0:TAB0]).then_inc(s_us, 1)

                    def step(g, s, lo, hi):
                        if lo == 0:
                            for i in range(3):
                                stage(i, i, i)
                            for i in range(2):
                                turn(i, i, i)
                        if hi <= GROUPS - 3:
                            turn(g + 2, (s + 2) % SLOTS, lo + 2)
                        if lo >= 3:
                            hold(act, s_acc, g - 2)
                        hold(act, s_ed, g + 1)
                        nc.scalar.activation(msg[:, s % 3, :, C:TAB0], ee[:, 2 + s % 2, :, :], ACT.Exp).then_inc(s_p, 1)
                        if lo >= 2:
                            copied(g - 2, s, lo - 2)
                        if hi <= GROUPS - 4:
                            stage(g + 3, (s + 3) % SLOTS, lo + 3)
                        if lo == GROUPS - 1:
                            copied(g - 1, s + 1, lo)
                            copied(g, s, lo)
                    sweep(act, GROUPS, step, SLOTS, AHEAD)

                @block.vector
                def _(v):
                    def hots(g, s, lo):
                        if lo >= SLOTS:
                            v.wait_ge(s_acc, g - SLOTS + 1)
                        one_hots(nc, env, oh[:, s, :, :], g).then_inc(s_oh, 1)

                    def add(g, s):
                        base = v.value_load(baseI[0:1, bass.ds(g, 1)], min_val=0, max_val=N)
                        v.wait_ge(s_flip, g + 1)
                        w = acc[:, :, bass.ds(base, W)]
                        nc.vector.tensor_tensor(out=w, in0=w,
                                                in1=pF[:, s % 2, 0:2 * W].rearrange("p (k n) -> p k n", k=2), op=ALU.add)
                        w = den[:, bass.ds(base, W)]
                        nc.vector.tensor_tensor(out=w, in0=w, in1=pF[0:H0, s % 2, 2 * W:3 * W], op=ALU.add).then_inc(s_add, 1)

                    def exponents(g, s, lo):
                        v.wait_ge(s_gat[s], (g // SLOTS + 1) * 16 * GT)
                        if lo >= 1:
                            v.wait_ge(s_ed, g)
                        v.wait_ge(s_E, g + 1)
                        nc.vector.tensor_reduce(
                            lg[:, :, :], pE[:, s % 2, 0:24 * GT].rearrange("p (j i c) -> p j c i", i=3, c=8), AX.X,
                            ALU.add).then_inc(s_lg, 1)
                        v.drain()
                        nc.vector.tensor_tensor(out=ee[:, 0, :, :], in0=rows[:, s, :, C:C + H0], in1=lg[:, :, 0:H0],
                                                op=ALU.add)
                        v.drain()
                        nc.vector.scalar_tensor_tensor(out=ee[:, 1, :, :], in0=ee[:, 0, :, :], scalar=0.2,
                                                       in1=ee[:, 0, :, :], op0=ALU.mult, op1=ALU.max)
                        v.drain()
                        nc.vector.tensor_tensor(out=ee[:, 0, :, :], in0=ee[:, 1, :, :], in1=lg[:, :, H0:8],
                                                op=ALU.subtract)
                        v.drain()
                        if lo >= 2:
                            v.wait_ge(s_p, g - 1)
                        nc.vector.tensor_scalar(ee[:, 2 + s % 2, :, :], ee[:, 0, :, :], 0.0, None, ALU.min)\
                          .then_inc(s_ed, 1)

                    def messages(g, s, lo):
                        v.wait_ge(s_p, g + 1)
                        nc.vector.tensor_tensor(
                            out=msg[:, s % 3, :, 0:C].rearrange("p j (h c) -> p j h c", h=H0),
                            in0=rows[:, s, :, 0:C].rearrange("p j (h c) -> p j h c", h=H0),
                            in1=msg[:, s % 3, :, C:TAB0].unsqueeze(3).broadcast_to([R, GT, H0, D0]), op=ALU.mult)\
                          .then_inc(s_msg, 1)

                    def step(g, s, lo, hi):
                        if lo == 0:
                            hots(0, 0, 0)
                            hots(1, 1, 1)
                        if hi <= GROUPS - 3:
                            hots(g + 2, (s + 2) % SLOTS, lo + 2)
                        exponents(g, s, lo)
                        if lo >= 4:
                            add(g - 4, s)
                        if lo >= 1:
                            messages(g - 1, (s - 1) % SLOTS, lo - 1)
                        if lo == GROUPS - 1:
                            messages(g, s, lo)
                            for i in (3, 2, 1, 0):
                                v.drain()
                                add(g - i, s + i)
                            v.drain()
                    sweep(v, GROUPS, step, SLOTS, AHEAD)

                @block.tensor
                def _(pe):
                    def turn(g, s, lo):
                        if lo >= 1:
                            pe.wait_ge(s_ohT, g)
                        hold(pe, s_oh, g + 1)
                        for j in range(GT):
                            last = nc.tensor.transpose(pT[:, 128 * j:128 * j + R], oh[:, s, j, :], ident[0:R, 0:R])
                        last.then_inc(s_T, 1)

                    def logits(g, s, lo):
                        pe.wait_ge(s_ohT, g + 1)
                        pe.wait_ge(s_dw[s], (g // SLOTS + 1) * 16)
                        if lo >= 2:
                            pe.wait_ge(s_lg, g - 1)
                        for j in range(GT):
                            last = nc.tensor.matmul(pE[:, s % 2, 24 * j:24 * j + 24], ohT[:, s % 2, j, :], dw[:, s, :],
                                                    start=True, stop=True)
                        last.then_inc(s_E, 1)

                    def sums(g, s, lo):
                        pe.wait_ge(s_msg, g + 1)
                        if lo >= 2:
                            pe.wait_ge(s_us, g - 1)
                        for j in range(GT):
                            h = W * (j % 2)
                            last = nc.tensor.matmul(pU[h:h + W, s % 2, 0:TAB0], oh[:, s, j, :], msg[:, s % 3, j, :],
                                                    start=j < 2, stop=j >= GT - 2)
                        last.then_inc(s_acc, 1)

                    def flip(g, s, lo):
                        pe.wait_ge(s_us, g + 1)
                        if lo >= 2:
                            pe.wait_ge(s_add, g - 1)
                        for k in range(2):
                            nc.tensor.matmul(pF[:, s % 2, k * W:k * W + W], us[:, s % 2, 128 * k:128 * k + 128],
                                             eye2[:, :], start=True, stop=True)
                        nc.tensor.matmul(pF[0:H0, s % 2, 2 * W:3 * W], us[:, s % 2, C:TAB0], eye2[:, :],
                                         start=True, stop=True).then_inc(s_flip, 1)

                    def step(g, s, lo, hi):
                        if lo == 0:
                            turn(0, 0, 0)
                            turn(1, 1, 1)
                            logits(0, 0, 0)
                        if hi <= GROUPS - 3:
                            turn(g + 2, (s + 2) % SLOTS, lo + 2)
                        if lo >= 2:
                            sums(g - 2, (s - 2) % SLOTS, lo - 2)
                        if lo >= 3:
                            flip(g - 3, s + 1, lo - 3)
                        if hi <= GROUPS - 2:
                            logits(g + 1, (s + 1) % SLOTS, lo + 1)
                        if lo == GROUPS - 1:
                            sums(g - 1, (s - 1) % SLOTS, lo - 1)
                            flip(g - 2, s, lo)
                            sums(g, s, lo)
                            flip(g - 1, s + 1, lo)
                            flip(g, s, lo)
                    sweep(pe, GROUPS, step, SLOTS, AHEAD)

        edge_passes(env, 0, [acc[:, :, :], den[:, :]], one_pass, s_gat,
                    s_dw + [s_ix, s_oh, s_T, s_ohT, s_E, s_lg, s_ed, s_p, s_msg, s_acc, s_us, s_flip, s_add])


def row_bc(ap, parts):
    return ap.rearrange("(o n) -> o n", o=1).broadcast_to([parts, ap.shape[0]])


def back0(env, acc, den):
    nc, a, sem, ident, ones, stats = (env[k] for k in ("nc", "a", "sem", "ident", "ones", "stats"))
    cv = env["chunk_view"]
    g0, g0b, pself = env["g0"], env["g0b"], env["pself"]
    x_v, tab_v, x1_v = cv(env["x_in"]), cv(env["tab0"]), cv(env["x_d"][0])
    with ExitStack() as ctx:
        sb = lambda n, s, d=F32: ctx.enter_context(nc.sbuf_tensor("b0_" + n, s, d))
        pb = lambda n, s: ctx.enter_context(nc.psum_tensor("b0_" + n, s, F32))
        w2 = sb("w2", [128, 2, C])
        crow = sb("crow", [1, 4, C])
        xt = sb("xt", [R, 2, 2, C])
        ht = sb("ht", [R, 2, 2, TAB0])
        xnT = sb("xnT", [128, 2, 2, CH])
        us = sb("us", [128, 2, 2, CH])
        ds_ = sb("ds", [H0, 2, CH])
        gT = sb("gT", [128, 2, CH])
        dn = sb("dn", [R, 2, H0])
        sc_all = sb("sc_all", [R, TILES, 2])
        sc = sb("sc", [R, 2, 2, 2])
        ya = sb("ya", [R, 2, C])
        yb = sb("yb", [R, 2, C])
        xx = sb("xx", [R, 2, 2, C])
        x1 = sb("x1", [R, 2, 2, C])
        xn1 = sb("xn1", [R, 2, 2, C])
        bn, mv, ve, rn, mhalf = (sb("bn", [R, 2, 6]), sb("mv", [R, 2, 2, 2]), sb("ve", [R, 2]), sb("rn", [R, 2, 2, 2]),
                                 sb("mhalf", [R, 2]))
        xT = sb("xT", [128, 2, 2, CH])
        pU, pN, pH, pO, pT = (pb("pU", [R, 2, 512]), pb("pN", [R, 512]), pb("pH", [128, 512]), pb("pO", [R, 2, 512]),
                              pb("pT", [128, 512]))
        pSum = pb("pSum", [128, 512])
        s_w, s_z = sem("b0_weights"), sem("b0_consts")
        s_ld = [sem("b0_load0"), sem("b0_load1")]
        s_st = [sem("b0_store0"), sem("b0_store1")]
        s_sx = [sem("b0_storeT0"), sem("b0_storeT1")]
        s_us, s_U, s_H, s_g, s_O, s_x1, s_var, s_rstd, s_rn, s_xn1, s_T, s_xT, s_dn, s_rd, s_sum, s_sc, s_xx = (
            sem("b0_" + n) for n in ("sums", "U", "H", "gelu", "O", "x1", "var", "rstd", "scales", "xn1", "T", "xT", "den",
                                     "read", "xsum", "xscale", "xx"))

        with nc.Block() as block:
            @block.sync
            def _(sp):
                sp.dma_start(w2[:, :, :], a["L0_mix_w2"].rearrange("(k p) n -> p k n", p=128)).then_inc(s_w, 16)
                sp.dma_start(crow[:, 2, :], row_bc(a["L0_gnn_bias"], 1)).then_inc(s_w, 16)
                sp.dma_start(crow[:, 3, :], row_bc(a["L0_mix_b2"], 1)).then_inc(s_w, 16)
                sp.wait_ge(s_w, 48)

            @block.gpsimd
            def _(pool):
                nc.gpsimd.memset(mhalf[:, :], -0.5)
                pool.drain()

        with nc.Block() as block:
            @block.vector
            def _(v):
                for t in range(2):
                    nc.vector.tensor_tensor(out=crow[:, t, :], in0=crow[:, 2, :], in1=crow[:, 3, :], op=ALU.add)
                nc.vector.tensor_scalar(sc_all[:, :, 0], stats[:, :, 0], 1.0, None, ALU.add)
                nc.vector.tensor_copy(sc_all[:, :, 1], stats[:, :, 1])
                v.drain()

        with nc.Block() as block:
            @block.sync
            def _(sp):
                def load(u, s):
                    rows_dma(sp, xt[:, s, :, :], x_v[u], s_ld[s])
                    rows_dma(sp, ht[:, s, :, :], tab_v[u], s_ld[s])
                    sp.dma_start(xnT[:, s, :, :], env["xnT_d"][0][:, :, bass.ds(u * CH, CH)]).then_inc(s_ld[s], 16)

                def store(u, s):
                    sp.wait_ge(s_x1, u + 1)
                    rows_dma(sp, x1_v[u], x1[:, s, :, :], s_st[s])
                    sp.wait_ge(s_xT, u + 1)
                    sp.dma_start(env["xnT_d"][1][:, :, bass.ds(u * CH, CH)], xT[:, s, :, :]).then_inc(s_sx[s], 16)

                def step(u, s, lo, hi):
                    if lo >= 2:
                        sp.wait_ge(s_xx, u - 1)
                        sp.wait_ge(s_rd, u - 1)
                        sp.wait_ge(s_H, u - 1)
                    load(u, s % 2)
                    if lo >= 3:
                        store(u - 3, (s + 1) % 2)
                sweep(sp, CHUNKS, step, 4)
                for u in range(CHUNKS - 3, CHUNKS):
                    store(u, u % 2)
                for i in range(2):
                    n = (CHUNKS + 1 - i) // 2
                    sp.wait_ge(s_st[i], 32 * n)
                    sp.wait_ge(s_sx[i], 16 * n)

            @block.scalar
            def _(act):
                def pick(u, s, lo):
                    if lo >= 2:
                        hold(act, s_U, u - 1)
                    nc.scalar.copy(us[:, s, :, :], acc[:, :, bass.ds(u * CH, CH)])
                    nc.scalar.copy(ds_[:, s, :], den[:, bass.ds(u * CH, CH)]).then_inc(s_us, 1)

                def inputs(u, s, lo):
                    hold(act, s_ld[s], (u // 2 + 1) * 80)
                    if lo >= 2:
                        hold(act, s_x1, u - 1)
                    hold(act, s_sc, u + 1)
                    for t in range(2):
                        last = nc.scalar.activation(xx[:, s, t, :], xt[:, s, t, :], ACT.Identity,
                                                    bias=sc[:, s, t, 1:2], scale=sc[:, s, t, 0:1])
                    last.then_inc(s_xx, 1)

                def normalize(u, s, lo):
                    if lo >= 2:
                        hold(act, s_sum, u - 1)
                    hold(act, s_rn, u + 1)
                    for t in range(2):
                        last = nc.scalar.activation(xn1[:, s, t, :], x1[:, s, t, :], ACT.Identity,
                                                    bias=rn[:, s, t, 1:2], scale=rn[:, s, t, 0:1])
                    last.then_inc(s_xn1, 1)

                def turn(u, s, lo):
                    if lo >= 2:
                        hold(act, s_sx[s], (u // 2) * 16)
                    hold(act, s_T, u + 1)
                    nc.scalar.copy(xT[:, s, :, :], pT[:, 0:2 * CH].rearrange("p (k n) -> p k n", k=2)).then_inc(s_xT, 1)

                def step(u, s, lo, hi):
                    if lo == 0:
                        pick(0, 0, 0)
                        inputs(0, 0, 0)
                    if hi <= CHUNKS - 2:
                        pick(u + 1, 1 - s, lo + 1)
                    if lo >= 1:
                        hold(act, s_O, u)
                    hold(act, s_H, u + 1)
                    for f in range(2):
                        last = nc.scalar.activation(gT[:, f, :], pH[:, f * CH:(f + 1) * CH], ACT.Gelu, bias=g0b[:, f:f + 1])
                    last.then_inc(s_g, 1)
                    if lo >= 1:
                        normalize(u - 1, 1 - s, lo - 1)
                    if hi <= CHUNKS - 2:
                        inputs(u + 1, 1 - s, lo + 1)
                    if lo >= 1:
                        turn(u - 1, 1 - s, lo - 1)
                    if lo == CHUNKS - 1:
                        normalize(u, s, lo)
                        turn(u, s, lo)
                sweep(act, CHUNKS, step)

            @block.gpsimd
            def _(pool):
                def step(u, s, lo, hi):
                    hold(pool, s_var, u + 1)
                    nc.gpsimd.tensor_tensor(out=rn[:, s, :, 0], in0=ve[:, :], in1=mhalf[:, :], op=ALU.pow)\
                      .then_inc(s_rstd, 1)
                sweep(pool, CHUNKS, step)

            @block.vector
            def _(v):
                def scales(u, s, lo):
                    if lo >= 2:
                        v.wait_ge(s_xx, u - 1)
                    nc.vector.tensor_copy(sc[:, s, :, :], sc_all[:, bass.ds(u * 2, 2), :]).then_inc(s_sc, 1)

                def finish(u, s):
                    v.wait_ge(s_rstd, u + 1)
                    nc.vector.scalar_tensor_tensor(out=rn[:, s, :, 1], in0=mv[:, s, :, 0], scalar=-1.0,
                                                   in1=rn[:, s, :, 0], op0=ALU.mult, op1=ALU.mult).then_inc(s_rn, 1)
                    v.drain()
                    nc.vector.tensor_copy(stats[:, bass.ds(u * 2, 2), :], rn[:, s, :, :])

                def step(u, s, lo, hi):
                    if lo == 0:
                        scales(0, 0, 0)
                    if hi <= CHUNKS - 2:
                        scales(u + 1, 1 - s, lo + 1)
                    v.wait_ge(s_ld[s], (u // 2 + 1) * 80)
                    v.wait_ge(s_U, u + 1)
                    nc.vector.tensor_tensor(out=dn[:, :, :], in0=pN[:, 0:2 * H0].rearrange("p (t h) -> p t h", t=2),
                                            in1=pself[:, bass.ds(u * 2, 2), :], op=ALU.add).then_inc(s_dn, 1)
                    nc.vector.tensor_tensor(
                        out=ya[:, :, :].rearrange("p t (h c) -> p t h c", h=H0),
                        in0=ht[:, s, :, 0:C].rearrange("p t (h c) -> p t h c", h=H0),
                        in1=pself[:, bass.ds(u * 2, 2), :].unsqueeze(3).broadcast_to([R, 2, H0, D0]), op=ALU.mult)
                    v.drain()
                    nc.vector.reciprocal(dn[:, :, :], dn[:, :, :])
                    nc.vector.tensor_tensor(out=yb[:, :, :], in0=ya[:, :, :],
                                            in1=pU[:, s, :].rearrange("p (t c) -> p t c", t=2), op=ALU.add)
                    v.drain().then_inc(s_rd, 1)
                    if lo >= 1:
                        finish(u - 1, 1 - s)
                    nc.vector.tensor_tensor(
                        out=ya[:, :, :].rearrange("p t (h c) -> p t h c", h=H0),
                        in0=yb[:, :, :].rearrange("p t (h c) -> p t h c", h=H0),
                        in1=dn[:, :, :].unsqueeze(3).broadcast_to([R, 2, H0, D0]), op=ALU.mult)
                    v.drain()
                    v.wait_ge(s_xx, u + 1)
                    nc.vector.tensor_tensor(out=yb[:, :, :], in0=ya[:, :, :], in1=xx[:, s, :, :], op=ALU.add)
                    v.drain()
                    v.wait_ge(s_O, u + 1)
                    if lo >= 2:
                        v.wait_ge(s_xn1, u - 1)
                        v.wait_ge(s_st[s], (u // 2) * 32)
                    nc.vector.tensor_tensor(out=x1[:, s, :, :], in0=yb[:, :, :],
                                            in1=pO[:, s, :].rearrange("p (t c) -> p t c", t=2), op=ALU.add)
                    v.drain().then_inc(s_x1, 1)
                    ln_stats(nc, v, x1[:, s, :, :], bn, mv[:, s, :, :], ve, s_var)
                    if lo == CHUNKS - 1:
                        finish(u, s)
                        v.drain()
                sweep(v, CHUNKS, step)

            @block.tensor
            def _(pe):
                def front(u, s, lo):
                    pe.wait_ge(s_us, u + 1)
                    if lo >= 2:
                        pe.wait_ge(s_rd, u - 1)
                    for t in range(2):
                        for k in range(2):
                            nc.tensor.transpose(pU[:, s, t * C + 128 * k:t * C + 128 * k + 128],
                                                us[:, s, k, t * R:t * R + R], ident[:, :])
                    if lo >= 1:
                        hold(pe, s_dn, u)
                    for t in range(2):
                        last = nc.tensor.transpose(pN[:, t * H0:t * H0 + H0], ds_[:, s, t * R:t * R + R],
                                                   ident[0:H0, 0:H0])
                    last.then_inc(s_U, 1)
                    pe.wait_ge(s_ld[s], (u // 2 + 1) * 80)
                    if lo >= 1:
                        pe.wait_ge(s_g, u)
                    for f in range(2):
                        for k in range(2):
                            last = nc.tensor.matmul(pH[:, f * CH:(f + 1) * CH], g0[:, k, 128 * f:128 * f + 128],
                                                    xnT[:, s, k, :], start=k == 0, stop=k == 1)
                    last.then_inc(s_H, 1)

                def turn(u, s, lo):
                    pe.wait_ge(s_xn1, u + 1)
                    if lo >= 1:
                        pe.wait_ge(s_xT, u)
                    for k in range(2):
                        for t in range(2):
                            last = nc.tensor.transpose(pT[:, k * CH + t * R:k * CH + t * R + R],
                                                       xn1[:, s, t, 128 * k:128 * k + 128], ident[0:R, 0:R])
                    last.then_inc(s_T, 1)
                    for k in range(2):
                        for t in range(2):
                            last = nc.tensor.matmul(pSum[:, k:k + 1], xn1[:, s, t, 128 * k:128 * k + 128], ones[0:R, 0:1],
                                                    start=False, stop=False, skip_group_check=True)
                    last.then_inc(s_sum, 1)

                def step(u, s, lo, hi):
                    if lo == 0:
                        front(0, 0, 0)
                    if lo >= 2:
                        pe.wait_ge(s_x1, u - 1)
                    nc.tensor.matmul(pO[:, s, :], ones[0:1, 0:R], crow[:, 0:2, :].rearrange("o t c -> o (t c)"), start=True,
                                     stop=False, skip_group_check=True)
                    pe.wait_ge(s_g, u + 1)
                    for t in range(2):
                        for f in range(2):
                            last = nc.tensor.matmul(pO[:, s, t * C:(t + 1) * C], gT[:, f, t * R:t * R + R], w2[:, f, :],
                                                    start=False, stop=t == 1 and f == 1, skip_group_check=True)
                    last.then_inc(s_O, 1)
                    if hi <= CHUNKS - 2:
                        front(u + 1, 1 - s, lo + 1)
                    if lo >= 1:
                        turn(u - 1, 1 - s, lo - 1)
                    if lo == CHUNKS - 1:
                        turn(u, s, lo)
                nc.tensor.matmul(pSum[:, 0:2], env["zeros"][0:1, 0:128], env["zeros"][0:1, 0:2], start=True, stop=False,
                                 skip_group_check=True)
                sweep(pe, CHUNKS, step)
                pe.drain()

        with nc.Block() as block:
            @block.vector
            def _(v):
                nc.vector.tensor_copy(env["x1sum"][:, :], pSum[:, 0:2])
                v.drain()


def ffn0(env):
    nc, a, sem, ident, ones, stats = (env[k] for k in ("nc", "a", "sem", "ident", "ones", "stats"))
    cv = env["chunk_view"]
    x1_v, x2_v = cv(env["x_d"][0]), cv(env["x_d"][1])
    NF = 2 * F0 // 128
    with ExitStack() as ctx:
        sb = lambda n, s, d=F32: ctx.enter_context(nc.sbuf_tensor("m_" + n, s, d))
        pb = lambda n, s: ctx.enter_context(nc.psum_tensor("m_" + n, s, F32))
        w1 = sb("w1", [128, 2, 2, F0])
        w2 = sb("w2", [128, NF, C])
        b1 = sb("b1", [128, NF])
        b2 = sb("b2", [R, 3, C])
        gam = sb("gam", [R, 2, C])
        wr = sb("wr", [128, 2, E8])
        br = sb("br", [1, E8])
        lg = sb("lg", [1, 8, E8])
        sm = sb("sm", [1, 8])
        ei = sb("ei", [1, 8], U32)
        wB = sb("wB", [128, 2])
        xnT = sb("xnT", [128, 4, 2, CH])
        x1 = sb("x1", [R, 4, 2, C])
        hT = sb("hT", [128, 2, NF, CH])
        ya = sb("ya", [R, 2, C])
        yb = sb("yb", [R, 2, C])
        xnb = sb("xnb", [R, 2, C])
        x2 = sb("x2", [R, 2, 2, C])
        xn2 = sb("xn2", [R, 2, 2, C])
        sc = sb("sc", [R, 2, 2])
        bn, mv, ve, rn, mhalf = (sb("bn", [R, 2, 6]), sb("mv", [R, 2, 2]), sb("ve", [R, 2]), sb("rn", [R, 2, 2]),
                                 sb("mhalf", [R, 2]))
        xT = sb("xT", [128, 2, 2, CH])
        pH, pO, pT = pb("pH", [128, NF // 2, 512]), pb("pO", [R, 512]), pb("pT", [128, 512])
        s_w, s_l, s_act, s_l2, s_e, s_wb = (sem("m_" + n) for n in ("weights", "logits", "exp", "l2", "experts", "wB"))
        s_ld = [sem(f"m_load{i}") for i in range(4)]
        s_st = [sem("m_store0"), sem("m_store1")]
        s_sx = [sem("m_storeT0"), sem("m_storeT1")]
        s_H, s_g, s_O, s_Or, s_x2, s_var, s_rstd, s_xn2, s_T, s_xT = (
            sem("m_" + n) for n in ("H", "gelu", "O", "Oread", "x2", "var", "rstd", "xn2", "T", "xT"))

        with nc.Block() as block:
            @block.sync
            def _(sp):
                sp.dma_start(wr[:, :, :], a["L0_ffn_Wr"].rearrange("(k p) n -> p k n", p=128)).then_inc(s_w, 16)
                sp.dma_start(br[:, :], row_bc(a["L0_ffn_br"], 1)).then_inc(s_w, 16)
                sp.dma_start(gam[:, 0, :], row_bc(a["L0_ffn_gamma"], R)).then_inc(s_w, 16)
                sp.dma_start(gam[:, 1, :], row_bc(a["L0_ffn_beta"], R)).then_inc(s_w, 16)
                sp.wait_ge(s_w, 64)
                sp.wait_ge(s_e, 1)
                for j in range(2):
                    e = sp.value_load(ei[0:1, j:j + 1], min_val=0, max_val=E8 - 1)
                    ix = bass.ds(e, 1)
                    sp.dma_start(w1[:, j, :, :], a["L0_ffn_W1"][ix].rearrange("e (k p) f -> p (e k) f", p=128))\
                      .then_inc(s_w, 16)
                    sp.dma_start(w2[:, j * NF // 2:(j + 1) * NF // 2, :],
                                 a["L0_ffn_W2"][ix].rearrange("e (f p) n -> p (e f) n", p=128)).then_inc(s_w, 16)
                    sp.dma_start(b1[:, j * NF // 2:(j + 1) * NF // 2],
                                 a["L0_ffn_b1"][ix].rearrange("e (f p) -> p (e f)", p=128)).then_inc(s_w, 16)
                    sp.dma_start(b2[:, j, :], a["L0_ffn_b2"][ix].broadcast_to([R, C])).then_inc(s_w, 16)
                sp.wait_ge(s_w, 64 + 128)

            @block.gpsimd
            def _(pool):
                nc.gpsimd.memset(mhalf[:, :], -0.5)
                pool.drain()

            @block.tensor
            def _(pe):
                pe.wait_ge(s_w, 64)
                for k in range(2):
                    last = nc.tensor.matmul(pO[0:1, 0:E8], env["x1sum"][:, k:k + 1], wr[:, k, :], start=k == 0, stop=k == 1)
                last.then_inc(s_l, 1)
                pe.wait_ge(s_wb, 1)
                nc.tensor.matmul(pT[:, 0:2], ones[0:1, :], sm[0:1, 6:8], start=True, stop=True).then_inc(s_l, 1)

            @block.scalar
            def _(act):
                for n, (i, w) in enumerate(((1, E8), (3, E8), (6, 2))):
                    act.wait_ge(s_l2, n + 1)
                    nc.scalar.activation(lg[:, i, 0:w], lg[:, i, 0:w], ACT.Exp).then_inc(s_act, 1)

            @block.vector
            def _(v):
                ts, tt = nc.vector.tensor_scalar, nc.vector.tensor_tensor
                v.wait_ge(s_w, 64)
                v.wait_ge(s_l, 1)
                nc.vector.scalar_tensor_tensor(out=lg[:, 0, :], in0=pO[0:1, 0:E8], scalar=1.0 / N, in1=br[:, :],
                                               op0=ALU.mult, op1=ALU.add)
                v.drain()

                def softmax(src, dst, n, w, m):
                    nc.vector.tensor_reduce(sm[:, m:m + 1], lg[:, src, 0:w], AX.X, ALU.max)
                    v.drain()
                    ts(lg[:, dst, 0:w], lg[:, src, 0:w], sm[:, m:m + 1], None, ALU.subtract).then_inc(s_l2, 1)
                    v.wait_ge(s_act, n + 1)
                    nc.vector.tensor_reduce(sm[:, m + 1:m + 2], lg[:, dst, 0:w], AX.X, ALU.add)
                    v.drain()
                    nc.vector.reciprocal(sm[:, m + 1:m + 2], sm[:, m + 1:m + 2])
                    v.drain()

                softmax(0, 1, 0, E8, 0)
                ts(lg[:, 1, :], lg[:, 1, :], sm[:, 1:2], None, ALU.mult)
                v.drain()
                ts(lg[:, 2, :], lg[:, 1, :], float(N) / CAPACITY, None, ALU.mult)
                v.drain()
                nc.vector.reciprocal(lg[:, 2, :], lg[:, 2, :])
                v.drain()
                ts(lg[:, 2, :], lg[:, 2, :], 1.0, None, ALU.min)
                v.drain()
                tt(out=lg[:, 4, :], in0=lg[:, 1, :], in1=lg[:, 2, :], op=ALU.mult)
                v.drain()
                softmax(4, 3, 1, E8, 2)
                ts(lg[:, 3, :], lg[:, 3, :], sm[:, 3:4], None, ALU.mult)
                v.drain()
                nc.vector.max(lg[:, 5, :], lg[:, 3, :])
                v.drain()
                nc.vector.max_index(ei[:, :], lg[:, 5, :], lg[:, 3, :])
                v.drain().then_inc(s_e, 1)
                softmax(5, 6, 2, 2, 4)
                ts(sm[:, 6:8], lg[:, 6, 0:2], sm[:, 5:6], None, ALU.mult)
                v.drain().then_inc(s_wb, 1)
                v.wait_ge(s_l, 2)
                nc.vector.tensor_copy(wB[:, :], pT[:, 0:2])
                v.drain()
                v.wait_ge(s_w, 64 + 128)
                for j in range(2):
                    w = w2[:, j * NF // 2:(j + 1) * NF // 2, :]
                    ts(w, w, wB[:, j:j + 1], None, ALU.mult)
                ts(b2[:, 2, :], b2[:, 0, :], wB[0:R, 0:1], None, ALU.mult)
                v.drain()
                nc.vector.scalar_tensor_tensor(out=b2[:, 0, :], in0=b2[:, 1, :], scalar=wB[0:R, 1:2], in1=b2[:, 2, :],
                                               op0=ALU.mult, op1=ALU.add)
                v.drain()

        with nc.Block() as block:
            @block.sync
            def _(sp):
                def load(u, s):
                    rows_dma(sp, x1[:, s, :, :], x1_v[u], s_ld[s])
                    sp.dma_start(xnT[:, s, :, :], env["xnT_d"][1][:, :, bass.ds(u * CH, CH)]).then_inc(s_ld[s], 16)

                def store(u, s):
                    sp.wait_ge(s_x2, u + 1)
                    rows_dma(sp, x2_v[u], x2[:, s, :, :], s_st[s])
                    sp.wait_ge(s_xT, u + 1)
                    sp.dma_start(env["xnT_d"][2][:, :, bass.ds(u * CH, CH)], xT[:, s, :, :]).then_inc(s_sx[s], 16)

                def step(u, s, lo, hi):
                    if lo >= 4:
                        sp.wait_ge(s_x2, u - 3)
                    load(u, s)
                    if lo >= 3:
                        store(u - 3, (s + 1) % 2)
                sweep(sp, CHUNKS, step, 4)
                for u in range(CHUNKS - 3, CHUNKS):
                    store(u, u % 2)
                for i in range(2):
                    n = (CHUNKS + 1 - i) // 2
                    sp.wait_ge(s_st[i], 32 * n)
                    sp.wait_ge(s_sx[i], 16 * n)

            @block.scalar
            def _(act):
                def turn(u, s, lo):
                    if lo >= 2:
                        hold(act, s_sx[s], (u // 2) * 16)
                    hold(act, s_T, u + 1)
                    nc.scalar.copy(xT[:, s, :, :], pT[:, 0:2 * CH].rearrange("p (k n) -> p k n", k=2)).then_inc(s_xT, 1)

                def step(u, s, lo, hi):
                    if lo >= 2:
                        hold(act, s_O, u - 1)
                    for f in range(NF):
                        if f % 2 == 0:
                            hold(act, s_H, NF // 2 * u + f // 2 + 1)
                        x = nc.scalar.activation(hT[:, s % 2, f, :], pH[:, f // 2, (f % 2) * CH:(f % 2 + 1) * CH], ACT.Gelu,
                                                 bias=b1[:, f:f + 1])
                        if f % 2:
                            x.then_inc(s_g, 1)
                    if lo >= 2:
                        turn(u - 2, s % 2, lo - 2)
                    if lo == CHUNKS - 1:
                        turn(u - 1, (s + 1) % 2, lo)
                        turn(u, s % 2, lo)
                sweep(act, CHUNKS, step, 4)

            @block.gpsimd
            def _(pool):
                def step(u, s, lo, hi):
                    for i in range(2):
                        hold(pool, s_var, 2 * u + i + 1)
                        nc.gpsimd.tensor_tensor(out=rn[:, :, 0], in0=ve[:, :], in1=mhalf[:, :], op=ALU.pow)\
                          .then_inc(s_rstd, 1)
                sweep(pool, CHUNKS, step)

            @block.vector
            def _(v):
                def step(u, q, lo, hi):
                    s = q % 2
                    v.wait_ge(s_ld[q], (u // 4 + 1) * 48)
                    nc.vector.tensor_copy(sc[:, :, :], stats[:, bass.ds(u * 2, 2), :])
                    v.drain()
                    for t in range(2):
                        nc.vector.tensor_scalar(xnb[:, t, :], x1[:, q, t, :], sc[:, t, 0:1], sc[:, t, 1:2],
                                                ALU.mult, ALU.add)
                    v.drain()
                    nc.vector.tensor_tensor(out=ya[:, :, :], in0=xnb[:, :, :],
                                            in1=b2[:, 0, :].unsqueeze(1).broadcast_to([R, 2, C]), op=ALU.add)
                    v.drain()
                    v.wait_ge(s_O, u + 1)
                    nc.vector.tensor_tensor(out=yb[:, :, :], in0=ya[:, :, :],
                                            in1=pO[:, :].rearrange("p (t c) -> p t c", t=2), op=ALU.add)
                    v.drain().then_inc(s_Or, 1)
                    ln_stats(nc, v, yb, bn, mv, ve, s_var)
                    v.wait_ge(s_rstd, 2 * u + 1)
                    ln_apply(nc, v, ya, yb, mv, rn)
                    v.drain()
                    nc.vector.tensor_tensor(out=yb[:, :, :], in0=ya[:, :, :],
                                            in1=gam[:, 0, :].unsqueeze(1).broadcast_to([R, 2, C]), op=ALU.mult)
                    nc.vector.tensor_tensor(out=xnb[:, :, :], in0=x1[:, q, :, :],
                                            in1=gam[:, 1, :].unsqueeze(1).broadcast_to([R, 2, C]), op=ALU.add)
                    v.drain()
                    if lo >= 2:
                        v.wait_ge(s_st[s], (u // 2) * 32)
                    nc.vector.tensor_tensor(out=x2[:, s, :, :], in0=xnb[:, :, :], in1=yb[:, :, :], op=ALU.add)
                    v.drain().then_inc(s_x2, 1)
                    ln_stats(nc, v, x2[:, s, :, :], bn, mv, ve, s_var)
                    v.wait_ge(s_rstd, 2 * u + 2)
                    if lo >= 2:
                        v.wait_ge(s_T, u - 1)
                    ln_apply(nc, v, xn2[:, s, :, :], x2[:, s, :, :], mv, rn).then_inc(s_xn2, 1)
                    nc.vector.tensor_copy(stats[:, bass.ds(u * 2, 2), :], rn[:, :, :])
                    v.drain()
                sweep(v, CHUNKS, step, 4)

            @block.tensor
            def _(pe):
                def hidden(u, s, lo):
                    pe.wait_ge(s_ld[s], (u // 4 + 1) * 48)
                    for f in range(NF):
                        if f % 2 == 0 and lo >= 1:
                            pe.wait_ge(s_g, NF // 2 * (u - 1) + f // 2 + 1)
                        j, c = f // (NF // 2), f % (NF // 2)
                        for k in range(2):
                            last = nc.tensor.matmul(pH[:, f // 2, (f % 2) * CH:(f % 2 + 1) * CH],
                                                    w1[:, j, k, 128 * c:128 * c + 128], xnT[:, s, k, :],
                                                    start=k == 0, stop=k == 1)
                        if f % 2:
                            last.then_inc(s_H, 1)

                def output(u, s, lo):
                    if lo >= 1:
                        pe.wait_ge(s_Or, u)
                    for t in range(2):
                        for f in range(NF):
                            if t == 0 and f % 2 == 0:
                                pe.wait_ge(s_g, NF // 2 * u + f // 2 + 1)
                            last = nc.tensor.matmul(pO[:, t * C:(t + 1) * C], hT[:, s % 2, f, t * R:t * R + R], w2[:, f, :],
                                                    start=f == 0, stop=f == NF - 1)
                    last.then_inc(s_O, 1)

                def turn(u, s, lo):
                    pe.wait_ge(s_xn2, u + 1)
                    if lo >= 1:
                        pe.wait_ge(s_xT, u)
                    for k in range(2):
                        for t in range(2):
                            last = nc.tensor.transpose(pT[:, k * CH + t * R:k * CH + t * R + R],
                                                       xn2[:, s, t, 128 * k:128 * k + 128], ident[0:R, 0:R])
                    last.then_inc(s_T, 1)

                def step(u, s, lo, hi):
                    if lo == 0:
                        hidden(0, 0, 0)
                    if hi <= CHUNKS - 2:
                        hidden(u + 1, (s + 1) % 4, lo + 1)
                    output(u, s, lo)
                    if lo >= 1:
                        turn(u - 1, (s + 1) % 2, lo - 1)
                    if lo == CHUNKS - 1:
                        turn(u, s % 2, lo)
                sweep(pe, CHUNKS, step, 4)


def front1(env):
    nc, a, sem, ident, ones = (env[k] for k in ("nc", "a", "sem", "ident", "ones"))
    cv = env["chunk_view"]
    tab_v = cv(env["tab1"])
    g1, attr = env["g1"], env["attr"]
    HID = 512
    with ExitStack() as ctx:
        sb = lambda n, s, d=F32: ctx.enter_context(nc.sbuf_tensor("f1_" + n, s, d))
        wq = sb("wq", [128, 4, C])
        wk = sb("wk", [128, 8, C])
        wo = sb("wo", [128, 2, HID])
        wkv = sb("wkv", [128, 2, 2 * HID])
        woT = sb("woT", [128, 4, C])
        lin = sb("lin", [128, 2, C])
        centre = sb("centre", [128, 128])
        xnT = sb("xnT", [128, 2, 2, CH])
        trow = sb("trow", [R, 2, 2, C])
        sq = sb("sq", [R, 2, HID])
        ss = sb("ss", [R, 2, 8])
        sd = sb("sd", [R, 2, 8])
        ri = sb("ri", [R, 2, 8])
        kvn = sb("kvn", [R, 2, 2 * HID])
        epst = sb("epst", [128, 1])
        mask = sb("mask", [128, 128])
        dT = sb("dT", [128, 4, 128])
        m1 = sb("m1", [128, 4, C])
        pb = lambda n, s: ctx.enter_context(nc.psum_tensor("f1_" + n, s, F32))
        pA, pKV, pY, pS = pb("pA", [128, 2, 512]), pb("pKV", [128, 4, 512]), pb("pY", [R, 512]), pb("pS", [128, 512])
        s_w, s_kvw, s_c, s_t, s_tc, s_m = (sem("f1_" + n) for n in ("weights", "kvweights", "consts", "T", "Tc", "mask"))
        s_ld = [sem("f1_load0"), sem("f1_load1")]
        s_st = [sem("f1_store0"), sem("f1_store1")]
        s_kv, s_sq, s_ss, s_sd, s_kvn, s_acc, s_Y, s_row = (
            sem("f1_" + n) for n in ("kv", "sq", "ss", "sd", "kvn", "acc", "Y", "rows"))
        s_dT, s_M, s_m1, s_G = (sem("f1_" + n) for n in ("dT", "M", "m1", "G"))
        wqkv = a["L1_mix_Wqkv"].rearrange("(i p) k -> p i k", p=128)

        with nc.Block() as block:
            @block.gpsimd
            def _(pool):
                nc.gpsimd.memset(lin[:, :, :], 0.0).then_inc(s_c, 1)
                nc.gpsimd.memset(epst[:, :], EPS)
                nc.gpsimd.memset(mask[:, :], 0.0)
                pool.drain()
                for h in range(2):
                    nc.gpsimd.memset(mask[64 * h:64 * h + 64, 64 * h:64 * h + 64], 1.0)
                    pool.drain()
                pool.drain().then_inc(s_m, 1)
                pool.wait_ge(s_t, 1)
                nc.gpsimd.tensor_scalar(mask[:, :], mask[:, :], 1.0 / N, None, ALU.mult)
                pool.drain()

            @block.sync
            def _(sp):
                sp.dma_start(wk[:, :, :], wqkv[:, 4:12, :]).then_inc(s_kvw, 16)
                sp.dma_start(wo[:, :, :], a["L1_mix_Wout"].rearrange("(k p) f -> p k f", p=128)).then_inc(s_kvw, 16)
                sp.dma_start(wq[:, :, :], wqkv[:, 0:4, :]).then_inc(s_w, 16)
                sp.dma_start(attr[:, :], a["node_vec1"].rearrange("(t p) o -> p (t o)", p=R)).then_inc(s_w, 16)
                sp.wait_ge(s_c, 1)
                sp.dma_start(lin[0:64, 0, 0:64], a["L1_gnn_lin1_w0"]).then_inc(s_w, 16)
                for k, p, c, u, n in vector_rows():
                    sp.dma_start(lin[p:p + 3 * (n - 1) + 1:3, k, 64 + 64 * c:128 + 64 * c],
                                 a["L1_gnn_lin1_w1"][u:u + n, :]).then_inc(s_w, 16)
                sp.wait_ge(s_w, 16 * (3 + len(vector_rows())))

            @block.tensor
            def _(pe):
                pe.wait_ge(s_kvw, 32)
                pe.wait_ge(s_m, 2)
                for n in range(6):
                    if n >= 2:
                        pe.wait_ge(s_tc, n - 1)
                    for i in range(4):
                        to = pA[:, n % 2, 128 * i:128 * i + 128]
                        if n < 4:
                            last = nc.tensor.matmul(to, wk[:, 4 * (n % 2) + i, 128 * (n // 2):128 * (n // 2) + 128],
                                                    centre[:, :], start=True, stop=True)
                        else:
                            last = nc.tensor.transpose(to, wo[:, i % 2, 128 * (2 * (n - 4) + i // 2):
                                                              128 * (2 * (n - 4) + i // 2) + 128], ident[:, :])
                    last.then_inc(s_t, 1)

            @block.vector
            def _(v):
                v.wait_ge(s_m, 1)
                nc.vector.scalar_tensor_tensor(out=centre[:, :], in0=mask[:, :], scalar=-1.0 / 64, in1=ident[:, :],
                                               op0=ALU.mult, op1=ALU.add).then_inc(s_m, 1)
                for n in range(6):
                    v.wait_ge(s_t, n + 1)
                    dst = (wkv[:, n // 2, HID * (n % 2):HID * (n % 2) + HID] if n < 4 else
                           woT[:, 2 * (n - 4):2 * (n - 4) + 2, :].rearrange("p k c -> p (k c)"))
                    nc.vector.tensor_copy(dst, pA[:, n % 2, :]).then_inc(s_tc, 1)
                v.wait_ge(s_w, 16 * (3 + len(vector_rows())))
                nc.vector.tensor_scalar(lin[:, :, :], lin[:, :, :], 0.125, None, ALU.mult)
                v.drain()

        with nc.Block() as block:
            @block.sync
            def _(sp):
                def store(u, s):
                    sp.wait_ge(s_row, u + 1)
                    rows_dma(sp, tab_v[u], trow[:, s, :, :], s_st[s])

                def step(u, s, lo, hi):
                    if lo >= 2:
                        sp.wait_ge(s_kv, (u - 1) * 4)
                    sp.dma_start(xnT[:, s, :, :], env["xnT_d"][2][:, :, bass.ds(u * CH, CH)]).then_inc(s_ld[s], 16)
                    if lo >= 1:
                        store(u - 1, 1 - s)
                    if lo == CHUNKS - 1:
                        store(u, s)
                sweep(sp, CHUNKS, step)
                for i in range(2):
                    sp.wait_ge(s_st[i], 32 * ((CHUNKS + 1 - i) // 2))

            @block.tensor
            def _(pe):
                def sums(u, t):
                    i = u * 2 + t
                    pe.wait_ge(s_kvn, 2 * i + 2)
                    for g in range(4):
                        last = nc.tensor.matmul(pS[:, 128 * g:128 * g + 128], kvn[:, t, HID + 128 * g:HID + 128 * g + 128],
                                                kvn[:, t, 128 * g:128 * g + 128], start=False, stop=False,
                                                skip_group_check=True)
                    last.then_inc(s_acc, 1)

                def step(u, s, lo, hi):
                    pe.wait_ge(s_ld[s], (u // 2 + 1) * 16)
                    for t in range(2):
                        for b in range(2):
                            hh = u * 4 + 2 * t + b
                            if lo >= 1:
                                pe.wait_ge(s_kvn, hh - 3)
                            for k in range(2):
                                last = nc.tensor.matmul(pKV[0:R, 2 * t + b, :], xnT[:, s, k, t * R:t * R + R],
                                                        wkv[:, k, HID * b:HID * b + HID], start=k == 0, stop=k == 1)
                            last.then_inc(s_kv, 1)
                        if t == 0:
                            if lo >= 1:
                                pe.wait_ge(s_row, u)
                            for q in range(2):
                                for k in range(2):
                                    last = nc.tensor.matmul(pY[:, q * C:q * C + C], xnT[:, s, k, q * R:q * R + R],
                                                            lin[:, k, :], start=k == 0, stop=k == 1)
                            last.then_inc(s_Y, 1)
                            if lo >= 1:
                                sums(u - 1, 0)
                        elif lo >= 1:
                            sums(u - 1, 1)

                nc.tensor.matmul(pS[:, :], env["zeros"][0:1, 0:128], env["zeros"][0:1, :], start=True, stop=False,
                                 skip_group_check=True)
                sweep(pe, CHUNKS, step)
                sums(CHUNKS - 1, 0)
                sums(CHUNKS - 1, 1)
                pe.drain()

            @block.scalar
            def _(act):
                def step(u, s, lo, hi):
                    for h in range(4):
                        hh = u * 4 + h
                        hold(act, s_kv, hh + 1)
                        if lo >= 1 or h >= 2:
                            hold(act, s_ss, hh - 1)
                        nc.scalar.activation(sq[:, h % 2, :], pKV[0:R, h, :], ACT.Square).then_inc(s_sq, 1)
                        hold(act, s_ss, hh + 1)
                        nc.scalar.activation(sd[:, h % 2, :], ss[:, h % 2, :], ACT.Sqrt, bias=epst[0:R, :],
                                             scale=1.0 / 64).then_inc(s_sd, 1)
                    if lo >= 2:
                        hold(act, s_st[s], (u // 2) * 32)
                    hold(act, s_Y, u + 1)
                    for t in range(2):
                        last = nc.scalar.activation(trow[:, s, t, :], pY[:, t * C:t * C + C], ACT.Copy,
                                                    scale=attr[:, bass.ds(u * 2 + t, 1)])
                    last.then_inc(s_row, 1)
                sweep(act, CHUNKS, step)

            @block.vector
            def _(v):
                def normalize(u, h, lo):
                    t, b = h // 2, h % 2
                    v.wait_ge(s_sd, u * 4 + h + 1)
                    nc.vector.reciprocal(ri[:, b, :], sd[:, b, :])
                    v.drain()
                    if lo >= 1:
                        v.wait_ge(s_acc, u * 2 + t - 1)
                    nc.vector.tensor_tensor(
                        out=kvn[:, t, HID * b:HID * b + HID].rearrange("p (h d) -> p h d", d=64),
                        in0=pKV[0:R, h, :].rearrange("p (h d) -> p h d", d=64),
                        in1=ri[:, b, :].unsqueeze(2).broadcast_to([R, 8, 64]), op=ALU.mult).then_inc(s_kvn, 1)

                def step(u, s, lo, hi):
                    for h in range(4):
                        hh = u * 4 + h
                        v.wait_ge(s_sq, hh + 1)
                        nc.vector.tensor_reduce(ss[:, h % 2, :], sq[:, h % 2, :].rearrange("p (h d) -> p h d", d=64), AX.X,
                                                ALU.add).then_inc(s_ss, 1)
                        if h >= 1:
                            normalize(u, h - 1, lo)
                        elif lo >= 1:
                            normalize(u - 1, 3, lo - 1)
                    if lo == CHUNKS - 1:
                        normalize(u, 3, lo)
                sweep(v, CHUNKS, step)

        with nc.Block() as block:
            @block.vector
            def _(v):
                for g in range(4):
                    nc.vector.tensor_tensor(out=dT[:, g, :], in0=pS[:, 128 * g:128 * g + 128], in1=mask[:, :], op=ALU.mult)
                v.drain().then_inc(s_dT, 1)
                for g in range(4):
                    v.wait_ge(s_M, g + 1)
                    nc.vector.tensor_copy(m1[:, g, :], pA[:, g % 2, 0:C]).then_inc(s_m1, 1)
                v.wait_ge(s_G, 1)
                nc.vector.tensor_copy(g1[:, :, :], pKV[:, 0:2, 0:C])
                v.drain()

            @block.tensor
            def _(pe):
                pe.wait_ge(s_dT, 1)
                for g in range(4):
                    if g >= 2:
                        pe.wait_ge(s_m1, g - 1)
                    nc.tensor.matmul(pA[:, g % 2, 0:C], dT[:, g, :], woT[:, g, :], start=True, stop=True).then_inc(s_M, 1)
                pe.wait_ge(s_m1, 4)
                for k in range(2):
                    for g in range(4):
                        last = nc.tensor.matmul(pKV[:, k, 0:C], wq[:, g, 128 * k:128 * k + 128], m1[:, g, :],
                                                start=g == 0, stop=g == 3)
                last.then_inc(s_G, 1)


def vector_rows():
    runs = []
    for c in range(3):
        for k in range(2):
            us = [u for u in range(64) if (64 + 3 * u + c) // 128 == k]
            runs.append((k, (64 + 3 * us[0] + c) % 128, c, us[0], len(us)))
    return runs


def edge_attrs(env, ea):
    nc, a, sem, ident = (env[k] for k in ("nc", "a", "sem", "ident"))
    with ExitStack() as ctx:
        st = ctx.enter_context(nc.sbuf_tensor("ea_st", [QB, NB, R * 4], F32))
        sc = ctx.enter_context(nc.sbuf_tensor("ea_sc", [QB, 4, NB, R], F32))
        pt = ctx.enter_context(nc.psum_tensor("ea_pt", [R, 8, 512], F32))
        s_ld, s_c, s_t, s_ev = sem("ea_load"), sem("ea_split"), sem("ea_T"), sem("ea_copied")
        with nc.Block() as block:
            @block.sync
            def _(sp):
                sp.dma_start(st[:, :, :], a["edge_attr_4"].rearrange("(b q e) c -> q b (e c)", q=QB, e=R)).then_inc(s_ld, 16)
                sp.wait_ge(s_ld, 16)

            @block.vector
            def _(v):
                v.wait_ge(s_ld, 16)
                for c in range(4):
                    nc.vector.tensor_copy(sc[:, c, :, :], st[:, :, :].rearrange("q b (e c) -> q b e c", c=4)[:, :, :, c])\
                      .then_inc(s_c, 1)
                for c in range(4):
                    for b in range(NB):
                        n = c * NB + b
                        v.wait_ge(s_t, n + 1)
                        nc.vector.tensor_copy(ea[:, QB * b:QB * (b + 1), c], pt[:, n % 8, 0:QB]).then_inc(s_ev, 1)
                v.drain()

            @block.tensor
            def _(pe):
                for c in range(4):
                    pe.wait_ge(s_c, c + 1)
                    for b in range(NB):
                        n = c * NB + b
                        if n >= 8:
                            pe.wait_ge(s_ev, n - 7)
                        nc.tensor.transpose(pt[:, n % 8, 0:QB], sc[:, c, b, :], ident[0:QB, 0:QB]).then_inc(s_t, 1)


def edges1(env, z, ea):
    nc, a, sem, ident = (env[k] for k in ("nc", "a", "sem", "ident"))
    srcI, baseI = env["srcI"], env["baseI"]
    PAIRS = (GT + 1) // 2
    with ExitStack() as ctx:
        sb = lambda n, s, d=F32: ctx.enter_context(nc.sbuf_tensor("e1_" + n, s, d))
        pb = lambda n, s: ctx.enter_context(nc.psum_tensor("e1_" + n, s, F32))
        ix = sb("ix", [R, SLOTS, GT], I32)
        rows = sb("rows", [R, 3, GT, C])
        es = sb("es", [R, SLOTS, GT, 8])
        esT = sb("esT", [8 * GT, 2, R])
        w1 = sb("w1", [8 * GT, PAIRS, 128])
        w2 = sb("w2", [128, 2, C])
        hT = sb("hT", [128, 2, PAIRS, R])
        ohu = sb("ohu", [R, GT, W])
        oh = sb("oh", [R, 2, GT, 4, W])
        msg = sb("msg", [R, 2, GT, 8, 64])
        us = sb("us", [128, 2, 512])
        pH = pb("pH", [128, 512])
        pT = pH[0:8 * GT, 128 * PAIRS:128 * PAIRS + R]
        pW, pU, pF = pb("pW", [R, 3, 512]), pb("pU", [128, 2, 512]), pb("pF", [128, 2, 512])
        s_wt, s_wz = sem("e1_weights"), sem("e1_zeroed")
        s_gat = env["s_rows"]
        s_es = [sem(f"e1_es{i}") for i in range(SLOTS)]
        s_ix, s_T, s_esT, s_F, s_h, s_W, s_msg, s_oh, s_acc, s_us, s_flip, s_add = (
            sem("e1_" + n) for n in ("ix", "T", "esT", "F", "silu", "W", "msg", "oh", "acc", "copied", "flip", "added"))
        SILU_NORM = 1.679
        blk = lambda s, j, i: msg[:, s, j, :, :].rearrange("p b c -> p (b c)")[:, 64 * i:64 * i + 64]

        with nc.Block() as block:
            @block.gpsimd
            def _(pool):
                nc.gpsimd.memset(w1[:, :, :], 0.0)
                nc.gpsimd.memset(w2[:, :, :], 0.0)
                for t in (env["b1_sc"], env["b1_lin2"]):
                    nc.gpsimd.memset(t[:, :, :], 0.0)
                pool.drain().then_inc(s_wz, 1)

            @block.sync
            def _(sp):
                sp.wait_ge(s_wz, 1)
                for j in range(GT):
                    sp.dma_start(w1[8 * j:8 * j + 8, j // 2, 64 * (j % 2):64 * (j % 2) + 64], a["L1_gnn_fc_w1"])\
                      .then_inc(s_wt, 16)
                for r in range(2):
                    for i, b in enumerate((0, 3, 2, 1)):
                        sp.dma_start(w2[64 * r:64 * r + 64, r, 64 * i:64 * i + 64],
                                     a["L1_gnn_fc_w2"][:, 64 * b:64 * b + 64]).then_inc(s_wt, 16)
                back1_loads(env, sp)
                sp.wait_ge(s_wt, 16 * (GT + 8))

        with nc.Block() as block:
            @block.vector
            def _(v):
                nc.vector.tensor_scalar(w2[:, :, :], w2[:, :, :], SILU_NORM / 8.0, None, ALU.mult)
                v.drain()
        es_v = a["edge_attr_8"].rearrange("(g j p) f -> g p j f", j=GT, p=R)

        def one_pass():
            with nc.Block() as block:
                @block.gpsimd
                def _(pool):
                    def step(g, s, lo, hi):
                        hold(pool, s_ix, g + 1)
                        for j in range(GT):
                            nc.gpsimd.indirect_dma_start(
                                out=rows[:, s % 3, j, :], out_offset=None, in_=env["tab1"],
                                in_offset=bass.IndirectOffsetOnAxis(ap=ix[:, s, j:j + 1], axis=0))\
                              .then_inc(s_gat[s], 16)
                    sweep(pool, GROUPS, step, SLOTS, AHEAD)

                @block.sync
                def _(sp):
                    def step(g, s, lo, hi):
                        if lo >= SLOTS:
                            sp.wait_ge(s_T, g - SLOTS + 1)
                        rows_dma(sp, es[:, s, :, :], es_v[g], s_es[s])
                    sweep(sp, GROUPS, step, SLOTS, AHEAD)

                @block.scalar
                def _(act):
                    def stage(g, s, lo):
                        if lo >= 3:
                            hold(act, s_msg, PAIRS * (g - 2))
                        nc.scalar.copy(ix[:, s, :], srcI[:, bass.ds(g * GT, GT)]).then_inc(s_ix, 1)

                    def front(g, s, lo):
                        if lo >= 2:
                            hold(act, s_F, g - 1)
                        hold(act, s_T, g + 1)
                        nc.scalar.copy(esT[:, s % 2, :], pT).then_inc(s_esT, 1)
                        if lo >= 2:
                            hold(act, s_W, PAIRS * (g - 1))
                        hold(act, s_F, g + 1)
                        nc.scalar.activation(hT[:, s % 2, :, :],
                                             pH[:, 0:128 * PAIRS].rearrange("p (i e) -> p i e", e=128)[:, :, 0:R],
                                             ACT.Silu, scale=8.0 ** -0.5).then_inc(s_h, 1)

                    def copied(g, s, lo):
                        if lo >= 2:
                            hold(act, s_flip, g - 1)
                        hold(act, s_acc, g + 1)
                        nc.scalar.copy(us[:, s % 2, :], pU[:, s % 2, :]).then_inc(s_us, 1)

                    def step(g, s, lo, hi):
                        if lo == 0:
                            for i in range(3):
                                stage(i, i, i)
                            front(0, 0, 0)
                        if lo >= 1 and hi <= GROUPS - 3:
                            stage(g + 2, (s + 2) % SLOTS, lo + 2)
                        if hi <= GROUPS - 2:
                            front(g + 1, (s + 1) % SLOTS, lo + 1)
                        if lo >= 1:
                            copied(g - 1, s + 1, lo - 1)
                        if lo == GROUPS - 1:
                            copied(g, s, lo)
                    sweep(act, GROUPS, step, SLOTS, AHEAD)

                @block.vector
                def _(v):
                    def add(g, s):
                        base = v.value_load(baseI[0:1, bass.ds(g, 1)], min_val=0, max_val=N)
                        v.wait_ge(s_flip, g + 1)
                        w = z[:, :, bass.ds(base, W)]
                        f = pF[:, s % 2, :].rearrange("p (k h n) -> p k h n", k=4, h=2)
                        nc.vector.tensor_tensor(out=w, in0=w, in1=f[:, :, 0, :], op=ALU.add)
                        v.drain()
                        nc.vector.tensor_tensor(out=w, in0=w, in1=f[:, :, 1, :], op=ALU.add).then_inc(s_add, 1)

                    def step(g, s, lo, hi):
                        if lo >= 1:
                            v.wait_ge(s_oh, g)
                        one_hots(nc, env, ohu[:, :, :], g)
                        v.drain()
                        if lo >= 2:
                            v.wait_ge(s_acc, g - 1)
                        nc.vector.tensor_tensor(
                            out=oh[:, s % 2, :, :, :], in0=ohu[:, :, :].unsqueeze(2).broadcast_to([R, GT, 4, W]),
                            in1=ea[:, bass.ds(g * GT, GT), :].unsqueeze(3).broadcast_to([R, GT, 4, W]), op=ALU.mult)\
                          .then_inc(s_oh, 1)
                        v.wait_ge(s_gat[s], (g // SLOTS + 1) * 16 * GT)
                        for j in range(GT):
                            if j % 2 == 0:
                                v.wait_ge(s_W, g * PAIRS + j // 2 + 1)
                            wj = pW[:, j // 2, 256 * (j % 2):256 * (j % 2) + 256]
                            wa = wj.rearrange("p (b q c) -> p b q c", b=2, q=2)
                            m = msg[:, s % 2, j, :, :].rearrange("p (b q) c -> p b q c", b=2)
                            nc.vector.tensor_tensor(out=m[:, :, 0, :], in0=wa[:, :, 0, :],
                                                    in1=rows[:, s % 3, j, 0:64].unsqueeze(1).broadcast_to([R, 2, 64]),
                                                    op=ALU.mult)
                            last = nc.vector.tensor_tensor(
                                out=m[:, :, 1:4, :], in0=wa[:, :, 1:2, :].broadcast_to([R, 2, 3, 64]),
                                in1=rows[:, s % 3, j, 64:256].rearrange("p (q c) -> p q c", q=3).unsqueeze(1)
                                .broadcast_to([R, 2, 3, 64]), op=ALU.mult)
                            if j % 2 or j == GT - 1:
                                last.then_inc(s_msg, 1)
                        if lo >= 3:
                            add(g - 3, s + 1)
                        if lo == GROUPS - 1:
                            for i in (2, 1, 0):
                                v.drain()
                                add(g - i, s + i)
                            v.drain()
                    sweep(v, GROUPS, step, SLOTS, AHEAD)

                @block.tensor
                def _(pe):
                    def front(g, s, lo):
                        if lo >= 1:
                            pe.wait_ge(s_h, g)
                        hold(pe, s_es[s], (g // SLOTS + 1) * 32)
                        nc.tensor.transpose(pT, es[:, s, :, :].rearrange("p j f -> p (j f)"), ident[0:R, 0:R])\
                          .then_inc(s_T, 1)

                    def first(g, s):
                        hold(pe, s_esT, g + 1)
                        for i in range(PAIRS):
                            last = nc.tensor.matmul(pH[:, 128 * i:128 * i + R], w1[:, i, :], esT[:, s % 2, :],
                                                    start=True, stop=True)
                        last.then_inc(s_F, 1)

                    def second(g, s, lo):
                        pe.wait_ge(s_h, g + 1)
                        for j in range(GT):
                            if lo >= 1 and j % 2 == 0:
                                pe.wait_ge(s_msg, (g - 1) * PAIRS + j // 2 + 1)
                            last = nc.tensor.matmul(pW[:, j // 2, 256 * (j % 2):256 * (j % 2) + 256],
                                                    hT[:, s % 2, j // 2, :], w2[:, j % 2, :], start=True, stop=True)
                            if j % 2 or j == GT - 1:
                                last.then_inc(s_W, 1)

                    def sums(g, s, lo):
                        pe.wait_ge(s_msg, (g + 1) * PAIRS)
                        pe.wait_ge(s_oh, g + 1)
                        if lo >= 2:
                            hold(pe, s_us, g - 1)
                        for pair in range(0, GT, 2):
                            for c in range(4):
                                for j in range(pair, min(pair + 2, GT)):
                                    h = W * (j % 2 if j < GT - 1 else c in (1, 2))
                                    m = msg[:, s % 2, j, :, :]
                                    u8 = pU[h:h + W, s % 2, :].rearrange("p (b c) -> p b c", b=8)
                                    last = nc.tensor.matmul(
                                        u8[:, 0:4, :] if c == 0 else u8[:, 3 + c:8:4 - c, :], oh[:, s % 2, j, c, :],
                                        m[:, 0:4, :] if c == 0 else m[:, 4:5 + c:c, :],
                                        start=pair + c == 0, stop=j == GT - 1 and c >= 2, skip_group_check=True)
                        last.then_inc(s_acc, 1)

                    def flip(g, s, lo):
                        pe.wait_ge(s_us, g + 1)
                        if lo >= 2:
                            pe.wait_ge(s_add, g - 1)
                        for k in range(4):
                            last = nc.tensor.transpose(pF[:, s % 2, 128 * k:128 * k + 128],
                                                       us[:, s % 2, 128 * k:128 * k + 128], ident[:, :])
                        last.then_inc(s_flip, 1)

                    def step(g, s, lo, hi):
                        if lo == 0:
                            front(0, 0, 0)
                            first(0, 0)
                        if hi <= GROUPS - 2:
                            front(g + 1, (s + 1) % SLOTS, lo + 1)
                        second(g, s, lo)
                        if hi <= GROUPS - 2:
                            first(g + 1, s + 1)
                        if lo >= 1:
                            sums(g - 1, s + 1, lo - 1)
                        if lo >= 2:
                            flip(g - 2, s, lo - 2)
                        if lo == GROUPS - 1:
                            flip(g - 1, s + 1, lo)
                            sums(g, s, lo)
                            flip(g, s, lo)
                    sweep(pe, GROUPS, step, SLOTS, AHEAD)

        edge_passes(env, 1, [z[:, :, :]], one_pass, s_gat,
                    s_es + [s_ix, s_T, s_esT, s_F, s_h, s_W, s_msg, s_oh, s_acc, s_us, s_flip, s_add])


def back1_loads(env, sp):
    a, s_w = env["a"], env["s_b1w"]
    sc_w, lin2, w1011 = env["b1_sc"], env["b1_lin2"], env["b1_w1011"]
    for r in range(2):
        for i, n in enumerate(("L1_gnn_lin2_w10", "L1_gnn_lin2_w11")):
            sp.dma_start(w1011[64 * r:64 * r + 64, i, :], a[n]).then_inc(s_w, 16)
    sp.dma_start(sc_w[0:64, 0, 0:64], a["L1_gnn_sc_w0"]).then_inc(s_w, 16)
    sp.dma_start(lin2[0:64, 0, 0:64], a["L1_gnn_lin2_w00"]).then_inc(s_w, 16)
    sp.dma_start(lin2[64:128, 3, 0:64], a["L1_gnn_lin2_w01"]).then_inc(s_w, 16)
    for k, p, c, u, n in vector_rows():
        sp.dma_start(sc_w[p:p + 3 * (n - 1) + 1:3, k, 64 + c:64 + 3 * 63 + c + 1:3],
                     a["L1_gnn_sc_w1"][u:u + n, :]).then_inc(s_w, 16)


def back1(env, z):
    nc, a, sem, ident, stats, attr = (env[k] for k in ("nc", "a", "sem", "ident", "stats", "attr"))
    cv = env["chunk_view"]
    x2_v, xn_v, out_v = cv(env["x_d"][1]), cv(env["xn3"]), cv(env["out"])
    wsel = env["wsel"]
    INV2 = 128.0 ** -0.5
    with ExitStack() as ctx:
        sb = lambda n, s, d=F32: ctx.enter_context(nc.sbuf_tensor("b1_" + n, s, d))
        pb = lambda n, s: ctx.enter_context(nc.psum_tensor("b1_" + n, s, F32))
        sc_w, lin2, w1011 = env["b1_sc"], env["b1_lin2"], env["b1_w1011"]
        bout = sb("bout", [R, C])
        wr = sb("wr", [R, C])
        br = sb("br", [R, 1])
        xt = sb("xt", [R, 2, 2, C])
        xnT = sb("xnT", [128, 2, 2, CH])
        zs = sb("zs", [128, 2, 4, CH])
        ga = sb("ga", [R, 2, C])
        ya = sb("ya", [R, 2, C])
        x3 = sb("x3", [R, 2, C])
        yy = sb("yy", [R, 2, 2, C])
        xn = sb("xn", [R, 2, 2, C])
        pr = sb("pr", [R, 2, C])
        bn, mv, ve, rn, mhalf = (sb("bn", [R, 2, 6]), sb("mv", [R, 2, 2]), sb("ve", [R, 2]), sb("rn", [R, 2, 2]),
                                 sb("mhalf", [R, 2]))
        pA, pB = pb("pA", [R, 2, 512]), pb("pB", [R, 2, 512])
        s_w = sem("b1_weights")
        s_ld = [sem("b1_load0"), sem("b1_load1")]
        s_st = [sem("b1_store0"), sem("b1_store1")]
        s_zs, s_A, s_ga, s_Br, s_var, s_rstd, s_xn, s_y = (
            sem("b1_" + n) for n in ("zs", "A", "gated", "read", "var", "rstd", "xn", "y"))
        vec = lambda t, k: t[:, k, 64:256].rearrange("p (v c) -> p v c", c=3)

        with nc.Block() as block:
            @block.gpsimd
            def _(pool):
                nc.gpsimd.memset(mhalf[:, :], -0.5)
                pool.drain()

            @block.sync
            def _(sp):
                sp.dma_start(bout[:, :], row_bc(a["L1_mix_bout"], R)).then_inc(s_w, 16)
                sp.dma_start(wr[:, :], a["L1_ffn_wr"].rearrange("k o -> o k").broadcast_to([R, C])).then_inc(s_w, 16)
                sp.dma_start(br[:, :], a["L1_ffn_br"].rearrange("(o n) -> o n", o=1).broadcast_to([R, 1])).then_inc(s_w, 16)
                sp.wait_ge(s_w, 48)

            @block.vector
            def _(v):
                v.wait_ge(env["s_b1w"], 16 * (7 + len(vector_rows())))
                for (b, p), w, c in zip(((0, 64), (1, 0), (1, 64), (2, 0), (2, 64), (3, 0)), (1, 1, 1, 0, 0, 0),
                                        (0, 1, 2) * 2):
                    nc.vector.tensor_copy(vec(lin2, b)[p:p + 64, :, c], w1011[p:p + 64, w, :])
                v.drain()
                nc.vector.tensor_scalar(sc_w[:, :, :], sc_w[:, :, :], SIN8 / 8.0, None, ALU.mult)
                nc.vector.tensor_scalar(lin2[:, :, :], lin2[:, :, :], COS8 * INV2 * 20.0 ** -0.5, None, ALU.mult)
                v.drain()
                nc.vector.tensor_scalar(lin2[64:128, 3, :], lin2[64:128, 3, :], INV_SQRT3, None, ALU.mult)
                v.drain()

        with nc.Block() as block:
            @block.sync
            def _(sp):
                def load(u, s):
                    rows_dma(sp, xt[:, s, :, :], x2_v[u], s_ld[s])
                    sp.dma_start(xnT[:, s, :, :], env["xnT_d"][2][:, :, bass.ds(u * CH, CH)]).then_inc(s_ld[s], 16)

                def store(u, s):
                    sp.wait_ge(s_y, u + 1)
                    rows_dma(sp, out_v[u], yy[:, s, :, :], s_st[s])
                    rows_dma(sp, xn_v[u], xn[:, s, :, :], s_st[s])

                def step(u, s, lo, hi):
                    if lo >= 2:
                        sp.wait_ge(s_Br, u - 1)
                        sp.wait_ge(s_A, u - 1)
                    load(u, s)
                    if lo >= 2:
                        store(u - 2, s)
                sweep(sp, CHUNKS, step)
                for u in (CHUNKS - 2, CHUNKS - 1):
                    store(u, u % 2)
                for i in range(2):
                    sp.wait_ge(s_st[i], 64 * ((CHUNKS + 1 - i) // 2))

            @block.gpsimd
            def _(pool):
                def step(u, s, lo, hi):
                    hold(pool, s_var, u + 1)
                    nc.gpsimd.tensor_tensor(out=rn[:, :, 0], in0=ve[:, :], in1=mhalf[:, :], op=ALU.pow)\
                      .then_inc(s_rstd, 1)
                sweep(pool, CHUNKS, step)

            @block.scalar
            def _(act):
                def pick(u, s, lo):
                    if lo >= 2:
                        hold(act, s_A, u - 1)
                    nc.scalar.copy(zs[:, s, :, :], z[:, :, bass.ds(u * CH, CH)]).then_inc(s_zs, 1)

                def step(u, s, lo, hi):
                    if lo == 0:
                        pick(0, 0, 0)
                    if hi <= CHUNKS - 2:
                        pick(u + 1, 1 - s, lo + 1)
                    if lo >= 1:
                        hold(act, s_Br, u)
                    hold(act, s_A, u + 1)
                    for t in range(2):
                        last = nc.scalar.activation(ga[:, t, :], pA[:, s, t * C:t * C + C], ACT.Copy,
                                                    scale=attr[:, bass.ds(u * 2 + t, 1)])
                    last.then_inc(s_ga, 1)
                sweep(act, CHUNKS, step)

            @block.vector
            def _(v):
                def step(u, s, lo, hi):
                    v.wait_ge(s_ld[s], (u // 2 + 1) * 48)
                    nc.vector.tensor_tensor(out=ya[:, :, :], in0=xt[:, s, :, :],
                                            in1=bout[:, :].unsqueeze(1).broadcast_to([R, 2, C]), op=ALU.add)
                    v.wait_ge(s_ga, u + 1)
                    nc.vector.tensor_tensor(out=x3[:, :, :], in0=ga[:, :, :],
                                            in1=pB[:, s, :].rearrange("p (t c) -> p t c", t=2), op=ALU.add)
                    v.drain()
                    nc.vector.tensor_tensor(out=x3[:, :, :], in0=x3[:, :, :], in1=ya[:, :, :], op=ALU.add)
                    v.drain().then_inc(s_Br, 1)
                    ln_stats(nc, v, x3, bn, mv, ve, s_var)
                    v.wait_ge(s_rstd, u + 1)
                    if lo >= 2:
                        v.wait_ge(s_st[s], (u // 2) * 64)
                    ln_apply(nc, v, xn[:, s, :, :], x3, mv, rn)
                    v.drain().then_inc(s_xn, 1)
                    nc.vector.tensor_tensor(out=yy[:, s, :, :], in0=x3[:, :, :], in1=xn[:, s, :, :], op=ALU.add)\
                      .then_inc(s_y, 1)
                    nc.vector.tensor_tensor(out=pr[:, :, :], in0=xn[:, s, :, :],
                                            in1=wr[:, :].unsqueeze(1).broadcast_to([R, 2, C]), op=ALU.mult)
                    v.drain()
                    nc.vector.tensor_reduce(wsel[:, bass.ds(u * 2, 2)], pr[:, :, :], AX.X, ALU.add)
                    v.drain()
                    if lo == CHUNKS - 1:
                        nc.vector.tensor_scalar(wsel[:, :], wsel[:, :], br[:, 0:1], None, ALU.add)
                        v.drain()
                sweep(v, CHUNKS, step)

            @block.tensor
            def _(pe):
                def products(u, s, lo):
                    pe.wait_ge(s_zs, u + 1)
                    pe.wait_ge(s_ld[s], (u // 2 + 1) * 48)
                    if lo >= 2:
                        pe.wait_ge(s_Br, u - 1)
                    for t in range(2):
                        tt = slice(t * R, t * R + R)
                        for k in range(2):
                            nc.tensor.matmul(pA[:, s, t * C:t * C + C], xnT[:, s, k, tt], sc_w[:, k, :],
                                             start=k == 0, stop=False)
                        for b in range(4):
                            nc.tensor.matmul(pA[:, s, t * C:t * C + C], zs[:, s, b, tt], lin2[:, b, :],
                                             start=False, stop=b == 3)
                        for k in range(2):
                            last = nc.tensor.matmul(pB[:, s, t * C:t * C + C], xnT[:, s, k, tt], env["g1"][:, k, :],
                                                    start=k == 0, stop=k == 1)
                    last.then_inc(s_A, 1)

                def step(u, s, lo, hi):
                    products(u, s, lo)
                sweep(pe, CHUNKS, step)


def ffn1(env):
    nc, a, sem, ident, ones, wsel = (env[k] for k in ("nc", "a", "sem", "ident", "ones", "wsel"))
    NF = F1 // 128
    LADDER = 15
    ROUNDS = 8
    CT = KEPT // R
    UNITS = -(-CT // 2)
    AT = 10
    tiles = lambda lo: 1 if lo == UNITS - 1 else 2
    with ExitStack() as ctx:
        sb = lambda n, s, d=F32: ctx.enter_context(nc.sbuf_tensor("o_" + n, s, d))
        pb = lambda n, s: ctx.enter_context(nc.psum_tensor("o_" + n, s, F32))
        w1 = sb("w1", [128, 2, F1])
        w2 = sb("w2", [128, NF, C])
        b1 = sb("b1", [128, NF])
        b2 = sb("b2", [R, C])
        before = sb("before", [R, R])
        rungI, rung = sb("rung_i", [R, LADDER], I32), sb("rung", [R, LADDER])
        wz = sb("wz", [R, TILES])
        half = sb("half", [R, TILES, 2])
        neg, flip, off = sb("neg", [R, TILES]), sb("flip", [R, TILES]), sb("off", [R, 2, TILES])
        key = sb("key", [R, 2, TILES])
        low = sb("low", [R, TILES])
        above, same = sb("above", [R, TILES]), sb("same", [R, TILES])
        thr, hit = sb("thr", [R, LADDER]), sb("hit", [R, LADDER])
        cmp_ = sb("cmp", [R, LADDER, TILES])
        cnt = sb("cnt", [R, LADDER])
        digit, base = sb("digit", [R, 1]), sb("found", [R, 2])
        last_ = sb("last", [R, 1 + TILES])
        scan = sb("scan", [R, 2, TILES])
        room = sb("room", [R, 1])
        sel = sb("sel", [R, TILES])
        coef = sb("coef", [R, TILES])
        cpart, crest = sb("cpart", [R, 3, TILES], BF16), sb("crest", [R, 2, TILES])
        pos, tile_no, place = sb("pos", [R, TILES]), sb("tile_no", [R, TILES]), sb("place", [R, TILES])
        stepI, steps = sb("steps_i", [R, CT + 1], I32), sb("steps", [R, CT + 1])
        colI, col = sb("col_i", [R, R], I32), sb("col", [R, R])
        tI, tF = sb("t_i", [R, TILES], I32), sb("t_f", [R, TILES])
        pI, pF = sb("p_i", [R, 1], I32), sb("p_f", [R, 1])
        ge = sb("ge", [R, TILES, CT + 1])
        oneB = sb("oneB", [R, TILES, CT])
        rhs = sb("rhs", [R, TILES, 5, CT], BF16)
        oneA = sb("oneA", [R, 2, AT, R], BF16)
        cidx, cI = sb("cidx", [R, CT]), sb("c_i", [R, CT], I32)
        cw = sb("cw", [R, 3, CT])
        ix = sb("ix", [R, 4, 2], I32)
        xg = sb("xg", [R, 4, 2, C])
        yg = sb("yg", [R, 4, 2, C])
        xnT = sb("xnT", [128, 2, 2, CH])
        hT = sb("hT", [128, 2, NF, CH])
        yo = sb("yo", [R, 4, 2, C])
        ot = sb("ot", [R, 2, 2, C])
        pH, pO, pS = pb("pH", [128, NF // 2, 512]), pb("pO", [R, 2, 512]), pb("pS", [R, 512])
        pT = pb("pT", [128, 512])
        s_w, s_rung, s_cnt, s_tot, s_A, s_B = (sem("o_" + n) for n in ("weights", "rungs", "counts", "totals", "onehots",
                                                                      "gathered"))
        s_gat, s_sc = env["s_rows"][0:4], env["s_rows"][4:6]
        s_ix, s_T, s_xT, s_H, s_g, s_O, s_y, s_o = (
            sem("o_" + n) for n in ("ix", "T", "xT", "H", "gelu", "O", "y", "out"))

        def select(v):
            ts, tt, stt = nc.vector.tensor_scalar, nc.vector.tensor_tensor, nc.vector.scalar_tensor_tensor
            ts(wz[:, :], wsel[:, :], 0.0, None, ALU.add)
            v.drain()
            nc.vector.tensor_copy(half[:, :, :], wz[:, :].bitcast(U16).rearrange("p (t h) -> p t h", h=2))
            v.drain()
            ts(neg[:, :], half[:, :, 1], 32768.0, None, ALU.is_ge)
            v.drain()
            ts(flip[:, :], neg[:, :], -2.0, 1.0, ALU.mult, ALU.add)
            ts(off[:, 0, :], neg[:, :], 65535.0, None, ALU.mult)
            ts(off[:, 1, :], neg[:, :], 32767.0, 32768.0, ALU.mult, ALU.add)
            v.drain()
            for i in range(2):
                tt(out=key[:, i, :], in0=half[:, :, i], in1=flip[:, :], op=ALU.mult)
            v.drain()
            tt(out=key[:, :, :], in0=key[:, :, :], in1=off[:, :, :], op=ALU.add)
            nc.vector.memset(base[:, :], 0.0)
            v.wait_ge(s_rung, 1)
            nc.vector.tensor_copy(rung[:, :], rungI[:, :])
            v.drain()
            for n in range(ROUNDS):
                i, step = n // 4, float(16 ** (3 - n % 4))
                k = key[:, 1, :] if i == 0 else low[:, :]
                ts(thr[:, :], rung[:, :], step, base[:, i:i + 1], ALU.mult, ALU.add)
                v.drain()
                tt(out=cmp_[:, :, :], in0=k.unsqueeze(1).broadcast_to([R, LADDER, TILES]),
                   in1=thr[:, :].unsqueeze(2).broadcast_to([R, LADDER, TILES]), op=ALU.is_ge)
                v.drain()
                nc.vector.tensor_reduce(cnt[:, :], cmp_[:, :, :], AX.X, ALU.add)
                v.drain().then_inc(s_cnt, 1)
                v.wait_ge(s_tot, n + 1)
                ts(hit[:, :], pS[:, 0:LADDER], float(KEPT), 0.0, ALU.is_ge, ALU.add, accum_out=digit[:, :])
                v.drain()
                stt(out=base[:, i:i + 1], in0=digit[:, :], scalar=step, in1=base[:, i:i + 1], op0=ALU.mult, op1=ALU.add)
                v.drain()
                if n == 3:
                    ts(above[:, :], key[:, 1, :], base[:, 0:1], None, ALU.is_gt)
                    ts(same[:, :], key[:, 1, :], base[:, 0:1], None, ALU.is_equal)
                    v.drain()
                    stt(out=low[:, :], in0=key[:, 0, :], scalar=1.0, in1=same[:, :], op0=ALU.add, op1=ALU.mult)
                    v.drain()
                    stt(out=low[:, :], in0=above[:, :], scalar=70000.0, in1=low[:, :], op0=ALU.mult, op1=ALU.add)
                    v.drain()
                    ts(low[:, :], low[:, :], -1.0, None, ALU.add)
                    v.drain()
            ts(above[:, :], low[:, :], base[:, 1:2], 0.0, ALU.is_gt, ALU.add, accum_out=last_[:, 0:1])
            ts(last_[:, 1:1 + TILES], low[:, :], base[:, 1:2], None, ALU.is_equal)
            v.drain().then_inc(s_cnt, 1)
            v.wait_ge(s_tot, ROUNDS + 1)
            ts(room[:, :], pS[:, 0:1], -1.0, float(KEPT), ALU.mult, ALU.add)
            q = before_each(v)
            stt(out=same[:, :], in0=scan[:, q, :], scalar=room[:, 0:1], in1=last_[:, 1:1 + TILES],
                op0=ALU.is_lt, op1=ALU.mult)
            v.drain()
            tt(out=sel[:, :], in0=same[:, :], in1=above[:, :], op=ALU.add)
            ts(room[:, :], room[:, :], -1.0, None, ALU.add)
            v.drain()
            stt(out=same[:, :], in0=scan[:, q, :], scalar=room[:, 0:1], in1=last_[:, 1:1 + TILES],
                op0=ALU.is_equal, op1=ALU.mult)
            v.drain()
            tt(out=coef[:, :], in0=sel[:, :], in1=same[:, :], op=ALU.subtract)
            nc.vector.tensor_copy(last_[:, 1:1 + TILES], sel[:, :])
            v.drain().then_inc(s_cnt, 1)
            tt(out=coef[:, :], in0=coef[:, :], in1=wsel[:, :], op=ALU.mult)
            v.drain()
            rest = coef[:, :]
            for i in range(3):
                nc.vector.tensor_copy(cpart[:, i, :], rest)
                v.drain()
                if i < 2:
                    tt(out=crest[:, i, :], in0=rest, in1=cpart[:, i, :], op=ALU.subtract)
                    v.drain()
                    rest = crest[:, i, :]
            v.wait_ge(s_rung, 2)
            for f, i in ((steps, stepI), (col, colI), (tF, tI), (pF, pI)):
                nc.vector.tensor_copy(f[:, :], i[:, :])
            v.wait_ge(s_tot, ROUNDS + 2)
            q = before_each(v)
            ts(pos[:, :], sel[:, :], -9999.0, 9999.0, ALU.mult, ALU.add)
            v.drain()
            tt(out=pos[:, :], in0=pos[:, :], in1=scan[:, q, :], op=ALU.add)
            v.drain()
            tt(out=ge[:, :, :], in0=pos[:, :].unsqueeze(2).broadcast_to([R, TILES, CT + 1]),
               in1=steps[:, :].unsqueeze(1).broadcast_to([R, TILES, CT + 1]), op=ALU.is_ge)
            v.drain()
            nc.vector.tensor_reduce(tile_no[:, :], ge[:, :, 1:CT + 1], AX.X, ALU.add)
            tt(out=oneB[:, :, :], in0=ge[:, :, 0:CT], in1=ge[:, :, 1:CT + 1], op=ALU.subtract)
            v.drain()
            stt(out=place[:, :], in0=tile_no[:, :], scalar=-float(R), in1=pos[:, :], op0=ALU.mult, op1=ALU.add)
            ts(rhs[:, :, 1, :], oneB[:, :, :], pF[:, 0:1], None, ALU.mult)
            for i, by in ((0, tF[:, :]), (2, cpart[:, 0, :]), (3, cpart[:, 1, :]), (4, cpart[:, 2, :])):
                tt(out=rhs[:, :, i, :], in0=oneB[:, :, :], in1=by.unsqueeze(2).broadcast_to([R, TILES, CT]), op=ALU.mult)
            v.drain()
            for b in range(TILES // AT):
                if b >= 2:
                    v.wait_ge(s_B, b - 1)
                tt(out=oneA[:, b % 2, :, :], in0=place[:, b * AT:(b + 1) * AT].unsqueeze(2).broadcast_to([R, AT, R]),
                   in1=col[:, :].unsqueeze(1).broadcast_to([R, AT, R]), op=ALU.is_equal).then_inc(s_A, 1)
            v.wait_ge(s_B, TILES // AT)
            nc.vector.tensor_copy(cw[:, 0:2, :], pS[:, 2 * CT:4 * CT].rearrange("p (i o) -> p i o", o=CT))
            nc.vector.tensor_copy(cidx[:, :], pS[:, CT:2 * CT])
            v.drain()
            stt(out=cI[:, :], in0=pS[:, 0:CT], scalar=float(R), in1=cidx[:, :], op0=ALU.mult, op1=ALU.add)
            tt(out=cw[:, 2, :], in0=cw[:, 0, :], in1=cw[:, 1, :], op=ALU.add)
            v.drain()
            tt(out=cw[:, 0, :], in0=cw[:, 2, :], in1=pS[:, 4 * CT:5 * CT], op=ALU.add)
            v.drain()

        def before_each(v):
            nc.vector.memset(scan[:, 0, 0:1], 0.0)
            nc.vector.tensor_copy(scan[:, 0, 1:TILES], pS[:, 1:TILES])
            v.drain()
            d, q = 1, 0
            while d < TILES:
                nc.vector.tensor_copy(scan[:, 1 - q, 0:d], scan[:, q, 0:d])
                nc.vector.tensor_tensor(out=scan[:, 1 - q, d:TILES], in0=scan[:, q, d:TILES],
                                        in1=scan[:, q, 0:TILES - d], op=ALU.add)
                v.drain()
                d, q = 2 * d, 1 - q
            nc.vector.tensor_tensor(out=scan[:, 1 - q, :], in0=scan[:, q, :], in1=pS[:, 64:64 + TILES], op=ALU.add)
            v.drain()
            return 1 - q

        with nc.Block() as block:
            @block.sync
            def _(sp):
                sp.dma_start(w1[:, :, :], a["L1_ffn_w1"].rearrange("(k p) f -> p k f", p=128)).then_inc(s_w, 16)
                sp.dma_start(b1[:, :], a["L1_ffn_b1"].rearrange("(f p) -> p f", p=128)).then_inc(s_w, 16)
                sp.dma_start(w2[:, :, :], a["L1_ffn_w2"].rearrange("(f p) n -> p f n", p=128)).then_inc(s_w, 16)
                sp.dma_start(b2[:, :], row_bc(a["L1_ffn_b2"], R)).then_inc(s_w, 16)
                sp.wait_ge(s_w, 64)

            @block.gpsimd
            def _(pool):
                nc.gpsimd.iota(rungI[:, :], pattern=[[1, LADDER]], base=1, channel_multiplier=0).then_inc(s_rung, 1)
                nc.gpsimd.iota(stepI[:, :], pattern=[[R, CT + 1]], base=0, channel_multiplier=0)
                nc.gpsimd.iota(colI[:, :], pattern=[[1, R]], base=0, channel_multiplier=0)
                nc.gpsimd.iota(tI[:, :], pattern=[[1, TILES]], base=0, channel_multiplier=0)
                nc.gpsimd.iota(pI[:, :], pattern=[[1, 1]], base=0, channel_multiplier=1)
                nc.gpsimd.memset(before[:, :], 1.0)
                pool.drain()
                nc.gpsimd.affine_select(out=before[:, :], in_=before[:, :], compare_op=ALU.is_gt, fill=0.0, base=0,
                                        pattern=[[1, R]], channel_multiplier=-1)
                pool.drain().then_inc(s_rung, 1)

            @block.tensor
            def _(pe):
                for n in range(ROUNDS):
                    pe.wait_ge(s_cnt, n + 1)
                    nc.tensor.matmul(pS[:, 0:LADDER], ones[0:R, 0:R], cnt[:, :], start=True, stop=True).then_inc(s_tot, 1)
                pe.wait_ge(s_rung, 2)
                for n in range(2):
                    pe.wait_ge(s_cnt, ROUNDS + n + 1)
                    nc.tensor.matmul(pS[:, 0:1 + TILES], ones[0:R, 0:R], last_[:, :], start=True, stop=True)
                    nc.tensor.matmul(pS[:, 64:64 + TILES], before[:, :], last_[:, 1:1 + TILES], start=True, stop=True)\
                      .then_inc(s_tot, 1)
                for b in range(TILES // AT):
                    pe.wait_ge(s_A, b + 1)
                    for i in range(AT):
                        t = b * AT + i
                        last = nc.tensor.matmul(pS[:, 0:5 * CT], oneA[:, b % 2, i, :],
                                                rhs[:, t, :, :].rearrange("p i o -> p (i o)"), start=t == 0,
                                                stop=t == TILES - 1)
                    last.then_inc(s_B, 1)

            @block.vector
            def _(v):
                select(v)

        with nc.Block() as block:
            @block.gpsimd
            def _(pool):
                offset = lambda s, t: bass.IndirectOffsetOnAxis(ap=ix[:, s, t:t + 1], axis=0)

                def gather(u, s, lo):
                    hold(pool, s_ix, u + 1)
                    for t in range(tiles(lo)):
                        for rows, table in ((xg, env["xn3"]), (yg, env["out"])):
                            nc.gpsimd.indirect_dma_start(out=rows[:, s, t, :], out_offset=None, in_=table,
                                                         in_offset=offset(s, t)).then_inc(s_gat[s], 16)

                def scatter(u, s, lo):
                    hold(pool, s_o, u + 1)
                    for t in range(tiles(lo)):
                        nc.gpsimd.indirect_dma_start(out=env["out"], out_offset=offset(s, t), in_=ot[:, s % 2, t, :],
                                                     in_offset=None).then_inc(s_sc[s % 2], 16)

                def step(u, s, lo, hi):
                    gather(u, s, lo)
                    if lo >= 3:
                        scatter(u - 3, (s + 1) % 4, lo - 3)
                sweep(pool, UNITS, step, 4)
                for u in range(UNITS - 3, UNITS):
                    scatter(u, u % 4, u)
                for i in range(2):
                    pool.wait_ge(s_sc[i], 16 * sum(tiles(u) for u in range(i, UNITS, 2)))

            @block.scalar
            def _(act):
                def inputs(u, s, lo):
                    if lo >= 2:
                        hold(act, s_H, (u - 1) * (NF // 2))
                    hold(act, s_T, u + 1)
                    n = R * tiles(lo)
                    nc.scalar.copy(xnT[:, s % 2, :, 0:n],
                                   pT[:, 0:2 * CH].rearrange("p (k n) -> p k n", k=2)[:, :, 0:n]).then_inc(s_xT, 1)

                def copied(u, s, lo):
                    if lo >= 4:
                        hold(act, s_o, u - 3)
                    hold(act, s_O, u + 1)
                    n = C * tiles(lo)
                    nc.scalar.copy(yo[:, s, :, :].rearrange("p t c -> p (t c)")[:, 0:n], pO[:, s % 2, 0:n])\
                      .then_inc(s_y, 1)

                def step(u, s, lo, hi):
                    if lo == 0:
                        inputs(0, 0, 0)
                    for f in range(NF):
                        if f % 2 == 0:
                            hold(act, s_H, NF // 2 * u + f // 2 + 1)
                        n = R * tiles(lo)
                        x = nc.scalar.activation(hT[:, s % 2, f, 0:n], pH[:, f // 2, (f % 2) * CH:(f % 2) * CH + n],
                                                 ACT.Gelu_apprx_tanh, bias=b1[:, f:f + 1])
                        if f % 2:
                            x.then_inc(s_g, 1)
                    if hi <= UNITS - 2:
                        inputs(u + 1, (s + 1) % 4, lo + 1)
                    if lo >= 1:
                        copied(u - 1, (s - 1) % 4, lo - 1)
                    if lo == UNITS - 1:
                        copied(u, s, lo)
                sweep(act, UNITS, step, 4)

            @block.tensor
            def _(pe):
                def turn(u, s, lo):
                    if lo >= 1:
                        pe.wait_ge(s_xT, u)
                    hold(pe, s_gat[s], (u // 4) * 64 + 32 * tiles(lo))
                    for k in range(2):
                        for t in range(tiles(lo)):
                            last = nc.tensor.transpose(pT[:, k * CH + t * R:k * CH + t * R + R],
                                                       xg[:, s, t, 128 * k:128 * k + 128], ident[0:R, 0:R])
                    last.then_inc(s_T, 1)

                def hidden(u, s, lo):
                    pe.wait_ge(s_xT, u + 1)
                    n = R * tiles(lo)
                    for f in range(NF):
                        if f % 2 == 0 and lo >= 1:
                            pe.wait_ge(s_g, NF // 2 * (u - 1) + f // 2 + 1)
                        for k in range(2):
                            last = nc.tensor.matmul(pH[:, f // 2, (f % 2) * CH:(f % 2) * CH + n],
                                                    w1[:, k, 128 * f:128 * f + 128], xnT[:, s % 2, k, 0:n],
                                                    start=k == 0, stop=k == 1)
                        if f % 2:
                            last.then_inc(s_H, 1)

                def step(u, s, lo, hi):
                    if lo == 0:
                        turn(0, 0, 0)
                        turn(1, 1, 1)
                        hidden(0, 0, 0)
                    if hi <= UNITS - 2:
                        hidden(u + 1, (s + 1) % 4, lo + 1)
                    if lo >= 2:
                        pe.wait_ge(s_y, u - 1)
                    for t in range(tiles(lo)):
                        for f in range(NF):
                            if t == 0 and f % 2 == 0:
                                pe.wait_ge(s_g, NF // 2 * u + f // 2 + 1)
                            last = nc.tensor.matmul(pO[:, s % 2, t * C:(t + 1) * C], hT[:, s % 2, f, t * R:t * R + R],
                                                    w2[:, f, :], start=f == 0, stop=f == NF - 1)
                        if t == 0 and hi <= UNITS - 3:
                            turn(u + 2, (s + 2) % 4, lo + 2)
                    last.then_inc(s_O, 1)
                sweep(pe, UNITS, step, 4, 2)

            @block.vector
            def _(v):
                def stage(u, s, lo):
                    if lo >= 4:
                        v.wait_ge(s_sc[s % 2], (u // 2 - 1) * 32)
                    n = tiles(lo)
                    nc.vector.tensor_copy(ix[:, s, 0:n], cI[:, bass.ds(u * 2, n)]).then_inc(s_ix, 1)

                def step(u, s, lo, hi):
                    if lo == 0:
                        for i in range(4):
                            stage(i, i, i)
                    n = tiles(lo)
                    y = yo[:, s, 0:n, :]
                    v.wait_ge(s_y, u + 1)
                    nc.vector.tensor_tensor(out=y, in0=y, in1=b2[:, :].unsqueeze(1).broadcast_to([R, n, C]), op=ALU.add)
                    v.drain()
                    nc.vector.tensor_tensor(out=y, in0=y, in1=cw[:, 0, bass.ds(u * 2, n)].unsqueeze(2)
                                            .broadcast_to([R, n, C]), op=ALU.mult)
                    v.drain()
                    if lo >= 2:
                        v.wait_ge(s_sc[s % 2], (u // 2) * 32)
                    v.wait_ge(s_gat[s], (u // 4) * 64 + 32 * n)
                    nc.vector.tensor_tensor(out=ot[:, s % 2, 0:n, :], in0=y, in1=yg[:, s, 0:n, :], op=ALU.add)\
                      .then_inc(s_o, 1)
                    if lo >= 1 and hi <= UNITS - 4:
                        stage(u + 3, (s + 3) % 4, lo + 3)
                sweep(v, UNITS, step, 4, 3)

        with nc.Block() as block:
            @block.gpsimd
            def _(pool):
                taken = [32 * sum(tiles(u) for u in range(i, UNITS, 4)) for i in range(4)]
                taken += [16 * sum(tiles(u) for u in range(i, UNITS, 2)) for i in range(2)]
                nc.gpsimd.inc_swdge_sem(env["s_rows"], taken, mode="sub")


@contextmanager
def phase(env):
    nc, used = env["nc"], []
    with ExitStack() as ctx:
        def sem(name):
            used.append(ctx.enter_context(nc.semaphore(name)))
            return used[-1]

        env["sem"] = sem
        yield
        with nc.Block() as block:
            @block.gpsimd
            def _(pool):
                for s in used:
                    pool.sem_clear(s)


def gps_kernel(nc, a, out):
    def dram(name, shape, dt=F32):
        return nc.dram_tensor(name, shape, dt).ap()

    def chunk_view(t):
        return t.rearrange("(u t p) c -> u p t c", t=2, p=R)

    with nc.allow_non_contiguous_dma(reason="bias columns and rows of a strided weight"), ExitStack() as ctx:
        sb = lambda n, s, d=F32: ctx.enter_context(nc.sbuf_tensor(n, s, d))
        env = dict(
            nc=nc, a=a, chunk_view=chunk_view, x_in=a["x"], out=out,
            tab0=dram("tab0", (N, TAB0)),
            dst_tab=dram("dst_tab", (NPAD, 24), BF16),
            tab1=dram("tab1", (N, C)),
            xnT_d=[dram(f"xnT{i}", (128, 2, N)) for i in range(3)],
            x_d=[dram(f"xres{i}", (N, C)) for i in range(2)],
            xn3=dram("xn3", (N, C)),
            gf_d=dram("group_range", (2, GROUPS)),
            ident=sb("ident", [128, 128]), ones=sb("ones", [128, 128]), zeros=sb("zeros", [1, 512]),
            stats=sb("stats", [R, TILES, 2]),
            spanI=sb("span", [1, 1], I32),
            g0=sb("mix0_g", [128, 2, C]), g0b=sb("mix0_b", [128, 2]), g1=sb("mix1_g", [128, 2, C]),
            pself=sb("pself", [R, TILES, H0]),
            x1sum=sb("x1sum", [128, 2]), attr=sb("node_attr", [R, TILES]), wsel=sb("wsel", [R, TILES]),
            srcI=sb("src", [R, ETILES], I32),
            dstRel=sb("dst_rel", [R, ETILES]),
            baseF=sb("base_f", [1, GROUPS]), baseI=sb("base", [1, GROUPS], I32),
            iotaI=sb("iota_i", [R, W], I32), iotaW=sb("iota", [R, W]))
        env["s_rows"] = [ctx.enter_context(nc.semaphore(f"edge_rows{i}")) for i in range(SLOTS)]
        ident, ones, zeros = env["ident"], env["ones"], env["zeros"]
        with phase(env):
            s_zero = env["sem"]("const_zeroed")
            with nc.Block() as block:
                @block.gpsimd
                def _(pool):
                    nc.gpsimd.memset(ident[:, :], 0.0).then_inc(s_zero, 1)
                    nc.gpsimd.memset(ones[:, :], 1.0)
                    nc.gpsimd.memset(zeros[:, :], 0.0)
                    pool.wait_ge(s_zero, 1)
                    nc.gpsimd.affine_select(out=ident[:, :], in_=ident[:, :], compare_op=ALU.not_equal, fill=1.0,
                                            base=0, pattern=[[-1, 128]], channel_multiplier=1)
                    pool.drain()
        with phase(env):
            edge_indices(env)
        with phase(env):
            front0(env)
        with ExitStack() as first:
            acc = first.enter_context(nc.sbuf_tensor("sum0", [128, 2, NPAD], F32))
            den = first.enter_context(nc.sbuf_tensor("den0", [H0, NPAD], F32))
            with phase(env):
                edges0(env, acc, den)
            with phase(env):
                back0(env, acc, den)
        with phase(env):
            ffn0(env)
        with phase(env):
            front1(env)
        with ExitStack() as second, phase(env):
            env["s_b1w"] = env["sem"]("b1_weights_early")
            z = second.enter_context(nc.sbuf_tensor("sum1", [128, 4, NPAD], F32))
            for name, shape in (("b1_sc", [128, 2, C]), ("b1_lin2", [128, 4, C]), ("b1_w1011", [128, 2, 64])):
                env[name] = second.enter_context(nc.sbuf_tensor(name, shape, F32))
            with ExitStack() as attrs:
                ea = attrs.enter_context(nc.sbuf_tensor("edge_attr", [R, ETILES, 4], F32))
                with phase(env):
                    edge_attrs(env, ea)
                with phase(env):
                    edges1(env, z, ea)
            with phase(env):
                back1(env, z)
        with phase(env):
            ffn1(env)


def kernel(**inputs):
    import numpy as np
    import concourse.bacc as bacc
    from concourse.bass_utils import run_bass_kernel_spmd

    nc = bacc.Bacc("TRN2", target_bir_lowering=False, num_devices=1)
    arrays, aps = {}, {}
    for name, value in inputs.items():
        if name == "L1_ffn_attention_mask":
            continue
        value = np.ascontiguousarray(value)
        arrays["in_" + name] = value
        aps[name] = nc.dram_tensor("in_" + name, value.shape, mybir.dt.from_np(value.dtype), kind="ExternalInput").ap()
    out = nc.dram_tensor("out_nodes", (N, C), F32, kind="ExternalOutput").ap()
    gps_kernel(nc, aps, out)
    result = run_bass_kernel_spmd(nc, [arrays], core_ids=[0])
    return result.results[0]["out_nodes"]
```
